# Optimizing a Trainium2 kernel written in Bass

```python
import numpy as np
import jax
import jax.numpy as jnp

def _softmax(x, axis=-1):
    return jax.nn.softmax(x, axis=axis)

def _gelu(x):
    return jax.nn.gelu(x, approximate=True)

def _silu(x):
    return jax.nn.silu(x)

def _sigmoid(x):
    return jax.nn.sigmoid(x)

def _layernorm(x, axis=-1, eps=1e-05):
    m = jnp.mean(x, axis=axis, keepdims=True)
    v = jnp.var(x, axis=axis, keepdims=True)
    return (x - m) / jnp.sqrt(v + eps)

def _scatter_add(tgt, idx, src, axis=0):
    return tgt.at[idx].add(src)

def _segment_sum(src, seg, n):
    return jax.ops.segment_sum(src, seg, n)
kernel_name = 'mk_perceiver_d2_seqx_r4_3895b4'

def setup_inputs(seed: int=0):
    np.random.seed(seed)
    _w = jnp.asarray

    def _rec_inputs():
        import jax
        import jax.numpy as jnp
        _rk = jax.random.key(seed)
        x = -0.0003929 + 0.9999 * jax.random.normal(jax.random.fold_in(_rk, 1), (64, 32, 256), jnp.float32)
        _lenS = 32 - jax.random.randint(jax.random.fold_in(_rk, 7), (64,), 0, max(1, 32 // 4) + 1, jnp.int32)
        _lenS2 = 257 - jax.random.randint(jax.random.fold_in(_rk, 8), (64,), 0, max(1, 257 // 4) + 1, jnp.int32)
        _ctx_1024P = jax.random.normal(jax.random.fold_in(_rk, 11), (64, 16, 256), jnp.float32)
        _ctx_1024c = jax.random.dirichlet(jax.random.fold_in(_rk, 511), 0.3 * jnp.ones((16,), jnp.float32), (64, 257))
        _ctx_1024t = jnp.einsum('bsk,bkd->bsd', _ctx_1024c, _ctx_1024P)
        _ctx_1024t = _ctx_1024t * jax.lax.rsqrt(jnp.mean(jnp.square(_ctx_1024t)) + 1e-12) * 0.953939
        ctx_1024 = 2.81802e-05 + 1.00001 * (_ctx_1024t + 0.3 * jax.random.normal(jax.random.fold_in(_rk, 611), (64, 257, 256), jnp.float32))
        _validS = jnp.arange(32)[None, :] < _lenS[:, None]
        _validS2 = jnp.arange(257)[None, :] < _lenS2[:, None]
        _causal = jnp.tril(jnp.ones((32, 32), dtype=bool))
        mask_SxS2_ik1 = jnp.where(jnp.broadcast_to(_validS2[0:1, :], (32, 257)), 1, 0).astype(jnp.int32)
        return (x, ctx_1024, mask_SxS2_ik1)
    x, ctx_1024, mask_SxS2_ik1 = _rec_inputs()

    def _L0_xattn_setup():
        import jax, jax.numpy as jnp
        import numpy as np
        B, N, M, D_MODEL, D_K, D_V = (8, 512, 512, 256, 256, 256)
        NEG = -1000000000.0
        key = jax.random.key(seed)
        ks = jax.random.split(key, 10)
        s = 1.0 / np.sqrt(D_MODEL)
        return {'querys': jax.random.normal(ks[0], (B, N, D_MODEL), jnp.float32), 'keys': jax.random.normal(ks[1], (B, M, D_MODEL), jnp.float32), 'values': jax.random.normal(ks[2], (B, M, D_MODEL), jnp.float32), 'mask': jax.random.randint(ks[3], (N, M), 0, 2, jnp.int32), 'Wq': jax.random.normal(ks[4], (D_K, D_MODEL), jnp.float32) * s, 'bq': jnp.zeros((D_K,), jnp.float32), 'Wk': jax.random.normal(ks[5], (D_K, D_MODEL), jnp.float32) * s, 'bk': jnp.zeros((D_K,), jnp.float32), 'Wv': jax.random.normal(ks[6], (D_V, D_MODEL), jnp.float32) * s, 'bv': jnp.zeros((D_V,), jnp.float32)}
    _L0_xattn_all = _L0_xattn_setup()
    _L0_xattn_in = {k: v for k, v in _L0_xattn_all.items() if k in ('Wq', 'bq', 'Wk', 'bk', 'Wv', 'bv')}
    del _L0_xattn_all

    def _L0_attn_setup():
        import jax, jax.numpy as jnp
        import numpy as np
        B, T, C = (8, 512, 256)
        HID = 4 * C
        EPS = 1e-05

        def layernorm(x, g, b):
            m = jnp.mean(x, axis=-1, keepdims=True)
            v = jnp.mean(jnp.square(x - m), axis=-1, keepdims=True)
            return (x - m) * jax.lax.rsqrt(v + EPS) * g + b

        def time_shift(x):
            return jnp.concatenate([jnp.zeros_like(x[:, :1]), x[:, :-1]], axis=1)

        def wkv(time_decay, time_first, k, v):
            w = -jnp.exp(time_decay)
            u = time_first
            kT = jnp.swapaxes(k, 0, 1)
            vT = jnp.swapaxes(v, 0, 1)

            def step(carry, kv):
                aa, bb, pp = carry
                kt, vt = kv
                ww = u + kt
                p = jnp.maximum(pp, ww)
                e1 = jnp.exp(pp - p)
                e2 = jnp.exp(ww - p)
                y = (e1 * aa + e2 * vt) / (e1 * bb + e2)
                ww2 = pp + w
                p2 = jnp.maximum(ww2, kt)
                e1b = jnp.exp(ww2 - p2)
                e2b = jnp.exp(kt - p2)
                return ((e1b * aa + e2b * vt, e1b * bb + e2b, p2), y)
            init = (jnp.zeros((k.shape[0], k.shape[2]), k.dtype), jnp.zeros((k.shape[0], k.shape[2]), k.dtype), jnp.full((k.shape[0], k.shape[2]), -1e+38, k.dtype))
            _, ys = jax.lax.scan(step, init, (kT, vT))
            return jnp.swapaxes(ys, 0, 1)
        key = jax.random.key(seed)
        ks = jax.random.split(key, 24)
        s = 0.02
        d = {'x': jax.random.normal(ks[0], (B, T, C), jnp.float32), 'ln1_g': jnp.ones((C,), jnp.float32), 'ln1_b': jnp.zeros((C,), jnp.float32), 'ln2_g': jnp.ones((C,), jnp.float32), 'ln2_b': jnp.zeros((C,), jnp.float32), 'time_decay': jax.random.normal(ks[1], (C,), jnp.float32) - 2.0, 'time_first': jax.random.normal(ks[2], (C,), jnp.float32) * 0.5 + np.log(0.3).astype(np.float32), 'tm_k': jax.random.uniform(ks[3], (1, 1, C), jnp.float32), 'tm_v': jax.random.uniform(ks[4], (1, 1, C), jnp.float32), 'tm_r': jax.random.uniform(ks[5], (1, 1, C), jnp.float32), 'Wk': jax.random.normal(ks[6], (C, C), jnp.float32) * s, 'Wv': jax.random.normal(ks[7], (C, C), jnp.float32) * s, 'Wr': jax.random.normal(ks[8], (C, C), jnp.float32) * s, 'Wo': jax.random.normal(ks[9], (C, C), jnp.float32) * s, 'cm_k': jax.random.uniform(ks[10], (1, 1, C), jnp.float32), 'cm_r': jax.random.uniform(ks[11], (1, 1, C), jnp.float32), 'Wck': jax.random.normal(ks[12], (HID, C), jnp.float32) * s, 'Wcr': jax.random.normal(ks[13], (C, C), jnp.float32) * s, 'Wcv': jax.random.normal(ks[14], (C, HID), jnp.float32) * s}
        return d
    _L0_attn_all = _L0_attn_setup()
    _L0_attn_in = {k: v for k, v in _L0_attn_all.items() if k in ('ln1_g', 'ln1_b', 'ln2_g', 'ln2_b', 'time_decay', 'time_first', 'tm_k', 'tm_v', 'tm_r', 'Wk', 'Wv', 'Wr', 'Wo', 'cm_k', 'cm_r', 'Wck', 'Wcr', 'Wcv')}
    del _L0_attn_all

    def _L0_ffn_setup():
        import jax, jax.numpy as jnp
        import numpy as np
        TOP_K = 2
        key = jax.random.key(seed)
        k1, k2, k3 = jax.random.split(key, 3)
        B, S, H, E = (4, 512, 256, 8)
        hidden_states = jax.random.normal(k1, (B, S, H), dtype=jnp.float32)
        Wg = jax.random.normal(k2, (H, E), dtype=jnp.float32) * H ** (-0.5)
        We = jax.random.normal(k3, (E, H, H), dtype=jnp.float32) * H ** (-0.5)
        be = jnp.zeros((E, H), dtype=jnp.float32)
        return {'hidden_states': hidden_states, 'Wg': Wg, 'We': We, 'be': be}
    _L0_ffn_all = _L0_ffn_setup()
    _L0_ffn_in = {k: v for k, v in _L0_ffn_all.items() if k in ('Wg', 'We', 'be')}
    del _L0_ffn_all

    def _L1_xattn_setup():
        import jax, jax.numpy as jnp
        import numpy as np
        EMBED_DIM = 256
        Q_HEADS = 16
        KV_HEADS = 8
        HEAD_DIM = EMBED_DIM // Q_HEADS
        KV_EMBED = HEAD_DIM * KV_HEADS
        GROUPS = Q_HEADS // KV_HEADS
        LN_EPS = 1e-05
        RMS_EPS = 1e-06

        def _rms_norm(x):
            return x * jax.lax.rsqrt(jnp.mean(jnp.square(x), axis=-1, keepdims=True) + RMS_EPS)

        def _act_quant(x):
            scale = 127.0 / jnp.maximum(jnp.max(jnp.abs(x), axis=-1, keepdims=True), 1e-05)
            return jnp.clip(jnp.round(x * scale), -128.0, 127.0) / scale

        def _weight_quant(w):
            scale = 1.0 / jnp.maximum(jnp.mean(jnp.abs(w)), 1e-05)
            return jnp.clip(jnp.round(w * scale), -1.0, 1.0) / scale

        def _ste(a, q):
            return a + jax.lax.stop_gradient(q - a)

        def bit_linear(x, w):
            xn = _rms_norm(x)
            xq = _ste(xn, _act_quant(xn))
            wq = _ste(w, _weight_quant(w))
            return jnp.einsum('bni,oi->bno', xq, wq)
        key = jax.random.key(seed)
        ks = jax.random.split(key, 6)
        B, N, S, D = (16, 256, 64, EMBED_DIM)
        s = D ** (-0.5)
        return {'x': jax.random.normal(ks[0], (B, N, D), jnp.float32), 'y': jax.random.normal(ks[1], (B, S, D), jnp.float32), 'wq': jax.random.normal(ks[2], (D, D), jnp.float32) * s, 'wk': jax.random.normal(ks[3], (KV_EMBED, D), jnp.float32) * s, 'wv': jax.random.normal(ks[4], (KV_EMBED, D), jnp.float32) * s, 'wo': jax.random.normal(ks[5], (D, D), jnp.float32) * s, 'ln_gamma': jnp.ones((D,), jnp.float32), 'ln_beta': jnp.zeros((D,), jnp.float32)}
    _L1_xattn_all = _L1_xattn_setup()
    _L1_xattn_in = {k: v for k, v in _L1_xattn_all.items() if k in ('wq', 'wk', 'wv', 'wo', 'ln_gamma', 'ln_beta')}
    del _L1_xattn_all

    def _L1_attn_setup():
        import jax, jax.numpy as jnp
        from jax import lax
        import numpy as np
        D_MODEL, D_STATE, D_CONV, EXPAND = (256, 16, 4, 2)
        D_INNER = D_MODEL * EXPAND
        BATCH, SEQ = (2, 512)
        LN_EPS = 1e-05

        def _forward(x, in_proj_w, in_proj_b, conv_w, conv_b, x_proj_w, x_proj_b, A_log, D, out_proj_w, out_proj_b, ln_gamma, ln_beta):
            d_state = A_log.shape[1]
            d_conv = conv_w.shape[-1]
            residual = x
            xz = x @ in_proj_w.T + in_proj_b
            x_main, z = jnp.split(xz, 2, axis=-1)
            xc = jnp.transpose(x_main, (0, 2, 1))
            xc = lax.conv_general_dilated(xc, conv_w, window_strides=(1,), padding=[(d_conv - 1, 0)], dimension_numbers=('NCH', 'OIH', 'NCH'), feature_group_count=xc.shape[1])
            xc = xc + conv_b[None, :, None]
            xc = jax.nn.silu(jnp.transpose(xc, (0, 2, 1)))
            ssm = xc @ x_proj_w.T + x_proj_b
            B_param = ssm[..., :d_state]
            C_param = ssm[..., d_state:2 * d_state]
            delta = jax.nn.softplus(ssm[..., -1:])
            A = -jnp.exp(A_log)

            def step(h, ts):
                dt, B_t, C_t, x_t = ts
                dA = jnp.exp(A[None] * dt[:, :, None])
                dBx = dt[:, :, None] * B_t[:, None, :] * x_t[:, :, None]
                h = dA * h + dBx
                y = jnp.einsum('bdn,bn->bd', h, C_t) + D * x_t
                return (h, y)
            h0 = jnp.zeros((x.shape[0], xc.shape[-1], d_state), xc.dtype)
            xs = (jnp.swapaxes(delta, 0, 1), jnp.swapaxes(B_param, 0, 1), jnp.swapaxes(C_param, 0, 1), jnp.swapaxes(xc, 0, 1))
            _, ys = lax.scan(step, h0, xs)
            y = jnp.swapaxes(ys, 0, 1)
            y = y * jax.nn.silu(z)
            y = y @ out_proj_w.T + out_proj_b
            r = y + residual
            mu = jnp.mean(r, axis=-1, keepdims=True)
            var = jnp.mean(jnp.square(r - mu), axis=-1, keepdims=True)
            return (r - mu) * lax.rsqrt(var + LN_EPS) * ln_gamma + ln_beta
        key = jax.random.key(seed)
        ks = jax.random.split(key, 6)
        x = jax.random.normal(ks[0], (BATCH, SEQ, D_MODEL), dtype=jnp.float32)
        in_proj_w = jax.random.normal(ks[1], (2 * D_INNER, D_MODEL), dtype=jnp.float32) * 0.02
        in_proj_b = jnp.zeros((2 * D_INNER,), jnp.float32)
        conv_w = jax.random.normal(ks[2], (D_INNER, 1, D_CONV), dtype=jnp.float32) * 0.2
        conv_b = jnp.zeros((D_INNER,), jnp.float32)
        x_proj_w = jax.random.normal(ks[3], (2 * D_STATE + 1, D_INNER), dtype=jnp.float32) * 0.02
        x_proj_b = jnp.zeros((2 * D_STATE + 1,), jnp.float32)
        A_log = jnp.log(jnp.tile(jnp.arange(1, D_STATE + 1, dtype=jnp.float32)[None, :], (D_INNER, 1)))
        D = jnp.ones((D_INNER,), jnp.float32)
        out_proj_w = jax.random.normal(ks[4], (D_MODEL, D_INNER), dtype=jnp.float32) * 0.02
        out_proj_b = jnp.zeros((D_MODEL,), jnp.float32)
        ln_gamma = jnp.ones((D_MODEL,), jnp.float32)
        ln_beta = jnp.zeros((D_MODEL,), jnp.float32)
        return dict(x=x, in_proj_w=in_proj_w, in_proj_b=in_proj_b, conv_w=conv_w, conv_b=conv_b, x_proj_w=x_proj_w, x_proj_b=x_proj_b, A_log=A_log, D=D, out_proj_w=out_proj_w, out_proj_b=out_proj_b, ln_gamma=ln_gamma, ln_beta=ln_beta)
    _L1_attn_all = _L1_attn_setup()
    _L1_attn_in = {k: v for k, v in _L1_attn_all.items() if k in ('in_proj_w', 'in_proj_b', 'conv_w', 'conv_b', 'x_proj_w', 'x_proj_b', 'A_log', 'D', 'out_proj_w', 'out_proj_b', 'ln_gamma', 'ln_beta')}
    del _L1_attn_all

    def _L1_ffn_setup():
        import jax, jax.numpy as jnp
        import numpy as np
        TEMPERATURE = 0.5
        CAPACITY_FACTOR = 1.25
        TOP_K = 1
        key = jax.random.key(seed)
        ks = jax.random.split(key, 5)
        B, S, D, H, E = (4, 512, 256, 512, 8)
        s = 0.02
        return {'x': jax.random.normal(ks[0], (B, S, D), jnp.float32), 'gate_w': jax.random.normal(ks[1], (E, D), jnp.float32) * s, 'gate_b': jnp.zeros((E,), jnp.float32), 'rms_w': jnp.ones((E,), jnp.float32), 'w1': jax.random.normal(ks[2], (E, D, H), jnp.float32) * s, 'b1': jnp.zeros((E, H), jnp.float32), 'w2': jax.random.normal(ks[3], (E, H, D), jnp.float32) * s, 'b2': jnp.zeros((E, D), jnp.float32)}
    _L1_ffn_all = _L1_ffn_setup()
    _L1_ffn_in = {k: v for k, v in _L1_ffn_all.items() if k in ('gate_w', 'gate_b', 'rms_w', 'w1', 'b1', 'w2', 'b2')}
    del _L1_ffn_all
    return {'x': x, 'ctx_1024': ctx_1024, 'mask_SxS2_ik1': mask_SxS2_ik1, 'L0_xattn_Wq': _L0_xattn_in['Wq'], 'L0_xattn_bq': _L0_xattn_in['bq'], 'L0_xattn_Wk': _L0_xattn_in['Wk'], 'L0_xattn_bk': _L0_xattn_in['bk'], 'L0_xattn_Wv': _L0_xattn_in['Wv'], 'L0_xattn_bv': _L0_xattn_in['bv'], 'L0_attn_ln1_g': _L0_attn_in['ln1_g'], 'L0_attn_ln1_b': _L0_attn_in['ln1_b'], 'L0_attn_ln2_g': _L0_attn_in['ln2_g'], 'L0_attn_ln2_b': _L0_attn_in['ln2_b'], 'L0_attn_time_decay': _L0_attn_in['time_decay'], 'L0_attn_time_first': _L0_attn_in['time_first'], 'L0_attn_tm_k': _L0_attn_in['tm_k'], 'L0_attn_tm_v': _L0_attn_in['tm_v'], 'L0_attn_tm_r': _L0_attn_in['tm_r'], 'L0_attn_Wk': _L0_attn_in['Wk'], 'L0_attn_Wv': _L0_attn_in['Wv'], 'L0_attn_Wr': _L0_attn_in['Wr'], 'L0_attn_Wo': _L0_attn_in['Wo'], 'L0_attn_cm_k': _L0_attn_in['cm_k'], 'L0_attn_cm_r': _L0_attn_in['cm_r'], 'L0_attn_Wck': _L0_attn_in['Wck'], 'L0_attn_Wcr': _L0_attn_in['Wcr'], 'L0_attn_Wcv': _L0_attn_in['Wcv'], 'L0_ffn_Wg': _L0_ffn_in['Wg'], 'L0_ffn_We': _L0_ffn_in['We'], 'L0_ffn_be': _L0_ffn_in['be'], 'L1_xattn_wq': _L1_xattn_in['wq'], 'L1_xattn_wk': _L1_xattn_in['wk'], 'L1_xattn_wv': _L1_xattn_in['wv'], 'L1_xattn_wo': _L1_xattn_in['wo'], 'L1_xattn_ln_gamma': _L1_xattn_in['ln_gamma'], 'L1_xattn_ln_beta': _L1_xattn_in['ln_beta'], 'L1_attn_in_proj_w': _L1_attn_in['in_proj_w'], 'L1_attn_in_proj_b': _L1_attn_in['in_proj_b'], 'L1_attn_conv_w': _L1_attn_in['conv_w'], 'L1_attn_conv_b': _L1_attn_in['conv_b'], 'L1_attn_x_proj_w': _L1_attn_in['x_proj_w'], 'L1_attn_x_proj_b': _L1_attn_in['x_proj_b'], 'L1_attn_A_log': _L1_attn_in['A_log'], 'L1_attn_D': _L1_attn_in['D'], 'L1_attn_out_proj_w': _L1_attn_in['out_proj_w'], 'L1_attn_out_proj_b': _L1_attn_in['out_proj_b'], 'L1_attn_ln_gamma': _L1_attn_in['ln_gamma'], 'L1_attn_ln_beta': _L1_attn_in['ln_beta'], 'L1_ffn_gate_w': _L1_ffn_in['gate_w'], 'L1_ffn_gate_b': _L1_ffn_in['gate_b'], 'L1_ffn_rms_w': _L1_ffn_in['rms_w'], 'L1_ffn_w1': _L1_ffn_in['w1'], 'L1_ffn_b1': _L1_ffn_in['b1'], 'L1_ffn_w2': _L1_ffn_in['w2'], 'L1_ffn_b2': _L1_ffn_in['b2']}

def reference(x, ctx_1024, mask_SxS2_ik1, L0_xattn_Wq, L0_xattn_bq, L0_xattn_Wk, L0_xattn_bk, L0_xattn_Wv, L0_xattn_bv, L0_attn_ln1_g, L0_attn_ln1_b, L0_attn_ln2_g, L0_attn_ln2_b, L0_attn_time_decay, L0_attn_time_first, L0_attn_tm_k, L0_attn_tm_v, L0_attn_tm_r, L0_attn_Wk, L0_attn_Wv, L0_attn_Wr, L0_attn_Wo, L0_attn_cm_k, L0_attn_cm_r, L0_attn_Wck, L0_attn_Wcr, L0_attn_Wcv, L0_ffn_Wg, L0_ffn_We, L0_ffn_be, L1_xattn_wq, L1_xattn_wk, L1_xattn_wv, L1_xattn_wo, L1_xattn_ln_gamma, L1_xattn_ln_beta, L1_attn_in_proj_w, L1_attn_in_proj_b, L1_attn_conv_w, L1_attn_conv_b, L1_attn_x_proj_w, L1_attn_x_proj_b, L1_attn_A_log, L1_attn_D, L1_attn_out_proj_w, L1_attn_out_proj_b, L1_attn_ln_gamma, L1_attn_ln_beta, L1_ffn_gate_w, L1_ffn_gate_b, L1_ffn_rms_w, L1_ffn_w1, L1_ffn_b1, L1_ffn_w2, L1_ffn_b2):
    import jax
    import jax.numpy as jnp

    def _L0_xattn_ref(querys, keys, values, mask, Wq, bq, Wk, bk, Wv, bv):
        import jax, jax.numpy as jnp
        import numpy as np
        B, N, M, D_MODEL, D_K, D_V = (8, 512, 512, 256, 256, 256)
        NEG = -1000000000.0
        q = querys @ Wq.T + bq
        k = keys @ Wk.T + bk
        v = values @ Wv.T + bv
        scores = jnp.einsum('bnd,bmd->bnm', q, k)
        scores = jnp.where(mask[None, :, :] == 0, NEG, scores)
        weights = jax.nn.softmax(scores, axis=2)
        out = jnp.einsum('bnm,bmd->bnd', weights, v)
        return out

    def _L0_attn_ref(x, ln1_g, ln1_b, ln2_g, ln2_b, time_decay, time_first, tm_k, tm_v, tm_r, Wk, Wv, Wr, Wo, cm_k, cm_r, Wck, Wcr, Wcv):
        import jax, jax.numpy as jnp
        import numpy as np
        B, T, C = (8, 512, 256)
        HID = 4 * C
        EPS = 1e-05

        def layernorm(x, g, b):
            m = jnp.mean(x, axis=-1, keepdims=True)
            v = jnp.mean(jnp.square(x - m), axis=-1, keepdims=True)
            return (x - m) * jax.lax.rsqrt(v + EPS) * g + b

        def time_shift(x):
            return jnp.concatenate([jnp.zeros_like(x[:, :1]), x[:, :-1]], axis=1)

        def wkv(time_decay, time_first, k, v):
            w = -jnp.exp(time_decay)
            u = time_first
            kT = jnp.swapaxes(k, 0, 1)
            vT = jnp.swapaxes(v, 0, 1)

            def step(carry, kv):
                aa, bb, pp = carry
                kt, vt = kv
                ww = u + kt
                p = jnp.maximum(pp, ww)
                e1 = jnp.exp(pp - p)
                e2 = jnp.exp(ww - p)
                y = (e1 * aa + e2 * vt) / (e1 * bb + e2)
                ww2 = pp + w
                p2 = jnp.maximum(ww2, kt)
                e1b = jnp.exp(ww2 - p2)
                e2b = jnp.exp(kt - p2)
                return ((e1b * aa + e2b * vt, e1b * bb + e2b, p2), y)
            init = (jnp.zeros((k.shape[0], k.shape[2]), k.dtype), jnp.zeros((k.shape[0], k.shape[2]), k.dtype), jnp.full((k.shape[0], k.shape[2]), -1e+38, k.dtype))
            _, ys = jax.lax.scan(step, init, (kT, vT))
            return jnp.swapaxes(ys, 0, 1)
        h = layernorm(x, ln1_g, ln1_b)
        hh = time_shift(h)
        xk = h * tm_k + hh * (1 - tm_k)
        xv = h * tm_v + hh * (1 - tm_v)
        xr = h * tm_r + hh * (1 - tm_r)
        k = jnp.einsum('btc,oc->bto', xk, Wk)
        v = jnp.einsum('btc,oc->bto', xv, Wv)
        sr = jax.nn.sigmoid(jnp.einsum('btc,oc->bto', xr, Wr))
        rwkv = sr * wkv(time_decay, time_first, k, v)
        x = x + jnp.einsum('btc,oc->bto', rwkv, Wo)
        h = layernorm(x, ln2_g, ln2_b)
        hh = time_shift(h)
        xk = h * cm_k + hh * (1 - cm_k)
        xr = h * cm_r + hh * (1 - cm_r)
        kk = jnp.einsum('btc,hc->bth', xk, Wck)
        kk = jnp.square(jax.nn.relu(kk))
        kv = jnp.einsum('bth,ch->btc', kk, Wcv)
        rkv = jax.nn.sigmoid(jnp.einsum('btc,oc->bto', xr, Wcr)) * kv
        return x + rkv

    def _L0_ffn_ref(hidden_states, Wg, We, be):
        import jax, jax.numpy as jnp
        import numpy as np
        TOP_K = 2
        B, S, H = hidden_states.shape
        T = B * S
        x = hidden_states.reshape(T, H)
        probs = jax.nn.softmax(x @ Wg, axis=-1)
        top_vals, top_idx = jax.lax.top_k(probs, TOP_K)
        gates = top_vals / jnp.sum(top_vals, axis=-1, keepdims=True)
        expert_out = jnp.einsum('th,ehd->etd', x, We) + be[:, None, :]
        tok = jnp.arange(T)[:, None]
        sel = expert_out[top_idx, tok, :]
        out = jnp.sum(gates[..., None] * sel, axis=1)
        return out.reshape(B, S, H)

    def _L1_xattn_ref(x, y, wq, wk, wv, wo, ln_gamma, ln_beta):
        import jax, jax.numpy as jnp
        import numpy as np
        EMBED_DIM = 256
        Q_HEADS = 16
        KV_HEADS = 8
        HEAD_DIM = EMBED_DIM // Q_HEADS
        KV_EMBED = HEAD_DIM * KV_HEADS
        GROUPS = Q_HEADS // KV_HEADS
        LN_EPS = 1e-05
        RMS_EPS = 1e-06

        def _rms_norm(x):
            return x * jax.lax.rsqrt(jnp.mean(jnp.square(x), axis=-1, keepdims=True) + RMS_EPS)

        def _act_quant(x):
            scale = 127.0 / jnp.maximum(jnp.max(jnp.abs(x), axis=-1, keepdims=True), 1e-05)
            return jnp.clip(jnp.round(x * scale), -128.0, 127.0) / scale

        def _weight_quant(w):
            scale = 1.0 / jnp.maximum(jnp.mean(jnp.abs(w)), 1e-05)
            return jnp.clip(jnp.round(w * scale), -1.0, 1.0) / scale

        def _ste(a, q):
            return a + jax.lax.stop_gradient(q - a)

        def bit_linear(x, w):
            xn = _rms_norm(x)
            xq = _ste(xn, _act_quant(xn))
            wq = _ste(w, _weight_quant(w))
            return jnp.einsum('bni,oi->bno', xq, wq)
        B, N, D = x.shape
        S = y.shape[1]
        q = bit_linear(x, wq).reshape(B, N, Q_HEADS, HEAD_DIM)
        k = bit_linear(y, wk).reshape(B, S, KV_HEADS, HEAD_DIM)
        v = bit_linear(y, wv).reshape(B, S, KV_HEADS, HEAD_DIM)
        q = jnp.transpose(q, (0, 2, 1, 3)) / HEAD_DIM ** 0.5
        q = q.reshape(B, KV_HEADS, GROUPS, N, HEAD_DIM)
        k = jnp.transpose(k, (0, 2, 1, 3))
        v = jnp.transpose(v, (0, 2, 1, 3))
        scores = jnp.einsum('bhgnd,bhsd->bhgns', q, k)
        attn = jax.nn.softmax(scores, axis=-1)
        out = jnp.einsum('bhgns,bhsd->bhgnd', attn, v)
        out = jnp.transpose(out, (0, 3, 1, 2, 4)).reshape(B, N, D)
        mu = jnp.mean(out, axis=-1, keepdims=True)
        var = jnp.mean(jnp.square(out - mu), axis=-1, keepdims=True)
        out = (out - mu) * jax.lax.rsqrt(var + LN_EPS) * ln_gamma + ln_beta
        return bit_linear(out, wo)

    def _L1_attn_ref(x, in_proj_w, in_proj_b, conv_w, conv_b, x_proj_w, x_proj_b, A_log, D, out_proj_w, out_proj_b, ln_gamma, ln_beta):
        import jax, jax.numpy as jnp
        from jax import lax
        import numpy as np
        D_MODEL, D_STATE, D_CONV, EXPAND = (256, 16, 4, 2)
        D_INNER = D_MODEL * EXPAND
        BATCH, SEQ = (2, 512)
        LN_EPS = 1e-05

        def _forward(x, in_proj_w, in_proj_b, conv_w, conv_b, x_proj_w, x_proj_b, A_log, D, out_proj_w, out_proj_b, ln_gamma, ln_beta):
            d_state = A_log.shape[1]
            d_conv = conv_w.shape[-1]
            residual = x
            xz = x @ in_proj_w.T + in_proj_b
            x_main, z = jnp.split(xz, 2, axis=-1)
            xc = jnp.transpose(x_main, (0, 2, 1))
            xc = lax.conv_general_dilated(xc, conv_w, window_strides=(1,), padding=[(d_conv - 1, 0)], dimension_numbers=('NCH', 'OIH', 'NCH'), feature_group_count=xc.shape[1])
            xc = xc + conv_b[None, :, None]
            xc = jax.nn.silu(jnp.transpose(xc, (0, 2, 1)))
            ssm = xc @ x_proj_w.T + x_proj_b
            B_param = ssm[..., :d_state]
            C_param = ssm[..., d_state:2 * d_state]
            delta = jax.nn.softplus(ssm[..., -1:])
            A = -jnp.exp(A_log)

            def step(h, ts):
                dt, B_t, C_t, x_t = ts
                dA = jnp.exp(A[None] * dt[:, :, None])
                dBx = dt[:, :, None] * B_t[:, None, :] * x_t[:, :, None]
                h = dA * h + dBx
                y = jnp.einsum('bdn,bn->bd', h, C_t) + D * x_t
                return (h, y)
            h0 = jnp.zeros((x.shape[0], xc.shape[-1], d_state), xc.dtype)
            xs = (jnp.swapaxes(delta, 0, 1), jnp.swapaxes(B_param, 0, 1), jnp.swapaxes(C_param, 0, 1), jnp.swapaxes(xc, 0, 1))
            _, ys = lax.scan(step, h0, xs)
            y = jnp.swapaxes(ys, 0, 1)
            y = y * jax.nn.silu(z)
            y = y @ out_proj_w.T + out_proj_b
            r = y + residual
            mu = jnp.mean(r, axis=-1, keepdims=True)
            var = jnp.mean(jnp.square(r - mu), axis=-1, keepdims=True)
            return (r - mu) * lax.rsqrt(var + LN_EPS) * ln_gamma + ln_beta
        return _forward(x, in_proj_w, in_proj_b, conv_w, conv_b, x_proj_w, x_proj_b, A_log, D, out_proj_w, out_proj_b, ln_gamma, ln_beta)

    def _L1_ffn_ref(x, gate_w, gate_b, rms_w, w1, b1, w2, b2):
        import jax, jax.numpy as jnp
        import numpy as np
        TEMPERATURE = 0.5
        CAPACITY_FACTOR = 1.25
        TOP_K = 1
        B, S, D = x.shape
        E = gate_w.shape[0]
        xf = x.reshape(-1, D)
        N = xf.shape[0]
        logits = xf @ gate_w.T + gate_b
        eps = jnp.finfo(logits.dtype).eps
        ms = jnp.mean(logits * logits, axis=-1, keepdims=True)
        logits = logits * jax.lax.rsqrt(ms + eps) * rms_w
        gates = jax.nn.softmax(logits / TEMPERATURE, axis=-1)
        g, idx = jax.lax.top_k(gates, TOP_K)
        g, idx = (g[:, 0], idx[:, 0])
        capacity = min(int(np.ceil(N * TOP_K / E * CAPACITY_FACTOR)), N)
        counts = jnp.zeros((E,), jnp.int32).at[idx].add(1)
        active = (counts > 0) & (capacity >= 1)
        mask = active[idx].astype(gates.dtype)
        masked = g * mask
        norm_g = masked / (masked + 1e-06)
        h = jax.nn.gelu(jnp.einsum('nd,edh->neh', xf, w1) + b1, approximate=False)
        y = jnp.einsum('neh,ehd->ned', h, w2) + b2
        out = (y * norm_g[:, None, None]).sum(axis=1)
        return out.reshape(B, S, D)
    x = x + _L0_xattn_ref(_layernorm(x, axis=-1), ctx_1024, ctx_1024, mask_SxS2_ik1, L0_xattn_Wq, L0_xattn_bq, L0_xattn_Wk, L0_xattn_bk, L0_xattn_Wv, L0_xattn_bv)
    x = x + _L0_attn_ref(_layernorm(x, axis=-1), L0_attn_ln1_g, L0_attn_ln1_b, L0_attn_ln2_g, L0_attn_ln2_b, L0_attn_time_decay, L0_attn_time_first, L0_attn_tm_k, L0_attn_tm_v, L0_attn_tm_r, L0_attn_Wk, L0_attn_Wv, L0_attn_Wr, L0_attn_Wo, L0_attn_cm_k, L0_attn_cm_r, L0_attn_Wck, L0_attn_Wcr, L0_attn_Wcv)
    x = x + _L0_ffn_ref(_layernorm(x, axis=-1), L0_ffn_Wg, L0_ffn_We, L0_ffn_be)
    x = x + _L1_xattn_ref(_layernorm(x, axis=-1), ctx_1024, L1_xattn_wq, L1_xattn_wk, L1_xattn_wv, L1_xattn_wo, L1_xattn_ln_gamma, L1_xattn_ln_beta)
    x = x + _L1_attn_ref(_layernorm(x, axis=-1), L1_attn_in_proj_w, L1_attn_in_proj_b, L1_attn_conv_w, L1_attn_conv_b, L1_attn_x_proj_w, L1_attn_x_proj_b, L1_attn_A_log, L1_attn_D, L1_attn_out_proj_w, L1_attn_out_proj_b, L1_attn_ln_gamma, L1_attn_ln_beta)
    x = x + _L1_ffn_ref(_layernorm(x, axis=-1), L1_ffn_gate_w, L1_ffn_gate_b, L1_ffn_rms_w, L1_ffn_w1, L1_ffn_b1, L1_ffn_w2, L1_ffn_b2)
    return x

_drawn_inputs = setup_inputs


def setup_inputs(seed=0):
    import zlib

    import numpy as np

    out = dict(_drawn_inputs(seed))
    spreads = {'L0_xattn_bq': (0.0, 0.1),
     'L0_xattn_bk': (0.0, 0.8),
     'L0_xattn_bv': (0.0, 0.1),
     'L0_attn_ln1_g': (1.0, 0.6),
     'L0_attn_ln1_b': (0.0, 0.8),
     'L0_attn_ln2_g': (1.0, 0.6),
     'L0_attn_ln2_b': (0.0, 0.73),
     'L0_ffn_be': (0.0, 0.293),
     'L1_xattn_ln_gamma': (1.0, 0.2),
     'L1_xattn_ln_beta': (0.0, 0.335),
     'L1_attn_in_proj_b': (0.0, 0.8),
     'L1_attn_conv_b': (0.0, 0.8),
     'L1_attn_x_proj_b': (0.0, 0.8),
     'L1_attn_D': (1.0, 0.6),
     'L1_attn_out_proj_b': (0.0, 0.277),
     'L1_attn_ln_gamma': (1.0, 0.2),
     'L1_attn_ln_beta': (0.0, 0.311),
     'L1_ffn_gate_b': (0.0, 0.8),
     'L1_ffn_rms_w': (1.0, 0.6),
     'L1_ffn_b1': (0.0, 0.45),
     'L1_ffn_b2': (0.0, 0.1)}
    factors = {'L0_attn_time_decay': 6.307,
     'L0_attn_time_first': 8.0,
     'L0_attn_tm_k': 8.0,
     'L0_attn_tm_v': 7.633,
     'L0_attn_tm_r': 8.0,
     'L0_attn_Wk': 7.114,
     'L0_attn_Wv': 2.858,
     'L0_attn_Wr': 8.0,
     'L0_attn_cm_k': 3.272,
     'L0_attn_cm_r': 8.0,
     'L0_attn_Wcr': 6.615,
     'L1_attn_in_proj_w': 8.0,
     'L1_attn_conv_w': 8.0,
     'L1_attn_x_proj_w': 8.0,
     'L1_attn_A_log': 8.0,
     'L1_attn_out_proj_w': 8.0,
     'L1_ffn_gate_w': 8.0}
    for name, (base, spread) in spreads.items():
        noise = np.random.default_rng([zlib.crc32(name.encode()), seed]).standard_normal(out[name].shape)
        drawn = base * np.exp(spread * noise) if base else spread * noise
        out[name] = jnp.asarray(drawn.astype(out[name].dtype))
    for name, factor in factors.items():
        out[name] = (out[name] * factor).astype(out[name].dtype)
    return out
```

```python
from contextlib import ExitStack

import numpy as np

import concourse.bass as bass
from concourse import mybir

FP32 = mybir.dt.float32
BF16 = mybir.dt.bfloat16
I32 = mybir.dt.int32
U32 = mybir.dt.uint32
ALU = mybir.AluOpType
ACT = mybir.ActivationFunctionType
AX = mybir.AxisListType

P = 128
B, T, C, M = 64, 32, 256, 257
CJ = C // P
TILES = B * T // P
BPT = P // T
KT_ = 4
BLOCKS = TILES // KT_
BT = KT_ * P
BB = KT_ * BPT
HID = 4 * C
E = 8
FH = 512
HEADS, KVH, HD = 16, 8, 16
DI, NS, TAPS = 512, 16, 4
DC = DI // P
NEG = -1.0e9
FAR = -1.0e38
LN_EPS, RMS_EPS = 1e-5, 1e-6
ROUND = 1.5 * 2.0 ** 23
F32_EPS = float(np.finfo(np.float32).eps)


class Steps:

    def __init__(self, sem, names, ahead=1):
        self.sem = sem
        self.ahead = ahead
        self.names = [n for item in names for n in ([item] if isinstance(item, str) else [item[0]] * item[1])]
        self.n = len(self.names)
        self.emitted = 0

    def start(self, eng):
        eng.sem_inc(self.sem, self.ahead * self.n)

    def __call__(self, name):
        want = self.names[self.emitted % self.n]
        assert want == name, (want, name)
        self.emitted += 1
        return self.sem

    def at(self, name, i, k=None):
        places = [p for p, n in enumerate(self.names) if n == name]
        place = places[-1] if k is None else places[k]
        return self.sem, (i + self.ahead) * self.n + place + 1


class Chip:
    pass


def tensors(nc, ctx, prefix):
    def sb(name, shape, dt=FP32):
        return ctx.enter_context(nc.sbuf_tensor(f"{prefix}_{name}", shape, dt))

    def ps(name, shape=(P, 512), dt=FP32):
        return ctx.enter_context(nc.psum_tensor(f"{prefix}_{name}", list(shape), dt))

    def sem(name):
        return ctx.enter_context(nc.semaphore(f"{prefix}_{name}"))

    return sb, ps, sem



LN_V = [("stats", 4), "sums", "diff", "between", "variance", "mean", "rstd", ("norm", 4)]
LN_A = ["std", ("features", CJ)]
LN_T = [("turned", CJ)]


class Norm:

    def __init__(self, sb, ps, banks=None, name="ln"):
        self.stats = sb(f"{name}_stats", [P, KT_, 6])
        self.sums = sb(f"{name}_sums", [P, KT_, 2])
        self.diff = sb(f"{name}_diff", [P, KT_])
        self.var = sb(f"{name}_var", [P, KT_])
        self.mean = sb(f"{name}_mean", [P, KT_])
        self.std = sb(f"{name}_std", [P, KT_])
        self.rstd = sb(f"{name}_rstd", [P, KT_])
        self.xn = sb(f"{name}_xn", [P, KT_, C])
        self.hT = sb(f"{name}_hT", [P, CJ, BT]) if name == "ln" else None
        self.ps = banks or [ps(f"{name}_ps{j}") for j in range(CJ)]
        self.src = None


def second_names(names):
    return [n + "2" if isinstance(n, str) else (n[0] + "2", n[1]) for n in names]


class second:

    def __init__(self, steps):
        self.steps = steps

    def __call__(self, name):
        return self.steps(name + "2")

    def at(self, name, i, k=None):
        return self.steps.at(name + "2", i, k)


def ln_vector(e, V, A, n, src, i, free):
    def tile(k):
        return n.src[:, k, :] if src is None else src[:, i * KT_ + k, :]

    for k in range(KT_):
        e.bn_stats(n.stats[:, k, :], tile(k)).then_inc(V("stats"), 1)
    e.wait_ge(*V.at("stats", i))
    e.tensor_tensor(n.sums[:, :, :], n.stats[:, :, 1:3], n.stats[:, :, 4:6], ALU.add).then_inc(V("sums"), 1)
    e.tensor_tensor(n.diff[:, :], n.stats[:, :, 1], n.stats[:, :, 4], ALU.subtract).then_inc(V("diff"), 1)
    e.wait_ge(*V.at("diff", i))
    e.scalar_tensor_tensor(n.var[:, :], n.diff[:, :], 0.25, n.diff[:, :], ALU.mult, ALU.mult).then_inc(V("between"), 1)
    e.wait_ge(*V.at("between", i))
    e.scalar_tensor_tensor(n.var[:, :], n.sums[:, :, 1], 1.0 / C, n.var[:, :], ALU.mult, ALU.add).then_inc(V("variance"), 1)
    e.tensor_scalar(n.mean[:, :], n.sums[:, :, 0], 0.5, None, ALU.mult).then_inc(V("mean"), 1)
    e.wait_ge(*A.at("std", i))
    e.reciprocal(n.rstd[:, :], n.std[:, :]).then_inc(V("rstd"), 1)
    e.wait_ge(*V.at("rstd", i))
    free()
    for k in range(KT_):
        e.tensor_scalar(n.xn[:, k, :], tile(k), n.mean[:, k:k + 1], n.rstd[:, k:k + 1],
                        ALU.subtract, ALU.mult).then_inc(V("norm"), 1)


def ln_scalar_std(e, V, A, n, i, c):
    e.wait_ge(*V.at("variance", i))
    e.activation(n.std[:, :], n.var[:, :], ACT.Sqrt, bias=c.eps[:, 0:1]).then_inc(A("std"), 1)


def ln_scalar_features(e, T_, A, n, i, free, gain=None, shift=None):
    free()
    for j in range(CJ):
        e.wait_ge(*T_.at("turned", i, j))
        if gain is None:
            e.activation(n.hT[:, j, :], n.ps[j][:, :], ACT.Copy).then_inc(A("features"), 1)
        else:
            e.activation(n.hT[:, j, :], n.ps[j][:, :], ACT.Identity, bias=shift[:, j:j + 1],
                         scale=gain[:, j:j + 1]).then_inc(A("features"), 1)


def ln_tensor(e, V, T_, n, i, c, free, src=None, step="norm"):
    src = src or n.xn
    free()
    e.wait_ge(*V.at(step, i))
    for j in range(CJ):
        for k in range(KT_):
            t = e.transpose(n.ps[j][:, k * P:(k + 1) * P], src[:, k, j * P:(j + 1) * P], c.ident[:, :])
        t.then_inc(T_("turned"), 1)



def load_all(nc, c):
    with ExitStack() as ctx:
        sb, ps, sem = tensors(nc, ctx, "ld")
        loaded, made = sem("loaded"), sem("made")
        block = ctx.enter_context(nc.Block())

        @block.sync
        def _(e):
            e.dma_start(c.X[:, :, :], c.d["x"]).then_inc(loaded, 16)
            e.dma_start(c.vecs[:, :], c.d["vecs"]).then_inc(loaded, 16)
            e.dma_start(c.rows[:, :], c.d["rows"]).then_inc(loaded, 16)
            e.dma_start(c.consts[:, :], c.d["ident"]).then_inc(loaded, 16)
            e.dma_start(c.small[:, :], c.d["small"]).then_inc(loaded, 16)
            e.wait_ge(loaded, 80)

        @block.vector
        def _(e):
            e.memset(c.eps[:, 0:1], LN_EPS).then_inc(made, 1)
            e.memset(c.eps[:, 1:2], RMS_EPS).then_inc(made, 1)
            e.memset(c.eps[:, 3:4], F32_EPS).then_inc(made, 1)
            e.memset(c.eps[:, 2:3], float(np.log(1e-5))).then_inc(made, 1)
            e.memset(c.ones[:, :], 1.0).then_inc(made, 1)
            e.wait_ge(loaded, 80)
            e.tensor_copy(c.identb[:, :], c.ident[:, :]).then_inc(made, 1)



def l0_queries(nc, c):
    with ExitStack() as ctx:
        sb, ps, sem = tensors(nc, ctx, "q0")
        wq = sb("wq", [P, CJ, C])
        wk = sb("wk", [P, CJ, C])
        fused = sb("fused", [P, CJ, C])
        side = sb("side", [P, 8])
        n = Norm(sb, ps)
        out_ps = [ps(f"out_ps{o}") for o in range(CJ)]
        fuse_ps = [ps(f"fuse_ps{j}") for j in range(CJ)]
        side_ps = ps("side_ps")
        qc_ps = ps("qc_ps")
        loaded, fused_ready, fuse_done, side_made = sem("loaded"), sem("fused"), sem("fuse_done"), sem("side_made")
        V = Steps(sem("vector"), LN_V + ["qc"])
        A = Steps(sem("scalar"), LN_A + [("qk", CJ)])
        T_ = Steps(sem("tensor"), LN_T + [("qk", CJ), "qc"])
        block = ctx.enter_context(nc.Block())
        bq, bk = c.vec["bq"], c.vec["bk"]

        @block.sync
        def _(e):
            e.dma_start(wq[:, :, :], c.d["l0_wq"]).then_inc(loaded, 16)
            e.dma_start(wk[:, :, :], c.d["l0_wk"]).then_inc(loaded, 16)

        @block.tensor
        def _(e):
            T_.start(e)
            e.wait_ge(loaded, 32)
            for j in range(CJ):
                for o in range(CJ):
                    m = e.matmul(fuse_ps[j][:, 0:C], wq[:, o, j * P:(j + 1) * P], wk[:, o, :],
                                 start=(o == 0), stop=(o == CJ - 1))
                m.then_inc(fuse_done, 1)
            for j in range(CJ):
                for w, b, at in ((wk, bq, 0), (wq, bk, 2)):
                    for o in range(CJ):
                        e.matmul(side_ps[:, at + j:at + j + 1], w[:, o, j * P:(j + 1) * P], b[:, o:o + 1],
                                 start=(o == 0), stop=(o == CJ - 1))
            for o in range(CJ):
                m = e.matmul(side_ps[0:1, 4:5], bq[:, o:o + 1], bk[:, o:o + 1], start=(o == 0), stop=(o == CJ - 1))
            m.then_inc(fuse_done, 1)
            with e.Fori(0, BLOCKS) as i:
                ln_tensor(e, V, T_, n, i, c, lambda: e.wait_ge(*A.at("features", i - 1)))
                e.wait_ge(*A.at("features", i))
                e.wait_ge(fused_ready, CJ)
                e.wait_ge(side_made, 2)
                for o in range(CJ):
                    e.wait_ge(*A.at("qk", i - 1, o))
                    for j in range(CJ):
                        m = e.matmul(out_ps[o][:, :], fused[:, j, o * P:(o + 1) * P], n.hT[:, j, :],
                                     start=(j == 0), stop=(j == CJ - 1))
                    m.then_inc(T_("qk"), 1)
                e.wait_ge(*V.at("qc", i - 1))
                for k in range(KT_):
                    for j in range(CJ):
                        e.matmul(qc_ps[:, k:k + 1], n.hT[:, j, k * P:(k + 1) * P], side[:, 2 + j:3 + j],
                                 start=(j == 0), stop=False)
                    m = e.matmul(qc_ps[:, k:k + 1], c.ones[0:1, 0:P], side[0:1, 4:5], start=False, stop=True)
                m.then_inc(T_("qc"), 1)

        @block.vector
        def _(e):
            V.start(e)
            e.wait_ge(fuse_done, 3)
            for j in range(CJ):
                e.tensor_copy(fused[:, j, :], fuse_ps[j][:, 0:C]).then_inc(fused_ready, 1)
            with e.Fori(0, BLOCKS) as i:
                ln_vector(e, V, A, n, c.X, i, lambda: e.wait_ge(*T_.at("turned", i - 1)))
                e.wait_ge(*T_.at("qc", i))
                e.tensor_copy(c.qc[:, bass.ds(i * KT_, KT_)], qc_ps[:, 0:KT_]).then_inc(V("qc"), 1)

        @block.scalar
        def _(e):
            A.start(e)
            e.wait_ge(fuse_done, 3)
            e.activation(side[:, 0:4], side_ps[:, 0:4], ACT.Copy).then_inc(side_made, 1)
            e.activation(side[0:1, 4:5], side_ps[0:1, 4:5], ACT.Copy).then_inc(side_made, 1)
            e.wait_ge(side_made, 2)
            with e.Fori(0, BLOCKS) as i:
                ln_scalar_std(e, V, A, n, i, c)
                ln_scalar_features(e, T_, A, n, i, lambda: e.wait_ge(*T_.at("qc", i - 1)))
                for o in range(CJ):
                    e.wait_ge(*T_.at("qk", i, o))
                    e.activation(c.qkT[:, o, bass.ds(i * BT, BT)], out_ps[o][:, :], ACT.Identity,
                                 bias=side[:, o:o + 1]).then_inc(A("qk"), 1)


def l0_attention(nc, c):
    with ExitStack() as ctx:
        sb, ps, sem = tensors(nc, ctx, "a0")
        wv = sb("wv", [P, CJ, C])
        mask_i = sb("mask_i", [P, M], I32)
        keep = sb("keep", [P, M])
        fill = sb("fill", [P, M])
        last_n = sb("last_n", [BPT, TILES, C])
        last_t = sb("last_t", [P, CJ, B])
        ctx_t = [sb(f"ctx_t{u}", [P, BPT, CJ, 2 * P]) for u in range(2)]
        ctx_n = [sb(f"ctx_n{u}", [P, BPT, 2, C]) for u in range(2)]
        qk = [sb(f"qk{u}", [P, CJ, P]) for u in range(2)]
        s = [sb(f"s{u}", [P, M]) for u in range(2)]
        p = [sb(f"p{u}", [P, M]) for u in range(2)]
        tiny = [sb(f"tiny{u}", [P, 16]) for u in range(2)]
        pt = [sb(f"pt{u}", [P, 2 * P]) for u in range(2)]
        pl = [sb(f"pl{u}", [BPT, P]) for u in range(2)]
        o = [sb(f"o{u}", [P, C]) for u in range(2)]
        ot = [sb(f"ot{u}", [P, CJ, P]) for u in range(2)]
        sq = sb("sq", [P, C])
        rounded = sb("rounded", [P, BPT * 2, C])
        qs = [sb(f"qs{u}", [P, 8]) for u in range(2)]
        ss = [sb(f"ss{u}", [P, 8]) for u in range(2)]
        root = [sb(f"root{u}", [P, 8]) for u in range(2)]
        s_ps = [ps(f"s_ps{u}") for u in range(2)]
        o_ps = [ps(f"o_ps{u}") for u in range(2)]
        pt_ps, ot_ps, y_ps = ps("pt_ps"), ps("ot_ps"), ps("y_ps")
        w_loaded, made, seen = sem("w_loaded"), sem("made"), sem("seen")
        t_loaded = [sem(f"t_loaded{u}") for u in range(2)]
        n_loaded = [sem(f"n_loaded{u}") for u in range(2)]
        V = Steps(sem("vector"), ["scored", "last", "last_s", "masked", "minus", "absmax", "keep_max",
                                  "keep_ss", "guard", "flip", "scale",
                                  "last_p", "inverse", "out", "whole", "added"], 2)
        A = Steps(sem("scalar"), ["exp", ("squares", 2 * BPT), "log", "root", "pt", "pl", "ot"], 2)
        T_ = Steps(sem("tensor"), ["scores", "pt", "out", "ot", "y"], 2)
        G = Steps(sem("pool"), ["qk", ("rounded", 2 * BPT)], 2)
        block = ctx.enter_context(nc.Block())

        @block.sync
        def _(e):
            e.dma_start(wv[:, :, :], c.d["l0_wv"]).then_inc(w_loaded, 16)
            for b in range(BPT):
                e.dma_start(mask_i[b * T:(b + 1) * T, :], c.d["mask"]).then_inc(w_loaded, 16)
            e.dma_start(last_n[:, :, :], c.d["ctx_last_n"]).then_inc(w_loaded, 16)
            e.dma_start(last_t[:, :, :], c.d["ctx_last_t"]).then_inc(w_loaded, 16)
            with e.Fori(0, TILES // 2) as h:
                for u in range(2):
                    t = h * 2 + u
                    e.wait_ge(*T_.at("scores", t - 2))
                    e.dma_start(ctx_t[u][:, :, :, :], c.d["ctx_t"][t]).then_inc(t_loaded[u], 16)
                    e.wait_ge(*T_.at("out", t - 2))
                    e.wait_ge(*A.at("squares", t - 2))
                    e.wait_ge(*V.at("absmax", t - 2))
                    e.wait_ge(*G.at("rounded", t - 2))
                    e.dma_start(ctx_n[u][:, :, :, :], c.d["ctx_n"][t]).then_inc(n_loaded[u], 16)

        @block.gpsimd
        def _(e):
            G.start(e)
            with e.Fori(0, TILES // 2) as h:
                for u in range(2):
                    t = h * 2 + u
                    e.wait_ge(*T_.at("scores", t - 2))
                    e.tensor_copy(qk[u][:, :, :], c.qkT[:, :, bass.ds(t * P, P)]).then_inc(G("qk"), 1)
                    e.wait_ge(*V.at("scale", t))
                    e.wait_ge(*V.at("whole", t - 1))
                    e.sem_inc(seen, 1)
                    for r in range(2 * BPT):
                        e.tensor_scalar(rounded[:, r, :], ctx_n[u][:, r // 2, r % 2, :], qs[u][:, r:r + 1], ROUND,
                                        ALU.mult, ALU.add).then_inc(G("rounded"), 1)

        @block.tensor
        def _(e):
            T_.start(e)
            e.wait_ge(w_loaded, 16 * 7)
            with e.Fori(0, TILES // 2) as h:
                for u in range(2):
                    t = h * 2 + u
                    e.wait_ge(*G.at("qk", t))
                    e.wait_ge(*V.at("scored", t - 2))
                    e.wait_ge(*V.at("last", t - 2))
                    e.wait_ge(t_loaded[u], (h + 1) * 16)
                    for j in range(CJ):
                        for b in range(BPT):
                            e.matmul(s_ps[u][b * T:(b + 1) * T, 0:2 * P], qk[u][:, j, b * T:(b + 1) * T],
                                     ctx_t[u][:, b, j, :], start=(j == 0), stop=(j == CJ - 1))
                    for j in range(CJ):
                        m = e.matmul(s_ps[u][:, 2 * P:2 * P + BPT], qk[u][:, j, :],
                                     last_t[:, j, bass.ds(t * BPT, BPT)], start=(j == 0), stop=(j == CJ - 1))
                    m.then_inc(T_("scores"), 1)
                    e.wait_ge(*A.at("exp", t))
                    e.wait_ge(*V.at("last_p", t))
                    e.wait_ge(*A.at("pl", t - 1))
                    for m in range(2):
                        e.transpose(pt_ps[:, m * P:(m + 1) * P], p[u][:, m * P:(m + 1) * P], c.ident[:, :])
                    e.transpose(pt_ps[0:BPT, 2 * P:3 * P], tiny[u][:, 8:8 + BPT], c.ident[:, :]).then_inc(T_("pt"), 1)
                    e.wait_ge(*A.at("pl", t))
                    e.wait_ge(n_loaded[u], (h + 1) * 16)
                    e.wait_ge(*V.at("out", t - 2))
                    e.matmul(o_ps[u][:, 0:C], pl[u][:, :], last_n[:, t, :], start=True, stop=False,
                             skip_group_check=True)
                    for k in range(2):
                        for b in range(BPT):
                            m = e.matmul(o_ps[u][b * T:(b + 1) * T, 0:C], pt[u][:, k * P + b * T:k * P + (b + 1) * T],
                                         ctx_n[u][:, b, k, :], start=False, stop=(k == 1), skip_group_check=True)
                    m.then_inc(T_("out"), 1)
                    e.wait_ge(*V.at("out", t))
                    e.wait_ge(*A.at("ot", t - 1))
                    for j in range(CJ):
                        m = e.transpose(ot_ps[:, j * P:(j + 1) * P], o[u][:, j * P:(j + 1) * P], c.ident[:, :])
                    m.then_inc(T_("ot"), 1)
                    e.wait_ge(*A.at("ot", t))
                    e.wait_ge(*V.at("added", t - 1))
                    for j in range(CJ):
                        e.matmul(y_ps[:, 0:C], ot[u][:, j, :], wv[:, j, :], start=(j == 0), stop=False)
                    e.matmul(y_ps[:, 0:C], c.ones[0:1, 0:P], c.row["bv"][0:1, :], start=False,
                             stop=True).then_inc(T_("y"), 1)

        @block.vector
        def _(e):
            V.start(e)
            e.wait_ge(w_loaded, 16 * 7)
            e.tensor_scalar(keep[:, :], mask_i[:, :], 0.0, None, ALU.not_equal).then_inc(made, 1)
            e.wait_ge(made, 1)
            e.tensor_scalar(fill[:, :], keep[:, :], 1.0, -NEG, ALU.subtract, ALU.mult).then_inc(made, 1)
            e.wait_ge(made, 2)
            with e.Fori(0, TILES // 2) as h:
                for u in range(2):
                    t = h * 2 + u
                    x, sc = tiny[u], s_ps[u]
                    e.wait_ge(*T_.at("scores", t))
                    e.wait_ge(*A.at("exp", t - 2))
                    e.scalar_tensor_tensor(s[u][:, 0:2 * P], sc[:, 0:2 * P], c.qc[:, bass.ds(t, 1)], keep[:, 0:2 * P],
                                           ALU.add, ALU.mult).then_inc(V("scored"), 1)
                    e.tensor_tensor_reduce(x[:, 0:4], sc[:, 2 * P:2 * P + BPT], c.own[:, :], 1.0, 0.0, ALU.mult,
                                           ALU.add, x[:, 4:5]).then_inc(V("last"), 1)
                    e.wait_ge(*V.at("last", t))
                    e.scalar_tensor_tensor(s[u][:, 2 * P:M], x[:, 4:5], c.qc[:, bass.ds(t, 1)], keep[:, 2 * P:M],
                                           ALU.add, ALU.mult).then_inc(V("last_s"), 1)
                    e.wait_ge(*V.at("last_s", t))
                    e.tensor_tensor(s[u][:, :], s[u][:, :], fill[:, :], ALU.add).then_inc(V("masked"), 1)
                    e.wait_ge(*V.at("masked", t))
                    e.tensor_reduce(x[:, 5:6], s[u][:, :], AX.X, ALU.max, negate=True).then_inc(V("minus"), 1)
                    e.wait_ge(n_loaded[u], (h + 1) * 16)
                    e.wait_ge(*G.at("rounded", t - 2))
                    e.tensor_reduce(qs[u][:, :], ctx_n[u][:, :, :, :].rearrange("p b k c -> p (b k) c"), AX.X, ALU.max,
                                    apply_absolute_value=True).then_inc(V("absmax"), 1)
                    e.wait_ge(*V.at("absmax", t))
                    e.tensor_copy(c.c_max[:, bass.ds(t * 2 * BPT, 2 * BPT)], qs[u][:, :]).then_inc(V("keep_max"), 1)
                    e.wait_ge(*A.at("root", t))
                    e.tensor_copy(c.c_ss[:, bass.ds(t * 2 * BPT, 2 * BPT)], ss[u][:, :]).then_inc(V("keep_ss"), 1)
                    e.wait_ge(*V.at("keep_ss", t))
                    e.tensor_tensor(qs[u][:, :], qs[u][:, :], root[u][:, :], ALU.max).then_inc(V("guard"), 1)
                    e.wait_ge(*V.at("guard", t))
                    e.reciprocal(qs[u][:, :], qs[u][:, :]).then_inc(V("flip"), 1)
                    e.wait_ge(*V.at("flip", t))
                    e.tensor_scalar(qs[u][:, :], qs[u][:, :], 127.0, None, ALU.mult).then_inc(V("scale"), 1)
                    e.wait_ge(*A.at("exp", t))
                    e.wait_ge(*T_.at("pt", t - 2))
                    e.tensor_scalar(x[:, 8:12], c.own[:, :], p[u][:, 2 * P:M], None, ALU.mult).then_inc(V("last_p"), 1)
                    e.reciprocal(x[:, 7:8], x[:, 6:7]).then_inc(V("inverse"), 1)
                    e.wait_ge(*V.at("inverse", t))
                    e.wait_ge(*T_.at("out", t))
                    e.wait_ge(*T_.at("ot", t - 2))
                    e.tensor_scalar(o[u][:, :], o_ps[u][:, 0:C], x[:, 7:8], None, ALU.mult).then_inc(V("out"), 1)
                    e.wait_ge(*G.at("rounded", t))
                    e.tensor_scalar(c.cq[:, bass.ds(t * 2 * BPT, 2 * BPT), :], rounded[:, :, :], ROUND, None,
                                    ALU.subtract).then_inc(V("whole"), 1)
                    e.wait_ge(*T_.at("y", t))
                    e.tensor_tensor(c.X[:, t, :], c.X[:, t, :], y_ps[:, 0:C], ALU.add).then_inc(V("added"), 1)

        @block.scalar
        def _(e):
            A.start(e)
            with e.Fori(0, TILES // 2) as h:
                for u in range(2):
                    t = h * 2 + u
                    x = tiny[u]
                    e.wait_ge(*V.at("minus", t))
                    e.wait_ge(*T_.at("pt", t - 2))
                    e.wait_ge(*V.at("inverse", t - 2))
                    e.activation(p[u][:, :], s[u][:, :], ACT.Exp, bias=x[:, 5:6],
                                 accum_out=x[:, 6:7]).then_inc(A("exp"), 1)
                    e.wait_ge(n_loaded[u], (h + 1) * 16)
                    e.wait_ge(*V.at("keep_ss", t - 2))
                    for r in range(2 * BPT):
                        e.wait_ge(*(A.at("squares", t, r - 1) if r else A.at("squares", t - 1)))
                        e.activation(sq[:, :], ctx_n[u][:, r // 2, r % 2, :], ACT.Square,
                                     accum_out=ss[u][:, r:r + 1]).then_inc(A("squares"), 1)
                    e.wait_ge(*A.at("squares", t))
                    e.wait_ge(*V.at("guard", t - 2))
                    e.activation(root[u][:, :], ss[u][:, :], ACT.Ln, scale=1.0 / C,
                                 bias=c.eps[:, 1:2]).then_inc(A("log"), 1)
                    e.wait_ge(*A.at("log", t))
                    e.activation(root[u][:, :], root[u][:, :], ACT.Exp, scale=0.5,
                                 bias=c.eps[:, 2:3]).then_inc(A("root"), 1)
                    e.wait_ge(*T_.at("pt", t))
                    e.wait_ge(*T_.at("out", t - 2))
                    e.activation(pt[u][:, :], pt_ps[:, 0:2 * P], ACT.Copy).then_inc(A("pt"), 1)
                    e.activation(pl[u][:, :], pt_ps[0:BPT, 2 * P:3 * P], ACT.Copy).then_inc(A("pl"), 1)
                    e.wait_ge(*T_.at("ot", t))
                    e.wait_ge(*T_.at("y", t - 2))
                    e.activation(ot[u][:, :, :].rearrange("p j t -> p (j t)"), ot_ps[:, 0:C], ACT.Copy).then_inc(A("ot"), 1)



def by_batch(ap):
    return ap.rearrange("p (g t) -> p g t", t=T)


def l0_time_mix(nc, c):
    with ExitStack() as ctx:
        sb, ps, sem = tensors(nc, ctx, "tm")
        w = {k: sb(f"w{k}", [P, CJ, C]) for k in "kvro"}
        n = Norm(sb, ps)
        xn0 = sb("xn0", [P, KT_, C])
        var2, std2, rstd2 = sb("var2", [P, KT_]), sb("std2", [P, KT_]), sb("rstd2", [P, KT_])
        tm = {k: sb(f"tm_{k}", [P, CJ]) for k in "kvr"}
        decay = sb("decay_row", [P, CJ * BT])
        wcol = sb("wcol", [P, CJ])
        dh = sb("dh", [P, CJ * BT])
        mix = {k: sb(f"mix_{k}", [P, CJ, BT]) for k in "kvr"}
        k_, v_, sr = sb("k", [P, CJ * BT]), sb("v", [P, CJ * BT]), sb("er", [P, CJ * BT])
        pp = sb("pp", [P, 1 + CJ * BT])
        aa = sb("aa", [P, 1 + CJ * BT])
        bb = sb("bb", [P, 1 + CJ * BT])
        z1, z2, z3, z4 = (sb(f"z{q}", [P, CJ * BT]) for q in range(1, 5))
        num, den = sb("num", [P, CJ * BT]), sb("den", [P, CJ * BT])
        gated = sb("gated", [P, CJ, BT])
        lin_ps = {k: [ps(f"{k}_ps{o}") for o in range(CJ)] for k in "kvr"}
        loaded, made = sem("loaded"), sem("made")
        V = Steps(sem("vector"), LN_V[:-1] + ["var2", "eps2", "both", ("norm", KT_), ("plain", KT_), "shift", "first",
                                              ("mix", 3 * CJ), "pp", "z2", ("z1", CJ), "cut_z1", "cut_pp",
                                              ("z4", CJ), ("z3", CJ), "e2", "z3b", "kv", "aa", "bb", "num", "den",
                                              "last_num", "last_num2", "den2", "inv", "gated", ("added", CJ)])
        A = Steps(sem("scalar"), LN_A[:1] + ["std2"] + LN_A[1:] + [("k", CJ), ("v", CJ), ("r", CJ), "e2b", "e1b", "e1", "e2"])
        T_ = Steps(sem("tensor"), LN_T + [("k", CJ), ("v", CJ), ("r", CJ), ("y", CJ)])
        block = ctx.enter_context(nc.Block())

        @block.sync
        def _(e):
            for k in "kvro":
                e.dma_start(w[k][:, :, :], c.d[f"l0_w{k}m"]).then_inc(loaded, 16)

        @block.tensor
        def _(e):
            T_.start(e)
            e.wait_ge(loaded, 64)
            with e.Fori(0, BLOCKS) as i:
                ln_tensor(e, V, T_, n, i, c, lambda: e.wait_ge(*V.at("added", i - 1)))
                for q, k in enumerate("kvr"):
                    e.wait_ge(*V.at("mix", i, 2 * q + 1))
                    for o in range(CJ):
                        e.wait_ge(*A.at(k, i - 1, o))
                        for j in range(CJ):
                            m = e.matmul(lin_ps[k][o][:, :], w[k][:, j, o * P:(o + 1) * P], mix[k][:, j, :],
                                         start=(j == 0), stop=(j == CJ - 1))
                        m.then_inc(T_(k), 1)
                e.wait_ge(*V.at("gated", i))
                e.wait_ge(*A.at("features", i))
                for b in range(CJ):
                    for k in (2 * b, 2 * b + 1):
                        for j in range(CJ):
                            m = e.matmul(n.ps[b][:, (k % 2) * C:(k % 2 + 1) * C], gated[:, j, k * P:(k + 1) * P],
                                         w["o"][:, j, :], start=(j == 0), stop=(j == CJ - 1))
                    m.then_inc(T_("y"), 1)

        @block.vector
        def _(e):
            V.start(e)
            for k in "kvr":
                e.tensor_scalar(tm[k][:, :], c.vec[f"tm_{k}"], 1.0, None, ALU.subtract).then_inc(made, 1)
            e.wait_ge(made, 4)
            e.tensor_scalar(wcol[:, :], wcol[:, :], -1.0, None, ALU.mult).then_inc(made, 1)
            e.memset(decay[:, :], 0.0).then_inc(made, 1)
            e.memset(pp[:, 0:1], FAR).then_inc(made, 1)
            e.memset(aa[:, 0:1], 0.0).then_inc(made, 1)
            e.memset(bb[:, 0:1], 0.0).then_inc(made, 1)
            e.wait_ge(made, 9)
            for j in range(CJ):
                e.tensor_scalar(decay[:, j * BT:(j + 1) * BT], decay[:, j * BT:(j + 1) * BT], wcol[:, j:j + 1], None,
                                ALU.add).then_inc(made, 1)
            e.wait_ge(made, 11)
            e.memset(by_batch(decay[:, :])[:, :, 0:1], FAR).then_inc(made, 1)
            e.wait_ge(made, 12)
            N = CJ * BT
            pp_now, pp_was, aa_was, bb_was = pp[:, 1:1 + N], pp[:, 0:N], aa[:, 0:N], bb[:, 0:N]
            first = c.vec["first"]

            def half(ap, j):
                return ap[:, j * BT:(j + 1) * BT]

            with e.Fori(0, BLOCKS) as i:
                def second():
                    e.wait_ge(*V.at("rstd", i))
                    e.tensor_tensor(var2[:, :], n.var[:, :], n.rstd[:, :], ALU.mult).then_inc(V("var2"), 1)
                    e.wait_ge(*V.at("var2", i))
                    e.tensor_tensor(var2[:, :], var2[:, :], n.rstd[:, :], ALU.mult).then_inc(V("eps2"), 1)
                    e.wait_ge(*A.at("std2", i))
                    e.reciprocal(rstd2[:, :], std2[:, :]).then_inc(V("both"), 1)
                    e.wait_ge(*V.at("both", i))
                    e.wait_ge(*T_.at("turned", i - 1))

                ln_vector(e, V, A, n, c.X, i, second)
                e.wait_ge(*V.at("norm", i))
                for k in range(KT_):
                    e.tensor_copy(xn0[:, k, :], n.xn[:, k, :]).then_inc(V("plain"), 1)
                e.wait_ge(*V.at("plain", i))
                h = n.hT[:, :, :].rearrange("p j t -> p (j t)")
                e.wait_ge(*A.at("features", i))
                e.tensor_tensor(by_batch(dh[:, :])[:, :, 1:T], by_batch(h)[:, :, 1:T], by_batch(h)[:, :, 0:T - 1],
                                ALU.subtract).then_inc(V("shift"), 1)
                e.tensor_copy(by_batch(dh[:, :])[:, :, 0:1], by_batch(h)[:, :, 0:1]).then_inc(V("first"), 1)
                e.wait_ge(*V.at("first", i))
                for k in "kvr":
                    e.wait_ge(*T_.at(k, i - 1))
                    for j in range(CJ):
                        e.scalar_tensor_tensor(mix[k][:, j, :], half(dh, j), tm[k][:, j:j + 1], n.hT[:, j, :],
                                               ALU.mult, ALU.add).then_inc(V("mix"), 1)
                e.wait_ge(*A.at("k", i))
                e.tensor_tensor_scan(pp_now, decay[:, :], k_[:, :], 0.0, ALU.add, ALU.max).then_inc(V("pp"), 1)
                e.wait_ge(*V.at("pp", i))
                e.tensor_tensor(z2[:, :], k_[:, :], pp_now, ALU.subtract).then_inc(V("z2"), 1)
                for j in range(CJ):
                    e.scalar_tensor_tensor(half(z1, j), half(pp_was, j), wcol[:, j:j + 1], half(pp_now, j), ALU.add,
                                           ALU.subtract).then_inc(V("z1"), 1)
                e.wait_ge(*V.at("z1", i))
                e.memset(by_batch(z1[:, :])[:, :, 0:1], FAR).then_inc(V("cut_z1"), 1)
                e.memset(by_batch(pp_was)[:, :, 0:1], FAR).then_inc(V("cut_pp"), 1)
                e.wait_ge(*V.at("cut_pp", i))
                for j in range(CJ):
                    e.scalar_tensor_tensor(half(z4, j), half(k_, j), first[:, j:j + 1], half(pp_was, j), ALU.add,
                                           ALU.max).then_inc(V("z4"), 1)
                e.wait_ge(*V.at("z4", i))
                for j in range(CJ):
                    e.scalar_tensor_tensor(half(z3, j), half(k_, j), first[:, j:j + 1], half(z4, j), ALU.add,
                                           ALU.subtract).then_inc(V("z3"), 1)
                e.wait_ge(*V.at("z3", i))
                e.tensor_tensor(z4[:, :], pp_was, z4[:, :], ALU.subtract).then_inc(V("e2"), 1)
                e.wait_ge(*A.at("v", i))
                e.wait_ge(*A.at("e2b", i))
                e.tensor_tensor(num[:, :], z2[:, :], v_[:, :], ALU.mult).then_inc(V("z3b"), 1)
                e.wait_ge(*V.at("z3b", i))
                e.wait_ge(*A.at("e1b", i))
                e.tensor_tensor_scan(aa[:, 1:1 + N], z1[:, :], num[:, :], 0.0, ALU.mult, ALU.add).then_inc(V("kv"), 1)
                e.tensor_tensor_scan(bb[:, 1:1 + N], z1[:, :], z2[:, :], 0.0, ALU.mult, ALU.add).then_inc(V("aa"), 1)
                e.wait_ge(*V.at("aa", i))
                e.wait_ge(*A.at("e2", i))
                e.tensor_tensor(num[:, :], z4[:, :], aa_was, ALU.mult).then_inc(V("bb"), 1)
                e.tensor_tensor(den[:, :], z4[:, :], bb_was, ALU.mult).then_inc(V("num"), 1)
                e.tensor_tensor(z2[:, :], z3[:, :], v_[:, :], ALU.mult).then_inc(V("den"), 1)
                e.wait_ge(*V.at("den", i))
                e.tensor_tensor(num[:, :], num[:, :], z2[:, :], ALU.add).then_inc(V("last_num"), 1)
                e.tensor_tensor(den[:, :], den[:, :], z3[:, :], ALU.add).then_inc(V("last_num2"), 1)
                e.wait_ge(*V.at("last_num2", i))
                e.wait_ge(*A.at("r", i))
                e.tensor_tensor(num[:, :], sr[:, :], num[:, :], ALU.mult).then_inc(V("den2"), 1)
                e.reciprocal(den[:, :], den[:, :]).then_inc(V("inv"), 1)
                e.wait_ge(*V.at("inv", i))
                e.wait_ge(*T_.at("y", i - 1))
                e.tensor_tensor(gated[:, :, :].rearrange("p j t -> p (j t)"), num[:, :], den[:, :],
                                ALU.mult).then_inc(V("gated"), 1)
                for b in range(CJ):
                    e.wait_ge(*T_.at("y", i, b))
                    e.tensor_tensor(c.XI[:, bass.ds(i * KT_ + 2 * b, 2), :], xn0[:, 2 * b:2 * b + 2, :],
                                    n.ps[b][:, :].rearrange("p (k f) -> p k f", k=2), ALU.add).then_inc(V("added"), 1)

        @block.scalar
        def _(e):
            A.start(e)
            e.activation(wcol[:, :], c.vec["decay"], ACT.Exp).then_inc(made, 1)
            with e.Fori(0, BLOCKS) as i:
                ln_scalar_std(e, V, A, n, i, c)
                e.wait_ge(*V.at("eps2", i))
                e.activation(std2[:, :], var2[:, :], ACT.Sqrt, bias=c.eps[:, 0:1]).then_inc(A("std2"), 1)
                ln_scalar_features(e, T_, A, n, i, lambda: e.wait_ge(*V.at("mix", i - 1)), c.vec["ln1_g"],
                                   c.vec["ln1_b"])
                for k, dst in (("k", k_), ("v", v_), ("r", sr)):
                    e.wait_ge(*V.at("den2", i - 1))
                    for o in range(CJ):
                        e.wait_ge(*T_.at(k, i, o))
                        e.activation(dst[:, o * BT:(o + 1) * BT], lin_ps[k][o][:, :],
                                     ACT.Sigmoid if k == "r" else ACT.Copy).then_inc(A(k), 1)
                e.wait_ge(*V.at("z2", i))
                e.activation(z2[:, :], z2[:, :], ACT.Exp).then_inc(A("e2b"), 1)
                e.wait_ge(*V.at("cut_z1", i))
                e.activation(z1[:, :], z1[:, :], ACT.Exp).then_inc(A("e1b"), 1)
                e.wait_ge(*V.at("z3", i))
                e.activation(z3[:, :], z3[:, :], ACT.Exp).then_inc(A("e1"), 1)
                e.wait_ge(*V.at("e2", i))
                e.activation(z4[:, :], z4[:, :], ACT.Exp).then_inc(A("e2"), 1)


def l0_channel_mix(nc, c):
    with ExitStack() as ctx:
        sb, ps, sem = tensors(nc, ctx, "cm")
        HC = HID // P
        wk, wv, wr = sb("wk", [P, CJ, HID]), sb("wv", [P, HC, C]), sb("wr", [P, CJ, C])
        n = Norm(sb, ps)
        tm = {k: sb(f"tm_{k}", [P, CJ]) for k in "kr"}
        dh = sb("dh", [P, CJ * BT])
        mix = {k: sb(f"mix_{k}", [P, CJ, BT]) for k in "kr"}
        relu = [sb(f"relu{u}", [P, BT]) for u in range(2)]
        kk = sb("kk", [P, HC, BT])
        gate = sb("gate", [P, KT_, C])
        k_ps = [ps(f"k_ps{u}") for u in range(2)]
        r_ps = [ps(f"r_ps{u}") for u in range(2)]
        v_ps = [ps(f"v_ps{u}") for u in range(2)]
        loaded, made = sem("loaded"), sem("made")
        V = Steps(sem("vector"), LN_V + ["shift", "first", ("mix", 2 * CJ), ("square", HC), ("rkv", 2), ("plus", 2), ("added", 2)])
        A = Steps(sem("scalar"), LN_A + [("relu", HC), ("gate", 2)])
        T_ = Steps(sem("tensor"), LN_T + [("k", HC), ("r", 2), ("v", 2)])
        block = ctx.enter_context(nc.Block())

        @block.sync
        def _(e):
            e.dma_start(wk[:, :, :], c.d["l0_wck"]).then_inc(loaded, 16)
            e.dma_start(wr[:, :, :], c.d["l0_wcr"]).then_inc(loaded, 16)
            e.dma_start(wv[:, :, :], c.d["l0_wcv"]).then_inc(loaded, 16)

        @block.tensor
        def _(e):
            T_.start(e)
            e.wait_ge(loaded, 48)
            with e.Fori(0, BLOCKS) as i:
                ln_tensor(e, V, T_, n, i, c, lambda: e.wait_ge(*A.at("features", i - 1)))
                e.wait_ge(*V.at("mix", i))
                for h in range(HC):
                    e.wait_ge(*(A.at("relu", i, h - 2) if h >= 2 else A.at("relu", i - 1)))
                    for j in range(CJ):
                        m = e.matmul(k_ps[h % 2][:, :], wk[:, j, h * P:(h + 1) * P], mix["k"][:, j, :],
                                     start=(j == 0), stop=(j == CJ - 1))
                    m.then_inc(T_("k"), 1)
                for b in range(2):
                    e.wait_ge(*A.at("gate", i - 1, b))
                    for k in (2 * b, 2 * b + 1):
                        for j in range(CJ):
                            m = e.matmul(r_ps[b][:, (k % 2) * C:(k % 2 + 1) * C], mix["r"][:, j, k * P:(k + 1) * P],
                                         wr[:, j, :], start=(j == 0), stop=(j == CJ - 1))
                    m.then_inc(T_("r"), 1)
                e.wait_ge(*V.at("square", i))
                for b in range(2):
                    e.wait_ge(*V.at("rkv", i - 1, b))
                    for k in (2 * b, 2 * b + 1):
                        for h in range(HC):
                            m = e.matmul(v_ps[b][:, (k % 2) * C:(k % 2 + 1) * C], kk[:, h, k * P:(k + 1) * P],
                                         wv[:, h, :], start=(h == 0), stop=(h == HC - 1))
                    m.then_inc(T_("v"), 1)

        @block.vector
        def _(e):
            V.start(e)
            for k in "kr":
                e.tensor_scalar(tm[k][:, :], c.vec[f"cm_{k}"], 1.0, None, ALU.subtract).then_inc(made, 1)
            e.wait_ge(made, 2)
            with e.Fori(0, BLOCKS) as i:
                ln_vector(e, V, A, n, c.XI, i, lambda: e.wait_ge(*T_.at("turned", i - 1)))
                h = n.hT[:, :, :].rearrange("p j t -> p (j t)")
                e.wait_ge(*A.at("features", i))
                e.tensor_tensor(by_batch(dh[:, :])[:, :, 1:T], by_batch(h)[:, :, 1:T], by_batch(h)[:, :, 0:T - 1],
                                ALU.subtract).then_inc(V("shift"), 1)
                e.tensor_copy(by_batch(dh[:, :])[:, :, 0:1], by_batch(h)[:, :, 0:1]).then_inc(V("first"), 1)
                e.wait_ge(*V.at("first", i))
                for k in "kr":
                    e.wait_ge(*T_.at(k, i - 1))
                    for j in range(CJ):
                        e.scalar_tensor_tensor(mix[k][:, j, :], dh[:, j * BT:(j + 1) * BT], tm[k][:, j:j + 1],
                                               n.hT[:, j, :], ALU.mult, ALU.add).then_inc(V("mix"), 1)
                e.wait_ge(*T_.at("v", i - 1))
                for q in range(HC):
                    e.wait_ge(*A.at("relu", i, q))
                    e.tensor_tensor(kk[:, q, :], relu[q % 2][:, :], relu[q % 2][:, :], ALU.mult).then_inc(V("square"), 1)
                for b in range(2):
                    e.wait_ge(*A.at("gate", i, b))
                    e.wait_ge(*T_.at("v", i, b))
                    g = gate[:, 2 * b:2 * b + 2, :]
                    e.tensor_tensor(g, g, v_ps[b][:, :].rearrange("p (k f) -> p k f", k=2), ALU.mult).then_inc(V("rkv"), 1)
                e.wait_ge(*V.at("rkv", i))
                for b in range(2):
                    tiles = bass.ds(i * KT_ + 2 * b, 2)
                    g = gate[:, 2 * b:2 * b + 2, :]
                    e.tensor_tensor(g, g, c.XI[:, tiles, :], ALU.add).then_inc(V("plus"), 1)
                e.wait_ge(*V.at("plus", i))
                for b in range(2):
                    tiles = bass.ds(i * KT_ + 2 * b, 2)
                    g = gate[:, 2 * b:2 * b + 2, :]
                    e.tensor_tensor(c.X[:, tiles, :], c.X[:, tiles, :], g, ALU.add).then_inc(V("added"), 1)

        @block.scalar
        def _(e):
            A.start(e)
            with e.Fori(0, BLOCKS) as i:
                ln_scalar_std(e, V, A, n, i, c)
                ln_scalar_features(e, T_, A, n, i, lambda: e.wait_ge(*V.at("mix", i - 1)), c.vec["ln2_g"],
                                   c.vec["ln2_b"])
                for h in range(HC):
                    e.wait_ge(*T_.at("k", i, h))
                    e.wait_ge(*(V.at("square", i, h - 2) if h >= 2 else V.at("square", i - 1)))
                    e.activation(relu[h % 2][:, :], k_ps[h % 2][:, :], ACT.Relu).then_inc(A("relu"), 1)
                for b in range(2):
                    e.wait_ge(*T_.at("r", i, b))
                    e.wait_ge(*V.at("added", i - 1))
                    e.activation(gate[:, 2 * b:2 * b + 2, :].rearrange("p k f -> p (k f)"), r_ps[b][:, :],
                                 ACT.Sigmoid).then_inc(A("gate"), 1)



def over(ap, shape, at):
    return ap.unsqueeze(at).broadcast_to(list(shape))


def l0_experts(nc, c):
    with ExitStack() as ctx:
        sb, ps, sem = tensors(nc, ctx, "mo")
        wg, we = sb("wg", [P, CJ, E]), sb("we", [P, CJ, E * C])
        n = Norm(sb, ps)
        lg, prob, top = sb("lg", [P, KT_, E]), sb("prob", [P, KT_, E]), sb("top", [P, KT_, 8])
        idx, idf = sb("idx", [P, KT_, 8], U32), sb("idf", [P, KT_, 8])
        big, both = sb("big", [P, KT_]), sb("both", [P, KT_])
        g0, g1, gate = sb("g0", [P, KT_, E]), sb("g1", [P, KT_, E]), sb("gate", [P, KT_, E])
        gate_t = sb("gate_t", [E, BT])
        g_ps, b_ps = ps("g_ps"), ps("b_ps")
        e_ps = [ps(f"e_ps{q}") for q in range(E // 2)]
        loaded, seen = sem("loaded"), sem("seen")
        V = Steps(sem("vector"), LN_V + ["logits", "big", "less", ("top", KT_), ("index", KT_), "float", "sum", "flip",
                                         "hot0", "hot1", "part0", "part1", "join", "gate"]
                  + KT_ * ([("expert", E)] + ["bias"]))
        A = Steps(sem("scalar"), LN_A + ["exp", "gate_t"])
        T_ = Steps(sem("tensor"), LN_T + ["logits", "gate_t"] + KT_ * ["bias", ("expert", E // 2)])
        block = ctx.enter_context(nc.Block())
        shape = [P, KT_, E]

        @block.sync
        def _(e):
            e.dma_start(wg[:, :, :], c.d["l0_wg"]).then_inc(loaded, 16)
            e.dma_start(we[:, :, :], c.d["l0_we"]).then_inc(loaded, 16)

        @block.tensor
        def _(e):
            T_.start(e)
            e.wait_ge(loaded, 32)
            with e.Fori(0, BLOCKS) as i:
                ln_tensor(e, V, T_, n, i, c, lambda: e.wait_ge(*A.at("features", i - 1)))
                e.wait_ge(*A.at("features", i))
                e.wait_ge(*A.at("gate_t", i - 1))
                for k in range(KT_):
                    for j in range(CJ):
                        m = e.matmul(g_ps[:, k * E:(k + 1) * E], n.hT[:, j, k * P:(k + 1) * P], wg[:, j, :],
                                     start=(j == 0), stop=(j == CJ - 1))
                m.then_inc(T_("logits"), 1)
                e.wait_ge(*V.at("gate", i))
                for k in range(KT_):
                    m = e.transpose(g_ps[0:E, k * P:(k + 1) * P], gate[:, k, :], c.ident[:, :])
                m.then_inc(T_("gate_t"), 1)
                e.wait_ge(*A.at("gate_t", i))
                for k in range(KT_):
                    e.wait_ge(*(V.at("bias", i, k - 1) if k else V.at("bias", i - 1)))
                    e.matmul(b_ps[:, 0:C], gate_t[:, k * P:(k + 1) * P], c.sm["be"][0:E, :], start=True,
                             stop=True).then_inc(T_("bias"), 1)
                    for q in range(E // 2):
                        e.wait_ge(*(V.at("expert", i, (k - 1) * E + 2 * q + 1) if k
                                    else V.at("expert", i - 1, (KT_ - 1) * E + 2 * q + 1)))
                        for j in range(CJ):
                            m = e.matmul(e_ps[q][:, :], n.hT[:, j, k * P:(k + 1) * P],
                                         we[:, j, q * 2 * C:(q + 1) * 2 * C], start=(j == 0), stop=(j == CJ - 1))
                        m.then_inc(T_("expert"), 1)

        @block.vector
        def _(e):
            V.start(e)
            with e.Fori(0, BLOCKS) as i:
                ln_vector(e, V, A, n, c.X, i, lambda: e.wait_ge(*T_.at("turned", i - 1)))
                e.wait_ge(*T_.at("logits", i))
                e.tensor_copy(lg[:, :, :].rearrange("p k e -> p (k e)"), g_ps[:, 0:KT_ * E]).then_inc(V("logits"), 1)
                e.wait_ge(*V.at("logits", i))
                e.tensor_reduce(big[:, :], lg[:, :, :], AX.X, ALU.max).then_inc(V("big"), 1)
                e.wait_ge(*V.at("big", i))
                e.tensor_tensor(lg[:, :, :], lg[:, :, :], over(big[:, :], shape, 2), ALU.subtract).then_inc(V("less"), 1)
                e.wait_ge(*A.at("exp", i))
                e.sem_inc(seen, 1)
                for k in range(KT_):
                    e.max(top[:, k, :], prob[:, k, :]).then_inc(V("top"), 1)
                e.wait_ge(*V.at("top", i))
                e.sem_inc(seen, 1)
                for k in range(KT_):
                    e.max_index(idx[:, k, :], top[:, k, :], prob[:, k, :]).then_inc(V("index"), 1)
                e.wait_ge(*V.at("index", i))
                e.tensor_copy(idf[:, :, :], idx[:, :, :]).then_inc(V("float"), 1)
                e.tensor_tensor(both[:, :], top[:, :, 0], top[:, :, 1], ALU.add).then_inc(V("sum"), 1)
                e.wait_ge(*V.at("sum", i))
                e.reciprocal(both[:, :], both[:, :]).then_inc(V("flip"), 1)
                e.tensor_tensor(g0[:, :, :], over(c.iota, shape, 1), idf[:, :, 0:1].broadcast_to(shape),
                                ALU.is_equal).then_inc(V("hot0"), 1)
                e.tensor_tensor(g1[:, :, :], over(c.iota, shape, 1), idf[:, :, 1:2].broadcast_to(shape),
                                ALU.is_equal).then_inc(V("hot1"), 1)
                e.wait_ge(*V.at("hot1", i))
                e.tensor_tensor(g0[:, :, :], g0[:, :, :], top[:, :, 0:1].broadcast_to(shape), ALU.mult).then_inc(V("part0"), 1)
                e.tensor_tensor(g1[:, :, :], g1[:, :, :], top[:, :, 1:2].broadcast_to(shape), ALU.mult).then_inc(V("part1"), 1)
                e.wait_ge(*V.at("part1", i))
                e.tensor_tensor(g0[:, :, :], g0[:, :, :], g1[:, :, :], ALU.add).then_inc(V("join"), 1)
                e.wait_ge(*V.at("join", i))
                e.tensor_tensor(gate[:, :, :], g0[:, :, :], over(both[:, :], shape, 2), ALU.mult).then_inc(V("gate"), 1)
                e.wait_ge(*V.at("gate", i))
                for k in range(KT_):
                    x = c.X[:, i * KT_ + k, :]
                    for q in range(E):
                        if q % 2 == 0:
                            e.wait_ge(*T_.at("expert", i, k * (E // 2) + q // 2))
                        if q:
                            e.wait_ge(*V.at("expert", i, k * E + q - 1))
                        e.scalar_tensor_tensor(x, e_ps[q // 2][:, (q % 2) * C:(q % 2 + 1) * C], gate[:, k, q:q + 1], x,
                                               ALU.mult, ALU.add).then_inc(V("expert"), 1)
                    e.wait_ge(*T_.at("bias", i, k))
                    e.wait_ge(*V.at("expert", i, k * E + E - 1))
                    e.tensor_tensor(x, x, b_ps[:, 0:C], ALU.add).then_inc(V("bias"), 1)

        @block.scalar
        def _(e):
            A.start(e)
            with e.Fori(0, BLOCKS) as i:
                ln_scalar_std(e, V, A, n, i, c)
                ln_scalar_features(e, T_, A, n, i, lambda: e.wait_ge(*T_.at("expert", i - 1)))
                e.wait_ge(*V.at("less", i))
                e.activation(prob[:, :, :].rearrange("p k e -> p (k e)"), lg[:, :, :].rearrange("p k e -> p (k e)"),
                             ACT.Exp).then_inc(A("exp"), 1)
                e.wait_ge(*T_.at("gate_t", i))
                e.activation(gate_t[:, :], g_ps[0:E, :], ACT.Copy).then_inc(A("gate_t"), 1)



QUANT_V = ["amax", "guard", "inv", "scale", ("round", KT_), "int", "rt_inv", "dequant"]
QUANT_A = [("squares", KT_), "rt"]


class Quant:

    def __init__(self, sb):
        self.ss, self.amax, self.rt = (sb(f"q_{k}", [P, KT_]) for k in ("ss", "amax", "rt"))
        self.guard, self.scale, self.factor = (sb(f"q_{k}", [P, KT_]) for k in ("guard", "scale", "factor"))
        self.junk = sb("q_junk", [P, C])
        self.big = sb("q_big", [P, KT_, C])
        self.ints = sb("q_ints", [P, KT_, C], BF16)


def quant_vector(e, V, A, q, src, ready, i, free):
    e.wait_ge(*ready)
    e.tensor_reduce(q.amax[:, :], src[:, :, :], AX.X, ALU.max, apply_absolute_value=True).then_inc(V("amax"), 1)
    e.wait_ge(*V.at("amax", i))
    e.wait_ge(*A.at("rt", i))
    e.scalar_tensor_tensor(q.guard[:, :], q.rt[:, :], 1e-5, q.amax[:, :], ALU.mult, ALU.max).then_inc(V("guard"), 1)
    e.wait_ge(*V.at("guard", i))
    e.reciprocal(q.scale[:, :], q.guard[:, :]).then_inc(V("inv"), 1)
    e.wait_ge(*V.at("inv", i))
    e.tensor_scalar(q.scale[:, :], q.scale[:, :], 127.0, None, ALU.mult).then_inc(V("scale"), 1)
    e.wait_ge(*V.at("scale", i))
    for k in range(KT_):
        e.tensor_scalar(q.big[:, k, :], src[:, k, :], q.scale[:, k:k + 1], ROUND, ALU.mult, ALU.add).then_inc(V("round"), 1)
    e.wait_ge(*V.at("round", i))
    free()
    e.tensor_scalar(q.ints[:, :, :], q.big[:, :, :], ROUND, None, ALU.subtract).then_inc(V("int"), 1)
    e.reciprocal(q.rt[:, :], q.rt[:, :]).then_inc(V("rt_inv"), 1)
    e.wait_ge(*V.at("rt_inv", i))
    e.scalar_tensor_tensor(q.factor[:, :], q.guard[:, :], 1.0 / 127.0, q.rt[:, :], ALU.mult,
                           ALU.mult).then_inc(V("dequant"), 1)


def quant_scalar(e, V, A, q, src, ready, i, c):
    e.wait_ge(*ready)
    e.wait_ge(*V.at("dequant", i - 1))
    for k in range(KT_):
        e.wait_ge(*(A.at("squares", i, k - 1) if k else A.at("squares", i - 1)))
        e.activation(q.junk[:, :], src[:, k, :], ACT.Square, accum_out=q.ss[:, k:k + 1]).then_inc(A("squares"), 1)
    e.wait_ge(*A.at("squares", i))
    e.activation(q.rt[:, :], q.ss[:, :], ACT.Sqrt, scale=1.0 / C, bias=c.eps[:, 1:2]).then_inc(A("rt"), 1)


def l1_prepare(nc, c):
    with ExitStack() as ctx:
        sb, ps, sem = tensors(nc, ctx, "pr")
        names = [("q", C), ("k", P), ("v", P), ("o", C)]
        w = {k: sb(f"w{k}", [P, CJ, o]) for k, o in names}
        part, mean, inv = sb("part", [P, 4]), sb("mean", [P, 4]), sb("inv", [P, 4])
        big = {k: sb(f"big{k}", [P, CJ, o]) for k, o in names}
        rt, guard = sb("rt", [P, 2 * B]), sb("guard", [P, 2 * B])
        lastq = sb("lastq", [B, 4])
        lastf = sb("lastf", [B, 4])
        last, last_big = sb("last", [B, C]), sb("last_big", [B, C])
        last_i = sb("last_i", [B, C], BF16)
        last_t = sb("last_t", [P, CJ, B], BF16)
        kv = sb("kv", [B, 2 * P])
        sum_ps, kv_ps, kt_ps = ps("sum_ps"), ps("kv_ps"), ps("kt_ps")
        t_ps = ps("t_ps", (P, 2 * 512), BF16)
        loaded, v, a, t, moved = sem("loaded"), sem("vector"), sem("scalar"), sem("tensor"), sem("moved")
        made = sem("made")
        block = ctx.enter_context(nc.Block())

        @block.sync
        def _(e):
            for k, _ in names:
                e.dma_start(w[k][:, :, :], c.d[f"l1_w{k}"]).then_inc(loaded, 16)
            e.dma_start(last[:, :], c.d["ctx_last"]).then_inc(loaded, 16)
            e.wait_ge(v, 26)
            e.dma_start(c.d["bounce"], kv[:, P:2 * P]).then_inc(moved, 16)
            e.wait_ge(moved, 16)

        @block.vector
        def _(e):
            e.wait_ge(loaded, 80)
            for q, (k, _) in enumerate(names):
                e.tensor_reduce(part[:, q:q + 1], w[k][:, :, :], AX.XY, ALU.add, apply_absolute_value=True).then_inc(v, 1)
            e.wait_ge(t, 1)
            for q, (_, o) in enumerate(names):
                e.tensor_scalar(mean[:, q:q + 1], sum_ps[:, q:q + 1], 1.0 / (C * o), 1e-5, ALU.mult, ALU.max).then_inc(v, 1)
            e.wait_ge(v, 8)
            e.reciprocal(inv[:, :], mean[:, :]).then_inc(v, 1)
            e.wait_ge(v, 9)
            for q, (k, _) in enumerate(names):
                e.tensor_scalar(big[k][:, :, :], w[k][:, :, :], inv[:, q:q + 1], ROUND, ALU.mult, ALU.add).then_inc(v, 1)
            e.wait_ge(v, 13)
            for k, _ in names:
                e.tensor_scalar(big[k][:, :, :], big[k][:, :, :], ROUND, 1.0, ALU.subtract, ALU.min).then_inc(v, 1)
            e.wait_ge(v, 17)
            e.tensor_scalar(c.wq[:, :, :], big["q"][:, :, :], -1.0, None, ALU.max).then_inc(v, 1)
            e.tensor_scalar(c.wkv[:, :, 0:P], big["k"][:, :, :], -1.0, None, ALU.max).then_inc(v, 1)
            e.tensor_scalar(c.wkv[:, :, P:2 * P], big["v"][:, :, :], -1.0, None, ALU.max).then_inc(v, 1)
            e.tensor_scalar(c.wo[:, :, :], big["o"][:, :, :], -1.0, None, ALU.max).then_inc(v, 1)
            e.tensor_scalar(c.wf[:, 0:1], mean[:, 0:1], HD ** -0.5, None, ALU.mult).then_inc(v, 1)
            e.tensor_copy(c.wf[:, 1:4], mean[:, 1:4]).then_inc(v, 1)
            e.tensor_reduce(lastq[:, 0:1], last[:, :], AX.X, ALU.max, apply_absolute_value=True).then_inc(v, 1)
            e.wait_ge(v, 24)
            e.wait_ge(a, 3)
            e.scalar_tensor_tensor(lastq[:, 2:3], lastq[:, 1:2], 1e-5, lastq[:, 0:1], ALU.mult, ALU.max).then_inc(made, 1)
            e.scalar_tensor_tensor(guard[:, :], rt[:, :], 1e-5, c.c_max[:, :], ALU.mult, ALU.max).then_inc(made, 1)
            e.wait_ge(made, 2)
            e.reciprocal(lastq[:, 3:4], lastq[:, 2:3]).then_inc(made, 1)
            e.reciprocal(rt[:, :], rt[:, :]).then_inc(made, 1)
            e.reciprocal(lastq[:, 1:2], lastq[:, 1:2]).then_inc(made, 1)
            e.wait_ge(made, 5)
            e.tensor_scalar(lastq[:, 3:4], lastq[:, 3:4], 127.0, None, ALU.mult).then_inc(made, 1)
            e.scalar_tensor_tensor(guard[:, :], guard[:, :], 1.0 / 127.0, rt[:, :], ALU.mult, ALU.mult).then_inc(made, 1)
            e.scalar_tensor_tensor(lastf[:, 1:2], lastq[:, 2:3], 1.0 / 127.0, lastq[:, 1:2], ALU.mult, ALU.mult).then_inc(made, 1)
            e.wait_ge(made, 8)
            e.tensor_scalar(c.kf[:, :], guard[:, :], mean[:, 1:2], None, ALU.mult).then_inc(made, 1)
            e.tensor_scalar(c.vf[:, :], guard[:, :], mean[:, 2:3], None, ALU.mult).then_inc(made, 1)
            e.tensor_scalar(lastf[:, 2:3], mean[0:B, 1:2], lastf[:, 1:2], None, ALU.mult).then_inc(made, 1)
            e.tensor_scalar(lastf[:, 3:4], mean[0:B, 2:3], lastf[:, 1:2], None, ALU.mult).then_inc(made, 1)
            e.tensor_scalar(last_big[:, :], last[:, :], lastq[:, 3:4], ROUND, ALU.mult, ALU.add).then_inc(made, 1)
            e.wait_ge(made, 13)
            e.tensor_scalar(last_i[:, :], last_big[:, :], ROUND, None, ALU.subtract).then_inc(made, 1)
            e.wait_ge(t, 2)
            e.tensor_copy(last_t[:, :, :].rearrange("p j b -> p (j b)"), t_ps[:, 0:CJ * B]).then_inc(made, 1)
            e.wait_ge(t, 3)
            e.tensor_scalar(kv[:, 0:P], kv_ps[0:B, 0:P], lastf[:, 2:3], None, ALU.mult).then_inc(v, 1)
            e.tensor_scalar(kv[:, P:2 * P], kv_ps[0:B, P:2 * P], lastf[:, 3:4], None, ALU.mult).then_inc(v, 1)
            e.wait_ge(t, 4)
            e.tensor_copy(c.k_last[:, :], kt_ps[:, 0:B]).then_inc(made, 1)

        @block.scalar
        def _(e):
            e.wait_ge(loaded, 80)
            e.activation(last_big[:, :], last[:, :], ACT.Square, accum_out=lastf[:, 0:1]).then_inc(a, 1)
            e.wait_ge(a, 1)
            e.activation(lastq[:, 1:2], lastf[:, 0:1], ACT.Sqrt, scale=1.0 / C, bias=c.eps[0:B, 1:2]).then_inc(a, 1)
            e.activation(rt[:, :], c.c_ss[:, :], ACT.Sqrt, scale=1.0 / C, bias=c.eps[:, 1:2]).then_inc(a, 1)

        @block.tensor
        def _(e):
            e.wait_ge(v, 4)
            e.matmul(sum_ps[:, 0:4], c.ones[:, :], part[:, :], start=True, stop=True).then_inc(t, 1)
            e.wait_ge(made, 14)
            for j in range(CJ):
                m = e.transpose(t_ps[:, j * B:(j + 1) * B], last_i[:, j * P:(j + 1) * P], c.identb[0:B, 0:B])
            m.then_inc(t, 1)
            e.wait_ge(made, 15)
            for j in range(CJ):
                m = e.matmul(kv_ps[0:B, 0:2 * P], last_t[:, j, :], c.wkv[:, j, :], start=(j == 0), stop=(j == CJ - 1))
            m.then_inc(t, 1)
            e.wait_ge(v, 26)
            e.transpose(kt_ps[:, 0:B], kv[:, 0:P], c.ident[0:B, 0:B]).then_inc(t, 1)


def l1_queries(nc, c):
    with ExitStack() as ctx:
        sb, ps, sem = tensors(nc, ctx, "q1")
        n, q = Norm(sb, ps), Quant(sb)
        f = sb("f", [P, KT_])
        xT = sb("xT", [P, CJ, BT], BF16)
        qn = sb("qn", [P, KT_, C])
        t_ps = [ps(f"t_ps{j}", (P, 2 * 512), BF16) for j in range(CJ)]
        q_ps = [ps(f"q_ps{b}") for b in range(2)]
        V = Steps(sem("vector"), LN_V + QUANT_V + ["factor", ("q", KT_)])
        A = Steps(sem("scalar"), LN_A[:1] + QUANT_A + [("xT", CJ), ("features", CJ)])
        T_ = Steps(sem("tensor"), [("ints_t", CJ), ("q", 2), ("turned", CJ)])
        block = ctx.enter_context(nc.Block())

        @block.vector
        def _(e):
            V.start(e)
            with e.Fori(0, BLOCKS) as i:
                ln_vector(e, V, A, n, c.X, i, lambda: None)
                quant_vector(e, V, A, q, n.xn, V.at("norm", i), i, lambda: e.wait_ge(*T_.at("ints_t", i - 1)))
                e.wait_ge(*V.at("dequant", i))
                e.tensor_scalar(f[:, :], q.factor[:, :], c.wf[:, 0:1], None, ALU.mult).then_inc(V("factor"), 1)
                e.wait_ge(*V.at("factor", i))
                e.wait_ge(*T_.at("turned", i - 1))
                for k in range(KT_):
                    e.wait_ge(*T_.at("q", i, k // 2))
                    e.tensor_scalar(qn[:, k, :], q_ps[k // 2][:, (k % 2) * C:(k % 2 + 1) * C], f[:, k:k + 1], None,
                                    ALU.mult).then_inc(V("q"), 1)

        @block.scalar
        def _(e):
            A.start(e)
            with e.Fori(0, BLOCKS) as i:
                ln_scalar_std(e, V, A, n, i, c)
                quant_scalar(e, V, A, q, n.xn, V.at("norm", i), i, c)
                e.wait_ge(*T_.at("q", i - 1))
                for j in range(CJ):
                    e.wait_ge(*T_.at("ints_t", i, j))
                    e.activation(xT[:, j, :], t_ps[j][:, 0:BT], ACT.Copy).then_inc(A("xT"), 1)
                for j in range(CJ):
                    e.wait_ge(*T_.at("turned", i, j))
                    e.activation(c.qT[:, j, bass.ds(i * BT, BT)], n.ps[j][:, :], ACT.Copy).then_inc(A("features"), 1)

        @block.tensor
        def _(e):
            T_.start(e)
            with e.Fori(0, BLOCKS) as i:
                e.wait_ge(*V.at("int", i))
                for j in range(CJ):
                    e.wait_ge(*A.at("xT", i - 1, j))
                    for k in range(KT_):
                        m = e.transpose(t_ps[j][:, k * P:(k + 1) * P], q.ints[:, k, j * P:(j + 1) * P], c.identb[:, :])
                    m.then_inc(T_("ints_t"), 1)
                e.wait_ge(*A.at("xT", i))
                for b in range(2):
                    e.wait_ge(*V.at("q", i - 1))
                    for k in (2 * b, 2 * b + 1):
                        for j in range(CJ):
                            m = e.matmul(q_ps[b][:, (k % 2) * C:(k % 2 + 1) * C], xT[:, j, k * P:(k + 1) * P],
                                         c.wq[:, j, :], start=(j == 0), stop=(j == CJ - 1))
                    m.then_inc(T_("q"), 1)
                ln_tensor(e, V, T_, n, i, c, lambda: e.wait_ge(*A.at("features", i - 1)), src=qn, step="q")


HALF = B // 4


def l1_keys(nc, c, half):
    with ExitStack() as ctx:
        sb, ps, sem = tensors(nc, ctx, f"k{half}")
        rows = [sb(f"rows{u}", [P, 2, C], BF16) for u in range(2)]
        xT = [sb(f"xT{u}", [P, CJ, 2 * P], BF16) for u in range(2)]
        kn = [sb(f"kn{u}", [P, 2, P]) for u in range(2)]
        t_ps = [ps(f"t_ps{u}", (P, 2 * 512), BF16) for u in range(2)]
        kv_ps = [ps(f"kv_ps{u}") for u in range(2)]
        kt_ps = [ps(f"kt_ps{u}") for u in range(2)]
        made, last = sem("made"), sem("last")
        V = Steps(sem("vector"), ["k", "v"], 2)
        A = Steps(sem("scalar"), ["xT", "kT"], 2)
        T_ = Steps(sem("tensor"), ["rows_t", "kv", "k_t"], 2)
        G = Steps(sem("pool"), ["rows"], 2)
        block = ctx.enter_context(nc.Block())
        first = half * HALF

        @block.sync
        def _(e):
            e.dma_start(c.v_last[0:1, :], c.d["bounce"][first:first + HALF, :].rearrange("(a b) f -> a (b f)", a=1))\
                .then_inc(last, 16)
            e.wait_ge(last, 16)

        @block.gpsimd
        def _(e):
            G.start(e)
            e.tensor_copy(c.kT[:, :, 2 * P], c.k_last[:, first:first + HALF]).then_inc(made, 1)
            with e.Fori(0, HALF // 2) as h:
                for u in range(2):
                    b = h * 2 + u
                    e.wait_ge(*T_.at("rows_t", b - 2))
                    e.tensor_copy(rows[u][:, :, :], c.cq[:, bass.ds(b * 2 + 2 * first, 2), :]).then_inc(G("rows"), 1)

        @block.tensor
        def _(e):
            T_.start(e)
            with e.Fori(0, HALF // 2) as h:
                for u in range(2):
                    b = h * 2 + u
                    e.wait_ge(*G.at("rows", b))
                    e.wait_ge(*A.at("xT", b - 2))
                    for j in range(CJ):
                        for m in range(2):
                            t = e.transpose(t_ps[u][:, (2 * j + m) * P:(2 * j + m + 1) * P],
                                            rows[u][:, m, j * P:(j + 1) * P], c.identb[:, :])
                    t.then_inc(T_("rows_t"), 1)
                    e.wait_ge(*A.at("xT", b))
                    e.wait_ge(*V.at("v", b - 2))
                    for m in range(2):
                        for j in range(CJ):
                            t = e.matmul(kv_ps[u][:, m * 2 * P:(m + 1) * 2 * P], xT[u][:, j, m * P:(m + 1) * P],
                                         c.wkv[:, j, :], start=(j == 0), stop=(j == CJ - 1))
                    t.then_inc(T_("kv"), 1)
                    e.wait_ge(*V.at("k", b))
                    e.wait_ge(*A.at("kT", b - 2))
                    for m in range(2):
                        t = e.transpose(kt_ps[u][:, m * P:(m + 1) * P], kn[u][:, m, :], c.ident[:, :])
                    t.then_inc(T_("k_t"), 1)

        @block.scalar
        def _(e):
            A.start(e)
            with e.Fori(0, HALF // 2) as h:
                for u in range(2):
                    b = h * 2 + u
                    e.wait_ge(*T_.at("rows_t", b))
                    e.wait_ge(*T_.at("kv", b - 2))
                    e.activation(xT[u][:, :, :].rearrange("p j m -> p (j m)"), t_ps[u][:, 0:2 * C],
                                 ACT.Copy).then_inc(A("xT"), 1)
                    e.wait_ge(*T_.at("k_t", b))
                    e.activation(c.kT[:, b, 0:2 * P], kt_ps[u][:, 0:2 * P], ACT.Copy).then_inc(A("kT"), 1)

        @block.vector
        def _(e):
            V.start(e)
            with e.Fori(0, HALF // 2) as h:
                for u in range(2):
                    b = h * 2 + u
                    shape = [P, 2, P]
                    r = bass.ds(b * 2 + 2 * first, 2)
                    kv = kv_ps[u][:, :].rearrange("p (m f) -> p m f", m=2)
                    e.wait_ge(*T_.at("kv", b))
                    e.wait_ge(*T_.at("k_t", b - 2))
                    e.tensor_tensor(kn[u][:, :, :], kv[:, :, 0:P], over(c.kf[:, r], shape, 2), ALU.mult).then_inc(V("k"), 1)
                    e.tensor_tensor(c.v[:, b, :, :], kv[:, :, P:2 * P], over(c.vf[:, r], shape, 2),
                                    ALU.mult).then_inc(V("v"), 1)
            e.wait_ge(made, 1)


def l1_attention(nc, c, half):
    with ExitStack() as ctx:
        sb, ps, sem = tensors(nc, ctx, f"t{half}")
        qd = [sb(f"qd{u}", [P, 2, KVH, T]) for u in range(2)]
        p = [[sb(f"p{u}{s}", [P, 2, M]) for s in range(2)] for u in range(2)]
        pt = [[sb(f"pt{u}{s}", [P, 2, 2, P]) for s in range(2)] for u in range(2)]
        pl = [[sb(f"pl{u}{s}", [1, 2 * P]) for s in range(2)] for u in range(2)]
        mx = [sb(f"mx{u}", [P, 2, 2]) for u in range(2)]
        tot = [sb(f"tot{u}", [P, 2, 2]) for u in range(2)]
        inv = [sb(f"inv{u}", [P, 2, 2]) for u in range(2)]
        s_ps = [ps(f"s_ps{s}", (P, 1024)) for s in range(2)]
        pt_ps = [ps(f"pt_ps{s}") for s in range(2)]
        pl_ps, o_ps = ps("pl_ps"), ps("o_ps")
        V = Steps(sem("vector"), [("max", 2), "pt", "inv", ("out", 4)], 2)
        A = Steps(sem("scalar"), [("exp", 4), "pl", "pt"], 2)
        T_ = Steps(sem("tensor"), [("scores", 2), ("pt", 2), "out"], 2)
        G = Steps(sem("pool"), [("qd", 2)], 2)
        block = ctx.enter_context(nc.Block())
        first = half * HALF
        U = BPT

        @block.gpsimd
        def _(e):
            G.start(e)
            with e.Fori(0, HALF // U) as h:
                for w in range(U):
                    b, u = h * U + w, w % 2
                    e.wait_ge(*T_.at("scores", b - 2))
                    for g in range(2):
                        e.tensor_tensor(qd[u][:, g, :, :], over(c.qT[:, g, bass.ds((b + first) * T, T)], [P, KVH, T], 1),
                                        over(c.group[:, :], [P, KVH, T], 2), ALU.mult).then_inc(G("qd"), 1)

        @block.tensor
        def _(e):
            T_.start(e)
            with e.Fori(0, HALF // U) as h:
                for w in range(U):
                    b, u = h * U + w, w % 2
                    e.wait_ge(*G.at("qd", b))
                    for s in range(2):
                        e.wait_ge(*A.at("exp", b - 1, 2 * s + 1))
                        for g in range(2):
                            m = e.matmul(s_ps[s][:, g * 512:g * 512 + M], qd[u][:, g, 4 * s:4 * s + 4, :],
                                         c.kT[:, b, :], start=True, stop=True)
                        m.then_inc(T_("scores"), 1)
                    e.wait_ge(*A.at("pl", b - 1))
                    for s in range(2):
                        e.wait_ge(*A.at("exp", b, 2 * s + 1))
                        e.wait_ge(*(A.at("pt", b - 1) if s else V.at("pt", b - 1)))
                        for m in range(2):
                            for g in range(2):
                                e.transpose(pt_ps[s][:, (2 * m + g) * P:(2 * m + g + 1) * P],
                                            p[u][s][:, g, m * P:(m + 1) * P], c.ident[:, :])
                        for g in range(2):
                            t = e.transpose(pl_ps[0:1, (2 * s + g) * P:(2 * s + g + 1) * P], p[u][s][:, g, 2 * P:M],
                                            c.ident[:, :])
                        t.then_inc(T_("pt"), 1)
                    e.wait_ge(*V.at("out", b - 1))
                    e.wait_ge(*A.at("pt", b))
                    e.wait_ge(*V.at("pt", b))
                    for s in range(2):
                        for g in range(2):
                            o = o_ps[:, (2 * s + g) * 64:(2 * s + g + 1) * 64]
                            e.matmul(o, pl[u][s][0:1, g * P:(g + 1) * P],
                                     c.v_last[0:1, bass.ds(b * P + 64 * s, 64)], start=True, stop=False)
                            for m in range(2):
                                t = e.matmul(o, pt[u][s][:, m, g, :], c.v[:, b, m, 64 * s:64 * s + 64], start=False,
                                             stop=(m == 1))
                    t.then_inc(T_("out"), 1)

        @block.scalar
        def _(e):
            A.start(e)
            with e.Fori(0, HALF // U) as h:
                for w in range(U):
                    b, u = h * U + w, w % 2
                    e.wait_ge(*T_.at("pt", b - 2))
                    e.wait_ge(*V.at("inv", b - 2))
                    for s in range(2):
                        e.wait_ge(*V.at("max", b, s))
                        for g in range(2):
                            e.activation(p[u][s][:, g, :], s_ps[s][:, g * 512:g * 512 + M], ACT.Exp,
                                         bias=mx[u][:, s, g:g + 1], accum_out=tot[u][:, s, g:g + 1]).then_inc(A("exp"), 1)
                    e.wait_ge(*T_.at("out", b - 2))
                    e.wait_ge(*T_.at("pt", b))
                    for s in range(2):
                        a = e.activation(pl[u][s][0:1, :], pl_ps[0:1, s * 2 * P:(s + 1) * 2 * P], ACT.Copy)
                        if s:
                            a.then_inc(A("pl"), 1)
                    e.activation(pt[u][1][:, :, :, :].rearrange("p m g r -> p (m g r)"), pt_ps[1][:, :],
                                 ACT.Copy).then_inc(A("pt"), 1)

        @block.vector
        def _(e):
            V.start(e)
            with e.Fori(0, HALF // U) as h:
                for w in range(U):
                    b, u = h * U + w, w % 2
                    e.wait_ge(*A.at("exp", b - 2))
                    for s in range(2):
                        e.wait_ge(*T_.at("scores", b, s))
                        e.tensor_reduce(mx[u][:, s, :], s_ps[s][:, :].rearrange("p (g m) -> p g m", g=2)[:, :, 0:M],
                                        AX.X, ALU.max, negate=True).then_inc(V("max"), 1)
                    e.wait_ge(*T_.at("pt", b, 0))
                    e.wait_ge(*T_.at("out", b - 2))
                    e.tensor_copy(pt[u][0][:, :, :, :].rearrange("p m g r -> p (m g r)"), pt_ps[0][:, :]).then_inc(V("pt"), 1)
                    e.wait_ge(*A.at("exp", b))
                    e.reciprocal(inv[u][:, :, :], tot[u][:, :, :]).then_inc(V("inv"), 1)
                    e.wait_ge(*V.at("inv", b))
                    e.wait_ge(*T_.at("out", b))
                    o = o_ps[:, 0:256].rearrange("p (s g f) -> p s g f", s=2, g=2)
                    tile = c.XA[:, first // BPT + h, :].rearrange("p (s k g d) -> p k s g d", s=2, k=4, g=2)
                    for k in range(4):
                        q = slice(32 * k, 32 * k + 32)
                        e.tensor_tensor(tile[32 * w:32 * w + 32, k, :, :, :], o[q, :, :, HD * k:HD * k + HD],
                                        over(inv[u][q, :, :], [T, 2, 2, HD], 3), ALU.mult).then_inc(V("out"), 1)


def l1_project(nc, c):
    with ExitStack() as ctx:
        sb, ps, sem = tensors(nc, ctx, "o1")
        n, q = Norm(sb, ps), Quant(sb)
        f = sb("f", [P, KT_])
        xT = sb("xT", [P, CJ, BT], BF16)
        t_ps = [ps(f"t_ps{j}", (P, 2 * 512), BF16) for j in range(CJ)]
        o_ps = [ps(f"o_ps{b}") for b in range(2)]
        V = Steps(sem("vector"), LN_V + ["gain", "shift"] + QUANT_V + ["factor", ("added", KT_)])
        A = Steps(sem("scalar"), LN_A[:1] + QUANT_A + [("xT", CJ)])
        T_ = Steps(sem("tensor"), [("ints_t", CJ), ("o", 2)])
        block = ctx.enter_context(nc.Block())

        @block.vector
        def _(e):
            V.start(e)
            rows = [P, KT_, C]
            with e.Fori(0, BLOCKS) as i:
                ln_vector(e, V, A, n, c.XA, i, lambda: None)
                e.wait_ge(*V.at("norm", i))
                y = n.xn[:, :, :]
                e.tensor_tensor(y, y, over(c.row["x_gamma"], rows, 1), ALU.mult).then_inc(V("gain"), 1)
                e.wait_ge(*V.at("gain", i))
                e.tensor_tensor(y, y, over(c.row["x_beta"], rows, 1), ALU.add).then_inc(V("shift"), 1)
                quant_vector(e, V, A, q, n.xn, V.at("shift", i), i, lambda: e.wait_ge(*T_.at("ints_t", i - 1)))
                e.wait_ge(*V.at("dequant", i))
                e.tensor_scalar(f[:, :], q.factor[:, :], c.wf[:, 3:4], None, ALU.mult).then_inc(V("factor"), 1)
                e.wait_ge(*V.at("factor", i))
                for k in range(KT_):
                    x = c.X[:, i * KT_ + k, :]
                    e.wait_ge(*T_.at("o", i, k // 2))
                    e.scalar_tensor_tensor(x, o_ps[k // 2][:, (k % 2) * C:(k % 2 + 1) * C], f[:, k:k + 1], x,
                                           ALU.mult, ALU.add).then_inc(V("added"), 1)

        @block.scalar
        def _(e):
            A.start(e)
            with e.Fori(0, BLOCKS) as i:
                ln_scalar_std(e, V, A, n, i, c)
                quant_scalar(e, V, A, q, n.xn, V.at("shift", i), i, c)
                e.wait_ge(*T_.at("o", i - 1))
                for j in range(CJ):
                    e.wait_ge(*T_.at("ints_t", i, j))
                    e.activation(xT[:, j, :], t_ps[j][:, 0:BT], ACT.Copy).then_inc(A("xT"), 1)

        @block.tensor
        def _(e):
            T_.start(e)
            with e.Fori(0, BLOCKS) as i:
                e.wait_ge(*V.at("int", i))
                for j in range(CJ):
                    e.wait_ge(*A.at("xT", i - 1, j))
                    for k in range(KT_):
                        m = e.transpose(t_ps[j][:, k * P:(k + 1) * P], q.ints[:, k, j * P:(j + 1) * P], c.identb[:, :])
                    m.then_inc(T_("ints_t"), 1)
                e.wait_ge(*A.at("xT", i))
                for b in range(2):
                    e.wait_ge(*V.at("added", i - 1))
                    for k in (2 * b, 2 * b + 1):
                        for j in range(CJ):
                            m = e.matmul(o_ps[b][:, (k % 2) * C:(k % 2 + 1) * C], xT[:, j, k * P:(k + 1) * P],
                                         c.wo[:, j, :], start=(j == 0), stop=(j == CJ - 1))
                    m.then_inc(T_("o"), 1)



def l1_state_space(nc, c):
    with ExitStack() as ctx:
        sb, ps, sem = tensors(nc, ctx, "ms")
        w_in, w_out = sb("w_in", [P, CJ, 2 * DI]), sb("w_out", [P, DC, C])
        w_x = sb("w_x", [P, DC, 2 * NS + 1])
        y_ps = [ps(f"y_ps{q}") for q in range(DC)]
        bc_ps = [ps(f"bc_ps{q}") for q in range(4)]
        n = Norm(sb, ps, y_ps[:2])
        n2 = Norm(sb, ps, y_ps[:2], "ln2")
        neg_a = sb("neg_a", [P, DC, NS])
        xm = sb("xm", [P, DC, BB, TAPS - 1 + T])
        acc = [sb(f"acc{u}", [P, BT]) for u in range(2)]
        xc, sz = sb("xc", [P, DC, BT]), sb("sz", [P, DC, BT])
        ssm = sb("ssm", [2 * NS, BT])
        lg, na, ez, wz, lz, dz, mz, step = (sb(f"dt_{k}", [P, KT_]) for k in ("lg", "na", "ez", "wz", "lz", "dz", "mz", "step"))
        dt = sb("dt", [P, BT])
        xdt = sb("xdt", [P, DC, BT])
        dA = [sb(f"dA{u}", [P, DC, BT]) for u in range(2)]
        u_ = sb("u", [P, DC, BT])
        h_ = sb("h", [P, DC, BT])
        hc = [sb(f"hc{u}", [P, DC, BT]) for u in range(2)]
        yg = sb("yg", [P, DC, BT])
        r = n2.src = sb("r", [P, KT_, C])
        loaded, made, seen = sem("loaded"), sem("made"), sem("seen")
        V = Steps(sem("vector"), LN_V + [("conv", DC * TAPS), "dt_lg", "dt_na", "dt_w", "dt_d", "dt_m", "dt_d1", "dt_inv", "dt_l1", "dt_zl",
                                              "dt_t", "dt", "xdt"] + NS * ["u", "h", "hc"]
                  + [("skip", DC), ("gated", DC), ("r1", 2), "r2"] + second_names(LN_V) + ["gain", "shift", "added"])
        A = Steps(sem("scalar"), LN_A + [("x", DC), ("silu", DC), ("z", DC), "ssm", "exp", "log", "DT"]
                  + NS * [("dA", DC)] + ["std2"])
        T_ = Steps(sem("tensor"), LN_T + [("x", DC), ("z", DC), "ssm", "dt_lg", "DT", "B", "C"] + (NS - 1) * ["B", "C", "y"]
                   + ["y", ("out", 2)])
        G = Steps(sem("pool"), NS * ["cut"])
        block = ctx.enter_context(nc.Block())
        flat = "p q t -> p (q t)"

        @block.sync
        def _(e):
            e.dma_start(w_in[:, :, :], c.d["l1_w_in"]).then_inc(loaded, 16)
            e.dma_start(w_x[:, :, :], c.d["l1_w_x"]).then_inc(loaded, 16)
            e.dma_start(w_out[:, :, :], c.d["l1_w_out"]).then_inc(loaded, 16)

        @block.tensor
        def _(e):
            T_.start(e)
            e.wait_ge(loaded, 48)

            def spread(bank, k):
                return e.matmul(bank[:, :], c.ident[0:2 * NS, k:k + 1].broadcast_to([2 * NS, P]), ssm[:, :],
                                start=True, stop=True)

            with e.Fori(0, BLOCKS) as i:
                ln_tensor(e, V, T_, n, i, c, lambda: e.wait_ge(*V.at("r1", i - 1)))
                e.wait_ge(*A.at("features", i))
                e.wait_ge(*V.at("hc", i - 1))
                for q in range(2 * DC):
                    if q >= DC:
                        e.wait_ge(*A.at("x", i, q - DC))
                    for j in range(CJ):
                        m = e.matmul(bc_ps[q % 4][:, :], w_in[:, j, q * P:(q + 1) * P], n.hT[:, j, :], start=(j == 0),
                                     stop=(j == CJ - 1))
                    m.then_inc(T_("x" if q < DC else "z"), 1)
                e.wait_ge(*A.at("silu", i))
                e.wait_ge(*A.at("z", i))
                for q in range(DC):
                    m = e.matmul(bc_ps[0][0:2 * NS, :], w_x[:, q, 0:2 * NS], xc[:, q, :], start=(q == 0), stop=(q == DC - 1))
                m.then_inc(T_("ssm"), 1)
                for k in range(KT_):
                    for q in range(DC):
                        m = e.matmul(bc_ps[1][:, k:k + 1], xc[:, q, k * P:(k + 1) * P], w_x[:, q, 2 * NS:2 * NS + 1],
                                     start=(q == 0), stop=(q == DC - 1))
                m.then_inc(T_("dt_lg"), 1)
                e.wait_ge(*V.at("dt", i))
                for k in range(KT_):
                    m = e.matmul(bc_ps[2][:, k * P:(k + 1) * P], step[:, k:k + 1].broadcast_to([P, P]), c.ident[:, :],
                                 start=True, stop=True)
                m.then_inc(T_("DT"), 1)
                e.wait_ge(*A.at("DT", i))

                def b_and_c(s):
                    if s >= 2:
                        e.wait_ge(*V.at("hc", i, s - 2))
                    spread(bc_ps[s % 2], s).then_inc(T_("B"), 1)
                    spread(bc_ps[2 + s % 2], NS + s).then_inc(T_("C"), 1)

                def add_state(s):
                    e.wait_ge(*V.at("hc", i, s))
                    for q in range(DC):
                        m = e.matmul(y_ps[q][:, :], c.ident[:, :], hc[s % 2][:, q, :], start=(s == 0), stop=(s == NS - 1))
                    m.then_inc(T_("y"), 1)

                b_and_c(0)
                for s in range(1, NS):
                    b_and_c(s)
                    add_state(s - 1)
                add_state(NS - 1)
                e.wait_ge(*V.at("gated", i))
                for b in range(2):
                    for k in (2 * b, 2 * b + 1):
                        for q in range(DC):
                            m = e.matmul(y_ps[b][:, (k % 2) * C:(k % 2 + 1) * C], yg[:, q, k * P:(k + 1) * P],
                                         w_out[:, q, :], start=(q == 0), stop=(q == DC - 1))
                    m.then_inc(T_("out"), 1)

        @block.gpsimd
        def _(e):
            G.start(e)
            with e.Fori(0, BLOCKS) as i:
                for s in range(NS):
                    e.wait_ge(*A.at("dA", i, s * DC + DC - 1))
                    e.sem_inc(seen, 1)
                    e.memset(by_batch(dA[s % 2][:, :, :].rearrange(flat))[:, :, 0:1], 0.0).then_inc(G("cut"), 1)

        @block.vector
        def _(e):
            V.start(e)
            e.memset(xm[:, :, :, :], 0.0).then_inc(made, 1)
            e.wait_ge(made, 2)
            e.tensor_scalar(neg_a[:, :, :], neg_a[:, :, :], -1.0, None, ALU.mult).then_inc(made, 1)
            taps = c.vec["conv_w"]
            with e.Fori(0, BLOCKS) as i:
                ln_vector(e, V, A, n, c.X, i, lambda: e.wait_ge(*T_.at("turned", i - 1)))
                for q in range(DC):
                    e.wait_ge(*A.at("x", i, q))
                    e.wait_ge(*(A.at("silu", i, q - 2) if q >= 2 else A.at("silu", i - 1)))
                    a = by_batch(acc[q % 2][:, :])
                    for k in range(TAPS):
                        x = xm[:, q, :, k:k + T]
                        w = taps[:, q * TAPS + k:q * TAPS + k + 1]
                        if k == 0:
                            e.tensor_scalar(a, x, w, None, ALU.mult).then_inc(V("conv"), 1)
                        else:
                            e.wait_ge(*V.at("conv", i, q * TAPS + k - 1))
                            e.scalar_tensor_tensor(a, x, w, a, ALU.mult, ALU.add).then_inc(V("conv"), 1)
                e.wait_ge(*T_.at("dt_lg", i))
                e.tensor_tensor(lg[:, :], bc_ps[1][:, 0:KT_], c.row["dt_b"].broadcast_to([P, KT_]), ALU.add).then_inc(V("dt_lg"), 1)
                e.wait_ge(*V.at("dt_lg", i))
                e.scalar_tensor_tensor(na[:, :], lg[:, :], -1.0, lg[:, :], ALU.mult, ALU.min).then_inc(V("dt_na"), 1)
                e.wait_ge(*A.at("exp", i))
                e.tensor_scalar(wz[:, :], ez[:, :], 1.0, None, ALU.add).then_inc(V("dt_w"), 1)
                e.wait_ge(*V.at("dt_w", i))
                e.tensor_scalar(dz[:, :], wz[:, :], 1.0, None, ALU.subtract).then_inc(V("dt_d"), 1)
                e.tensor_scalar(mz[:, :], wz[:, :], 1.0, None, ALU.is_equal).then_inc(V("dt_m"), 1)
                e.wait_ge(*V.at("dt_m", i))
                e.tensor_tensor(dz[:, :], dz[:, :], mz[:, :], ALU.add).then_inc(V("dt_d1"), 1)
                e.wait_ge(*V.at("dt_d1", i))
                e.reciprocal(dz[:, :], dz[:, :]).then_inc(V("dt_inv"), 1)
                e.wait_ge(*A.at("log", i))
                e.tensor_tensor(lz[:, :], lz[:, :], mz[:, :], ALU.add).then_inc(V("dt_l1"), 1)
                e.wait_ge(*V.at("dt_l1", i))
                e.tensor_tensor(lz[:, :], lz[:, :], dz[:, :], ALU.mult).then_inc(V("dt_zl"), 1)
                e.wait_ge(*V.at("dt_zl", i))
                e.tensor_tensor(lz[:, :], lz[:, :], ez[:, :], ALU.mult).then_inc(V("dt_t"), 1)
                e.wait_ge(*V.at("dt_t", i))
                e.scalar_tensor_tensor(step[:, :], lg[:, :], 0.0, lz[:, :], ALU.max, ALU.add).then_inc(V("dt"), 1)
                e.wait_ge(*A.at("DT", i))
                shape = [P, DC, BT]
                e.tensor_tensor(xdt[:, :, :], xc[:, :, :], over(dt[:, :], shape, 1), ALU.mult).then_inc(V("xdt"), 1)
                e.wait_ge(*V.at("xdt", i))
                for s in range(NS):
                    e.wait_ge(*T_.at("B", i, s))
                    e.tensor_tensor(u_[:, :, :], xdt[:, :, :], over(bc_ps[s % 2][:, :], shape, 1), ALU.mult).then_inc(V("u"), 1)
                    e.wait_ge(*V.at("u", i, s))
                    e.wait_ge(*G.at("cut", i, s))
                    e.tensor_tensor_scan(h_[:, :, :].rearrange(flat), dA[s % 2][:, :, :].rearrange(flat),
                                         u_[:, :, :].rearrange(flat), 0.0, ALU.mult, ALU.add).then_inc(V("h"), 1)
                    e.wait_ge(*V.at("h", i, s))
                    e.wait_ge(*T_.at("C", i, s))
                    e.wait_ge(*(T_.at("y", i, s - 2) if s >= 2 else T_.at("y", i - 1)))
                    e.tensor_tensor(hc[s % 2][:, :, :], h_[:, :, :], over(bc_ps[2 + s % 2][:, :], shape, 1),
                                    ALU.mult).then_inc(V("hc"), 1)
                e.wait_ge(*T_.at("y", i))
                for q in range(DC):
                    e.scalar_tensor_tensor(yg[:, q, :], xc[:, q, :], c.vec["D"][:, q:q + 1], y_ps[q][:, :], ALU.mult,
                                           ALU.add).then_inc(V("skip"), 1)
                e.wait_ge(*A.at("z", i))
                for q in range(DC):
                    e.wait_ge(*V.at("skip", i, q))
                    e.tensor_tensor(yg[:, q, :], yg[:, q, :], sz[:, q, :], ALU.mult).then_inc(V("gated"), 1)
                for b in range(2):
                    e.wait_ge(*T_.at("out", i, b))
                    e.tensor_tensor(r[:, 2 * b:2 * b + 2, :], n.xn[:, 2 * b:2 * b + 2, :],
                                    y_ps[b][:, :].rearrange("p (k f) -> p k f", k=2), ALU.add).then_inc(V("r1"), 1)
                e.wait_ge(*V.at("r1", i))
                rows = [P, KT_, C]
                e.tensor_tensor(r[:, :, :], r[:, :, :], over(c.row["out_b"], rows, 1), ALU.add).then_inc(V("r2"), 1)
                e.wait_ge(*V.at("r2", i))
                ln_vector(e, second(V), second(A), n2, None, i, lambda: None)
                e.wait_ge(*V.at("norm2", i))
                y = n2.xn[:, :, :]
                e.tensor_tensor(y, y, over(c.row["m_gamma"], rows, 1), ALU.mult).then_inc(V("gain"), 1)
                e.wait_ge(*V.at("gain", i))
                e.tensor_tensor(y, y, over(c.row["m_beta"], rows, 1), ALU.add).then_inc(V("shift"), 1)
                e.wait_ge(*V.at("shift", i))
                x = c.X[:, bass.ds(i * KT_, KT_), :]
                e.tensor_tensor(x, x, y, ALU.add).then_inc(V("added"), 1)

        @block.scalar
        def _(e):
            A.start(e)
            e.activation(neg_a[:, :, :].rearrange("p q s -> p (q s)"), c.vec["A_log"], ACT.Exp).then_inc(made, 1)
            e.wait_ge(made, 3)
            with e.Fori(0, BLOCKS) as i:
                ln_scalar_std(e, V, A, n, i, c)
                ln_scalar_features(e, T_, A, n, i, lambda: e.wait_ge(*T_.at("z", i - 1)))
                bias = c.vec["in_b"]
                e.wait_ge(*V.at("conv", i - 1))
                for q in range(DC):
                    e.wait_ge(*T_.at("x", i, q))
                    e.activation(xm[:, q, :, TAPS - 1:], by_batch(bc_ps[q][:, :]), ACT.Identity,
                                 bias=bias[:, q:q + 1]).then_inc(A("x"), 1)
                e.wait_ge(*V.at("skip", i - 1))
                e.wait_ge(*T_.at("ssm", i - 1))
                for q in range(DC):
                    e.wait_ge(*V.at("conv", i, q * TAPS + TAPS - 1))
                    e.activation(xc[:, q, :], acc[q % 2][:, :], ACT.Silu,
                                 bias=c.vec["conv_b"][:, q:q + 1]).then_inc(A("silu"), 1)
                e.wait_ge(*V.at("gated", i - 1))
                for q in range(DC):
                    e.wait_ge(*T_.at("z", i, q))
                    e.activation(sz[:, q, :], bc_ps[q][:, :], ACT.Silu,
                                 bias=bias[:, DC + q:DC + q + 1]).then_inc(A("z"), 1)
                e.wait_ge(*T_.at("ssm", i))
                e.wait_ge(*T_.at("C", i - 1))
                e.activation(ssm[:, :], bc_ps[0][0:2 * NS, :], ACT.Identity,
                             bias=c.sm["xp_b"][0:2 * NS, :]).then_inc(A("ssm"), 1)
                e.wait_ge(*V.at("dt_na", i))
                e.activation(ez[:, :], na[:, :], ACT.Exp).then_inc(A("exp"), 1)
                e.wait_ge(*V.at("dt_w", i))
                e.activation(lz[:, :], wz[:, :], ACT.Ln).then_inc(A("log"), 1)
                e.wait_ge(*T_.at("DT", i))
                e.activation(dt[:, :], bc_ps[2][:, :], ACT.Copy).then_inc(A("DT"), 1)
                e.wait_ge(*A.at("DT", i))
                for s in range(NS):
                    e.wait_ge(*(V.at("h", i, s - 2) if s >= 2 else V.at("h", i - 1)))
                    for q in range(DC):
                        e.activation(dA[s % 2][:, q, :], dt[:, :], ACT.Exp, scale=neg_a[:, q, s:s + 1]).then_inc(A("dA"), 1)
                ln_scalar_std(e, second(V), second(A), n2, i, c)



def l1_experts(nc, c):
    with ExitStack() as ctx:
        sb, ps, sem = tensors(nc, ctx, "fe")
        FJ = FH // P
        wg = sb("wg", [P, CJ, E])
        w1 = [sb(f"w1_{q}", [P, CJ, FH]) for q in range(E)]
        w2 = [sb(f"w2_{q}", [P, FJ, C]) for q in range(E)]
        n = Norm(sb, ps)
        lg, sq = sb("lg", [P, KT_, E]), sb("sq", [P, KT_, E])
        ms, big, tot = sb("ms", [P, KT_]), sb("big", [P, KT_]), sb("tot", [P, KT_])
        hid = [sb(f"hid{u}", [P, FJ, BT]) for u in range(2)]
        h_ps = [ps(f"h_ps{u}") for u in range(2)]
        y_ps = [ps(f"y_ps{k}") for k in range(KT_)]
        g_loaded = sem("g_loaded")
        w_loaded = [sem(f"w_loaded{q}") for q in range(E)]
        V = Steps(sem("vector"), LN_V + ["logits", "square", "mean_sq", "flip", "scaled", "weighted", "big", "less", "sum",
                                         "g", "g_eps", "g_inv", "norm_g", ("added", KT_)])
        A = Steps(sem("scalar"), LN_A + ["rms", "exp", ("gelu", E * FJ)])
        T_ = Steps(sem("tensor"), LN_T + ["logits", ("hidden", FJ)] + [("hidden", FJ), "y"] * (E - 1) + ["y"])
        block = ctx.enter_context(nc.Block())
        shape = [P, KT_, E]
        flat = "p k e -> p (k e)"

        @block.sync
        def _(e):
            e.dma_start(wg[:, :, :], c.d["l1_wg"]).then_inc(g_loaded, 16)
            for q in range(E):
                e.dma_start(w1[q][:, :, :], c.d["l1_w1"][q]).then_inc(w_loaded[q], 16)
                e.dma_start(w2[q][:, :, :], c.d["l1_w2"][q]).then_inc(w_loaded[q], 16)

        @block.tensor
        def _(e):
            T_.start(e)
            e.wait_ge(g_loaded, 16)

            def hidden(i, q):
                e.wait_ge(w_loaded[q], 32)
                for f in range(FJ):
                    at = q * FJ + f
                    e.wait_ge(*(A.at("gelu", i, at - 2) if at >= 2 else A.at("gelu", i - 1, E * FJ - 2 + at)))
                    for j in range(CJ):
                        m = e.matmul(h_ps[f % 2][:, :], w1[q][:, j, f * P:(f + 1) * P], n.hT[:, j, :], start=(j == 0),
                                     stop=(j == CJ - 1))
                    m.then_inc(T_("hidden"), 1)

            def combine(i, q):
                e.wait_ge(*A.at("gelu", i, q * FJ + FJ - 1))
                for k in range(KT_):
                    for f in range(FJ):
                        m = e.matmul(y_ps[k][:, 0:C], hid[q % 2][:, f, k * P:(k + 1) * P], w2[q][:, f, :],
                                     start=False, stop=(q == E - 1 and f == FJ - 1))
                m.then_inc(T_("y"), 1)

            with e.Fori(0, BLOCKS) as i:
                ln_tensor(e, V, T_, n, i, c, lambda: e.wait_ge(*V.at("logits", i - 1)))
                e.wait_ge(*A.at("features", i))
                for k in range(KT_):
                    for j in range(CJ):
                        m = e.matmul(n.ps[0][:, k * E:(k + 1) * E], n.hT[:, j, k * P:(k + 1) * P], wg[:, j, :],
                                     start=(j == 0), stop=(j == CJ - 1))
                m.then_inc(T_("logits"), 1)
                hidden(i, 0)
                for k in range(KT_):
                    e.wait_ge(*V.at("added", i - 1, k))
                    e.matmul(y_ps[k][:, 0:C], c.ones[0:E, 0:P], c.sm["b2"][0:E, :], start=True, stop=False)
                for q in range(1, E):
                    hidden(i, q)
                    combine(i, q - 1)
                combine(i, E - 1)

        @block.scalar
        def _(e):
            A.start(e)
            with e.Fori(0, BLOCKS) as i:
                ln_scalar_std(e, V, A, n, i, c)
                ln_scalar_features(e, T_, A, n, i, lambda: e.wait_ge(*T_.at("hidden", i - 1)))
                e.wait_ge(*V.at("mean_sq", i))
                e.activation(ms[:, :], ms[:, :], ACT.Sqrt, scale=1.0 / E, bias=c.eps[:, 3:4]).then_inc(A("rms"), 1)
                e.wait_ge(*V.at("less", i))
                e.activation(sq[:, :, :].rearrange(flat), lg[:, :, :].rearrange(flat), ACT.Exp,
                             scale=2.0).then_inc(A("exp"), 1)
                for q in range(E):
                    for f in range(FJ):
                        e.wait_ge(*T_.at("hidden", i, q * FJ + f))
                        if f == 0:
                            e.wait_ge(*(T_.at("y", i, q - 2) if q >= 2 else T_.at("y", i - 1, E - 2 + q)))
                        e.activation(hid[q % 2][:, f, :], h_ps[f % 2][:, :], ACT.Gelu,
                                     bias=c.vec["b1"][:, q * FJ + f:q * FJ + f + 1]).then_inc(A("gelu"), 1)

        @block.vector
        def _(e):
            V.start(e)
            with e.Fori(0, BLOCKS) as i:
                ln_vector(e, V, A, n, c.X, i, lambda: e.wait_ge(*T_.at("turned", i - 1)))
                e.wait_ge(*T_.at("logits", i))
                e.tensor_tensor(lg[:, :, :], n.ps[0][:, 0:KT_ * E].rearrange("p (k e) -> p k e", k=KT_),
                                over(c.row["gate_b"], shape, 1), ALU.add).then_inc(V("logits"), 1)
                e.wait_ge(*V.at("logits", i))
                e.tensor_tensor(sq[:, :, :], lg[:, :, :], lg[:, :, :], ALU.mult).then_inc(V("square"), 1)
                e.wait_ge(*V.at("square", i))
                e.tensor_reduce(ms[:, :], sq[:, :, :], AX.X, ALU.add).then_inc(V("mean_sq"), 1)
                e.wait_ge(*A.at("rms", i))
                e.reciprocal(ms[:, :], ms[:, :]).then_inc(V("flip"), 1)
                e.wait_ge(*V.at("flip", i))
                e.tensor_tensor(lg[:, :, :], lg[:, :, :], over(ms[:, :], shape, 2), ALU.mult).then_inc(V("scaled"), 1)
                e.wait_ge(*V.at("scaled", i))
                e.tensor_tensor(lg[:, :, :], lg[:, :, :], over(c.row["rms_w"], shape, 1), ALU.mult).then_inc(V("weighted"), 1)
                e.wait_ge(*V.at("weighted", i))
                e.tensor_reduce(big[:, :], lg[:, :, :], AX.X, ALU.max).then_inc(V("big"), 1)
                e.wait_ge(*V.at("big", i))
                e.tensor_tensor(lg[:, :, :], lg[:, :, :], over(big[:, :], shape, 2), ALU.subtract).then_inc(V("less"), 1)
                e.wait_ge(*A.at("exp", i))
                e.tensor_reduce(tot[:, :], sq[:, :, :], AX.X, ALU.add).then_inc(V("sum"), 1)
                e.wait_ge(*V.at("sum", i))
                e.reciprocal(tot[:, :], tot[:, :]).then_inc(V("g"), 1)
                e.wait_ge(*V.at("g", i))
                e.tensor_scalar(big[:, :], tot[:, :], 1e-6, None, ALU.add).then_inc(V("g_eps"), 1)
                e.wait_ge(*V.at("g_eps", i))
                e.reciprocal(big[:, :], big[:, :]).then_inc(V("g_inv"), 1)
                e.wait_ge(*V.at("g_inv", i))
                e.tensor_tensor(tot[:, :], tot[:, :], big[:, :], ALU.mult).then_inc(V("norm_g"), 1)
                e.wait_ge(*V.at("norm_g", i))
                e.wait_ge(*T_.at("y", i))
                for k in range(KT_):
                    x = c.X[:, i * KT_ + k, :]
                    e.scalar_tensor_tensor(x, y_ps[k][:, 0:C], tot[:, k:k + 1], x, ALU.mult, ALU.add).then_inc(V("added"), 1)



VECS = [("bq", 2), ("bk", 2), ("ln1_g", 2), ("ln1_b", 2), ("ln2_g", 2), ("ln2_b", 2), ("decay", 2), ("first", 2),
        ("tm_k", 2), ("tm_v", 2), ("tm_r", 2), ("cm_k", 2), ("cm_r", 2), ("in_b", 8), ("conv_w", 16), ("conv_b", 4),
        ("D", 4), ("A_log", 64), ("b1", 32)]
ROWS = [("bv", C), ("x_gamma", C), ("x_beta", C), ("out_b", C), ("m_gamma", C), ("m_beta", C), ("gate_b", E),
        ("rms_w", E), ("dt_b", 1)]
SMALL = [("be", C), ("b2", C), ("xp_b", 1)]


def named(tensor, table):
    out, at = {}, 0
    for name, n in table:
        out[name] = tensor[:, at:at + n]
        at += n
    return out, at


def build(nc, d, stages=range(1, 7)):
    c = Chip()
    c.d = d
    with ExitStack() as ctx:
        sb, ps, sem = tensors(nc, ctx, "c")
        c.X = sb("x", [P, TILES, C])
        c.vecs = sb("vecs", [P, sum(n for _, n in VECS)])
        c.rows = sb("rows", [P, sum(n for _, n in ROWS)])
        c.small = sb("small", [33, sum(n for _, n in SMALL)])
        c.vec, _ = named(c.vecs, VECS)
        c.row, _ = named(c.rows, ROWS)
        c.sm, _ = named(c.small, SMALL)
        c.consts = sb("consts", [P, P + 20])
        c.ident = c.consts[:, 0:P]
        c.own = c.consts[:, P:P + 4]
        c.group = c.consts[:, P + 4:P + 12]
        c.iota = c.consts[:, P + 12:P + 20]
        c.identb = sb("identb", [P, P], BF16)
        c.eps = sb("eps", [P, 4])
        c.ones = sb("ones", [P, P])
        c.c_max = sb("c_max", [P, 2 * B])
        c.c_ss = sb("c_ss", [P, 2 * B])
        load_all(nc, c)
        with ExitStack() as mid:
            c.cq = mid.enter_context(nc.sbuf_tensor("c_cq", [P, 2 * B, C], BF16))
            if 1 in stages:
                with ExitStack() as one:
                    c.qkT = one.enter_context(nc.sbuf_tensor("c_qkT", [P, CJ, B * T], FP32))
                    c.qc = one.enter_context(nc.sbuf_tensor("c_qc", [P, TILES], FP32))
                    l0_queries(nc, c)
                    l0_attention(nc, c)
            if 2 in stages:
                with ExitStack() as two:
                    c.XI = two.enter_context(nc.sbuf_tensor("c_XI", [P, TILES, C], FP32))
                    l0_time_mix(nc, c)
                    l0_channel_mix(nc, c)
            if 3 in stages:
                l0_experts(nc, c)
            if 4 in stages:
                with ExitStack() as four:
                    def sb4(name, shape, dt=FP32):
                        return four.enter_context(nc.sbuf_tensor(f"c_{name}", shape, dt))

                    c.wq, c.wkv, c.wo = (sb4(k, [P, CJ, C], BF16) for k in ("wq", "wkv", "wo"))
                    c.wf = sb4("wf", [P, 4])
                    c.kf, c.vf = sb4("kf", [P, 2 * B]), sb4("vf", [P, 2 * B])
                    c.k_last, c.v_last = sb4("k_last", [P, B]), sb4("v_last", [1, HALF * P])
                    c.qT = sb4("qT", [P, 2, B * T])
                    l1_prepare(nc, c)
                    l1_queries(nc, c)
                    c.XA = sb4("XA", [P, TILES, C])
                    with ExitStack() as kv:
                        c.kT = kv.enter_context(nc.sbuf_tensor("c_kT", [P, HALF, M], FP32))
                        c.v = kv.enter_context(nc.sbuf_tensor("c_v", [P, HALF, 2, P], FP32))
                        for half in range(B // HALF):
                            l1_keys(nc, c, half)
                            l1_attention(nc, c, half)
                    l1_project(nc, c)
        if 5 in stages:
            l1_state_space(nc, c)
        if 6 in stages:
            l1_experts(nc, c)
        store(nc, c)


def store(nc, c):
    with ExitStack() as ctx:
        sb, ps, sem = tensors(nc, ctx, "st")
        stored = sem("stored")
        block = ctx.enter_context(nc.Block())

        @block.sync
        def _(e):
            e.dma_start(c.d["out"], c.X[:, :, :]).then_inc(stored, 16)
            e.wait_ge(stored, 16)


def layout(i):
    f = {k: np.asarray(v) for k, v in i.items()}

    def feat(w):
        w = w.T
        return np.ascontiguousarray(w.reshape(-1, P, w.shape[1]).transpose(1, 0, 2))

    def nat(w):
        return np.ascontiguousarray(w.reshape(-1, P, w.shape[1]).transpose(1, 0, 2))

    def vec(v):
        return v.reshape(-1, P).T

    ctxm = f["ctx_1024"]
    a = {}
    a["x"] = f["x"].reshape(TILES, P, C).transpose(1, 0, 2)
    main, last = ctxm[:, :2 * P, :], ctxm[:, 2 * P, :]
    a["ctx_n"] = main.reshape(TILES, BPT, 2, P, C).transpose(0, 3, 1, 2, 4)
    a["ctx_t"] = main.reshape(TILES, BPT, 2 * P, CJ, P).transpose(0, 4, 1, 3, 2)
    a["ctx_last_n"] = last.reshape(TILES, BPT, C).transpose(1, 0, 2)
    a["ctx_last_t"] = last.reshape(B, CJ, P).transpose(2, 1, 0)
    a["mask"] = f["mask_SxS2_ik1"]
    a["l0_wq"], a["l0_wk"], a["l0_wv"] = nat(f["L0_xattn_Wq"]), nat(f["L0_xattn_Wk"]), feat(f["L0_xattn_Wv"])
    for k, n in (("km", "Wk"), ("vm", "Wv"), ("rm", "Wr"), ("om", "Wo"), ("ck", "Wck"), ("cr", "Wcr"), ("cv", "Wcv")):
        a[f"l0_w{k}"] = feat(f[f"L0_attn_{n}"])
    a["l0_wg"] = nat(f["L0_ffn_Wg"])
    a["l0_we"] = f["L0_ffn_We"].reshape(E, CJ, P, C).transpose(2, 1, 0, 3).reshape(P, CJ, E * C)
    a["l1_wg"] = feat(f["L1_ffn_gate_w"])
    a["l1_w1"] = f["L1_ffn_w1"].reshape(E, CJ, P, FH).transpose(0, 2, 1, 3)
    a["l1_w2"] = f["L1_ffn_w2"].reshape(E, FH // P, P, C).transpose(0, 2, 1, 3)
    a["l1_w_in"], a["l1_w_x"] = feat(f["L1_attn_in_proj_w"]), feat(f["L1_attn_x_proj_w"])
    a["l1_w_out"] = feat(f["L1_attn_out_proj_w"])
    wq = f["L1_xattn_wq"].reshape(KVH, 2, HD, C).transpose(1, 0, 2, 3).reshape(C, C)
    a["l1_wq"], a["l1_wk"], a["l1_wv"], a["l1_wo"] = (feat(w) for w in (wq, f["L1_xattn_wk"], f["L1_xattn_wv"],
                                                                         f["L1_xattn_wo"]))
    a["ctx_last"] = last
    v = {"bq": f["L0_xattn_bq"], "bk": f["L0_xattn_bk"], "ln1_g": f["L0_attn_ln1_g"], "ln1_b": f["L0_attn_ln1_b"],
         "ln2_g": f["L0_attn_ln2_g"], "ln2_b": f["L0_attn_ln2_b"], "decay": f["L0_attn_time_decay"],
         "first": f["L0_attn_time_first"], "tm_k": f["L0_attn_tm_k"], "tm_v": f["L0_attn_tm_v"],
         "tm_r": f["L0_attn_tm_r"], "cm_k": f["L0_attn_cm_k"], "cm_r": f["L0_attn_cm_r"],
         "in_b": f["L1_attn_in_proj_b"], "conv_b": f["L1_attn_conv_b"], "D": f["L1_attn_D"]}
    v = {k: vec(x.reshape(-1)) for k, x in v.items()}
    v["conv_w"] = f["L1_attn_conv_w"].reshape(DC, P, TAPS).transpose(1, 0, 2).reshape(P, -1)
    v["A_log"] = f["L1_attn_A_log"].reshape(DC, P, NS).transpose(1, 0, 2).reshape(P, -1)
    v["b1"] = f["L1_ffn_b1"].reshape(E, FH // P, P).transpose(2, 0, 1).reshape(P, -1)
    a["vecs"] = np.concatenate([v[n] for n, _ in VECS], 1)
    r = {"bv": f["L0_xattn_bv"], "x_gamma": f["L1_xattn_ln_gamma"], "x_beta": f["L1_xattn_ln_beta"],
         "out_b": f["L1_attn_out_proj_b"], "m_gamma": f["L1_attn_ln_gamma"], "m_beta": f["L1_attn_ln_beta"],
         "gate_b": f["L1_ffn_gate_b"], "rms_w": f["L1_ffn_rms_w"],
         "dt_b": f["L1_attn_x_proj_b"][2 * NS:]}
    a["rows"] = np.broadcast_to(np.concatenate([r[n] for n, _ in ROWS])[None], (P, sum(n for _, n in ROWS)))
    small = np.zeros((33, sum(n for _, n in SMALL)), np.float32)
    small[:E, 0:C], small[:E, C:2 * C], small[:, 2 * C] = f["L0_ffn_be"], f["L1_ffn_b2"], f["L1_attn_x_proj_b"]
    a["small"] = small
    p = np.arange(P)[:, None]
    a["ident"] = np.concatenate([np.eye(P), p // T == np.arange(4), p // HD == np.arange(8),
                                 np.broadcast_to(np.arange(8), (P, 8))], 1).astype(np.float32)
    return {k: np.ascontiguousarray(x) for k, x in a.items()}


def kernel(**inputs):
    from concourse import bacc
    from concourse.bass_utils import run_bass_kernel_spmd

    nc = bacc.Bacc("TRN2", target_bir_lowering=False, num_devices=1)
    arrays = {f"in_{k}": a for k, a in layout(inputs).items()}
    d = {k[3:]: nc.dram_tensor(k, a.shape, mybir.dt.from_np(a.dtype), kind="ExternalInput").ap()
         for k, a in arrays.items()}
    out = nc.dram_tensor("out", (TILES, P, C), FP32, kind="ExternalOutput").ap()
    d["bounce"] = nc.dram_tensor("bounce", (B, P), FP32, kind="Internal").ap()
    d["out"] = out.rearrange("t p c -> p t c")
    build(nc, d)
    r = run_bass_kernel_spmd(nc, [arrays], core_ids=[0])
    return r.results[0]["out"].reshape(B, T, C)
```

```python
from contextlib import ExitStack

import numpy as np

import concourse.bass as bass
from concourse import mybir

FP32 = mybir.dt.float32
BF16 = mybir.dt.bfloat16
FP16 = mybir.dt.float16
I32 = mybir.dt.int32
U32 = mybir.dt.uint32
ALU = mybir.AluOpType
ACT = mybir.ActivationFunctionType
AX = mybir.AxisListType

P = 128
B, T, C, M = 64, 32, 256, 257
CJ = C // P
TILES = B * T // P
BPT = P // T
KT_ = 4
BLOCKS = TILES // KT_
BT = KT_ * P
BB = KT_ * BPT
HID = 4 * C
E = 8
FH = 512
FJ = FH // P
HEADS, KVH, HD = 16, 8, 16
DI, NS, TAPS = 512, 16, 4
DC = DI // P
NEG = -1.0e9
FAR = -1.0e38
LN_EPS, RMS_EPS = 1e-5, 1e-6
ROUND = 1.5 * 2.0 ** 23
W_SCALE = 128.0
F32_EPS = float(np.finfo(np.float32).eps)


class Steps:

    def __init__(self, sem, names, ahead=1):
        self.sem = sem
        self.ahead = ahead
        self.names = [n for item in names for n in ([item] if isinstance(item, str) else [item[0]] * item[1])]
        self.n = len(self.names)
        self.emitted = 0
        self.before = 0

    def start(self, eng):
        if self.before == 0:
            eng.sem_inc(self.sem, self.ahead * self.n)

    def __call__(self, name):
        want = self.names[self.emitted % self.n]
        assert want == name, (want, name)
        self.emitted += 1
        return self.sem

    def at(self, name, i, k=None):
        places = [p for p, n in enumerate(self.names) if n == name]
        place = places[-1] if k is None else places[k]
        return self.sem, (i + self.before + self.ahead) * self.n + place + 1


class Chip:
    pass


class Shared:

    def __init__(self, nc, ctx, prefix):
        self.nc, self.ctx, self.prefix = nc, ctx, prefix
        self.made = {}

    def sem(self, name):
        if name not in self.made:
            self.made[name] = self.ctx.enter_context(self.nc.semaphore(f"{self.prefix}_{name}"))
        return self.made[name]

    def steps(self, name, names, before, ahead=2):
        key = "steps " + name
        if key not in self.made:
            self.made[key] = Steps(self.sem(name), names, ahead)
        self.made[key].before = before
        return self.made[key]


def tensors(nc, ctx, prefix):
    def sb(name, shape, dt=FP32):
        return ctx.enter_context(nc.sbuf_tensor(f"{prefix}_{name}", shape, dt))

    def ps(name, shape=(P, 512), dt=FP32):
        return ctx.enter_context(nc.psum_tensor(f"{prefix}_{name}", list(shape), dt))

    def sem(name):
        return ctx.enter_context(nc.semaphore(f"{prefix}_{name}"))

    return sb, ps, sem



LN_V = [("stats", 4), "sums", "diff", "between", "variance", "mean", "rstd", ("norm", 4)]
LN_A = ["std", ("features", CJ)]
LN_T = [("turned", CJ)]


class Norm:

    def __init__(self, sb, ps, banks=None, name="ln", tiles=KT_):
        self.tiles = tiles
        self.stats = sb(f"{name}_stats", [P, tiles, 6])
        self.sums = sb(f"{name}_sums", [P, tiles, 2])
        self.diff = sb(f"{name}_diff", [P, tiles])
        self.var = sb(f"{name}_var", [P, tiles])
        self.mean = sb(f"{name}_mean", [P, tiles])
        self.std = sb(f"{name}_std", [P, tiles])
        self.rstd = sb(f"{name}_rstd", [P, tiles])
        self.xn = sb(f"{name}_xn", [P, tiles, C])
        self.hT = sb(f"{name}_hT", [P, CJ, tiles * P]) if name == "ln" else None
        self.ps = banks or [ps(f"{name}_ps{j}") for j in range(CJ)]
        self.src = None


def second_names(names):
    return [n + "2" if isinstance(n, str) else (n[0] + "2", n[1]) for n in names]


class second:

    def __init__(self, steps):
        self.steps = steps

    def __call__(self, name):
        return self.steps(name + "2")

    def at(self, name, i, k=None):
        return self.steps.at(name + "2", i, k)


def ln_vector(e, V, A, n, src, i, free):
    def tile(k):
        return n.src[:, k, :] if src is None else src[:, i * n.tiles + k, :]

    for k in range(n.tiles):
        e.bn_stats(n.stats[:, k, :], tile(k)).then_inc(V("stats"), 1)
    e.wait_ge(*V.at("stats", i))
    e.tensor_tensor(n.sums[:, :, :], n.stats[:, :, 1:3], n.stats[:, :, 4:6], ALU.add).then_inc(V("sums"), 1)
    e.tensor_tensor(n.diff[:, :], n.stats[:, :, 1], n.stats[:, :, 4], ALU.subtract).then_inc(V("diff"), 1)
    e.wait_ge(*V.at("diff", i))
    e.scalar_tensor_tensor(n.var[:, :], n.diff[:, :], 0.25, n.diff[:, :], ALU.mult, ALU.mult).then_inc(V("between"), 1)
    e.wait_ge(*V.at("between", i))
    e.scalar_tensor_tensor(n.var[:, :], n.sums[:, :, 1], 1.0 / C, n.var[:, :], ALU.mult, ALU.add).then_inc(V("variance"), 1)
    e.tensor_scalar(n.mean[:, :], n.sums[:, :, 0], 0.5, None, ALU.mult).then_inc(V("mean"), 1)
    e.wait_ge(*A.at("std", i))
    e.reciprocal(n.rstd[:, :], n.std[:, :]).then_inc(V("rstd"), 1)
    e.wait_ge(*V.at("rstd", i))
    free()
    for k in range(n.tiles):
        e.tensor_scalar(n.xn[:, k, :], tile(k), n.mean[:, k:k + 1], n.rstd[:, k:k + 1],
                        ALU.subtract, ALU.mult).then_inc(V("norm"), 1)


def ln_scalar_std(e, V, A, n, i, c):
    e.wait_ge(*V.at("variance", i))
    e.activation(n.std[:, :], n.var[:, :], ACT.Sqrt, bias=c.eps[:, 0:1]).then_inc(A("std"), 1)


def ln_scalar_features(e, T_, A, n, i, free, gain=None, shift=None):
    free()
    for j in range(CJ):
        e.wait_ge(*T_.at("turned", i, j))
        if gain is None:
            e.activation(n.hT[:, j, :], n.ps[j][:, :], ACT.Copy).then_inc(A("features"), 1)
        else:
            e.activation(n.hT[:, j, :], n.ps[j][:, :], ACT.Identity, bias=shift[:, j:j + 1],
                         scale=gain[:, j:j + 1]).then_inc(A("features"), 1)


def ln_tensor(e, V, T_, n, i, c, free, src=None, step="norm"):
    src = src or n.xn
    free()
    e.wait_ge(*V.at(step, i))
    for j in range(CJ):
        for k in range(KT_):
            t = e.transpose(n.ps[j][:, k * P:(k + 1) * P], src[:, k, j * P:(j + 1) * P], c.ident[:, :])
        t.then_inc(T_("turned"), 1)



ALL_V = [(n[0], TILES) if isinstance(n, tuple) else n for n in LN_V]
ALL_A = ["std"] + BLOCKS * CJ * ["features", "rounded"]
ALL_T = [("turned", BLOCKS * CJ)]
ALL_G = [("rest", BLOCKS * CJ)]


def all_tensor(e, V, A, T_, n, c):
    for i in range(BLOCKS):
        for j in range(CJ):
            if i:
                e.wait_ge(*A.at("rounded", 0, (i - 1) * CJ + j))
            e.wait_ge(*V.at("norm", 0, i * KT_ + KT_ - 1))
            for k in range(KT_):
                t = e.transpose(n.ps[j][:, k * P:(k + 1) * P], n.xn[:, i * KT_ + k, j * P:(j + 1) * P], c.ident[:, :])
            t.then_inc(T_("turned"), 1)


def all_scalar(e, T_, A, n, parts):
    for i in range(BLOCKS):
        for j in range(CJ):
            e.wait_ge(*T_.at("turned", 0, i * CJ + j))
            e.activation(n.hT[:, j, i * BT:(i + 1) * BT], n.ps[j][:, :], ACT.Copy).then_inc(A("features"), 1)
            e.activation(parts[0][:, j, i * BT:(i + 1) * BT], n.ps[j][:, :], ACT.Copy).then_inc(A("rounded"), 1)


def all_pool(e, A, G, n, parts):
    for i in range(BLOCKS):
        for j in range(CJ):
            e.wait_ge(*A.at("rounded", 0, i * CJ + j))
            at = slice(i * BT, (i + 1) * BT)
            e.tensor_tensor(parts[1][:, j, at], n.hT[:, j, at], parts[0][:, j, at], ALU.subtract).then_inc(G("rest"), 1)



def load_all(nc, c):
    with ExitStack() as ctx:
        sb, ps, sem = tensors(nc, ctx, "ld")
        loaded, made = sem("loaded"), sem("made")
        block = ctx.enter_context(nc.Block())

        @block.sync
        def _(e):
            e.dma_start(c.X[:, :, :], c.d["x"]).then_inc(loaded, 16)
            e.dma_start(c.vecs[:, :], c.d["vecs"]).then_inc(loaded, 16)
            e.dma_start(c.rows[:, :], c.d["rows"]).then_inc(loaded, 16)
            e.dma_start(c.consts[:, :], c.d["ident"]).then_inc(loaded, 16)
            e.dma_start(c.small[:, :], c.d["small"]).then_inc(loaded, 16)
            e.wait_ge(loaded, 80)

        @block.vector
        def _(e):
            e.memset(c.eps[:, 0:1], LN_EPS).then_inc(made, 1)
            e.memset(c.eps[:, 1:2], RMS_EPS).then_inc(made, 1)
            e.memset(c.eps[:, 3:4], F32_EPS).then_inc(made, 1)
            e.memset(c.eps[:, 2:3], float(np.log(1e-5))).then_inc(made, 1)
            e.memset(c.ones[:, :], 1.0).then_inc(made, 1)
            e.wait_ge(loaded, 80)
            e.tensor_copy(c.identb[:, :], c.ident[:, :]).then_inc(made, 1)
            e.tensor_copy(c.identh[:, :], c.ident[:, :]).then_inc(made, 1)



def l0_queries(nc, c):
    with ExitStack() as ctx:
        sb, ps, sem = tensors(nc, ctx, "q0")
        wq = sb("wq", [P, CJ, C])
        wk = sb("wk", [P, CJ, C])
        fused = sb("fused", [P, CJ, C])
        side = sb("side", [P, 8])
        n = Norm(sb, ps)
        out_ps = [ps(f"out_ps{o}") for o in range(CJ)]
        fuse_ps = [ps(f"fuse_ps{j}") for j in range(CJ)]
        side_ps = ps("side_ps")
        qc_ps = ps("qc_ps")
        loaded, fused_ready, fuse_done, side_made = sem("loaded"), sem("fused"), sem("fuse_done"), sem("side_made")
        V = Steps(sem("vector"), LN_V + ["qc"])
        A = Steps(sem("scalar"), LN_A + [("qk", CJ)])
        T_ = Steps(sem("tensor"), LN_T + [("qk", CJ), "qc"])
        block = ctx.enter_context(nc.Block())
        bq, bk = c.vec["bq"], c.vec["bk"]

        @block.sync
        def _(e):
            e.dma_start(wq[:, :, :], c.d["l0_wq"]).then_inc(loaded, 16)
            e.dma_start(wk[:, :, :], c.d["l0_wk"]).then_inc(loaded, 16)

        @block.tensor
        def _(e):
            T_.start(e)
            e.wait_ge(loaded, 32)
            for j in range(CJ):
                for o in range(CJ):
                    m = e.matmul(fuse_ps[j][:, 0:C], wq[:, o, j * P:(j + 1) * P], wk[:, o, :],
                                 start=(o == 0), stop=(o == CJ - 1))
                m.then_inc(fuse_done, 1)
            for j in range(CJ):
                for w, b, at in ((wk, bq, 0), (wq, bk, 2)):
                    for o in range(CJ):
                        e.matmul(side_ps[:, at + j:at + j + 1], w[:, o, j * P:(j + 1) * P], b[:, o:o + 1],
                                 start=(o == 0), stop=(o == CJ - 1))
            for o in range(CJ):
                m = e.matmul(side_ps[0:1, 4:5], bq[:, o:o + 1], bk[:, o:o + 1], start=(o == 0), stop=(o == CJ - 1))
            m.then_inc(fuse_done, 1)
            with e.Fori(0, BLOCKS) as i:
                ln_tensor(e, V, T_, n, i, c, lambda: e.wait_ge(*A.at("features", i - 1)))
                e.wait_ge(*A.at("features", i))
                e.wait_ge(fused_ready, CJ)
                e.wait_ge(side_made, 2)
                for o in range(CJ):
                    e.wait_ge(*A.at("qk", i - 1, o))
                    for j in range(CJ):
                        m = e.matmul(out_ps[o][:, :], fused[:, j, o * P:(o + 1) * P], n.hT[:, j, :],
                                     start=(j == 0), stop=(j == CJ - 1))
                    m.then_inc(T_("qk"), 1)
                e.wait_ge(*V.at("qc", i - 1))
                for k in range(KT_):
                    for j in range(CJ):
                        e.matmul(qc_ps[:, k:k + 1], n.hT[:, j, k * P:(k + 1) * P], side[:, 2 + j:3 + j],
                                 start=(j == 0), stop=False)
                    m = e.matmul(qc_ps[:, k:k + 1], c.ones[0:1, 0:P], side[0:1, 4:5], start=False, stop=True)
                m.then_inc(T_("qc"), 1)

        @block.vector
        def _(e):
            V.start(e)
            e.wait_ge(fuse_done, 3)
            for j in range(CJ):
                e.tensor_copy(fused[:, j, :], fuse_ps[j][:, 0:C]).then_inc(fused_ready, 1)
            with e.Fori(0, BLOCKS) as i:
                ln_vector(e, V, A, n, c.X, i, lambda: e.wait_ge(*T_.at("turned", i - 1)))
                e.wait_ge(*T_.at("qc", i))
                e.tensor_copy(c.qc[:, bass.ds(i * KT_, KT_)], qc_ps[:, 0:KT_]).then_inc(V("qc"), 1)

        @block.scalar
        def _(e):
            A.start(e)
            e.wait_ge(fuse_done, 3)
            e.activation(side[:, 0:4], side_ps[:, 0:4], ACT.Copy).then_inc(side_made, 1)
            e.activation(side[0:1, 4:5], side_ps[0:1, 4:5], ACT.Copy).then_inc(side_made, 1)
            e.wait_ge(side_made, 2)
            with e.Fori(0, BLOCKS) as i:
                ln_scalar_std(e, V, A, n, i, c)
                ln_scalar_features(e, T_, A, n, i, lambda: e.wait_ge(*T_.at("qc", i - 1)))
                for o in range(CJ):
                    e.wait_ge(*T_.at("qk", i, o))
                    e.activation(c.qkT[:, o, bass.ds(i * BT, BT)], out_ps[o][:, :], ACT.Identity,
                                 bias=side[:, o:o + 1]).then_inc(A("qk"), 1)


def l0_attention(nc, c):
    with ExitStack() as ctx:
        sb, ps, sem = tensors(nc, ctx, "a0")
        wv = sb("wv", [P, CJ, C])
        mask_i = sb("mask_i", [P, M], I32)
        keep = sb("keep", [P, M])
        fill = sb("fill", [P, M])
        last_n = sb("last_n", [BPT, TILES, C])
        last_t = sb("last_t", [P, CJ, B])
        ctx_t = [sb(f"ctx_t{u}", [P, BPT, CJ, 2 * P]) for u in range(2)]
        ctx_n = [sb(f"ctx_n{u}", [P, BPT, 2, C]) for u in range(2)]
        qk = [sb(f"qk{u}", [P, CJ, P]) for u in range(2)]
        s = [sb(f"s{u}", [P, M]) for u in range(2)]
        p = [sb(f"p{u}", [P, M]) for u in range(2)]
        tiny = [sb(f"tiny{u}", [P, 16]) for u in range(2)]
        pt = [sb(f"pt{u}", [P, 2 * P]) for u in range(2)]
        pl = [sb(f"pl{u}", [BPT, P]) for u in range(2)]
        o = [sb(f"o{u}", [P, C]) for u in range(2)]
        ot = [sb(f"ot{u}", [P, CJ, P]) for u in range(2)]
        sq = sb("sq", [P, C])
        rounded = sb("rounded", [P, BPT * 2, C])
        qs = [sb(f"qs{u}", [P, 8]) for u in range(2)]
        ss = [sb(f"ss{u}", [P, 8]) for u in range(2)]
        root = [sb(f"root{u}", [P, 8]) for u in range(2)]
        s_ps = [ps(f"s_ps{u}") for u in range(2)]
        o_ps = [ps(f"o_ps{u}") for u in range(2)]
        pt_ps, ot_ps, y_ps = ps("pt_ps"), ps("ot_ps"), ps("y_ps")
        w_loaded, made, seen = sem("w_loaded"), sem("made"), sem("seen")
        t_loaded = [sem(f"t_loaded{u}") for u in range(2)]
        n_loaded = [sem(f"n_loaded{u}") for u in range(2)]
        def step(name, n=1):
            return Steps(sem(name), [("done", n)], 2)

        chain = Steps(sem("chain"), ["scored", "last", "last_s", "masked", "minus"], 2)
        weights = Steps(sem("weights"), ["last_p", "inverse"], 2)
        absmax, outs, whole, added = step("absmax"), step("outs"), step("whole"), step("added")
        scale = Steps(sem("scale"), ["keep_max", "keep_ss", "guard", "flip", "scale"], 2)
        exp, squares, kept, ot_kept = step("exp"), step("squares", 2 * BPT), step("kept", 2), step("ot_kept")
        root_s = Steps(sem("root"), ["log", "root"], 2)
        scores, turned, summed, ot_turned, projected = (step(k) for k in ("scores", "turned", "summed", "ot_turned", "projected"))
        qk_made, roundings = step("qk_made"), step("roundings", 2 * BPT)
        block = ctx.enter_context(nc.Block())

        def over_tiles(e, turns):
            turns(0, 0, 1)
            with e.Fori(0, TILES // 2 - 1) as h:
                turns(h * 2 + 1, 1, h + 1)
                turns(h * 2 + 2, 0, h + 2)
            turns(TILES - 1, 1, TILES // 2)

        def first(t):
            return isinstance(t, int) and t == 0

        def last(t):
            return isinstance(t, int) and t == TILES - 1

        @block.sync
        def _(e):
            e.dma_start(wv[:, :, :], c.d["l0_wv"]).then_inc(w_loaded, 16)
            for b in range(BPT):
                e.dma_start(mask_i[b * T:(b + 1) * T, :], c.d["mask"]).then_inc(w_loaded, 16)
            e.dma_start(last_n[:, :, :], c.d["ctx_last_n"]).then_inc(w_loaded, 16)
            e.dma_start(last_t[:, :, :], c.d["ctx_last_t"]).then_inc(w_loaded, 16)
            with e.Fori(0, TILES // 2) as h:
                for u in range(2):
                    t = h * 2 + u
                    e.wait_ge(*scores.at("done", t - 2))
                    e.dma_start(ctx_t[u][:, :, :, :], c.d["ctx_t"][t]).then_inc(t_loaded[u], 16)
                    e.wait_ge(*summed.at("done", t - 2))
                    e.wait_ge(*squares.at("done", t - 2))
                    e.wait_ge(*absmax.at("done", t - 2))
                    e.wait_ge(*roundings.at("done", t - 2))
                    e.dma_start(ctx_n[u][:, :, :, :], c.d["ctx_n"][t]).then_inc(n_loaded[u], 16)

        @block.gpsimd
        def _(e):
            def take_qk(t, u):
                e.wait_ge(*scores.at("done", t - 2))
                e.tensor_copy(qk[u][:, :, :], c.qkT[:, :, bass.ds(t * P, P)]).then_inc(qk_made("done"), 1)

            def turns(t, u, n):
                if not last(t):
                    take_qk(t + 1, 1 - u)
                e.wait_ge(*scale.at("scale", t))
                e.wait_ge(*whole.at("done", t - 1))
                e.sem_inc(seen, 1)
                for r in range(2 * BPT):
                    e.tensor_scalar(rounded[:, r, :], ctx_n[u][:, r // 2, r % 2, :], qs[u][:, r:r + 1], ROUND,
                                    ALU.mult, ALU.add).then_inc(roundings("done"), 1)

            for each in (qk_made, roundings):
                each.start(e)
            take_qk(0, 0)
            over_tiles(e, turns)

        @block.tensor
        def _(e):
            def score(t, u, n):
                e.wait_ge(*qk_made.at("done", t))
                e.wait_ge(*chain.at("last", t - 2))
                e.wait_ge(t_loaded[u], n * 16)
                for j in range(CJ):
                    for b in range(BPT):
                        e.matmul(s_ps[u][b * T:(b + 1) * T, 0:2 * P], qk[u][:, j, b * T:(b + 1) * T],
                                 ctx_t[u][:, b, j, :], start=(j == 0), stop=(j == CJ - 1))
                for j in range(CJ):
                    m = e.matmul(s_ps[u][:, 2 * P:2 * P + BPT], qk[u][:, j, :],
                                 last_t[:, j, bass.ds(t * BPT, BPT)], start=(j == 0), stop=(j == CJ - 1))
                m.then_inc(scores("done"), 1)

            def turn(t, u):
                e.wait_ge(*exp.at("done", t))
                e.wait_ge(*weights.at("last_p", t))
                e.wait_ge(*kept.at("done", t - 1))
                for m in range(2):
                    e.transpose(pt_ps[:, m * P:(m + 1) * P], p[u][:, m * P:(m + 1) * P], c.ident[:, :])
                e.transpose(pt_ps[0:BPT, 2 * P:3 * P], tiny[u][:, 8:8 + BPT], c.ident[:, :]).then_inc(turned("done"), 1)

            def weigh(t, u, n):
                e.wait_ge(*kept.at("done", t))
                e.wait_ge(n_loaded[u], n * 16)
                e.wait_ge(*outs.at("done", t - 2))
                e.matmul(o_ps[u][:, 0:C], pl[u][:, :], last_n[:, t, :], start=True, stop=False,
                         skip_group_check=True)
                for k in range(2):
                    for b in range(BPT):
                        m = e.matmul(o_ps[u][b * T:(b + 1) * T, 0:C], pt[u][:, k * P + b * T:k * P + (b + 1) * T],
                                     ctx_n[u][:, b, k, :], start=False, stop=(k == 1), skip_group_check=True)
                m.then_inc(summed("done"), 1)

            def turn_out(t, u):
                e.wait_ge(*outs.at("done", t))
                e.wait_ge(*ot_kept.at("done", t - 1))
                for j in range(CJ):
                    m = e.transpose(ot_ps[:, j * P:(j + 1) * P], o[u][:, j * P:(j + 1) * P], c.ident[:, :])
                m.then_inc(ot_turned("done"), 1)

            def project(t, u):
                e.wait_ge(*ot_kept.at("done", t))
                e.wait_ge(*added.at("done", t - 1))
                for j in range(CJ):
                    e.matmul(y_ps[:, 0:C], ot[u][:, j, :], wv[:, j, :], start=(j == 0), stop=False)
                e.matmul(y_ps[:, 0:C], c.ones[0:1, 0:P], c.row["bv"][0:1, :], start=False,
                         stop=True).then_inc(projected("done"), 1)

            def turns(t, u, n):
                turn(t, u)
                if not last(t):
                    score(t + 1, 1 - u, n + u)
                if not first(t):
                    turn_out(t - 1, 1 - u)
                weigh(t, u, n)
                if not first(t):
                    project(t - 1, 1 - u)

            for each in (scores, turned, summed, ot_turned, projected):
                each.start(e)
            e.wait_ge(w_loaded, 16 * 7)
            score(0, 0, 1)
            over_tiles(e, turns)
            turn_out(TILES - 1, 1)
            project(TILES - 1, 1)

        @block.vector
        def _(e):
            def largest(t, u, n):
                e.wait_ge(n_loaded[u], n * 16)
                e.wait_ge(*roundings.at("done", t - 2))
                e.tensor_reduce(qs[u][:, :], ctx_n[u][:, :, :, :].rearrange("p b k c -> p (b k) c"), AX.X, ALU.max,
                                apply_absolute_value=True).then_inc(absmax("done"), 1)

            def mask(t, u):
                x, sc = tiny[u], s_ps[u]
                e.wait_ge(*scores.at("done", t))
                e.wait_ge(*exp.at("done", t - 2))
                e.scalar_tensor_tensor(s[u][:, 0:2 * P], sc[:, 0:2 * P], c.qc[:, bass.ds(t, 1)], keep[:, 0:2 * P],
                                       ALU.add, ALU.mult).then_inc(chain("scored"), 1)
                e.tensor_tensor_reduce(x[:, 0:4], sc[:, 2 * P:2 * P + BPT], c.own[:, :], 1.0, 0.0, ALU.mult,
                                       ALU.add, x[:, 4:5]).then_inc(chain("last"), 1)
                e.wait_ge(*chain.at("last", t))
                e.scalar_tensor_tensor(s[u][:, 2 * P:M], x[:, 4:5], c.qc[:, bass.ds(t, 1)], keep[:, 2 * P:M],
                                       ALU.add, ALU.mult).then_inc(chain("last_s"), 1)
                e.wait_ge(*chain.at("last_s", t))
                e.tensor_tensor(s[u][:, :], s[u][:, :], fill[:, :], ALU.add).then_inc(chain("masked"), 1)
                e.wait_ge(*chain.at("masked", t))
                e.tensor_reduce(x[:, 5:6], s[u][:, :], AX.X, ALU.max, negate=True).then_inc(chain("minus"), 1)

            def weight(t, u):
                x = tiny[u]
                e.wait_ge(*exp.at("done", t))
                e.wait_ge(*turned.at("done", t - 2))
                e.tensor_scalar(x[:, 8:12], c.own[:, :], p[u][:, 2 * P:M], None, ALU.mult).then_inc(weights("last_p"), 1)
                e.reciprocal(x[:, 7:8], x[:, 6:7]).then_inc(weights("inverse"), 1)

            def rescale(t, u):
                e.wait_ge(*absmax.at("done", t))
                e.tensor_copy(c.c_max[:, bass.ds(t * 2 * BPT, 2 * BPT)], qs[u][:, :]).then_inc(scale("keep_max"), 1)
                e.wait_ge(*root_s.at("root", t))
                e.tensor_copy(c.c_ss[:, bass.ds(t * 2 * BPT, 2 * BPT)], ss[u][:, :]).then_inc(scale("keep_ss"), 1)
                e.wait_ge(*scale.at("keep_ss", t))
                e.tensor_tensor(qs[u][:, :], qs[u][:, :], root[u][:, :], ALU.max).then_inc(scale("guard"), 1)
                e.wait_ge(*scale.at("guard", t))
                e.reciprocal(qs[u][:, :], qs[u][:, :]).then_inc(scale("flip"), 1)
                e.wait_ge(*scale.at("flip", t))
                e.tensor_scalar(qs[u][:, :], qs[u][:, :], 127.0, None, ALU.mult).then_inc(scale("scale"), 1)

            def divide(t, u):
                e.wait_ge(*weights.at("inverse", t))
                e.wait_ge(*summed.at("done", t))
                e.wait_ge(*ot_turned.at("done", t - 2))
                e.tensor_scalar(o[u][:, :], o_ps[u][:, 0:C], tiny[u][:, 7:8], None, ALU.mult).then_inc(outs("done"), 1)

            def keep_rounded(t):
                e.wait_ge(*roundings.at("done", t))
                e.tensor_scalar(c.cq[:, bass.ds(t * 2 * BPT, 2 * BPT), :], rounded[:, :, :], ROUND, None,
                                ALU.subtract).then_inc(whole("done"), 1)

            def add(t):
                e.wait_ge(*projected.at("done", t))
                e.tensor_tensor(c.X[:, t, :], c.X[:, t, :], y_ps[:, 0:C], ALU.add).then_inc(added("done"), 1)

            def turns(t, u, n):
                if not last(t):
                    largest(t + 1, 1 - u, n + u)
                    mask(t + 1, 1 - u)
                divide(t, u)
                if not last(t):
                    weight(t + 1, 1 - u)
                keep_rounded(t)
                if not first(t):
                    add(t - 1)
                if not last(t):
                    rescale(t + 1, 1 - u)

            for each in (chain, weights, absmax, outs, whole, added, scale):
                each.start(e)
            e.wait_ge(w_loaded, 16 * 7)
            e.tensor_scalar(keep[:, :], mask_i[:, :], 0.0, None, ALU.not_equal).then_inc(made, 1)
            e.wait_ge(made, 1)
            e.tensor_scalar(fill[:, :], keep[:, :], 1.0, -NEG, ALU.subtract, ALU.mult).then_inc(made, 1)
            e.wait_ge(made, 2)
            mask(0, 0)
            weight(0, 0)
            largest(0, 0, 1)
            rescale(0, 0)
            over_tiles(e, turns)
            add(TILES - 1)

        @block.scalar
        def _(e):
            def exponentials(t, u):
                x = tiny[u]
                e.wait_ge(*chain.at("minus", t))
                e.wait_ge(*turned.at("done", t - 2))
                e.wait_ge(*weights.at("inverse", t - 2))
                e.activation(p[u][:, :], s[u][:, :], ACT.Exp, bias=x[:, 5:6],
                             accum_out=x[:, 6:7]).then_inc(exp("done"), 1)

            def square(t, u, n):
                e.wait_ge(n_loaded[u], n * 16)
                e.wait_ge(*scale.at("keep_ss", t - 2))
                for r in range(2 * BPT):
                    e.wait_ge(*(squares.at("done", t, r - 1) if r else squares.at("done", t - 1)))
                    e.activation(sq[:, :], ctx_n[u][:, r // 2, r % 2, :], ACT.Square,
                                 accum_out=ss[u][:, r:r + 1]).then_inc(squares("done"), 1)

            def roots(t, u):
                e.wait_ge(*squares.at("done", t))
                e.wait_ge(*scale.at("guard", t - 2))
                e.activation(root[u][:, :], ss[u][:, :], ACT.Ln, scale=1.0 / C,
                             bias=c.eps[:, 1:2]).then_inc(root_s("log"), 1)
                e.wait_ge(*root_s.at("log", t))
                e.activation(root[u][:, :], root[u][:, :], ACT.Exp, scale=0.5,
                             bias=c.eps[:, 2:3]).then_inc(root_s("root"), 1)

            def keep_turned(t, u):
                e.wait_ge(*turned.at("done", t))
                e.wait_ge(*summed.at("done", t - 2))
                e.activation(pt[u][:, :], pt_ps[:, 0:2 * P], ACT.Copy).then_inc(kept("done"), 1)
                e.activation(pl[u][:, :], pt_ps[0:BPT, 2 * P:3 * P], ACT.Copy).then_inc(kept("done"), 1)

            def keep_out(t, u):
                e.wait_ge(*ot_turned.at("done", t))
                e.wait_ge(*projected.at("done", t - 2))
                e.activation(ot[u][:, :, :].rearrange("p j t -> p (j t)"), ot_ps[:, 0:C], ACT.Copy).then_inc(ot_kept("done"), 1)

            def turns(t, u, n):
                keep_turned(t, u)
                if not last(t):
                    square(t + 1, 1 - u, n + u)
                if not first(t):
                    keep_out(t - 1, 1 - u)
                if not last(t):
                    exponentials(t + 1, 1 - u)
                    roots(t + 1, 1 - u)

            for each in (exp, squares, kept, ot_kept, root_s):
                each.start(e)
            exponentials(0, 0)
            square(0, 0, 1)
            roots(0, 0)
            over_tiles(e, turns)
            keep_out(TILES - 1, 1)



def by_batch(ap):
    return ap.rearrange("p (g t) -> p g t", t=T)


def l0_time_mix(nc, c):
    with ExitStack() as ctx:
        sb, ps, sem = tensors(nc, ctx, "tm")
        w = {k: sb(f"w{k}", [P, CJ, C]) for k in "kvro"}
        n = Norm(sb, ps)
        xn0 = sb("xn0", [P, KT_, C])
        var2, std2, rstd2 = sb("var2", [P, KT_]), sb("std2", [P, KT_]), sb("rstd2", [P, KT_])
        tm = {k: sb(f"tm_{k}", [P, CJ]) for k in "kvr"}
        decay = sb("decay_row", [P, CJ * BT])
        wcol = sb("wcol", [P, CJ])
        dh = sb("dh", [P, CJ * BT])
        mix = {k: sb(f"mix_{k}", [P, CJ, BT]) for k in "kvr"}
        k_, v_, sr = sb("k", [P, CJ * BT]), sb("v", [P, CJ * BT]), sb("er", [P, CJ * BT])
        pp = sb("pp", [P, 1 + CJ * BT])
        aa = sb("aa", [P, 1 + CJ * BT])
        bb = sb("bb", [P, 1 + CJ * BT])
        z1, z2, z3, z4 = (sb(f"z{q}", [P, CJ * BT]) for q in range(1, 5))
        num, den = sb("num", [P, CJ * BT]), sb("den", [P, CJ * BT])
        gated = sb("gated", [P, CJ, BT])
        lin_ps = {k: [ps(f"{k}_ps{o}") for o in range(CJ)] for k in "kvr"}
        loaded, made = sem("loaded"), sem("made")
        V = Steps(sem("vector"), LN_V[:-1] + ["var2", "eps2", "both", ("norm", KT_), ("plain", KT_), "shift", "first",
                                              ("mix", 3 * CJ), "pp", "z2", ("z1", CJ), "cut_z1", "cut_pp",
                                              ("z4", CJ), ("z3", CJ), "e2", "z3b", "kv", "aa", "bb", "num", "den",
                                              "last_num", "last_num2", "den2", "inv", "gated", ("added", CJ)])
        A = Steps(sem("scalar"), LN_A[:1] + ["std2"] + LN_A[1:] + [("k", CJ), ("v", CJ), ("r", CJ), "e2b", "e1b", "e1", "e2"])
        T_ = Steps(sem("tensor"), LN_T + [("k", CJ), ("v", CJ), ("r", CJ), ("y", CJ)])
        block = ctx.enter_context(nc.Block())

        @block.sync
        def _(e):
            for k in "kvro":
                e.dma_start(w[k][:, :, :], c.d[f"l0_w{k}m"]).then_inc(loaded, 16)

        @block.tensor
        def _(e):
            T_.start(e)
            e.wait_ge(loaded, 64)
            with e.Fori(0, BLOCKS) as i:
                ln_tensor(e, V, T_, n, i, c, lambda: e.wait_ge(*V.at("added", i - 1)))
                for q, k in enumerate("kvr"):
                    e.wait_ge(*V.at("mix", i, 2 * q + 1))
                    for o in range(CJ):
                        e.wait_ge(*A.at(k, i - 1, o))
                        for j in range(CJ):
                            m = e.matmul(lin_ps[k][o][:, :], w[k][:, j, o * P:(o + 1) * P], mix[k][:, j, :],
                                         start=(j == 0), stop=(j == CJ - 1))
                        m.then_inc(T_(k), 1)
                e.wait_ge(*V.at("gated", i))
                e.wait_ge(*A.at("features", i))
                for b in range(CJ):
                    for k in (2 * b, 2 * b + 1):
                        for j in range(CJ):
                            m = e.matmul(n.ps[b][:, (k % 2) * C:(k % 2 + 1) * C], gated[:, j, k * P:(k + 1) * P],
                                         w["o"][:, j, :], start=(j == 0), stop=(j == CJ - 1))
                    m.then_inc(T_("y"), 1)

        @block.vector
        def _(e):
            V.start(e)
            for k in "kvr":
                e.tensor_scalar(tm[k][:, :], c.vec[f"tm_{k}"], 1.0, None, ALU.subtract).then_inc(made, 1)
            e.wait_ge(made, 4)
            e.tensor_scalar(wcol[:, :], wcol[:, :], -1.0, None, ALU.mult).then_inc(made, 1)
            e.memset(decay[:, :], 0.0).then_inc(made, 1)
            e.memset(pp[:, 0:1], FAR).then_inc(made, 1)
            e.memset(aa[:, 0:1], 0.0).then_inc(made, 1)
            e.memset(bb[:, 0:1], 0.0).then_inc(made, 1)
            e.wait_ge(made, 9)
            for j in range(CJ):
                e.tensor_scalar(decay[:, j * BT:(j + 1) * BT], decay[:, j * BT:(j + 1) * BT], wcol[:, j:j + 1], None,
                                ALU.add).then_inc(made, 1)
            e.wait_ge(made, 11)
            e.memset(by_batch(decay[:, :])[:, :, 0:1], FAR).then_inc(made, 1)
            e.wait_ge(made, 12)
            N = CJ * BT
            pp_now, pp_was, aa_was, bb_was = pp[:, 1:1 + N], pp[:, 0:N], aa[:, 0:N], bb[:, 0:N]
            first = c.vec["first"]

            def half(ap, j):
                return ap[:, j * BT:(j + 1) * BT]

            with e.Fori(0, BLOCKS) as i:
                def second():
                    e.wait_ge(*V.at("rstd", i))
                    e.tensor_tensor(var2[:, :], n.var[:, :], n.rstd[:, :], ALU.mult).then_inc(V("var2"), 1)
                    e.wait_ge(*V.at("var2", i))
                    e.tensor_tensor(var2[:, :], var2[:, :], n.rstd[:, :], ALU.mult).then_inc(V("eps2"), 1)
                    e.wait_ge(*A.at("std2", i))
                    e.reciprocal(rstd2[:, :], std2[:, :]).then_inc(V("both"), 1)
                    e.wait_ge(*V.at("both", i))
                    e.wait_ge(*T_.at("turned", i - 1))

                ln_vector(e, V, A, n, c.X, i, second)
                e.wait_ge(*V.at("norm", i))
                for k in range(KT_):
                    e.tensor_copy(xn0[:, k, :], n.xn[:, k, :]).then_inc(V("plain"), 1)
                e.wait_ge(*V.at("plain", i))
                h = n.hT[:, :, :].rearrange("p j t -> p (j t)")
                e.wait_ge(*A.at("features", i))
                e.tensor_tensor(by_batch(dh[:, :])[:, :, 1:T], by_batch(h)[:, :, 1:T], by_batch(h)[:, :, 0:T - 1],
                                ALU.subtract).then_inc(V("shift"), 1)
                e.tensor_copy(by_batch(dh[:, :])[:, :, 0:1], by_batch(h)[:, :, 0:1]).then_inc(V("first"), 1)
                e.wait_ge(*V.at("first", i))
                for k in "kvr":
                    e.wait_ge(*T_.at(k, i - 1))
                    for j in range(CJ):
                        e.scalar_tensor_tensor(mix[k][:, j, :], half(dh, j), tm[k][:, j:j + 1], n.hT[:, j, :],
                                               ALU.mult, ALU.add).then_inc(V("mix"), 1)
                e.wait_ge(*A.at("k", i))
                e.tensor_tensor_scan(pp_now, decay[:, :], k_[:, :], 0.0, ALU.add, ALU.max).then_inc(V("pp"), 1)
                e.wait_ge(*V.at("pp", i))
                e.tensor_tensor(z2[:, :], k_[:, :], pp_now, ALU.subtract).then_inc(V("z2"), 1)
                for j in range(CJ):
                    e.scalar_tensor_tensor(half(z1, j), half(pp_was, j), wcol[:, j:j + 1], half(pp_now, j), ALU.add,
                                           ALU.subtract).then_inc(V("z1"), 1)
                e.wait_ge(*V.at("z1", i))
                e.memset(by_batch(z1[:, :])[:, :, 0:1], FAR).then_inc(V("cut_z1"), 1)
                e.memset(by_batch(pp_was)[:, :, 0:1], FAR).then_inc(V("cut_pp"), 1)
                e.wait_ge(*V.at("cut_pp", i))
                for j in range(CJ):
                    e.scalar_tensor_tensor(half(z4, j), half(k_, j), first[:, j:j + 1], half(pp_was, j), ALU.add,
                                           ALU.max).then_inc(V("z4"), 1)
                e.wait_ge(*V.at("z4", i))
                for j in range(CJ):
                    e.scalar_tensor_tensor(half(z3, j), half(k_, j), first[:, j:j + 1], half(z4, j), ALU.add,
                                           ALU.subtract).then_inc(V("z3"), 1)
                e.wait_ge(*V.at("z3", i))
                e.tensor_tensor(z4[:, :], pp_was, z4[:, :], ALU.subtract).then_inc(V("e2"), 1)
                e.wait_ge(*A.at("v", i))
                e.wait_ge(*A.at("e2b", i))
                e.tensor_tensor(num[:, :], z2[:, :], v_[:, :], ALU.mult).then_inc(V("z3b"), 1)
                e.wait_ge(*V.at("z3b", i))
                e.wait_ge(*A.at("e1b", i))
                e.tensor_tensor_scan(aa[:, 1:1 + N], z1[:, :], num[:, :], 0.0, ALU.mult, ALU.add).then_inc(V("kv"), 1)
                e.tensor_tensor_scan(bb[:, 1:1 + N], z1[:, :], z2[:, :], 0.0, ALU.mult, ALU.add).then_inc(V("aa"), 1)
                e.wait_ge(*V.at("aa", i))
                e.wait_ge(*A.at("e2", i))
                e.tensor_tensor(num[:, :], z4[:, :], aa_was, ALU.mult).then_inc(V("bb"), 1)
                e.tensor_tensor(den[:, :], z4[:, :], bb_was, ALU.mult).then_inc(V("num"), 1)
                e.tensor_tensor(z2[:, :], z3[:, :], v_[:, :], ALU.mult).then_inc(V("den"), 1)
                e.wait_ge(*V.at("den", i))
                e.tensor_tensor(num[:, :], num[:, :], z2[:, :], ALU.add).then_inc(V("last_num"), 1)
                e.tensor_tensor(den[:, :], den[:, :], z3[:, :], ALU.add).then_inc(V("last_num2"), 1)
                e.wait_ge(*V.at("last_num2", i))
                e.wait_ge(*A.at("r", i))
                e.tensor_tensor(num[:, :], sr[:, :], num[:, :], ALU.mult).then_inc(V("den2"), 1)
                e.reciprocal(den[:, :], den[:, :]).then_inc(V("inv"), 1)
                e.wait_ge(*V.at("inv", i))
                e.wait_ge(*T_.at("y", i - 1))
                e.tensor_tensor(gated[:, :, :].rearrange("p j t -> p (j t)"), num[:, :], den[:, :],
                                ALU.mult).then_inc(V("gated"), 1)
                for b in range(CJ):
                    e.wait_ge(*T_.at("y", i, b))
                    e.tensor_tensor(c.XI[:, bass.ds(i * KT_ + 2 * b, 2), :], xn0[:, 2 * b:2 * b + 2, :],
                                    n.ps[b][:, :].rearrange("p (k f) -> p k f", k=2), ALU.add).then_inc(V("added"), 1)

        @block.scalar
        def _(e):
            A.start(e)
            e.activation(wcol[:, :], c.vec["decay"], ACT.Exp).then_inc(made, 1)
            with e.Fori(0, BLOCKS) as i:
                ln_scalar_std(e, V, A, n, i, c)
                e.wait_ge(*V.at("eps2", i))
                e.activation(std2[:, :], var2[:, :], ACT.Sqrt, bias=c.eps[:, 0:1]).then_inc(A("std2"), 1)
                ln_scalar_features(e, T_, A, n, i, lambda: e.wait_ge(*V.at("mix", i - 1)), c.vec["ln1_g"],
                                   c.vec["ln1_b"])
                for k, dst in (("k", k_), ("v", v_), ("r", sr)):
                    e.wait_ge(*V.at("den2", i - 1))
                    for o in range(CJ):
                        e.wait_ge(*T_.at(k, i, o))
                        e.activation(dst[:, o * BT:(o + 1) * BT], lin_ps[k][o][:, :],
                                     ACT.Sigmoid if k == "r" else ACT.Copy).then_inc(A(k), 1)
                e.wait_ge(*V.at("z2", i))
                e.activation(z2[:, :], z2[:, :], ACT.Exp).then_inc(A("e2b"), 1)
                e.wait_ge(*V.at("cut_z1", i))
                e.activation(z1[:, :], z1[:, :], ACT.Exp).then_inc(A("e1b"), 1)
                e.wait_ge(*V.at("z3", i))
                e.activation(z3[:, :], z3[:, :], ACT.Exp).then_inc(A("e1"), 1)
                e.wait_ge(*V.at("e2", i))
                e.activation(z4[:, :], z4[:, :], ACT.Exp).then_inc(A("e2"), 1)


def l0_channel_mix(nc, c):
    with ExitStack() as ctx:
        sb, ps, sem = tensors(nc, ctx, "cm")
        HC = HID // P
        wk, wv, wr = sb("wk", [P, CJ, HID]), sb("wv", [P, HC, C]), sb("wr", [P, CJ, C])
        n = Norm(sb, ps)
        tm = {k: sb(f"tm_{k}", [P, CJ]) for k in "kr"}
        dh = sb("dh", [P, CJ * BT])
        mix = {k: sb(f"mix_{k}", [P, CJ, BT]) for k in "kr"}
        relu = [sb(f"relu{u}", [P, BT]) for u in range(2)]
        kk = sb("kk", [P, HC, BT])
        gate = sb("gate", [P, KT_, C])
        k_ps = [ps(f"k_ps{u}") for u in range(2)]
        r_ps = [ps(f"r_ps{u}") for u in range(2)]
        v_ps = [ps(f"v_ps{u}") for u in range(2)]
        loaded, made = sem("loaded"), sem("made")
        V = Steps(sem("vector"), LN_V + ["shift", "first", ("mix", 2 * CJ), ("square", HC), ("rkv", 2), ("plus", 2), ("added", 2)])
        A = Steps(sem("scalar"), LN_A + [("relu", HC), ("gate", 2)])
        T_ = Steps(sem("tensor"), LN_T + [("k", HC), ("r", 2), ("v", 2)])
        block = ctx.enter_context(nc.Block())

        @block.sync
        def _(e):
            e.dma_start(wk[:, :, :], c.d["l0_wck"]).then_inc(loaded, 16)
            e.dma_start(wr[:, :, :], c.d["l0_wcr"]).then_inc(loaded, 16)
            e.dma_start(wv[:, :, :], c.d["l0_wcv"]).then_inc(loaded, 16)

        @block.tensor
        def _(e):
            T_.start(e)
            e.wait_ge(loaded, 48)
            with e.Fori(0, BLOCKS) as i:
                ln_tensor(e, V, T_, n, i, c, lambda: e.wait_ge(*A.at("features", i - 1)))
                e.wait_ge(*V.at("mix", i))
                for h in range(HC):
                    e.wait_ge(*(A.at("relu", i, h - 2) if h >= 2 else A.at("relu", i - 1)))
                    for j in range(CJ):
                        m = e.matmul(k_ps[h % 2][:, :], wk[:, j, h * P:(h + 1) * P], mix["k"][:, j, :],
                                     start=(j == 0), stop=(j == CJ - 1))
                    m.then_inc(T_("k"), 1)
                for b in range(2):
                    e.wait_ge(*A.at("gate", i - 1, b))
                    for k in (2 * b, 2 * b + 1):
                        for j in range(CJ):
                            m = e.matmul(r_ps[b][:, (k % 2) * C:(k % 2 + 1) * C], mix["r"][:, j, k * P:(k + 1) * P],
                                         wr[:, j, :], start=(j == 0), stop=(j == CJ - 1))
                    m.then_inc(T_("r"), 1)
                e.wait_ge(*V.at("square", i))
                for b in range(2):
                    e.wait_ge(*V.at("rkv", i - 1, b))
                    for k in (2 * b, 2 * b + 1):
                        for h in range(HC):
                            m = e.matmul(v_ps[b][:, (k % 2) * C:(k % 2 + 1) * C], kk[:, h, k * P:(k + 1) * P],
                                         wv[:, h, :], start=(h == 0), stop=(h == HC - 1))
                    m.then_inc(T_("v"), 1)

        @block.vector
        def _(e):
            V.start(e)
            for k in "kr":
                e.tensor_scalar(tm[k][:, :], c.vec[f"cm_{k}"], 1.0, None, ALU.subtract).then_inc(made, 1)
            e.wait_ge(made, 2)
            with e.Fori(0, BLOCKS) as i:
                ln_vector(e, V, A, n, c.XI, i, lambda: e.wait_ge(*T_.at("turned", i - 1)))
                h = n.hT[:, :, :].rearrange("p j t -> p (j t)")
                e.wait_ge(*A.at("features", i))
                e.tensor_tensor(by_batch(dh[:, :])[:, :, 1:T], by_batch(h)[:, :, 1:T], by_batch(h)[:, :, 0:T - 1],
                                ALU.subtract).then_inc(V("shift"), 1)
                e.tensor_copy(by_batch(dh[:, :])[:, :, 0:1], by_batch(h)[:, :, 0:1]).then_inc(V("first"), 1)
                e.wait_ge(*V.at("first", i))
                for k in "kr":
                    e.wait_ge(*T_.at(k, i - 1))
                    for j in range(CJ):
                        e.scalar_tensor_tensor(mix[k][:, j, :], dh[:, j * BT:(j + 1) * BT], tm[k][:, j:j + 1],
                                               n.hT[:, j, :], ALU.mult, ALU.add).then_inc(V("mix"), 1)
                e.wait_ge(*T_.at("v", i - 1))
                for q in range(HC):
                    e.wait_ge(*A.at("relu", i, q))
                    e.tensor_tensor(kk[:, q, :], relu[q % 2][:, :], relu[q % 2][:, :], ALU.mult).then_inc(V("square"), 1)
                for b in range(2):
                    e.wait_ge(*A.at("gate", i, b))
                    e.wait_ge(*T_.at("v", i, b))
                    g = gate[:, 2 * b:2 * b + 2, :]
                    e.tensor_tensor(g, g, v_ps[b][:, :].rearrange("p (k f) -> p k f", k=2), ALU.mult).then_inc(V("rkv"), 1)
                e.wait_ge(*V.at("rkv", i))
                for b in range(2):
                    tiles = bass.ds(i * KT_ + 2 * b, 2)
                    g = gate[:, 2 * b:2 * b + 2, :]
                    e.tensor_tensor(g, g, c.XI[:, tiles, :], ALU.add).then_inc(V("plus"), 1)
                e.wait_ge(*V.at("plus", i))
                for b in range(2):
                    tiles = bass.ds(i * KT_ + 2 * b, 2)
                    g = gate[:, 2 * b:2 * b + 2, :]
                    e.tensor_tensor(c.X[:, tiles, :], c.X[:, tiles, :], g, ALU.add).then_inc(V("added"), 1)

        @block.scalar
        def _(e):
            A.start(e)
            with e.Fori(0, BLOCKS) as i:
                ln_scalar_std(e, V, A, n, i, c)
                ln_scalar_features(e, T_, A, n, i, lambda: e.wait_ge(*V.at("mix", i - 1)), c.vec["ln2_g"],
                                   c.vec["ln2_b"])
                for h in range(HC):
                    e.wait_ge(*T_.at("k", i, h))
                    e.wait_ge(*(V.at("square", i, h - 2) if h >= 2 else V.at("square", i - 1)))
                    e.activation(relu[h % 2][:, :], k_ps[h % 2][:, :], ACT.Relu).then_inc(A("relu"), 1)
                for b in range(2):
                    e.wait_ge(*T_.at("r", i, b))
                    e.wait_ge(*V.at("added", i - 1))
                    e.activation(gate[:, 2 * b:2 * b + 2, :].rearrange("p k f -> p (k f)"), r_ps[b][:, :],
                                 ACT.Sigmoid).then_inc(A("gate"), 1)



def over(ap, shape, at):
    return ap.unsqueeze(at).broadcast_to(list(shape))


def l0_gates(nc, c):
    with ExitStack() as ctx:
        sb, ps, sem = tensors(nc, ctx, "mg")
        wg, we = sb("wg", [P, CJ, E]), [sb(f"we{j}", [P, E * C]) for j in range(CJ)]
        n = Norm(sb, ps, tiles=TILES)
        lg, prob, top = sb("lg", [P, TILES, E]), sb("prob", [P, TILES, E]), sb("top", [P, TILES, 8])
        idx, idf = sb("idx", [P, TILES, 8], U32), sb("idf", [P, TILES, 8])
        big, both = sb("big", [P, TILES]), sb("both", [P, TILES])
        g0, g1, gate = sb("g0", [P, TILES, E]), sb("g1", [P, TILES, E]), c.gate
        g_ps, t_ps = ps("g_ps"), [ps(f"t_ps{i}") for i in range(BLOCKS)]
        loaded, seen, w_loaded = sem("loaded"), sem("seen"), [sem(f"w_loaded{j}") for j in range(CJ)]
        V = Steps(sem("vector"), ALL_V + ["logits", "big", "less", ("top", TILES), ("index", TILES), "float", "sum",
                                          "flip", "hot0", "hot1", "part0", "part1", "join", "gate"])
        A = Steps(sem("scalar"), ALL_A + ["exp", ("gate_t", BLOCKS)])
        T_ = Steps(sem("tensor"), ALL_T + ["logits", ("gate_t", BLOCKS)])
        G = Steps(sem("pool"), CJ * ["scaled", "w0", "w1"] + ALL_G)
        block = ctx.enter_context(nc.Block())
        shape = [P, TILES, E]

        @block.sync
        def _(e):
            e.dma_start(wg[:, :, :], c.d["l0_wg"]).then_inc(loaded, 16)
            for j in range(CJ):
                e.dma_start(we[j][:, :], c.d["l0_we"][:, j, :]).then_inc(w_loaded[j], 16)

        @block.tensor
        def _(e):
            T_.start(e)
            all_tensor(e, V, A, T_, n, c)
            e.wait_ge(loaded, 16)
            for k in range(TILES):
                if k % KT_ == 0:
                    e.wait_ge(*A.at("features", 0, k // KT_ * CJ + CJ - 1))
                for j in range(CJ):
                    m = e.matmul(g_ps[:, k * E:(k + 1) * E], n.hT[:, j, k * P:(k + 1) * P], wg[:, j, :],
                                 start=(j == 0), stop=(j == CJ - 1))
            m.then_inc(T_("logits"), 1)
            e.wait_ge(*V.at("gate", 0))
            for i in range(BLOCKS):
                for k in range(KT_):
                    m = e.transpose(t_ps[i][0:E, k * P:(k + 1) * P], gate[:, i * KT_ + k, :], c.ident[:, :])
                m.then_inc(T_("gate_t"), 1)

        @block.gpsimd
        def _(e):
            G.start(e)
            for j in range(CJ):
                e.wait_ge(w_loaded[j], 16)
                e.tensor_scalar(we[j][:, :], we[j][:, :], W_SCALE, None, ALU.mult).then_inc(G("scaled"), 1)
                e.wait_ge(*G.at("scaled", 0, j))
                e.tensor_copy(c.we[0][:, j, :], we[j][:, :]).then_inc(G("w0"), 1)
                e.wait_ge(*G.at("w0", 0, j))
                e.tensor_tensor(c.we[1][:, j, :], we[j][:, :], c.we[0][:, j, :], ALU.subtract).then_inc(G("w1"), 1)
            all_pool(e, A, G, n, c.parts)

        @block.vector
        def _(e):
            V.start(e)
            ln_vector(e, V, A, n, c.X, 0, lambda: None)
            e.wait_ge(*T_.at("logits", 0))
            e.tensor_copy(lg[:, :, :].rearrange("p k e -> p (k e)"), g_ps[:, 0:TILES * E]).then_inc(V("logits"), 1)
            e.wait_ge(*V.at("logits", 0))
            e.tensor_reduce(big[:, :], lg[:, :, :], AX.X, ALU.max).then_inc(V("big"), 1)
            e.wait_ge(*V.at("big", 0))
            e.tensor_tensor(lg[:, :, :], lg[:, :, :], over(big[:, :], shape, 2), ALU.subtract).then_inc(V("less"), 1)
            e.wait_ge(*A.at("exp", 0))
            e.sem_inc(seen, 1)
            for k in range(TILES):
                e.max(top[:, k, :], prob[:, k, :]).then_inc(V("top"), 1)
            e.wait_ge(*V.at("top", 0))
            e.sem_inc(seen, 1)
            for k in range(TILES):
                e.max_index(idx[:, k, :], top[:, k, :], prob[:, k, :]).then_inc(V("index"), 1)
            e.wait_ge(*V.at("index", 0))
            e.tensor_copy(idf[:, :, :], idx[:, :, :]).then_inc(V("float"), 1)
            e.tensor_tensor(both[:, :], top[:, :, 0], top[:, :, 1], ALU.add).then_inc(V("sum"), 1)
            e.wait_ge(*V.at("sum", 0))
            e.reciprocal(both[:, :], both[:, :]).then_inc(V("flip"), 1)
            e.tensor_tensor(g0[:, :, :], over(c.iota, shape, 1), idf[:, :, 0:1].broadcast_to(shape),
                            ALU.is_equal).then_inc(V("hot0"), 1)
            e.tensor_tensor(g1[:, :, :], over(c.iota, shape, 1), idf[:, :, 1:2].broadcast_to(shape),
                            ALU.is_equal).then_inc(V("hot1"), 1)
            e.wait_ge(*V.at("hot1", 0))
            e.tensor_tensor(g0[:, :, :], g0[:, :, :], top[:, :, 0:1].broadcast_to(shape), ALU.mult).then_inc(V("part0"), 1)
            e.tensor_tensor(g1[:, :, :], g1[:, :, :], top[:, :, 1:2].broadcast_to(shape), ALU.mult).then_inc(V("part1"), 1)
            e.wait_ge(*V.at("part1", 0))
            e.tensor_tensor(g0[:, :, :], g0[:, :, :], g1[:, :, :], ALU.add).then_inc(V("join"), 1)
            e.wait_ge(*V.at("join", 0))
            e.tensor_tensor(gate[:, :, :], g0[:, :, :], over(both[:, :], shape, 2), ALU.mult).then_inc(V("gate"), 1)

        @block.scalar
        def _(e):
            A.start(e)
            ln_scalar_std(e, V, A, n, 0, c)
            all_scalar(e, T_, A, n, c.parts)
            e.wait_ge(*V.at("less", 0))
            e.activation(prob[:, :, :].rearrange("p k e -> p (k e)"), lg[:, :, :].rearrange("p k e -> p (k e)"),
                         ACT.Exp).then_inc(A("exp"), 1)
            for i in range(BLOCKS):
                e.wait_ge(*T_.at("gate_t", 0, i))
                e.activation(c.gate_t[:, i * BT:(i + 1) * BT], t_ps[i][0:E, :], ACT.Copy).then_inc(A("gate_t"), 1)


def l0_experts(nc, c):
    with ExitStack() as ctx:
        sb, ps, sem = tensors(nc, ctx, "mo")
        h = [sb(f"h{u}", [P, 2, CJ, P], FP16) for u in range(2)]
        gate_t = [sb(f"gate_t{u}", [E, P]) for u in range(2)]
        b_ps = ps("b_ps")
        e_ps = [ps(f"e_ps{q}") for q in range(E // 2)]
        V = Steps(sem("vector"), ["scaled"] + [("expert", E)] + ["bias"], 2)
        A = Steps(sem("scalar"), [("part", 2), "gate_t"], 2)
        T_ = Steps(sem("tensor"), [("expert", E // 2), "bias"], 2)
        g = [sb(f"g{u}", [P, E]) for u in range(2)]
        block = ctx.enter_context(nc.Block())

        @block.scalar
        def _(e):
            A.start(e)
            with e.Fori(0, TILES // 2) as i:
                for u in range(2):
                    t = i * 2 + u
                    e.wait_ge(*T_.at("bias", t - 2))
                    for x in range(2):
                        e.activation(h[u][:, x, :, :], c.parts[x][:, :, bass.ds(t * P, P)], ACT.Copy).then_inc(A("part"), 1)
                    e.activation(gate_t[u][:, :], c.gate_t[:, bass.ds(t * P, P)], ACT.Copy).then_inc(A("gate_t"), 1)

        @block.tensor
        def _(e):
            T_.start(e)
            with e.Fori(0, TILES // 2) as i:
                for u in range(2):
                    t = i * 2 + u
                    e.wait_ge(*A.at("part", t))
                    for q in range(E // 2):
                        e.wait_ge(*V.at("expert", t - 1, 2 * q + 1))
                        for j in range(CJ):
                            for x, w in ((0, 0), (0, 1), (1, 0)):
                                m = e.matmul(e_ps[q][:, :], h[u][:, x, j, :], c.we[w][:, j, q * 2 * C:(q + 1) * 2 * C],
                                             start=(j == 0 and x + w == 0), stop=(j == CJ - 1 and x == 1))
                        m.then_inc(T_("expert"), 1)
                    e.wait_ge(*A.at("gate_t", t))
                    e.wait_ge(*V.at("bias", t - 1))
                    e.matmul(b_ps[:, 0:C], gate_t[u][:, :], c.sm["be"][0:E, :], start=True, stop=True).then_inc(T_("bias"), 1)

        @block.vector
        def _(e):
            V.start(e)
            with e.Fori(0, TILES // 2) as i:
                for u in range(2):
                    t = i * 2 + u
                    x = c.X[:, t, :]
                    e.wait_ge(*V.at("expert", t - 2))
                    e.tensor_scalar(g[u][:, :], c.gate[:, t, :], 1.0 / W_SCALE, None, ALU.mult).then_inc(V("scaled"), 1)
                    e.wait_ge(*V.at("scaled", t))
                    for q in range(E):
                        if q % 2 == 0:
                            e.wait_ge(*T_.at("expert", t, q // 2))
                        if q:
                            e.wait_ge(*V.at("expert", t, q - 1))
                        e.scalar_tensor_tensor(x, e_ps[q // 2][:, (q % 2) * C:(q % 2 + 1) * C], g[u][:, q:q + 1], x,
                                               ALU.mult, ALU.add).then_inc(V("expert"), 1)
                    e.wait_ge(*T_.at("bias", t))
                    e.wait_ge(*V.at("expert", t))
                    e.tensor_tensor(x, x, b_ps[:, 0:C], ALU.add).then_inc(V("bias"), 1)



QUANT_V = ["amax", "guard", "inv", "scale", ("round", KT_), "int", "rt_inv", "dequant"]
QUANT_A = [("squares", KT_), "rt"]


class Quant:

    def __init__(self, sb):
        self.ss, self.amax, self.rt = (sb(f"q_{k}", [P, KT_]) for k in ("ss", "amax", "rt"))
        self.guard, self.scale, self.factor = (sb(f"q_{k}", [P, KT_]) for k in ("guard", "scale", "factor"))
        self.junk = sb("q_junk", [P, C])
        self.big = sb("q_big", [P, KT_, C])
        self.ints = sb("q_ints", [P, KT_, C], BF16)


def quant_vector(e, V, A, q, src, ready, i, free):
    e.wait_ge(*ready)
    e.tensor_reduce(q.amax[:, :], src[:, :, :], AX.X, ALU.max, apply_absolute_value=True).then_inc(V("amax"), 1)
    e.wait_ge(*V.at("amax", i))
    e.wait_ge(*A.at("rt", i))
    e.scalar_tensor_tensor(q.guard[:, :], q.rt[:, :], 1e-5, q.amax[:, :], ALU.mult, ALU.max).then_inc(V("guard"), 1)
    e.wait_ge(*V.at("guard", i))
    e.reciprocal(q.scale[:, :], q.guard[:, :]).then_inc(V("inv"), 1)
    e.wait_ge(*V.at("inv", i))
    e.tensor_scalar(q.scale[:, :], q.scale[:, :], 127.0, None, ALU.mult).then_inc(V("scale"), 1)
    e.wait_ge(*V.at("scale", i))
    for k in range(KT_):
        e.tensor_scalar(q.big[:, k, :], src[:, k, :], q.scale[:, k:k + 1], ROUND, ALU.mult, ALU.add).then_inc(V("round"), 1)
    e.wait_ge(*V.at("round", i))
    free()
    e.tensor_scalar(q.ints[:, :, :], q.big[:, :, :], ROUND, None, ALU.subtract).then_inc(V("int"), 1)
    e.reciprocal(q.rt[:, :], q.rt[:, :]).then_inc(V("rt_inv"), 1)
    e.wait_ge(*V.at("rt_inv", i))
    e.scalar_tensor_tensor(q.factor[:, :], q.guard[:, :], 1.0 / 127.0, q.rt[:, :], ALU.mult,
                           ALU.mult).then_inc(V("dequant"), 1)


def quant_scalar(e, V, A, q, src, ready, i, c):
    e.wait_ge(*ready)
    e.wait_ge(*V.at("dequant", i - 1))
    for k in range(KT_):
        e.wait_ge(*(A.at("squares", i, k - 1) if k else A.at("squares", i - 1)))
        e.activation(q.junk[:, :], src[:, k, :], ACT.Square, accum_out=q.ss[:, k:k + 1]).then_inc(A("squares"), 1)
    e.wait_ge(*A.at("squares", i))
    e.activation(q.rt[:, :], q.ss[:, :], ACT.Sqrt, scale=1.0 / C, bias=c.eps[:, 1:2]).then_inc(A("rt"), 1)


def l1_prepare(nc, c):
    with ExitStack() as ctx:
        sb, ps, sem = tensors(nc, ctx, "pr")
        names = [("q", C), ("k", P), ("v", P), ("o", C)]
        w = {k: sb(f"w{k}", [P, CJ, o]) for k, o in names}
        part, mean, inv = sb("part", [P, 4]), sb("mean", [P, 4]), sb("inv", [P, 4])
        big = {k: sb(f"big{k}", [P, CJ, o]) for k, o in names}
        rt, guard = sb("rt", [P, 2 * B]), sb("guard", [P, 2 * B])
        lastq = sb("lastq", [B, 4])
        lastf = sb("lastf", [B, 4])
        last, last_big = sb("last", [B, C]), sb("last_big", [B, C])
        last_i = sb("last_i", [B, C], BF16)
        last_t = sb("last_t", [P, CJ, B], BF16)
        kv = sb("kv", [B, 2 * P])
        k_parts = sb("k_parts", [B, 2, 2, P // 2], FP16)
        sum_ps, kv_ps, kt_ps = ps("sum_ps"), ps("kv_ps"), ps("kt_ps", (P, 2 * 512), FP16)
        t_ps = ps("t_ps", (P, 2 * 512), BF16)
        loaded, v, a, t, moved = sem("loaded"), sem("vector"), sem("scalar"), sem("tensor"), sem("moved")
        made, split = sem("made"), sem("split")
        block = ctx.enter_context(nc.Block())

        @block.sync
        def _(e):
            for k, _ in names:
                e.dma_start(w[k][:, :, :], c.d[f"l1_w{k}"]).then_inc(loaded, 16)
            e.dma_start(last[:, :], c.d["ctx_last"]).then_inc(loaded, 16)
            e.wait_ge(v, 26)
            e.dma_start(c.d["bounce"], kv[:, P:2 * P]).then_inc(moved, 16)
            e.wait_ge(moved, 16)

        @block.vector
        def _(e):
            e.wait_ge(loaded, 80)
            for q, (k, _) in enumerate(names):
                e.tensor_reduce(part[:, q:q + 1], w[k][:, :, :], AX.XY, ALU.add, apply_absolute_value=True).then_inc(v, 1)
            e.wait_ge(t, 1)
            for q, (_, o) in enumerate(names):
                e.tensor_scalar(mean[:, q:q + 1], sum_ps[:, q:q + 1], 1.0 / (C * o), 1e-5, ALU.mult, ALU.max).then_inc(v, 1)
            e.wait_ge(v, 8)
            e.reciprocal(inv[:, :], mean[:, :]).then_inc(v, 1)
            e.wait_ge(v, 9)
            for q, (k, _) in enumerate(names):
                e.tensor_scalar(big[k][:, :, :], w[k][:, :, :], inv[:, q:q + 1], ROUND, ALU.mult, ALU.add).then_inc(v, 1)
            e.wait_ge(v, 13)
            for k, _ in names:
                e.tensor_scalar(big[k][:, :, :], big[k][:, :, :], ROUND, 1.0, ALU.subtract, ALU.min).then_inc(v, 1)
            e.wait_ge(v, 17)
            e.tensor_scalar(c.wq[:, :, :], big["q"][:, :, :], -1.0, None, ALU.max).then_inc(v, 1)
            e.tensor_scalar(c.wkv[:, :, 0:P], big["k"][:, :, :], -1.0, None, ALU.max).then_inc(v, 1)
            e.tensor_scalar(c.wkv[:, :, P:2 * P], big["v"][:, :, :], -1.0, None, ALU.max).then_inc(v, 1)
            e.tensor_scalar(c.wo[:, :, :], big["o"][:, :, :], -1.0, None, ALU.max).then_inc(v, 1)
            e.tensor_scalar(c.wf[:, 0:1], mean[:, 0:1], HD ** -0.5, None, ALU.mult).then_inc(v, 1)
            e.tensor_copy(c.wf[:, 1:4], mean[:, 1:4]).then_inc(v, 1)
            e.tensor_reduce(lastq[:, 0:1], last[:, :], AX.X, ALU.max, apply_absolute_value=True).then_inc(v, 1)
            e.wait_ge(v, 24)
            e.wait_ge(a, 3)
            e.scalar_tensor_tensor(lastq[:, 2:3], lastq[:, 1:2], 1e-5, lastq[:, 0:1], ALU.mult, ALU.max).then_inc(made, 1)
            e.scalar_tensor_tensor(guard[:, :], rt[:, :], 1e-5, c.c_max[:, :], ALU.mult, ALU.max).then_inc(made, 1)
            e.wait_ge(made, 2)
            e.reciprocal(lastq[:, 3:4], lastq[:, 2:3]).then_inc(made, 1)
            e.reciprocal(rt[:, :], rt[:, :]).then_inc(made, 1)
            e.reciprocal(lastq[:, 1:2], lastq[:, 1:2]).then_inc(made, 1)
            e.wait_ge(made, 5)
            e.tensor_scalar(lastq[:, 3:4], lastq[:, 3:4], 127.0, None, ALU.mult).then_inc(made, 1)
            e.scalar_tensor_tensor(guard[:, :], guard[:, :], 1.0 / 127.0, rt[:, :], ALU.mult, ALU.mult).then_inc(made, 1)
            e.scalar_tensor_tensor(lastf[:, 1:2], lastq[:, 2:3], 1.0 / 127.0, lastq[:, 1:2], ALU.mult, ALU.mult).then_inc(made, 1)
            e.wait_ge(made, 8)
            e.tensor_scalar(c.kf[:, :], guard[:, :], mean[:, 1:2], None, ALU.mult).then_inc(made, 1)
            e.tensor_scalar(c.vf[:, :], guard[:, :], mean[:, 2:3], None, ALU.mult).then_inc(made, 1)
            e.tensor_scalar(lastf[:, 2:3], mean[0:B, 1:2], lastf[:, 1:2], None, ALU.mult).then_inc(made, 1)
            e.tensor_scalar(lastf[:, 3:4], mean[0:B, 2:3], lastf[:, 1:2], None, ALU.mult).then_inc(made, 1)
            e.tensor_scalar(last_big[:, :], last[:, :], lastq[:, 3:4], ROUND, ALU.mult, ALU.add).then_inc(made, 1)
            e.wait_ge(made, 13)
            e.tensor_scalar(last_i[:, :], last_big[:, :], ROUND, None, ALU.subtract).then_inc(made, 1)
            e.wait_ge(t, 2)
            e.tensor_copy(last_t[:, :, :].rearrange("p j b -> p (j b)"), t_ps[:, 0:CJ * B]).then_inc(made, 1)
            e.wait_ge(t, 3)
            e.tensor_scalar(kv[:, 0:P], kv_ps[0:B, 0:P], lastf[:, 2:3], None, ALU.mult).then_inc(v, 1)
            e.tensor_scalar(kv[:, P:2 * P], kv_ps[0:B, P:2 * P], lastf[:, 3:4], None, ALU.mult).then_inc(v, 1)
            k = kv[:, 0:P].rearrange("b (s f) -> b s f", s=2)
            e.wait_ge(v, 26)
            e.tensor_copy(k_parts[:, :, 0, :], k).then_inc(split, 1)
            e.wait_ge(split, 1)
            e.tensor_tensor(k_parts[:, :, 1, :], k, k_parts[:, :, 0, :], ALU.subtract).then_inc(split, 1)
            e.memset(c.v_last[:, :, :, :], 0.0).then_inc(split, 1)
            e.tensor_tensor(c.mask[:, :], c.group[:, 0:4], c.group[:, 4:8], ALU.add).then_inc(split, 1)
            e.wait_ge(t, 4)
            e.tensor_copy(c.k_last[:, :, :].rearrange("p s b -> p (s b)"), kt_ps[:, 0:2 * B]).then_inc(made, 1)

        @block.scalar
        def _(e):
            e.wait_ge(loaded, 80)
            e.activation(last_big[:, :], last[:, :], ACT.Square, accum_out=lastf[:, 0:1]).then_inc(a, 1)
            e.wait_ge(a, 1)
            e.activation(lastq[:, 1:2], lastf[:, 0:1], ACT.Sqrt, scale=1.0 / C, bias=c.eps[0:B, 1:2]).then_inc(a, 1)
            e.activation(rt[:, :], c.c_ss[:, :], ACT.Sqrt, scale=1.0 / C, bias=c.eps[:, 1:2]).then_inc(a, 1)

        @block.tensor
        def _(e):
            e.wait_ge(v, 4)
            e.matmul(sum_ps[:, 0:4], c.ones[:, :], part[:, :], start=True, stop=True).then_inc(t, 1)
            e.wait_ge(made, 14)
            for j in range(CJ):
                m = e.transpose(t_ps[:, j * B:(j + 1) * B], last_i[:, j * P:(j + 1) * P], c.identb[0:B, 0:B])
            m.then_inc(t, 1)
            e.wait_ge(made, 15)
            for j in range(CJ):
                m = e.matmul(kv_ps[0:B, 0:2 * P], last_t[:, j, :], c.wkv[:, j, :], start=(j == 0), stop=(j == CJ - 1))
            m.then_inc(t, 1)
            e.wait_ge(split, 2)
            for s in range(2):
                m = e.transpose(kt_ps[:, s * B:(s + 1) * B], k_parts[:, s, :, :].rearrange("b x f -> b (x f)"),
                                c.identh[0:B, 0:B])
            m.then_inc(t, 1)


def l1_queries(nc, c):
    with ExitStack() as ctx:
        sb, ps, sem = tensors(nc, ctx, "q1")
        parts_ps = [ps(f"parts_ps{j}", (P, 2 * 512), FP16) for j in range(2)]
        n, q = Norm(sb, ps, banks=parts_ps), Quant(sb)
        f = sb("f", [P, KT_])
        xT = sb("xT", [P, CJ, BT], BF16)
        qn = sb("qn", [P, KT_, C])
        parts = [sb(f"parts{x}", [P, KT_, 4, 2, P // 2], FP16) for x in range(2)]
        t_ps = [ps(f"t_ps{j}", (P, 2 * 512), BF16) for j in range(CJ)]
        q_ps = [ps(f"q_ps{b}") for b in range(2)]
        V = Steps(sem("vector"), LN_V + QUANT_V + ["factor", ("q", KT_)])
        A = Steps(sem("scalar"), LN_A[:1] + QUANT_A + [("xT", CJ), ("rounded", 2), ("features", 4)])
        T_ = Steps(sem("tensor"), [("ints_t", CJ), ("q", 2), ("turned", 4)])
        G = Steps(sem("pool"), [("rest", 2)])

        def copy_of(t, dup):
            return t[:, :, :, dup, :].rearrange("p k c f -> p (k c) f")

        def in_parts(t):
            return t[:, :, :].rearrange("p k (c f) -> p (k c) f", f=P // 2)

        block = ctx.enter_context(nc.Block())

        @block.vector
        def _(e):
            V.start(e)
            with e.Fori(0, BLOCKS) as i:
                ln_vector(e, V, A, n, c.X, i, lambda: None)
                quant_vector(e, V, A, q, n.xn, V.at("norm", i), i, lambda: e.wait_ge(*T_.at("ints_t", i - 1)))
                e.wait_ge(*V.at("dequant", i))
                e.tensor_scalar(f[:, :], q.factor[:, :], c.wf[:, 0:1], None, ALU.mult).then_inc(V("factor"), 1)
                e.wait_ge(*V.at("factor", i))
                e.wait_ge(*G.at("rest", i - 1))
                for k in range(KT_):
                    e.wait_ge(*T_.at("q", i, k // 2))
                    e.tensor_scalar(qn[:, k, :], q_ps[k // 2][:, (k % 2) * C:(k % 2 + 1) * C], f[:, k:k + 1], None,
                                    ALU.mult).then_inc(V("q"), 1)

        @block.scalar
        def _(e):
            A.start(e)
            with e.Fori(0, BLOCKS) as i:
                ln_scalar_std(e, V, A, n, i, c)
                quant_scalar(e, V, A, q, n.xn, V.at("norm", i), i, c)
                e.wait_ge(*T_.at("q", i - 1))
                for j in range(CJ):
                    e.wait_ge(*T_.at("ints_t", i, j))
                    e.activation(xT[:, j, :], t_ps[j][:, 0:BT], ACT.Copy).then_inc(A("xT"), 1)
                e.wait_ge(*V.at("q", i))
                e.wait_ge(*T_.at("turned", i - 1, 1))
                for dup in range(2):
                    e.activation(copy_of(parts[0], dup), in_parts(qn), ACT.Copy).then_inc(A("rounded"), 1)
                for r in range(4):
                    e.wait_ge(*T_.at("turned", i, r))
                    e.activation(c.qT[:, 2 * r:2 * r + 2, bass.ds(i * BT, BT)],
                                 parts_ps[r % 2][:, :].rearrange("p (s t) -> p s t", s=2), ACT.Copy)\
                        .then_inc(A("features"), 1)

        @block.gpsimd
        def _(e):
            G.start(e)
            with e.Fori(0, BLOCKS) as i:
                e.wait_ge(*A.at("rounded", i))
                e.wait_ge(*T_.at("turned", i - 1))
                for dup in range(2):
                    e.tensor_tensor(copy_of(parts[1], dup), in_parts(qn), copy_of(parts[0], dup),
                                    ALU.subtract).then_inc(G("rest"), 1)

        @block.tensor
        def _(e):
            T_.start(e)
            with e.Fori(0, BLOCKS) as i:
                e.wait_ge(*V.at("int", i))
                for j in range(CJ):
                    e.wait_ge(*A.at("xT", i - 1, j))
                    for k in range(KT_):
                        m = e.transpose(t_ps[j][:, k * P:(k + 1) * P], q.ints[:, k, j * P:(j + 1) * P], c.identb[:, :])
                    m.then_inc(T_("ints_t"), 1)
                e.wait_ge(*A.at("xT", i))
                for b in range(2):
                    e.wait_ge(*V.at("q", i - 1))
                    for k in (2 * b, 2 * b + 1):
                        for j in range(CJ):
                            m = e.matmul(q_ps[b][:, (k % 2) * C:(k % 2 + 1) * C], xT[:, j, k * P:(k + 1) * P],
                                         c.wq[:, j, :], start=(j == 0), stop=(j == CJ - 1))
                    m.then_inc(T_("q"), 1)
                for r in range(4):
                    e.wait_ge(*A.at("features", i if r >= 2 else i - 1, (r - 2) % 4))
                    e.wait_ge(*(A.at("rounded", i) if r < 2 else G.at("rest", i)))
                    for s in range(2):
                        for k in range(KT_):
                            m = e.transpose(parts_ps[r % 2][:, s * BT + k * P:s * BT + (k + 1) * P],
                                            parts[r // 2][:, k, 2 * (r % 2) + s, :, :].rearrange("p d f -> p (d f)"),
                                            c.identh[:, :])
                    m.then_inc(T_("turned"), 1)


BQ = B // 4


def l1_keys(nc, c, shared, quarter):
    with ExitStack() as ctx:
        sb, ps, _ = tensors(nc, ctx, f"k{quarter}")
        rows = [sb(f"rows{u}", [P, 2, C], BF16) for u in range(2)]
        xT = [sb(f"xT{u}", [P, CJ, 2 * P], BF16) for u in range(2)]
        kn = [sb(f"kn{u}", [P, 4, P // 2]) for u in range(2)]
        parts = [sb(f"parts{u}", [P, 4, 2, P // 2], FP16) for u in range(2)]
        t_ps = [ps(f"t_ps{u}", (P, 2 * 512), BF16) for u in range(2)]
        kv_ps = [ps(f"kv_ps{u}") for u in range(2)]
        kt_ps = [ps(f"kt_ps{u}", (P, 2 * 512), FP16) for u in range(2)]
        before = quarter * BQ
        made, last = shared.sem("made"), shared.sem("last")
        V = shared.steps("vector", ["k", "v", "rounded"], before)
        xT_kept, kT_kept = (shared.steps(f"{x}_kept", ["done"], before) for x in ("xT", "kT"))
        rows_t, kv_t, k_t = (shared.steps(f"{x}_t", ["done"], before) for x in ("rows", "kv", "k"))
        G = shared.steps("pool", ["rest"], before)
        fetched = [shared.sem(f"fetched{u}") for u in range(2)]
        block = ctx.enter_context(nc.Block())
        first = quarter * BQ

        @block.sync
        def _(e):
            for t in range(4):
                s = t // 2
                e.dma_start(c.v_last[t:t + 1, :, t, :],
                            c.d["bounce"][first:first + BQ, 64 * s:64 * s + 64].rearrange("(a b) f -> a b f", a=1))\
                    .then_inc(last, 16)
            with e.Fori(0, BQ // 2) as h:
                for u in range(2):
                    b = h * 2 + u
                    e.wait_ge(*rows_t.at("done", b - 2))
                    e.dma_start(rows[u][:, :, :], c.cq[:, bass.ds(b * 2 + 2 * first, 2), :]).then_inc(fetched[u], 16)
            e.wait_ge(last, 64 * (quarter + 1))

        @block.gpsimd
        def _(e):
            G.start(e)
            for s in range(2):
                e.tensor_copy(c.kT[:, :, s, 2 * P], c.k_last[:, s, first:first + BQ]).then_inc(made, 1)
            with e.Fori(0, BQ // 2) as h:
                for u in range(2):
                    b = h * 2 + u
                    e.wait_ge(*V.at("rounded", b))
                    e.wait_ge(*k_t.at("done", b - 2))
                    e.tensor_tensor(parts[u][:, :, 1, :], kn[u][:, :, :], parts[u][:, :, 0, :],
                                    ALU.subtract).then_inc(G("rest"), 1)

        @block.tensor
        def _(e):
            def turn_rows(b, u, nth):
                e.wait_ge(fetched[u], (nth + before // 2) * 16)
                e.wait_ge(*xT_kept.at("done", b - 2))
                for j in range(CJ):
                    for m in range(2):
                        t = e.transpose(t_ps[u][:, (2 * j + m) * P:(2 * j + m + 1) * P],
                                        rows[u][:, m, j * P:(j + 1) * P], c.identb[:, :])
                t.then_inc(rows_t("done"), 1)

            def project(b, u):
                e.wait_ge(*xT_kept.at("done", b))
                e.wait_ge(*V.at("v", b - 2))
                for m in range(2):
                    for j in range(CJ):
                        t = e.matmul(kv_ps[u][:, m * 2 * P:(m + 1) * 2 * P], xT[u][:, j, m * P:(m + 1) * P],
                                     c.wkv[:, j, :], start=(j == 0), stop=(j == CJ - 1))
                t.then_inc(kv_t("done"), 1)

            def turn_keys(b, u):
                e.wait_ge(*G.at("rest", b))
                e.wait_ge(*kT_kept.at("done", b - 2))
                for m in range(2):
                    for s in range(2):
                        t = e.transpose(kt_ps[u][:, (2 * s + m) * P:(2 * s + m + 1) * P],
                                        parts[u][:, 2 * m + s, :, :].rearrange("p x f -> p (x f)"), c.identh[:, :])
                t.then_inc(k_t("done"), 1)

            for s in (rows_t, kv_t, k_t):
                s.start(e)
            turn_rows(0, 0, 1)
            project(0, 0)
            turn_rows(1, 1, 1)
            with e.Fori(0, BQ // 2 - 1) as h:
                for w in range(2):
                    b, u = h * 2 + w + 1, 1 - w
                    project(b, u)
                    turn_rows(b + 1, 1 - u, h + 2)
                    turn_keys(b - 1, 1 - u)
            project(BQ - 1, 1)
            turn_keys(BQ - 2, 0)
            turn_keys(BQ - 1, 1)

        @block.scalar
        def _(e):
            def keep_rows(b, u):
                e.wait_ge(*rows_t.at("done", b))
                e.wait_ge(*kv_t.at("done", b - 2))
                e.activation(xT[u][:, :, :].rearrange("p j m -> p (j m)"), t_ps[u][:, 0:2 * C],
                             ACT.Copy).then_inc(xT_kept("done"), 1)

            def keep_keys(b, u):
                e.wait_ge(*k_t.at("done", b))
                e.activation(c.kT[:, b, :, 0:2 * P], kt_ps[u][:, 0:4 * P].rearrange("p (s m) -> p s m", s=2),
                             ACT.Copy).then_inc(kT_kept("done"), 1)

            xT_kept.start(e)
            kT_kept.start(e)
            keep_rows(0, 0)
            keep_rows(1, 1)
            with e.Fori(0, BQ // 2 - 1) as h:
                for u in range(2):
                    b = h * 2 + u
                    keep_keys(b, u)
                    keep_rows(b + 2, u)
            keep_keys(BQ - 2, 0)
            keep_keys(BQ - 1, 1)

        @block.vector
        def _(e):
            V.start(e)
            with e.Fori(0, BQ // 2) as h:
                for u in range(2):
                    b = h * 2 + u
                    r = bass.ds(b * 2 + 2 * first, 2)
                    kv = kv_ps[u][:, :].rearrange("p (m f) -> p m f", m=2)
                    e.wait_ge(*kv_t.at("done", b))
                    e.wait_ge(*G.at("rest", b - 2))
                    e.tensor_tensor(kn[u][:, :, :].rearrange("p (m s) f -> p m (s f)", m=2), kv[:, :, 0:P],
                                    over(c.kf[:, r], [P, 2, P], 2), ALU.mult).then_inc(V("k"), 1)
                    e.tensor_tensor(c.v[:, b, :, :], kv[:, :, P:2 * P], over(c.vf[:, r], [P, 2, P], 2),
                                    ALU.mult).then_inc(V("v"), 1)
                    e.wait_ge(*k_t.at("done", b - 2))
                    e.wait_ge(*V.at("k", b))
                    e.tensor_copy(parts[u][:, :, 0, :], kn[u][:, :, :]).then_inc(V("rounded"), 1)
            e.wait_ge(made, 2 * (quarter + 1))


def l1_attention(nc, c, shared, quarter):
    with ExitStack() as ctx:
        sb, ps, _ = tensors(nc, ctx, f"t{quarter}")
        qd = [[sb(f"qd{u}{s}", [P, 4, 4, T], FP16) for s in range(2)] for u in range(2)]
        p = [sb(f"p{u}", [P, 4, M]) for u in range(2)]
        pt = [[sb(f"pt{u}{s}", [P, 2, 2, P]) for s in range(2)] for u in range(2)]
        pl = [sb(f"pl{u}", [4, P]) for u in range(2)]
        mx = [sb(f"mx{u}", [P, 4]) for u in range(2)]
        tot = [sb(f"tot{u}", [P, 4]) for u in range(2)]
        inv = [sb(f"inv{u}", [P, 2, 2]) for u in range(2)]
        s_ps = [ps(f"s_ps{s}", (P, 1024)) for s in range(2)]
        pt_ps = [ps(f"pt_ps{s}") for s in range(2)]
        pl_ps, o_ps = ps("pl_ps"), ps("o_ps")

        def step(name, n=1):
            return shared.steps(name, [("done", n)], quarter * BQ)

        made_q = [step(f"made_q{s}") for s in range(2)]
        scores = [step(f"scores{s}") for s in range(2)]
        turned = [step(f"turned{s}") for s in range(2)]
        outs = step("outs")
        maxes = [step(f"max{s}") for s in range(2)]
        kept0, inverse, divided = step("kept0"), step("inverse"), step("divided", 4)
        exps = [step(f"exps{s}", 2) for s in range(2)]
        kept1, kept_last = step("kept1"), step("kept_last")
        block = ctx.enter_context(nc.Block())
        first = quarter * BQ

        @block.gpsimd
        def _(e):
            for s in range(2):
                made_q[s].start(e)
            with e.Fori(0, BQ // 2) as h:
                for u in range(2):
                    b = h * 2 + u
                    for s in range(2):
                        e.wait_ge(*scores[s].at("done", b - 2))
                        q = c.qT[:, :, bass.ds((b + first) * T, T)].rearrange("p (x s) t -> p x s t", s=2)[:, :, s, :]
                        e.tensor_tensor(qd[u][s][:, :, :, :], over(q, [P, 4, 4, T], 2),
                                        over(over(c.mask[:, :], [P, 4, T], 2), [P, 4, 4, T], 1),
                                        ALU.mult).then_inc(made_q[s]("done"), 1)

        @block.tensor
        def _(e):
            def score(b, u, s):
                e.wait_ge(*made_q[s].at("done", b))
                e.wait_ge(*exps[s].at("done", b - 1))
                for g in range(2):
                    for x in range(2):
                        m = e.matmul(s_ps[s][:, g * 512:g * 512 + M], qd[u][s][:, 2 * x + g, :, :], c.kT[:, b, s, :],
                                     start=(x == 0), stop=(x == 1))
                m.then_inc(scores[s]("done"), 1)

            def turn(b, u, s):
                e.wait_ge(*exps[s].at("done", b))
                e.wait_ge(*(kept1 if s else kept0).at("done", b - 1))
                for m in range(2):
                    for g in range(2):
                        t = e.transpose(pt_ps[s][:, (2 * m + g) * P:(2 * m + g + 1) * P],
                                        p[u][:, 2 * s + g, m * P:(m + 1) * P], c.ident[:, :])
                if s:
                    e.wait_ge(*kept_last.at("done", b - 1))
                    t = e.transpose(pl_ps[0:4, 0:P], p[u][:, :, 2 * P], c.ident[:, :])
                t.then_inc(turned[s]("done"), 1)

            def out(b, u):
                e.wait_ge(*divided.at("done", b - 1))
                e.wait_ge(*kept_last.at("done", b))
                e.wait_ge(*kept0.at("done", b))
                e.wait_ge(*kept1.at("done", b))
                e.matmul(o_ps[:, 0:4 * 64], pl[u][:, :], c.v_last[:, b, :, :].rearrange("t a f -> t (a f)"),
                         start=True, stop=False, skip_group_check=True)
                for t in range(4):
                    s, g = divmod(t, 2)
                    for m in range(2):
                        i = e.matmul(o_ps[:, t * 64:(t + 1) * 64], pt[u][s][:, m, g, :],
                                     c.v[:, b, m, 64 * s:64 * s + 64], start=False, stop=(m == 1),
                                     skip_group_check=True)
                i.then_inc(outs("done"), 1)

            def turns(b, u, last=BQ):
                turn(b, u, 1)
                if last > 1:
                    score(b + 1, 1 - u, 1)
                    turn(b + 1, 1 - u, 0)
                if last > 2:
                    score(b + 2, u, 0)
                out(b, u)

            for s in (*scores, *turned, outs):
                s.start(e)
            score(0, 0, 0)
            score(0, 0, 1)
            turn(0, 0, 0)
            score(1, 1, 0)
            with e.Fori(0, BQ // 2 - 1) as h:
                for u in range(2):
                    turns(h * 2 + u, u)
            turns(BQ - 2, 0, 2)
            turns(BQ - 1, 1, 1)

        @block.scalar
        def _(e):
            def exp(b, u, s):
                e.wait_ge(*maxes[s].at("done", b))
                e.wait_ge(*turned[s].at("done", b - 2))
                e.wait_ge(*inverse.at("done", b - 2))
                for g in range(2):
                    t = 2 * s + g
                    e.activation(p[u][:, t, :], s_ps[s][:, g * 512:g * 512 + M], ACT.Exp, bias=mx[u][:, t:t + 1],
                                 accum_out=tot[u][:, t:t + 1]).then_inc(exps[s]("done"), 1)

            def keep(b, u):
                e.wait_ge(*turned[1].at("done", b))
                e.wait_ge(*outs.at("done", b - 2))
                e.activation(pt[u][1][:, :, :, :].rearrange("p m g r -> p (m g r)"), pt_ps[1][:, :],
                             ACT.Copy).then_inc(kept1("done"), 1)
                e.activation(pl[u][:, :], pl_ps[0:4, 0:P], ACT.Copy).then_inc(kept_last("done"), 1)

            def turns(b, u, last=BQ):
                keep(b, u)
                if last > 1:
                    exp(b + 1, 1 - u, 1)
                if last > 2:
                    exp(b + 2, u, 0)

            for s in (*exps, kept1, kept_last):
                s.start(e)
            exp(0, 0, 0)
            exp(0, 0, 1)
            exp(1, 1, 0)
            with e.Fori(0, BQ // 2 - 1) as h:
                for u in range(2):
                    turns(h * 2 + u, u)
            turns(BQ - 2, 0, 2)
            turns(BQ - 1, 1, 1)

        @block.vector
        def _(e):
            def maximum(b, u, s):
                e.wait_ge(*scores[s].at("done", b))
                e.wait_ge(*exps[s].at("done", b - 2))
                e.tensor_reduce(mx[u][:, 2 * s:2 * s + 2], s_ps[s][:, :].rearrange("p (g m) -> p g m", g=2)[:, :, 0:M],
                                AX.X, ALU.max, negate=True).then_inc(maxes[s]("done"), 1)

            def keep(b, u):
                e.wait_ge(*turned[0].at("done", b))
                e.wait_ge(*outs.at("done", b - 2))
                e.tensor_copy(pt[u][0][:, :, :, :].rearrange("p m g r -> p (m g r)"),
                              pt_ps[0][:, :]).then_inc(kept0("done"), 1)

            def divide(b, w, tile):
                u = w % 2
                e.wait_ge(*exps[0].at("done", b))
                e.wait_ge(*exps[1].at("done", b))
                e.wait_ge(*divided.at("done", b - 2))
                e.reciprocal(inv[u][:, :, :].rearrange("p s g -> p (s g)"), tot[u][:, :]).then_inc(inverse("done"), 1)
                e.wait_ge(*inverse.at("done", b))
                e.wait_ge(*outs.at("done", b))
                o = o_ps[:, 0:256].rearrange("p (s g f) -> p s g f", s=2, g=2)
                x = c.XA[:, tile, :].rearrange("p (s k g d) -> p k s g d", s=2, k=4, g=2)
                for k in range(4):
                    q = slice(32 * k, 32 * k + 32)
                    e.tensor_tensor(x[32 * w:32 * w + 32, k, :, :, :], o[q, :, :, HD * k:HD * k + HD],
                                    over(inv[u][q, :, :], [T, 2, 2, HD], 3), ALU.mult).then_inc(divided("done"), 1)

            def turns(b, w, tile, last=BQ):
                u = w % 2
                if last > 1:
                    maximum(b + 1, 1 - u, 1)
                    keep(b + 1, 1 - u)
                if last > 2:
                    maximum(b + 2, u, 0)
                divide(b, w, tile)

            for s in (*maxes, kept0, inverse, divided):
                s.start(e)
            maximum(0, 0, 0)
            maximum(0, 0, 1)
            keep(0, 0)
            maximum(1, 1, 0)
            with e.Fori(0, BQ // BPT - 1) as h:
                for w in range(BPT):
                    turns(h * BPT + w, w, h)
            for w in range(BPT):
                turns(BQ - BPT + w, w, BQ // BPT - 1, BPT - w)


def l1_project(nc, c, quarter):
    with ExitStack() as ctx:
        sb, ps, sem = tensors(nc, ctx, f"o{quarter}")
        n, q = Norm(sb, ps), Quant(sb)
        f = sb("f", [P, KT_])
        xT = sb("xT", [P, CJ, BT], BF16)
        t_ps = [ps(f"t_ps{j}", (P, 2 * 512), BF16) for j in range(CJ)]
        o_ps = [ps(f"o_ps{b}") for b in range(2)]
        V = Steps(sem("vector"), LN_V + ["gain", "shift"] + QUANT_V + ["factor", ("added", KT_)])
        A = Steps(sem("scalar"), LN_A[:1] + QUANT_A + [("xT", CJ)])
        T_ = Steps(sem("tensor"), [("ints_t", CJ), ("o", 2)])
        block = ctx.enter_context(nc.Block())
        i = 0

        @block.vector
        def _(e):
            V.start(e)
            rows = [P, KT_, C]
            ln_vector(e, V, A, n, c.XA, i, lambda: None)
            e.wait_ge(*V.at("norm", i))
            y = n.xn[:, :, :]
            e.tensor_tensor(y, y, over(c.row["x_gamma"], rows, 1), ALU.mult).then_inc(V("gain"), 1)
            e.wait_ge(*V.at("gain", i))
            e.tensor_tensor(y, y, over(c.row["x_beta"], rows, 1), ALU.add).then_inc(V("shift"), 1)
            quant_vector(e, V, A, q, n.xn, V.at("shift", i), i, lambda: e.wait_ge(*T_.at("ints_t", i - 1)))
            e.wait_ge(*V.at("dequant", i))
            e.tensor_scalar(f[:, :], q.factor[:, :], c.wf[:, 3:4], None, ALU.mult).then_inc(V("factor"), 1)
            e.wait_ge(*V.at("factor", i))
            for k in range(KT_):
                x = c.X[:, quarter * KT_ + k, :]
                e.wait_ge(*T_.at("o", i, k // 2))
                e.scalar_tensor_tensor(x, o_ps[k // 2][:, (k % 2) * C:(k % 2 + 1) * C], f[:, k:k + 1], x,
                                       ALU.mult, ALU.add).then_inc(V("added"), 1)

        @block.scalar
        def _(e):
            A.start(e)
            ln_scalar_std(e, V, A, n, i, c)
            quant_scalar(e, V, A, q, n.xn, V.at("shift", i), i, c)
            e.wait_ge(*T_.at("o", i - 1))
            for j in range(CJ):
                e.wait_ge(*T_.at("ints_t", i, j))
                e.activation(xT[:, j, :], t_ps[j][:, 0:BT], ACT.Copy).then_inc(A("xT"), 1)

        @block.tensor
        def _(e):
            T_.start(e)
            e.wait_ge(*V.at("int", i))
            for j in range(CJ):
                e.wait_ge(*A.at("xT", i - 1, j))
                for k in range(KT_):
                    m = e.transpose(t_ps[j][:, k * P:(k + 1) * P], q.ints[:, k, j * P:(j + 1) * P], c.identb[:, :])
                m.then_inc(T_("ints_t"), 1)
            e.wait_ge(*A.at("xT", i))
            for b in range(2):
                e.wait_ge(*V.at("added", i - 1))
                for k in (2 * b, 2 * b + 1):
                    for j in range(CJ):
                        m = e.matmul(o_ps[b][:, (k % 2) * C:(k % 2 + 1) * C], xT[:, j, k * P:(k + 1) * P],
                                     c.wo[:, j, :], start=(j == 0), stop=(j == CJ - 1))
                m.then_inc(T_("o"), 1)



def l1_state_space(nc, c):
    with ExitStack() as ctx:
        sb, ps, sem = tensors(nc, ctx, "ms")
        w_in, w_out = sb("w_in", [P, CJ, 2 * DI]), sb("w_out", [P, DC, C])
        w_x = sb("w_x", [P, DC, 2 * NS + 1])
        y_ps = [ps(f"y_ps{q}") for q in range(DC)]
        bc_ps = [ps(f"bc_ps{q}") for q in range(4)]
        n = Norm(sb, ps, y_ps[:2])
        n2 = Norm(sb, ps, y_ps[:2], "ln2")
        neg_a = sb("neg_a", [P, DC, NS])
        xm = sb("xm", [P, DC, BB, TAPS - 1 + T])
        acc = [sb(f"acc{u}", [P, BT]) for u in range(2)]
        xc, sz = sb("xc", [P, DC, BT]), sb("sz", [P, DC, BT])
        ssm = sb("ssm", [2 * NS, BT])
        lg, na, ez, wz, lz, dz, mz, step = (sb(f"dt_{k}", [P, KT_]) for k in ("lg", "na", "ez", "wz", "lz", "dz", "mz", "step"))
        dt = sb("dt", [P, BT])
        xdt = sb("xdt", [P, DC, BT])
        dA = [sb(f"dA{u}", [P, DC, BT]) for u in range(2)]
        u_ = sb("u", [P, DC, BT])
        h_ = sb("h", [P, DC, BT])
        hc = [sb(f"hc{u}", [P, DC, BT]) for u in range(2)]
        yg = sb("yg", [P, DC, BT])
        r = n2.src = sb("r", [P, KT_, C])
        loaded, made, seen = sem("loaded"), sem("made"), sem("seen")
        V = Steps(sem("vector"), LN_V + [("conv", DC * TAPS), "dt_lg", "dt_na", "dt_w", "dt_d", "dt_m", "dt_d1", "dt_inv", "dt_l1", "dt_zl",
                                              "dt_t", "dt", "xdt"] + NS * ["u", "h", "hc"]
                  + [("skip", DC), ("gated", DC), ("r1", 2), "r2"] + second_names(LN_V) + ["gain", "shift", "added"])
        A = Steps(sem("scalar"), LN_A + [("x", DC), ("silu", DC), ("z", DC), "ssm", "exp", "log", "DT"]
                  + NS * [("dA", DC)] + ["std2"])
        T_ = Steps(sem("tensor"), LN_T + [("x", DC), ("z", DC), "ssm", "dt_lg", "DT", "B", "C"] + (NS - 1) * ["B", "C", "y"]
                   + ["y", ("out", 2)])
        G = Steps(sem("pool"), NS * ["cut"])
        block = ctx.enter_context(nc.Block())
        flat = "p q t -> p (q t)"

        @block.sync
        def _(e):
            e.dma_start(w_in[:, :, :], c.d["l1_w_in"]).then_inc(loaded, 16)
            e.dma_start(w_x[:, :, :], c.d["l1_w_x"]).then_inc(loaded, 16)
            e.dma_start(w_out[:, :, :], c.d["l1_w_out"]).then_inc(loaded, 16)

        @block.tensor
        def _(e):
            T_.start(e)
            e.wait_ge(loaded, 48)

            def spread(bank, k):
                return e.matmul(bank[:, :], c.ident[0:2 * NS, k:k + 1].broadcast_to([2 * NS, P]), ssm[:, :],
                                start=True, stop=True)

            with e.Fori(0, BLOCKS) as i:
                ln_tensor(e, V, T_, n, i, c, lambda: e.wait_ge(*V.at("r1", i - 1)))
                e.wait_ge(*A.at("features", i))
                e.wait_ge(*V.at("hc", i - 1))
                for q in range(2 * DC):
                    if q >= DC:
                        e.wait_ge(*A.at("x", i, q - DC))
                    for j in range(CJ):
                        m = e.matmul(bc_ps[q % 4][:, :], w_in[:, j, q * P:(q + 1) * P], n.hT[:, j, :], start=(j == 0),
                                     stop=(j == CJ - 1))
                    m.then_inc(T_("x" if q < DC else "z"), 1)
                e.wait_ge(*A.at("silu", i))
                e.wait_ge(*A.at("z", i))
                for q in range(DC):
                    m = e.matmul(bc_ps[0][0:2 * NS, :], w_x[:, q, 0:2 * NS], xc[:, q, :], start=(q == 0), stop=(q == DC - 1))
                m.then_inc(T_("ssm"), 1)
                for k in range(KT_):
                    for q in range(DC):
                        m = e.matmul(bc_ps[1][:, k:k + 1], xc[:, q, k * P:(k + 1) * P], w_x[:, q, 2 * NS:2 * NS + 1],
                                     start=(q == 0), stop=(q == DC - 1))
                m.then_inc(T_("dt_lg"), 1)
                e.wait_ge(*V.at("dt", i))
                for k in range(KT_):
                    m = e.matmul(bc_ps[2][:, k * P:(k + 1) * P], step[:, k:k + 1].broadcast_to([P, P]), c.ident[:, :],
                                 start=True, stop=True)
                m.then_inc(T_("DT"), 1)
                e.wait_ge(*A.at("DT", i))

                def b_and_c(s):
                    if s >= 2:
                        e.wait_ge(*V.at("hc", i, s - 2))
                    spread(bc_ps[s % 2], s).then_inc(T_("B"), 1)
                    spread(bc_ps[2 + s % 2], NS + s).then_inc(T_("C"), 1)

                def add_state(s):
                    e.wait_ge(*V.at("hc", i, s))
                    for q in range(DC):
                        m = e.matmul(y_ps[q][:, :], c.ident[:, :], hc[s % 2][:, q, :], start=(s == 0), stop=(s == NS - 1))
                    m.then_inc(T_("y"), 1)

                b_and_c(0)
                for s in range(1, NS):
                    b_and_c(s)
                    add_state(s - 1)
                add_state(NS - 1)
                e.wait_ge(*V.at("gated", i))
                for b in range(2):
                    for k in (2 * b, 2 * b + 1):
                        for q in range(DC):
                            m = e.matmul(y_ps[b][:, (k % 2) * C:(k % 2 + 1) * C], yg[:, q, k * P:(k + 1) * P],
                                         w_out[:, q, :], start=(q == 0), stop=(q == DC - 1))
                    m.then_inc(T_("out"), 1)

        @block.gpsimd
        def _(e):
            G.start(e)
            with e.Fori(0, BLOCKS) as i:
                for s in range(NS):
                    e.wait_ge(*A.at("dA", i, s * DC + DC - 1))
                    e.sem_inc(seen, 1)
                    e.memset(by_batch(dA[s % 2][:, :, :].rearrange(flat))[:, :, 0:1], 0.0).then_inc(G("cut"), 1)

        @block.vector
        def _(e):
            V.start(e)
            e.memset(xm[:, :, :, :], 0.0).then_inc(made, 1)
            e.wait_ge(made, 2)
            e.tensor_scalar(neg_a[:, :, :], neg_a[:, :, :], -1.0, None, ALU.mult).then_inc(made, 1)
            taps = c.vec["conv_w"]
            with e.Fori(0, BLOCKS) as i:
                ln_vector(e, V, A, n, c.X, i, lambda: e.wait_ge(*T_.at("turned", i - 1)))
                for q in range(DC):
                    e.wait_ge(*A.at("x", i, q))
                    e.wait_ge(*(A.at("silu", i, q - 2) if q >= 2 else A.at("silu", i - 1)))
                    a = by_batch(acc[q % 2][:, :])
                    for k in range(TAPS):
                        x = xm[:, q, :, k:k + T]
                        w = taps[:, q * TAPS + k:q * TAPS + k + 1]
                        if k == 0:
                            e.tensor_scalar(a, x, w, None, ALU.mult).then_inc(V("conv"), 1)
                        else:
                            e.wait_ge(*V.at("conv", i, q * TAPS + k - 1))
                            e.scalar_tensor_tensor(a, x, w, a, ALU.mult, ALU.add).then_inc(V("conv"), 1)
                e.wait_ge(*T_.at("dt_lg", i))
                e.tensor_tensor(lg[:, :], bc_ps[1][:, 0:KT_], c.row["dt_b"].broadcast_to([P, KT_]), ALU.add).then_inc(V("dt_lg"), 1)
                e.wait_ge(*V.at("dt_lg", i))
                e.scalar_tensor_tensor(na[:, :], lg[:, :], -1.0, lg[:, :], ALU.mult, ALU.min).then_inc(V("dt_na"), 1)
                e.wait_ge(*A.at("exp", i))
                e.tensor_scalar(wz[:, :], ez[:, :], 1.0, None, ALU.add).then_inc(V("dt_w"), 1)
                e.wait_ge(*V.at("dt_w", i))
                e.tensor_scalar(dz[:, :], wz[:, :], 1.0, None, ALU.subtract).then_inc(V("dt_d"), 1)
                e.tensor_scalar(mz[:, :], wz[:, :], 1.0, None, ALU.is_equal).then_inc(V("dt_m"), 1)
                e.wait_ge(*V.at("dt_m", i))
                e.tensor_tensor(dz[:, :], dz[:, :], mz[:, :], ALU.add).then_inc(V("dt_d1"), 1)
                e.wait_ge(*V.at("dt_d1", i))
                e.reciprocal(dz[:, :], dz[:, :]).then_inc(V("dt_inv"), 1)
                e.wait_ge(*A.at("log", i))
                e.tensor_tensor(lz[:, :], lz[:, :], mz[:, :], ALU.add).then_inc(V("dt_l1"), 1)
                e.wait_ge(*V.at("dt_l1", i))
                e.tensor_tensor(lz[:, :], lz[:, :], dz[:, :], ALU.mult).then_inc(V("dt_zl"), 1)
                e.wait_ge(*V.at("dt_zl", i))
                e.tensor_tensor(lz[:, :], lz[:, :], ez[:, :], ALU.mult).then_inc(V("dt_t"), 1)
                e.wait_ge(*V.at("dt_t", i))
                e.scalar_tensor_tensor(step[:, :], lg[:, :], 0.0, lz[:, :], ALU.max, ALU.add).then_inc(V("dt"), 1)
                e.wait_ge(*A.at("DT", i))
                shape = [P, DC, BT]
                e.tensor_tensor(xdt[:, :, :], xc[:, :, :], over(dt[:, :], shape, 1), ALU.mult).then_inc(V("xdt"), 1)
                e.wait_ge(*V.at("xdt", i))
                for s in range(NS):
                    e.wait_ge(*T_.at("B", i, s))
                    e.tensor_tensor(u_[:, :, :], xdt[:, :, :], over(bc_ps[s % 2][:, :], shape, 1), ALU.mult).then_inc(V("u"), 1)
                    e.wait_ge(*V.at("u", i, s))
                    e.wait_ge(*G.at("cut", i, s))
                    e.tensor_tensor_scan(h_[:, :, :].rearrange(flat), dA[s % 2][:, :, :].rearrange(flat),
                                         u_[:, :, :].rearrange(flat), 0.0, ALU.mult, ALU.add).then_inc(V("h"), 1)
                    e.wait_ge(*V.at("h", i, s))
                    e.wait_ge(*T_.at("C", i, s))
                    e.wait_ge(*(T_.at("y", i, s - 2) if s >= 2 else T_.at("y", i - 1)))
                    e.tensor_tensor(hc[s % 2][:, :, :], h_[:, :, :], over(bc_ps[2 + s % 2][:, :], shape, 1),
                                    ALU.mult).then_inc(V("hc"), 1)
                e.wait_ge(*T_.at("y", i))
                for q in range(DC):
                    e.scalar_tensor_tensor(yg[:, q, :], xc[:, q, :], c.vec["D"][:, q:q + 1], y_ps[q][:, :], ALU.mult,
                                           ALU.add).then_inc(V("skip"), 1)
                e.wait_ge(*A.at("z", i))
                for q in range(DC):
                    e.wait_ge(*V.at("skip", i, q))
                    e.tensor_tensor(yg[:, q, :], yg[:, q, :], sz[:, q, :], ALU.mult).then_inc(V("gated"), 1)
                for b in range(2):
                    e.wait_ge(*T_.at("out", i, b))
                    e.tensor_tensor(r[:, 2 * b:2 * b + 2, :], n.xn[:, 2 * b:2 * b + 2, :],
                                    y_ps[b][:, :].rearrange("p (k f) -> p k f", k=2), ALU.add).then_inc(V("r1"), 1)
                e.wait_ge(*V.at("r1", i))
                rows = [P, KT_, C]
                e.tensor_tensor(r[:, :, :], r[:, :, :], over(c.row["out_b"], rows, 1), ALU.add).then_inc(V("r2"), 1)
                e.wait_ge(*V.at("r2", i))
                ln_vector(e, second(V), second(A), n2, None, i, lambda: None)
                e.wait_ge(*V.at("norm2", i))
                y = n2.xn[:, :, :]
                e.tensor_tensor(y, y, over(c.row["m_gamma"], rows, 1), ALU.mult).then_inc(V("gain"), 1)
                e.wait_ge(*V.at("gain", i))
                e.tensor_tensor(y, y, over(c.row["m_beta"], rows, 1), ALU.add).then_inc(V("shift"), 1)
                e.wait_ge(*V.at("shift", i))
                x = c.X[:, bass.ds(i * KT_, KT_), :]
                e.tensor_tensor(x, x, y, ALU.add).then_inc(V("added"), 1)

        @block.scalar
        def _(e):
            A.start(e)
            e.activation(neg_a[:, :, :].rearrange("p q s -> p (q s)"), c.vec["A_log"], ACT.Exp).then_inc(made, 1)
            e.wait_ge(made, 3)
            with e.Fori(0, BLOCKS) as i:
                ln_scalar_std(e, V, A, n, i, c)
                ln_scalar_features(e, T_, A, n, i, lambda: e.wait_ge(*T_.at("z", i - 1)))
                bias = c.vec["in_b"]
                e.wait_ge(*V.at("conv", i - 1))
                for q in range(DC):
                    e.wait_ge(*T_.at("x", i, q))
                    e.activation(xm[:, q, :, TAPS - 1:], by_batch(bc_ps[q][:, :]), ACT.Identity,
                                 bias=bias[:, q:q + 1]).then_inc(A("x"), 1)
                e.wait_ge(*V.at("skip", i - 1))
                e.wait_ge(*T_.at("ssm", i - 1))
                for q in range(DC):
                    e.wait_ge(*V.at("conv", i, q * TAPS + TAPS - 1))
                    e.activation(xc[:, q, :], acc[q % 2][:, :], ACT.Silu,
                                 bias=c.vec["conv_b"][:, q:q + 1]).then_inc(A("silu"), 1)
                e.wait_ge(*V.at("gated", i - 1))
                for q in range(DC):
                    e.wait_ge(*T_.at("z", i, q))
                    e.activation(sz[:, q, :], bc_ps[q][:, :], ACT.Silu,
                                 bias=bias[:, DC + q:DC + q + 1]).then_inc(A("z"), 1)
                e.wait_ge(*T_.at("ssm", i))
                e.wait_ge(*T_.at("C", i - 1))
                e.activation(ssm[:, :], bc_ps[0][0:2 * NS, :], ACT.Identity,
                             bias=c.sm["xp_b"][0:2 * NS, :]).then_inc(A("ssm"), 1)
                e.wait_ge(*V.at("dt_na", i))
                e.activation(ez[:, :], na[:, :], ACT.Exp).then_inc(A("exp"), 1)
                e.wait_ge(*V.at("dt_w", i))
                e.activation(lz[:, :], wz[:, :], ACT.Ln).then_inc(A("log"), 1)
                e.wait_ge(*T_.at("DT", i))
                e.activation(dt[:, :], bc_ps[2][:, :], ACT.Copy).then_inc(A("DT"), 1)
                e.wait_ge(*A.at("DT", i))
                for s in range(NS):
                    e.wait_ge(*(V.at("h", i, s - 2) if s >= 2 else V.at("h", i - 1)))
                    for q in range(DC):
                        e.activation(dA[s % 2][:, q, :], dt[:, :], ACT.Exp, scale=neg_a[:, q, s:s + 1]).then_inc(A("dA"), 1)
                ln_scalar_std(e, second(V), second(A), n2, i, c)



def l1_gates(nc, c):
    with ExitStack() as ctx:
        sb, ps, sem = tensors(nc, ctx, "fg")
        wg = sb("wg", [P, CJ, E])
        n = Norm(sb, ps, tiles=TILES)
        lg, sq = sb("lg", [P, TILES, E]), sb("sq", [P, TILES, E])
        ms, big, tot = sb("ms", [P, TILES]), sb("big", [P, TILES]), sb("tot", [P, TILES])
        g_ps = ps("g_ps")
        g_loaded = sem("g_loaded")
        V = Steps(sem("vector"), ALL_V + ["logits", "square", "mean_sq", "flip", "scaled", "weighted", "big", "less", "sum",
                                          "g", "g_eps", "g_inv", "norm_g"])
        A = Steps(sem("scalar"), ALL_A + ["rms", "exp"])
        T_ = Steps(sem("tensor"), ALL_T + ["logits"])
        G = Steps(sem("pool"), ALL_G)
        block = ctx.enter_context(nc.Block())
        shape = [P, TILES, E]
        flat = "p k e -> p (k e)"

        @block.sync
        def _(e):
            e.dma_start(wg[:, :, :], c.d["l1_wg"]).then_inc(g_loaded, 16)
            for q in range(E):
                e.dma_start(c.w1[q][:, :, :], c.d["l1_w1"][q]).then_inc(c.w_loaded[q], 16)
                e.dma_start(c.w2[q][:, :, :], c.d["l1_w2"][q]).then_inc(c.w_loaded[q], 16)

        @block.tensor
        def _(e):
            T_.start(e)
            all_tensor(e, V, A, T_, n, c)
            e.wait_ge(g_loaded, 16)
            for k in range(TILES):
                if k % KT_ == 0:
                    e.wait_ge(*A.at("features", 0, k // KT_ * CJ + CJ - 1))
                for j in range(CJ):
                    m = e.matmul(g_ps[:, k * E:(k + 1) * E], n.hT[:, j, k * P:(k + 1) * P], wg[:, j, :],
                                 start=(j == 0), stop=(j == CJ - 1))
            m.then_inc(T_("logits"), 1)

        @block.gpsimd
        def _(e):
            G.start(e)
            all_pool(e, A, G, n, c.parts)

        @block.scalar
        def _(e):
            A.start(e)
            ln_scalar_std(e, V, A, n, 0, c)
            all_scalar(e, T_, A, n, c.parts)
            e.wait_ge(*V.at("mean_sq", 0))
            e.activation(ms[:, :], ms[:, :], ACT.Sqrt, scale=1.0 / E, bias=c.eps[:, 3:4]).then_inc(A("rms"), 1)
            e.wait_ge(*V.at("less", 0))
            e.activation(sq[:, :, :].rearrange(flat), lg[:, :, :].rearrange(flat), ACT.Exp,
                         scale=2.0).then_inc(A("exp"), 1)

        @block.vector
        def _(e):
            V.start(e)
            ln_vector(e, V, A, n, c.X, 0, lambda: None)
            e.wait_ge(*T_.at("logits", 0))
            e.tensor_tensor(lg[:, :, :], g_ps[:, 0:TILES * E].rearrange("p (k e) -> p k e", k=TILES),
                            over(c.row["gate_b"], shape, 1), ALU.add).then_inc(V("logits"), 1)
            e.wait_ge(*V.at("logits", 0))
            e.tensor_tensor(sq[:, :, :], lg[:, :, :], lg[:, :, :], ALU.mult).then_inc(V("square"), 1)
            e.wait_ge(*V.at("square", 0))
            e.tensor_reduce(ms[:, :], sq[:, :, :], AX.X, ALU.add).then_inc(V("mean_sq"), 1)
            e.wait_ge(*A.at("rms", 0))
            e.reciprocal(ms[:, :], ms[:, :]).then_inc(V("flip"), 1)
            e.wait_ge(*V.at("flip", 0))
            e.tensor_tensor(lg[:, :, :], lg[:, :, :], over(ms[:, :], shape, 2), ALU.mult).then_inc(V("scaled"), 1)
            e.wait_ge(*V.at("scaled", 0))
            e.tensor_tensor(lg[:, :, :], lg[:, :, :], over(c.row["rms_w"], shape, 1), ALU.mult).then_inc(V("weighted"), 1)
            e.wait_ge(*V.at("weighted", 0))
            e.tensor_reduce(big[:, :], lg[:, :, :], AX.X, ALU.max).then_inc(V("big"), 1)
            e.wait_ge(*V.at("big", 0))
            e.tensor_tensor(lg[:, :, :], lg[:, :, :], over(big[:, :], shape, 2), ALU.subtract).then_inc(V("less"), 1)
            e.wait_ge(*A.at("exp", 0))
            e.tensor_reduce(tot[:, :], sq[:, :, :], AX.X, ALU.add).then_inc(V("sum"), 1)
            e.wait_ge(*V.at("sum", 0))
            e.reciprocal(tot[:, :], tot[:, :]).then_inc(V("g"), 1)
            e.wait_ge(*V.at("g", 0))
            e.tensor_scalar(big[:, :], tot[:, :], 1e-6, None, ALU.add).then_inc(V("g_eps"), 1)
            e.wait_ge(*V.at("g_eps", 0))
            e.reciprocal(big[:, :], big[:, :]).then_inc(V("g_inv"), 1)
            e.wait_ge(*V.at("g_inv", 0))
            e.scalar_tensor_tensor(c.norm_g[:, :], tot[:, :], 1.0 / W_SCALE, big[:, :], ALU.mult,
                                   ALU.mult).then_inc(V("norm_g"), 1)


def l1_experts(nc, c):
    with ExitStack() as ctx:
        sb, ps, sem = tensors(nc, ctx, "fe")
        w1 = [[sb(f"w1_{u}{x}", [P, CJ, FH], FP16) for x in range(2)] for u in range(E)]
        w2 = [[sb(f"w2_{u}{x}", [P, FJ, C], FP16) for x in range(2)] for u in range(E)]
        scale = sb("scale", [E, P])
        g = [sb(f"g{u}", [P, BT]) for u in range(2)]
        hid = [[sb(f"hid{u}{x}", [P, FJ, BT], FP16) for x in range(2)] for u in range(2)]
        h_ps = [ps(f"h_ps{u}") for u in range(4)]
        y_ps = [ps(f"y_ps{k}") for k in range(KT_)]
        N = E * FJ
        made = sem("made")
        V = Steps(sem("vector"), N * ["rounded", "rest"] + [("added", KT_)])
        A = Steps(sem("scalar"), [("gelu", N)])
        T_ = Steps(sem("tensor"), [("hidden", FJ)] + [("hidden", FJ), "y"] * (E - 1) + ["y"])
        G = Steps(sem("pool"), E * [f"{w}_{step}" for w in ("w1", "w2") for step in ("scaled", "rounded", "rest")])
        block = ctx.enter_context(nc.Block())
        products = ((0, 0), (0, 1), (1, 0))

        @block.gpsimd
        def _(e):
            G.start(e)
            for q in range(E):
                e.wait_ge(c.w_loaded[q], 32)
                for name, w, parts in (("w1", c.w1[q][:, :, :], w1[q]), ("w2", c.w2[q][:, :, :], w2[q])):
                    e.tensor_scalar(w, w, W_SCALE, None, ALU.mult).then_inc(G(f"{name}_scaled"), 1)
                    e.wait_ge(*G.at(f"{name}_scaled", 0, q))
                    e.tensor_copy(parts[0][:, :, :], w).then_inc(G(f"{name}_rounded"), 1)
                    e.wait_ge(*G.at(f"{name}_rounded", 0, q))
                    e.tensor_tensor(parts[1][:, :, :], w, parts[0][:, :, :], ALU.subtract).then_inc(G(f"{name}_rest"), 1)

        @block.tensor
        def _(e):
            T_.start(e)
            e.wait_ge(made, 1)

            def hidden(i, q):
                e.wait_ge(*G.at("w2_rest", 0, q))
                for f in range(FJ):
                    at = q * FJ + f
                    e.wait_ge(*(A.at("gelu", i, at - 4) if at >= 4 else A.at("gelu", i - 1, N - 4 + at)))
                    for j in range(CJ):
                        for w, x in products:
                            m = e.matmul(h_ps[f][:, :], w1[q][w][:, j, f * P:(f + 1) * P],
                                         c.parts[x][:, j, bass.ds(i * BT, BT)], start=(j == 0 and w + x == 0),
                                         stop=(j == CJ - 1 and w == 1))
                    m.then_inc(T_("hidden"), 1)

            def combine(i, q):
                e.wait_ge(*V.at("rest", i, q * FJ + FJ - 1))
                for k in range(KT_):
                    for f in range(FJ):
                        for x, w in products:
                            m = e.matmul(y_ps[k][:, 0:C], hid[q % 2][x][:, f, k * P:(k + 1) * P], w2[q][w][:, f, :],
                                         start=False, stop=(q == E - 1 and f == FJ - 1 and x == 1))
                m.then_inc(T_("y"), 1)

            with e.Fori(0, BLOCKS) as i:
                hidden(i, 0)
                for k in range(KT_):
                    e.wait_ge(*V.at("added", i - 1, k))
                    e.matmul(y_ps[k][:, 0:C], scale[:, :], c.sm["b2"][0:E, :], start=True, stop=False)
                for q in range(1, E):
                    hidden(i, q)
                    combine(i, q - 1)
                combine(i, E - 1)

        @block.scalar
        def _(e):
            A.start(e)
            with e.Fori(0, BLOCKS) as i:
                for q in range(E):
                    for f in range(FJ):
                        at = q * FJ + f
                        e.wait_ge(*T_.at("hidden", i, at))
                        e.wait_ge(*(V.at("rest", i, at - 2) if at >= 2 else V.at("rest", i - 1, N - 2 + at)))
                        e.activation(g[f % 2][:, :], h_ps[f][:, :], ACT.Gelu, scale=1.0 / W_SCALE,
                                     bias=c.vec["b1"][:, at:at + 1]).then_inc(A("gelu"), 1)

        @block.vector
        def _(e):
            V.start(e)
            e.memset(scale[:, :], W_SCALE).then_inc(made, 1)
            with e.Fori(0, BLOCKS) as i:
                for q in range(E):
                    for f in range(FJ):
                        at = q * FJ + f
                        part = hid[q % 2]
                        e.wait_ge(*A.at("gelu", i, at))
                        if f == 0:
                            e.wait_ge(*(T_.at("y", i, q - 2) if q >= 2 else T_.at("y", i - 1, E - 2 + q)))
                        e.tensor_copy(part[0][:, f, :], g[f % 2][:, :]).then_inc(V("rounded"), 1)
                        e.wait_ge(*V.at("rounded", i, at))
                        e.tensor_tensor(part[1][:, f, :], g[f % 2][:, :], part[0][:, f, :],
                                        ALU.subtract).then_inc(V("rest"), 1)
                e.wait_ge(*T_.at("y", i))
                for k in range(KT_):
                    x = c.X[:, i * KT_ + k, :]
                    e.scalar_tensor_tensor(x, y_ps[k][:, 0:C], c.norm_g[:, bass.ds(i * KT_ + k, 1)], x, ALU.mult,
                                           ALU.add).then_inc(V("added"), 1)



VECS = [("bq", 2), ("bk", 2), ("ln1_g", 2), ("ln1_b", 2), ("ln2_g", 2), ("ln2_b", 2), ("decay", 2), ("first", 2),
        ("tm_k", 2), ("tm_v", 2), ("tm_r", 2), ("cm_k", 2), ("cm_r", 2), ("in_b", 8), ("conv_w", 16), ("conv_b", 4),
        ("D", 4), ("A_log", 64), ("b1", 32)]
ROWS = [("bv", C), ("x_gamma", C), ("x_beta", C), ("out_b", C), ("m_gamma", C), ("m_beta", C), ("gate_b", E),
        ("rms_w", E), ("dt_b", 1)]
SMALL = [("be", C), ("b2", C), ("xp_b", 1)]


def named(tensor, table):
    out, at = {}, 0
    for name, n in table:
        out[name] = tensor[:, at:at + n]
        at += n
    return out, at


def build(nc, d, stages=range(1, 7)):
    c = Chip()
    c.d = d
    with ExitStack() as ctx:
        sb, ps, sem = tensors(nc, ctx, "c")
        c.X = sb("x", [P, TILES, C])
        c.vecs = sb("vecs", [P, sum(n for _, n in VECS)])
        c.rows = sb("rows", [P, sum(n for _, n in ROWS)])
        c.small = sb("small", [33, sum(n for _, n in SMALL)])
        c.vec, _ = named(c.vecs, VECS)
        c.row, _ = named(c.rows, ROWS)
        c.sm, _ = named(c.small, SMALL)
        c.consts = sb("consts", [P, P + 20])
        c.ident = c.consts[:, 0:P]
        c.own = c.consts[:, P:P + 4]
        c.group = c.consts[:, P + 4:P + 12]
        c.iota = c.consts[:, P + 12:P + 20]
        c.identb = sb("identb", [P, P], BF16)
        c.identh = sb("identh", [P, P], FP16)
        c.eps = sb("eps", [P, 4])
        c.ones = sb("ones", [P, P])
        c.c_max = sb("c_max", [P, 2 * B])
        c.c_ss = sb("c_ss", [P, 2 * B])
        load_all(nc, c)
        with ExitStack() as mid:
            c.cq = mid.enter_context(nc.sbuf_tensor("c_cq", [P, 2 * B, C], BF16))
            if 1 in stages:
                with ExitStack() as one:
                    c.qkT = one.enter_context(nc.sbuf_tensor("c_qkT", [P, CJ, B * T], FP32))
                    c.qc = one.enter_context(nc.sbuf_tensor("c_qc", [P, TILES], FP32))
                    l0_queries(nc, c)
                    l0_attention(nc, c)
            if 2 in stages:
                with ExitStack() as two:
                    c.XI = two.enter_context(nc.sbuf_tensor("c_XI", [P, TILES, C], FP32))
                    l0_time_mix(nc, c)
                    l0_channel_mix(nc, c)
            if 3 in stages:
                with ExitStack() as three:
                    def sb3(name, shape, dt=FP32):
                        return three.enter_context(nc.sbuf_tensor(f"c_{name}", shape, dt))

                    c.parts = [sb3(f"parts{x}", [P, CJ, B * T], FP16) for x in range(2)]
                    c.we = [sb3(f"we{x}", [P, CJ, E * C], FP16) for x in range(2)]
                    c.gate, c.gate_t = sb3("gate", [P, TILES, E]), sb3("gate_t", [E, B * T])
                    l0_gates(nc, c)
                    l0_experts(nc, c)
            if 4 in stages:
                with ExitStack() as four:
                    def sb4(name, shape, dt=FP32):
                        return four.enter_context(nc.sbuf_tensor(f"c_{name}", shape, dt))

                    c.wq, c.wkv, c.wo = (sb4(k, [P, CJ, C], BF16) for k in ("wq", "wkv", "wo"))
                    c.wf = sb4("wf", [P, 4])
                    c.kf, c.vf = sb4("kf", [P, 2 * B]), sb4("vf", [P, 2 * B])
                    c.k_last = sb4("k_last", [P, 2, B], FP16)
                    c.v_last = sb4("v_last", [4, BQ, 4, P // 2])
                    c.mask = sb4("mask", [P, 4])
                    c.qT = sb4("qT", [P, 8, B * T], FP16)
                    l1_prepare(nc, c)
                    l1_queries(nc, c)
                    c.XA = sb4("XA", [P, KT_, C])
                    with ExitStack() as kv:
                        c.kT = kv.enter_context(nc.sbuf_tensor("c_kT", [P, BQ, 2, M], FP16))
                        c.v = kv.enter_context(nc.sbuf_tensor("c_v", [P, BQ, 2, P], FP32))
                        shared = Shared(nc, kv, "keys"), Shared(nc, kv, "att")
                        for quarter in range(B // BQ):
                            l1_keys(nc, c, shared[0], quarter)
                            l1_attention(nc, c, shared[1], quarter)
                            l1_project(nc, c, quarter)
        if 5 in stages:
            l1_state_space(nc, c)
        if 6 in stages:
            with ExitStack() as six:
                def sb6(name, shape, dt=FP32):
                    return six.enter_context(nc.sbuf_tensor(f"c_{name}", shape, dt))

                c.w1 = [sb6(f"w1_{q}", [P, CJ, FH]) for q in range(E)]
                c.w2 = [sb6(f"w2_{q}", [P, FJ, C]) for q in range(E)]
                c.w_loaded = [six.enter_context(nc.semaphore(f"c_w_loaded{q}")) for q in range(E)]
                c.parts = [sb6(f"f_parts{x}", [P, CJ, B * T], FP16) for x in range(2)]
                c.norm_g = sb6("norm_g", [P, TILES])
                l1_gates(nc, c)
                l1_experts(nc, c)
        store(nc, c)


def store(nc, c):
    with ExitStack() as ctx:
        sb, ps, sem = tensors(nc, ctx, "st")
        stored = sem("stored")
        block = ctx.enter_context(nc.Block())

        @block.sync
        def _(e):
            e.dma_start(c.d["out"], c.X[:, :, :]).then_inc(stored, 16)
            e.wait_ge(stored, 16)


def layout(i):
    f = {k: np.asarray(v) for k, v in i.items()}

    def feat(w):
        w = w.T
        return np.ascontiguousarray(w.reshape(-1, P, w.shape[1]).transpose(1, 0, 2))

    def nat(w):
        return np.ascontiguousarray(w.reshape(-1, P, w.shape[1]).transpose(1, 0, 2))

    def vec(v):
        return v.reshape(-1, P).T

    ctxm = f["ctx_1024"]
    a = {}
    a["x"] = f["x"].reshape(TILES, P, C).transpose(1, 0, 2)
    main, last = ctxm[:, :2 * P, :], ctxm[:, 2 * P, :]
    a["ctx_n"] = main.reshape(TILES, BPT, 2, P, C).transpose(0, 3, 1, 2, 4)
    a["ctx_t"] = main.reshape(TILES, BPT, 2 * P, CJ, P).transpose(0, 4, 1, 3, 2)
    a["ctx_last_n"] = last.reshape(TILES, BPT, C).transpose(1, 0, 2)
    a["ctx_last_t"] = last.reshape(B, CJ, P).transpose(2, 1, 0)
    a["mask"] = f["mask_SxS2_ik1"]
    a["l0_wq"], a["l0_wk"], a["l0_wv"] = nat(f["L0_xattn_Wq"]), nat(f["L0_xattn_Wk"]), feat(f["L0_xattn_Wv"])
    for k, n in (("km", "Wk"), ("vm", "Wv"), ("rm", "Wr"), ("om", "Wo"), ("ck", "Wck"), ("cr", "Wcr"), ("cv", "Wcv")):
        a[f"l0_w{k}"] = feat(f[f"L0_attn_{n}"])
    a["l0_wg"] = nat(f["L0_ffn_Wg"])
    a["l0_we"] = f["L0_ffn_We"].reshape(E, CJ, P, C).transpose(2, 1, 0, 3).reshape(P, CJ, E * C)
    a["l1_wg"] = feat(f["L1_ffn_gate_w"])
    a["l1_w1"] = f["L1_ffn_w1"].reshape(E, CJ, P, FH).transpose(0, 2, 1, 3)
    a["l1_w2"] = f["L1_ffn_w2"].reshape(E, FH // P, P, C).transpose(0, 2, 1, 3)
    a["l1_w_in"], a["l1_w_x"] = feat(f["L1_attn_in_proj_w"]), feat(f["L1_attn_x_proj_w"])
    a["l1_w_out"] = feat(f["L1_attn_out_proj_w"])
    wq = f["L1_xattn_wq"].reshape(KVH, 2, HD, C).transpose(1, 0, 2, 3).reshape(C, C)
    a["l1_wq"], a["l1_wk"], a["l1_wv"], a["l1_wo"] = (feat(w) for w in (wq, f["L1_xattn_wk"], f["L1_xattn_wv"],
                                                                         f["L1_xattn_wo"]))
    a["ctx_last"] = last
    v = {"bq": f["L0_xattn_bq"], "bk": f["L0_xattn_bk"], "ln1_g": f["L0_attn_ln1_g"], "ln1_b": f["L0_attn_ln1_b"],
         "ln2_g": f["L0_attn_ln2_g"], "ln2_b": f["L0_attn_ln2_b"], "decay": f["L0_attn_time_decay"],
         "first": f["L0_attn_time_first"], "tm_k": f["L0_attn_tm_k"], "tm_v": f["L0_attn_tm_v"],
         "tm_r": f["L0_attn_tm_r"], "cm_k": f["L0_attn_cm_k"], "cm_r": f["L0_attn_cm_r"],
         "in_b": f["L1_attn_in_proj_b"], "conv_b": f["L1_attn_conv_b"], "D": f["L1_attn_D"]}
    v = {k: vec(x.reshape(-1)) for k, x in v.items()}
    v["conv_w"] = f["L1_attn_conv_w"].reshape(DC, P, TAPS).transpose(1, 0, 2).reshape(P, -1)
    v["A_log"] = f["L1_attn_A_log"].reshape(DC, P, NS).transpose(1, 0, 2).reshape(P, -1)
    v["b1"] = f["L1_ffn_b1"].reshape(E, FH // P, P).transpose(2, 0, 1).reshape(P, -1)
    a["vecs"] = np.concatenate([v[n] for n, _ in VECS], 1)
    r = {"bv": f["L0_xattn_bv"], "x_gamma": f["L1_xattn_ln_gamma"], "x_beta": f["L1_xattn_ln_beta"],
         "out_b": f["L1_attn_out_proj_b"], "m_gamma": f["L1_attn_ln_gamma"], "m_beta": f["L1_attn_ln_beta"],
         "gate_b": f["L1_ffn_gate_b"], "rms_w": f["L1_ffn_rms_w"],
         "dt_b": f["L1_attn_x_proj_b"][2 * NS:]}
    a["rows"] = np.broadcast_to(np.concatenate([r[n] for n, _ in ROWS])[None], (P, sum(n for _, n in ROWS)))
    small = np.zeros((33, sum(n for _, n in SMALL)), np.float32)
    small[:E, 0:C], small[:E, C:2 * C], small[:, 2 * C] = f["L0_ffn_be"], f["L1_ffn_b2"], f["L1_attn_x_proj_b"]
    a["small"] = small
    p = np.arange(P)[:, None]
    a["ident"] = np.concatenate([np.eye(P), p // T == np.arange(4), p // HD == np.arange(8),
                                 np.broadcast_to(np.arange(8), (P, 8))], 1).astype(np.float32)
    return {k: np.ascontiguousarray(x) for k, x in a.items()}


def kernel(**inputs):
    from concourse import bacc
    from concourse.bass_utils import run_bass_kernel_spmd

    nc = bacc.Bacc("TRN2", target_bir_lowering=False, num_devices=1)
    arrays = {f"in_{k}": a for k, a in layout(inputs).items()}
    d = {k[3:]: nc.dram_tensor(k, a.shape, mybir.dt.from_np(a.dtype), kind="ExternalInput").ap()
         for k, a in arrays.items()}
    out = nc.dram_tensor("out", (TILES, P, C), FP32, kind="ExternalOutput").ap()
    d["bounce"] = nc.dram_tensor("bounce", (B, P), FP32, kind="Internal").ap()
    d["out"] = out.rearrange("t p c -> p t c")
    build(nc, d)
    r = run_bass_kernel_spmd(nc, [arrays], core_ids=[0])
    return r.results[0]["out"].reshape(B, T, C)
```

```python
from contextlib import ExitStack

import numpy as np

import concourse.bass as bass
from concourse import mybir

FP32 = mybir.dt.float32
BF16 = mybir.dt.bfloat16
FP16 = mybir.dt.float16
I32 = mybir.dt.int32
U32 = mybir.dt.uint32
ALU = mybir.AluOpType
ACT = mybir.ActivationFunctionType
AX = mybir.AxisListType

P = 128
B, T, C, M = 64, 32, 256, 257
CJ = C // P
TILES = B * T // P
BPT = P // T
KT_ = 4
BLOCKS = TILES // KT_
BT = KT_ * P
BB = KT_ * BPT
HID = 4 * C
E = 8
FH = 512
FJ = FH // P
HEADS, KVH, HD = 16, 8, 16
DI, NS, TAPS = 512, 16, 4
DC = DI // P
NR = 2 * NS + 1
NEG = -1.0e9
FAR = -1.0e38
LN_EPS, RMS_EPS = 1e-5, 1e-6
ROUND = 1.5 * 2.0 ** 23
W_SCALE = 128.0
F32_EPS = float(np.finfo(np.float32).eps)


class Steps:

    def __init__(self, sem, names, ahead=1):
        self.sem = sem
        self.ahead = ahead
        self.names = [n for item in names for n in ([item] if isinstance(item, str) else [item[0]] * item[1])]
        self.n = len(self.names)
        self.emitted = 0
        self.before = 0

    def start(self, eng):
        if self.before == 0:
            eng.sem_inc(self.sem, self.ahead * self.n)

    def __call__(self, name):
        want = self.names[self.emitted % self.n]
        assert want == name, (want, name)
        self.emitted += 1
        return self.sem

    def at(self, name, i, k=None):
        places = [p for p, n in enumerate(self.names) if n == name]
        place = places[-1] if k is None else places[k]
        return self.sem, (i + self.before + self.ahead) * self.n + place + 1


class Chip:
    pass


class Shared:

    def __init__(self, nc, ctx, prefix):
        self.nc, self.ctx, self.prefix = nc, ctx, prefix
        self.made = {}

    def sem(self, name):
        if name not in self.made:
            self.made[name] = self.ctx.enter_context(self.nc.semaphore(f"{self.prefix}_{name}"))
        return self.made[name]

    def steps(self, name, names, before, ahead=2):
        key = "steps " + name
        if key not in self.made:
            self.made[key] = Steps(self.sem(name), names, ahead)
        self.made[key].before = before
        return self.made[key]


def tensors(nc, ctx, prefix):
    def sb(name, shape, dt=FP32):
        return ctx.enter_context(nc.sbuf_tensor(f"{prefix}_{name}", shape, dt))

    def ps(name, shape=(P, 512), dt=FP32):
        return ctx.enter_context(nc.psum_tensor(f"{prefix}_{name}", list(shape), dt))

    def sem(name):
        return ctx.enter_context(nc.semaphore(f"{prefix}_{name}"))

    return sb, ps, sem



LN_V = [("stats", 4), "sums", "diff", "between", "variance", "mean", "rstd", ("norm", 4)]
LN_A = ["std", ("features", CJ)]
LN_T = [("turned", CJ)]


class Norm:

    def __init__(self, sb, ps, banks=None, name="ln", tiles=KT_, xn=None):
        self.tiles = tiles
        self.stats = sb(f"{name}_stats", [P, tiles, 6])
        self.sums = sb(f"{name}_sums", [P, tiles, 2])
        self.diff = sb(f"{name}_diff", [P, tiles])
        self.var = sb(f"{name}_var", [P, tiles])
        self.mean = sb(f"{name}_mean", [P, tiles])
        self.std = sb(f"{name}_std", [P, tiles])
        self.rstd = sb(f"{name}_rstd", [P, tiles])
        self.xn = sb(f"{name}_xn", [P, tiles, C]) if xn is None else xn
        self.hT = sb(f"{name}_hT", [P, CJ, tiles * P]) if name == "ln" else None
        self.ps = banks or [ps(f"{name}_ps{j}") for j in range(CJ)]
        self.src = None


def second_names(names):
    return [n + "2" if isinstance(n, str) else (n[0] + "2", n[1]) for n in names]


class second:

    def __init__(self, steps):
        self.steps = steps

    def __call__(self, name):
        return self.steps(name + "2")

    def at(self, name, i, k=None):
        return self.steps.at(name + "2", i, k)


def ln_vector(e, V, A, n, src, i, free, stats=True):
    def tile(k):
        return n.src[:, k, :] if src is None else src[:, i * n.tiles + k, :]

    for k in range(n.tiles if stats else 0):
        e.bn_stats(n.stats[:, k, :], tile(k)).then_inc(V("stats"), 1)
    e.wait_ge(*V.at("stats", i))
    e.tensor_tensor(n.sums[:, :, :], n.stats[:, :, 1:3], n.stats[:, :, 4:6], ALU.add).then_inc(V("sums"), 1)
    e.tensor_tensor(n.diff[:, :], n.stats[:, :, 1], n.stats[:, :, 4], ALU.subtract).then_inc(V("diff"), 1)
    e.wait_ge(*V.at("diff", i))
    e.scalar_tensor_tensor(n.var[:, :], n.diff[:, :], 0.25, n.diff[:, :], ALU.mult, ALU.mult).then_inc(V("between"), 1)
    e.wait_ge(*V.at("between", i))
    e.scalar_tensor_tensor(n.var[:, :], n.sums[:, :, 1], 1.0 / C, n.var[:, :], ALU.mult, ALU.add).then_inc(V("variance"), 1)
    e.tensor_scalar(n.mean[:, :], n.sums[:, :, 0], 0.5, None, ALU.mult).then_inc(V("mean"), 1)
    e.wait_ge(*A.at("std", i))
    e.reciprocal(n.rstd[:, :], n.std[:, :]).then_inc(V("rstd"), 1)
    e.wait_ge(*V.at("rstd", i))
    free()
    for k in range(n.tiles):
        e.tensor_scalar(n.xn[:, k, :], tile(k), n.mean[:, k:k + 1], n.rstd[:, k:k + 1],
                        ALU.subtract, ALU.mult).then_inc(V("norm"), 1)


def ln_scalar_std(e, V, A, n, i, c):
    e.wait_ge(*V.at("variance", i))
    e.activation(n.std[:, :], n.var[:, :], ACT.Sqrt, bias=c.eps[:, 0:1]).then_inc(A("std"), 1)


def ln_scalar_features(e, T_, A, n, i, free, gain=None, shift=None):
    free()
    for j in range(CJ):
        e.wait_ge(*T_.at("turned", i, j))
        if gain is None:
            e.activation(n.hT[:, j, :], n.ps[j][:, :], ACT.Copy).then_inc(A("features"), 1)
        else:
            e.activation(n.hT[:, j, :], n.ps[j][:, :], ACT.Identity, bias=shift[:, j:j + 1],
                         scale=gain[:, j:j + 1]).then_inc(A("features"), 1)


def ln_tensor(e, V, T_, n, i, c, free, src=None, step="norm"):
    src = src or n.xn
    free()
    e.wait_ge(*V.at(step, i))
    for j in range(CJ):
        for k in range(KT_):
            t = e.transpose(n.ps[j][:, k * P:(k + 1) * P], src[:, k, j * P:(j + 1) * P], c.ident[:, :])
        t.then_inc(T_("turned"), 1)



ALL_V = [(n[0], TILES) if isinstance(n, tuple) else n for n in LN_V]
ALL_A = ["std"] + BLOCKS * CJ * ["features", "rounded"]
ALL_T = [("turned", BLOCKS * CJ)]
ALL_G = [("rest", BLOCKS * CJ)]


def all_tensor(e, V, A, T_, n, c):
    for i in range(BLOCKS):
        for j in range(CJ):
            if i:
                e.wait_ge(*A.at("rounded", 0, (i - 1) * CJ + j))
            e.wait_ge(*V.at("norm", 0, i * KT_ + KT_ - 1))
            for k in range(KT_):
                t = e.transpose(n.ps[j][:, k * P:(k + 1) * P], n.xn[:, i * KT_ + k, j * P:(j + 1) * P], c.ident[:, :])
            t.then_inc(T_("turned"), 1)


def all_scalar(e, T_, A, n, parts):
    for i in range(BLOCKS):
        for j in range(CJ):
            e.wait_ge(*T_.at("turned", 0, i * CJ + j))
            e.activation(n.hT[:, j, i * BT:(i + 1) * BT], n.ps[j][:, :], ACT.Copy).then_inc(A("features"), 1)
            e.activation(parts[0][:, j, i * BT:(i + 1) * BT], n.ps[j][:, :], ACT.Copy).then_inc(A("rounded"), 1)


def all_pool(e, A, G, n, parts):
    for i in range(BLOCKS):
        for j in range(CJ):
            e.wait_ge(*A.at("rounded", 0, i * CJ + j))
            at = slice(i * BT, (i + 1) * BT)
            e.tensor_tensor(parts[1][:, j, at], n.hT[:, j, at], parts[0][:, j, at], ALU.subtract).then_inc(G("rest"), 1)



def load_all(nc, c):
    with ExitStack() as ctx:
        sb, ps, sem = tensors(nc, ctx, "ld")
        loaded, made = sem("loaded"), sem("made")
        block = ctx.enter_context(nc.Block())

        @block.sync
        def _(e):
            e.dma_start(c.X[:, :, :], c.d["x"]).then_inc(loaded, 16)
            e.dma_start(c.vecs[:, :], c.d["vecs"]).then_inc(loaded, 16)
            e.dma_start(c.rows[:, :], c.d["rows"]).then_inc(loaded, 16)
            e.dma_start(c.consts[:, :], c.d["ident"]).then_inc(loaded, 16)
            e.dma_start(c.small[:, :], c.d["small"]).then_inc(loaded, 16)
            e.wait_ge(loaded, 80)

        @block.vector
        def _(e):
            e.memset(c.eps[:, 0:1], LN_EPS).then_inc(made, 1)
            e.memset(c.eps[:, 1:2], RMS_EPS).then_inc(made, 1)
            e.memset(c.eps[:, 3:4], F32_EPS).then_inc(made, 1)
            e.memset(c.eps[:, 2:3], float(np.log(1e-5))).then_inc(made, 1)
            e.memset(c.ones[:, :], 1.0).then_inc(made, 1)
            e.wait_ge(loaded, 80)
            e.tensor_copy(c.identb[:, :], c.ident[:, :]).then_inc(made, 1)
            e.tensor_copy(c.identh[:, :], c.ident[:, :]).then_inc(made, 1)



def l0_queries(nc, c):
    with ExitStack() as ctx:
        sb, ps, sem = tensors(nc, ctx, "q0")
        wq = sb("wq", [P, CJ, C])
        wk = sb("wk", [P, CJ, C])
        fused = sb("fused", [P, CJ, C])
        side = sb("side", [P, 8])
        n = Norm(sb, ps)
        out_ps = [ps(f"out_ps{o}") for o in range(CJ)]
        fuse_ps = [ps(f"fuse_ps{j}") for j in range(CJ)]
        side_ps = ps("side_ps")
        qc_ps = ps("qc_ps")
        loaded, fused_ready, fuse_done, side_made = sem("loaded"), sem("fused"), sem("fuse_done"), sem("side_made")
        V = Steps(sem("vector"), LN_V + ["qc"])
        A = Steps(sem("scalar"), LN_A + [("qk", CJ)])
        T_ = Steps(sem("tensor"), LN_T + [("qk", CJ), "qc"])
        block = ctx.enter_context(nc.Block())
        bq, bk = c.vec["bq"], c.vec["bk"]

        @block.sync
        def _(e):
            e.dma_start(wq[:, :, :], c.d["l0_wq"]).then_inc(loaded, 16)
            e.dma_start(wk[:, :, :], c.d["l0_wk"]).then_inc(loaded, 16)

        @block.tensor
        def _(e):
            T_.start(e)
            e.wait_ge(loaded, 32)
            for j in range(CJ):
                for o in range(CJ):
                    m = e.matmul(fuse_ps[j][:, 0:C], wq[:, o, j * P:(j + 1) * P], wk[:, o, :],
                                 start=(o == 0), stop=(o == CJ - 1))
                m.then_inc(fuse_done, 1)
            for j in range(CJ):
                for w, b, at in ((wk, bq, 0), (wq, bk, 2)):
                    for o in range(CJ):
                        e.matmul(side_ps[:, at + j:at + j + 1], w[:, o, j * P:(j + 1) * P], b[:, o:o + 1],
                                 start=(o == 0), stop=(o == CJ - 1))
            for o in range(CJ):
                m = e.matmul(side_ps[0:1, 4:5], bq[:, o:o + 1], bk[:, o:o + 1], start=(o == 0), stop=(o == CJ - 1))
            m.then_inc(fuse_done, 1)
            with e.Fori(0, BLOCKS) as i:
                ln_tensor(e, V, T_, n, i, c, lambda: e.wait_ge(*A.at("features", i - 1)))
                e.wait_ge(*A.at("features", i))
                e.wait_ge(fused_ready, CJ)
                e.wait_ge(side_made, 2)
                for o in range(CJ):
                    e.wait_ge(*A.at("qk", i - 1, o))
                    for j in range(CJ):
                        m = e.matmul(out_ps[o][:, :], fused[:, j, o * P:(o + 1) * P], n.hT[:, j, :],
                                     start=(j == 0), stop=(j == CJ - 1))
                    m.then_inc(T_("qk"), 1)
                e.wait_ge(*V.at("qc", i - 1))
                for k in range(KT_):
                    for j in range(CJ):
                        e.matmul(qc_ps[:, k:k + 1], n.hT[:, j, k * P:(k + 1) * P], side[:, 2 + j:3 + j],
                                 start=(j == 0), stop=False)
                    m = e.matmul(qc_ps[:, k:k + 1], c.ones[0:1, 0:P], side[0:1, 4:5], start=False, stop=True)
                m.then_inc(T_("qc"), 1)

        @block.vector
        def _(e):
            V.start(e)
            e.wait_ge(fuse_done, 3)
            for j in range(CJ):
                e.tensor_copy(fused[:, j, :], fuse_ps[j][:, 0:C]).then_inc(fused_ready, 1)
            with e.Fori(0, BLOCKS) as i:
                ln_vector(e, V, A, n, c.X, i, lambda: e.wait_ge(*T_.at("turned", i - 1)))
                e.wait_ge(*T_.at("qc", i))
                e.tensor_copy(c.qc[:, bass.ds(i * KT_, KT_)], qc_ps[:, 0:KT_]).then_inc(V("qc"), 1)

        @block.scalar
        def _(e):
            A.start(e)
            e.wait_ge(fuse_done, 3)
            e.activation(side[:, 0:4], side_ps[:, 0:4], ACT.Copy).then_inc(side_made, 1)
            e.activation(side[0:1, 4:5], side_ps[0:1, 4:5], ACT.Copy).then_inc(side_made, 1)
            e.wait_ge(side_made, 2)
            with e.Fori(0, BLOCKS) as i:
                ln_scalar_std(e, V, A, n, i, c)
                ln_scalar_features(e, T_, A, n, i, lambda: e.wait_ge(*T_.at("qc", i - 1)))
                for o in range(CJ):
                    e.wait_ge(*T_.at("qk", i, o))
                    e.activation(c.qkT[:, o, bass.ds(i * BT, BT)], out_ps[o][:, :], ACT.Identity,
                                 bias=side[:, o:o + 1]).then_inc(A("qk"), 1)


def l0_attention(nc, c):
    with ExitStack() as ctx:
        sb, ps, sem = tensors(nc, ctx, "a0")
        wv = sb("wv", [P, CJ, C])
        mask_i = sb("mask_i", [P, M], I32)
        keep = sb("keep", [P, M])
        fill = sb("fill", [P, M])
        last_n = sb("last_n", [BPT, TILES, C])
        last_t = sb("last_t", [P, CJ, B])
        ctx_t = [sb(f"ctx_t{u}", [P, BPT, CJ, 2 * P]) for u in range(2)]
        ctx_n = [sb(f"ctx_n{u}", [P, BPT, 2, C]) for u in range(2)]
        qk = [sb(f"qk{u}", [P, CJ, P]) for u in range(2)]
        s = [sb(f"s{u}", [P, M]) for u in range(2)]
        p = [sb(f"p{u}", [P, M]) for u in range(2)]
        tiny = [sb(f"tiny{u}", [P, 16]) for u in range(2)]
        pt = [sb(f"pt{u}", [P, 2 * P]) for u in range(2)]
        pl = [sb(f"pl{u}", [BPT, P]) for u in range(2)]
        o = [sb(f"o{u}", [P, C]) for u in range(2)]
        ot = [sb(f"ot{u}", [P, CJ, P]) for u in range(2)]
        sq = sb("sq", [P, C])
        rounded = sb("rounded", [P, BPT * 2, C])
        qs = [sb(f"qs{u}", [P, 8]) for u in range(2)]
        ss = [sb(f"ss{u}", [P, 8]) for u in range(2)]
        root = [sb(f"root{u}", [P, 8]) for u in range(2)]
        s_ps = [ps(f"s_ps{u}") for u in range(2)]
        o_ps = [ps(f"o_ps{u}") for u in range(2)]
        pt_ps, ot_ps, y_ps = ps("pt_ps"), ps("ot_ps"), ps("y_ps")
        w_loaded, made, seen = sem("w_loaded"), sem("made"), sem("seen")
        t_loaded = [sem(f"t_loaded{u}") for u in range(2)]
        n_loaded = [sem(f"n_loaded{u}") for u in range(2)]
        def step(name, n=1):
            return Steps(sem(name), [("done", n)], 2)

        chain = Steps(sem("chain"), ["scored", "last", "last_s", "masked", "minus"], 2)
        weights = Steps(sem("weights"), ["last_p", "inverse"], 2)
        absmax, outs, whole, added = step("absmax"), step("outs"), step("whole"), step("added")
        scale = Steps(sem("scale"), ["keep_max", "keep_ss", "guard", "flip", "scale"], 2)
        exp, squares, kept, ot_kept = step("exp"), step("squares", 2 * BPT), step("kept", 2), step("ot_kept")
        root_s = Steps(sem("root"), ["log", "root"], 2)
        scores, turned, summed, ot_turned, projected = (step(k) for k in ("scores", "turned", "summed", "ot_turned", "projected"))
        qk_made, roundings = step("qk_made"), step("roundings", 2 * BPT)
        block = ctx.enter_context(nc.Block())

        def over_tiles(e, turns):
            turns(0, 0, 1)
            with e.Fori(0, TILES // 2 - 1) as h:
                turns(h * 2 + 1, 1, h + 1)
                turns(h * 2 + 2, 0, h + 2)
            turns(TILES - 1, 1, TILES // 2)

        def first(t):
            return isinstance(t, int) and t == 0

        def last(t):
            return isinstance(t, int) and t == TILES - 1

        @block.sync
        def _(e):
            e.dma_start(wv[:, :, :], c.d["l0_wv"]).then_inc(w_loaded, 16)
            for b in range(BPT):
                e.dma_start(mask_i[b * T:(b + 1) * T, :], c.d["mask"]).then_inc(w_loaded, 16)
            e.dma_start(last_n[:, :, :], c.d["ctx_last_n"]).then_inc(w_loaded, 16)
            e.dma_start(last_t[:, :, :], c.d["ctx_last_t"]).then_inc(w_loaded, 16)
            with e.Fori(0, TILES // 2) as h:
                for u in range(2):
                    t = h * 2 + u
                    e.wait_ge(*scores.at("done", t - 2))
                    e.dma_start(ctx_t[u][:, :, :, :], c.d["ctx_t"][t]).then_inc(t_loaded[u], 16)
                    e.wait_ge(*summed.at("done", t - 2))
                    e.wait_ge(*squares.at("done", t - 2))
                    e.wait_ge(*absmax.at("done", t - 2))
                    e.wait_ge(*roundings.at("done", t - 2))
                    e.dma_start(ctx_n[u][:, :, :, :], c.d["ctx_n"][t]).then_inc(n_loaded[u], 16)

        @block.gpsimd
        def _(e):
            def take_qk(t, u):
                e.wait_ge(*scores.at("done", t - 2))
                e.tensor_copy(qk[u][:, :, :], c.qkT[:, :, bass.ds(t * P, P)]).then_inc(qk_made("done"), 1)

            def turns(t, u, n):
                if not last(t):
                    take_qk(t + 1, 1 - u)
                e.wait_ge(*scale.at("scale", t))
                e.wait_ge(*whole.at("done", t - 1))
                e.sem_inc(seen, 1)
                for r in range(2 * BPT):
                    e.tensor_scalar(rounded[:, r, :], ctx_n[u][:, r // 2, r % 2, :], qs[u][:, r:r + 1], ROUND,
                                    ALU.mult, ALU.add).then_inc(roundings("done"), 1)

            for each in (qk_made, roundings):
                each.start(e)
            take_qk(0, 0)
            over_tiles(e, turns)

        @block.tensor
        def _(e):
            def score(t, u, n):
                e.wait_ge(*qk_made.at("done", t))
                e.wait_ge(*chain.at("last", t - 2))
                e.wait_ge(t_loaded[u], n * 16)
                for j in range(CJ):
                    for b in range(BPT):
                        e.matmul(s_ps[u][b * T:(b + 1) * T, 0:2 * P], qk[u][:, j, b * T:(b + 1) * T],
                                 ctx_t[u][:, b, j, :], start=(j == 0), stop=(j == CJ - 1))
                for j in range(CJ):
                    m = e.matmul(s_ps[u][:, 2 * P:2 * P + BPT], qk[u][:, j, :],
                                 last_t[:, j, bass.ds(t * BPT, BPT)], start=(j == 0), stop=(j == CJ - 1))
                m.then_inc(scores("done"), 1)

            def turn(t, u):
                e.wait_ge(*exp.at("done", t))
                e.wait_ge(*weights.at("last_p", t))
                e.wait_ge(*kept.at("done", t - 1))
                for m in range(2):
                    e.transpose(pt_ps[:, m * P:(m + 1) * P], p[u][:, m * P:(m + 1) * P], c.ident[:, :])
                e.transpose(pt_ps[0:BPT, 2 * P:3 * P], tiny[u][:, 8:8 + BPT], c.ident[:, :]).then_inc(turned("done"), 1)

            def weigh(t, u, n):
                e.wait_ge(*kept.at("done", t))
                e.wait_ge(n_loaded[u], n * 16)
                e.wait_ge(*outs.at("done", t - 2))
                e.matmul(o_ps[u][:, 0:C], pl[u][:, :], last_n[:, t, :], start=True, stop=False,
                         skip_group_check=True)
                for k in range(2):
                    for b in range(BPT):
                        m = e.matmul(o_ps[u][b * T:(b + 1) * T, 0:C], pt[u][:, k * P + b * T:k * P + (b + 1) * T],
                                     ctx_n[u][:, b, k, :], start=False, stop=(k == 1), skip_group_check=True)
                m.then_inc(summed("done"), 1)

            def turn_out(t, u):
                e.wait_ge(*outs.at("done", t))
                e.wait_ge(*ot_kept.at("done", t - 1))
                for j in range(CJ):
                    m = e.transpose(ot_ps[:, j * P:(j + 1) * P], o[u][:, j * P:(j + 1) * P], c.ident[:, :])
                m.then_inc(ot_turned("done"), 1)

            def project(t, u):
                e.wait_ge(*ot_kept.at("done", t))
                e.wait_ge(*added.at("done", t - 1))
                for j in range(CJ):
                    e.matmul(y_ps[:, 0:C], ot[u][:, j, :], wv[:, j, :], start=(j == 0), stop=False)
                e.matmul(y_ps[:, 0:C], c.ones[0:1, 0:P], c.row["bv"][0:1, :], start=False,
                         stop=True).then_inc(projected("done"), 1)

            def turns(t, u, n):
                turn(t, u)
                if not last(t):
                    score(t + 1, 1 - u, n + u)
                if not first(t):
                    turn_out(t - 1, 1 - u)
                weigh(t, u, n)
                if not first(t):
                    project(t - 1, 1 - u)

            for each in (scores, turned, summed, ot_turned, projected):
                each.start(e)
            e.wait_ge(w_loaded, 16 * 7)
            score(0, 0, 1)
            over_tiles(e, turns)
            turn_out(TILES - 1, 1)
            project(TILES - 1, 1)

        @block.vector
        def _(e):
            def largest(t, u, n):
                e.wait_ge(n_loaded[u], n * 16)
                e.wait_ge(*roundings.at("done", t - 2))
                e.tensor_reduce(qs[u][:, :], ctx_n[u][:, :, :, :].rearrange("p b k c -> p (b k) c"), AX.X, ALU.max,
                                apply_absolute_value=True).then_inc(absmax("done"), 1)

            def mask(t, u):
                x, sc = tiny[u], s_ps[u]
                e.wait_ge(*scores.at("done", t))
                e.wait_ge(*exp.at("done", t - 2))
                e.scalar_tensor_tensor(s[u][:, 0:2 * P], sc[:, 0:2 * P], c.qc[:, bass.ds(t, 1)], keep[:, 0:2 * P],
                                       ALU.add, ALU.mult).then_inc(chain("scored"), 1)
                e.tensor_tensor_reduce(x[:, 0:4], sc[:, 2 * P:2 * P + BPT], c.own[:, :], 1.0, 0.0, ALU.mult,
                                       ALU.add, x[:, 4:5]).then_inc(chain("last"), 1)
                e.wait_ge(*chain.at("last", t))
                e.scalar_tensor_tensor(s[u][:, 2 * P:M], x[:, 4:5], c.qc[:, bass.ds(t, 1)], keep[:, 2 * P:M],
                                       ALU.add, ALU.mult).then_inc(chain("last_s"), 1)
                e.wait_ge(*chain.at("last_s", t))
                e.tensor_tensor(s[u][:, :], s[u][:, :], fill[:, :], ALU.add).then_inc(chain("masked"), 1)
                e.wait_ge(*chain.at("masked", t))
                e.tensor_reduce(x[:, 5:6], s[u][:, :], AX.X, ALU.max, negate=True).then_inc(chain("minus"), 1)

            def weight(t, u):
                x = tiny[u]
                e.wait_ge(*exp.at("done", t))
                e.wait_ge(*turned.at("done", t - 2))
                e.tensor_scalar(x[:, 8:12], c.own[:, :], p[u][:, 2 * P:M], None, ALU.mult).then_inc(weights("last_p"), 1)
                e.reciprocal(x[:, 7:8], x[:, 6:7]).then_inc(weights("inverse"), 1)

            def rescale(t, u):
                e.wait_ge(*absmax.at("done", t))
                e.tensor_copy(c.c_max[:, bass.ds(t * 2 * BPT, 2 * BPT)], qs[u][:, :]).then_inc(scale("keep_max"), 1)
                e.wait_ge(*root_s.at("root", t))
                e.tensor_copy(c.c_ss[:, bass.ds(t * 2 * BPT, 2 * BPT)], ss[u][:, :]).then_inc(scale("keep_ss"), 1)
                e.wait_ge(*scale.at("keep_ss", t))
                e.tensor_tensor(qs[u][:, :], qs[u][:, :], root[u][:, :], ALU.max).then_inc(scale("guard"), 1)
                e.wait_ge(*scale.at("guard", t))
                e.reciprocal(qs[u][:, :], qs[u][:, :]).then_inc(scale("flip"), 1)
                e.wait_ge(*scale.at("flip", t))
                e.tensor_scalar(qs[u][:, :], qs[u][:, :], 127.0, None, ALU.mult).then_inc(scale("scale"), 1)

            def divide(t, u):
                e.wait_ge(*weights.at("inverse", t))
                e.wait_ge(*summed.at("done", t))
                e.wait_ge(*ot_turned.at("done", t - 2))
                e.tensor_scalar(o[u][:, :], o_ps[u][:, 0:C], tiny[u][:, 7:8], None, ALU.mult).then_inc(outs("done"), 1)

            def keep_rounded(t):
                e.wait_ge(*roundings.at("done", t))
                e.tensor_scalar(c.cq[:, bass.ds(t * 2 * BPT, 2 * BPT), :], rounded[:, :, :], ROUND, None,
                                ALU.subtract).then_inc(whole("done"), 1)

            def add(t):
                e.wait_ge(*projected.at("done", t))
                e.tensor_tensor(c.X[:, t, :], c.X[:, t, :], y_ps[:, 0:C], ALU.add).then_inc(added("done"), 1)

            def turns(t, u, n):
                if not last(t):
                    largest(t + 1, 1 - u, n + u)
                    mask(t + 1, 1 - u)
                divide(t, u)
                if not last(t):
                    weight(t + 1, 1 - u)
                keep_rounded(t)
                if not first(t):
                    add(t - 1)
                if not last(t):
                    rescale(t + 1, 1 - u)

            for each in (chain, weights, absmax, outs, whole, added, scale):
                each.start(e)
            e.wait_ge(w_loaded, 16 * 7)
            e.tensor_scalar(keep[:, :], mask_i[:, :], 0.0, None, ALU.not_equal).then_inc(made, 1)
            e.wait_ge(made, 1)
            e.tensor_scalar(fill[:, :], keep[:, :], 1.0, -NEG, ALU.subtract, ALU.mult).then_inc(made, 1)
            e.wait_ge(made, 2)
            mask(0, 0)
            weight(0, 0)
            largest(0, 0, 1)
            rescale(0, 0)
            over_tiles(e, turns)
            add(TILES - 1)

        @block.scalar
        def _(e):
            def exponentials(t, u):
                x = tiny[u]
                e.wait_ge(*chain.at("minus", t))
                e.wait_ge(*turned.at("done", t - 2))
                e.wait_ge(*weights.at("inverse", t - 2))
                e.activation(p[u][:, :], s[u][:, :], ACT.Exp, bias=x[:, 5:6],
                             accum_out=x[:, 6:7]).then_inc(exp("done"), 1)

            def square(t, u, n):
                e.wait_ge(n_loaded[u], n * 16)
                e.wait_ge(*scale.at("keep_ss", t - 2))
                for r in range(2 * BPT):
                    e.wait_ge(*(squares.at("done", t, r - 1) if r else squares.at("done", t - 1)))
                    e.activation(sq[:, :], ctx_n[u][:, r // 2, r % 2, :], ACT.Square,
                                 accum_out=ss[u][:, r:r + 1]).then_inc(squares("done"), 1)

            def roots(t, u):
                e.wait_ge(*squares.at("done", t))
                e.wait_ge(*scale.at("guard", t - 2))
                e.activation(root[u][:, :], ss[u][:, :], ACT.Ln, scale=1.0 / C,
                             bias=c.eps[:, 1:2]).then_inc(root_s("log"), 1)
                e.wait_ge(*root_s.at("log", t))
                e.activation(root[u][:, :], root[u][:, :], ACT.Exp, scale=0.5,
                             bias=c.eps[:, 2:3]).then_inc(root_s("root"), 1)

            def keep_turned(t, u):
                e.wait_ge(*turned.at("done", t))
                e.wait_ge(*summed.at("done", t - 2))
                e.activation(pt[u][:, :], pt_ps[:, 0:2 * P], ACT.Copy).then_inc(kept("done"), 1)
                e.activation(pl[u][:, :], pt_ps[0:BPT, 2 * P:3 * P], ACT.Copy).then_inc(kept("done"), 1)

            def keep_out(t, u):
                e.wait_ge(*ot_turned.at("done", t))
                e.wait_ge(*projected.at("done", t - 2))
                e.activation(ot[u][:, :, :].rearrange("p j t -> p (j t)"), ot_ps[:, 0:C], ACT.Copy).then_inc(ot_kept("done"), 1)

            def turns(t, u, n):
                keep_turned(t, u)
                if not last(t):
                    square(t + 1, 1 - u, n + u)
                if not first(t):
                    keep_out(t - 1, 1 - u)
                if not last(t):
                    exponentials(t + 1, 1 - u)
                    roots(t + 1, 1 - u)

            for each in (exp, squares, kept, ot_kept, root_s):
                each.start(e)
            exponentials(0, 0)
            square(0, 0, 1)
            roots(0, 0)
            over_tiles(e, turns)
            keep_out(TILES - 1, 1)



def by_batch(ap):
    return ap.rearrange("p (g t) -> p g t", t=T)


def l0_time_mix(nc, c):
    with ExitStack() as ctx:
        sb, ps, sem = tensors(nc, ctx, "tm")
        w = {k: sb(f"w{k}", [P, CJ, C]) for k in "kvro"}
        n = Norm(sb, ps)
        xn0 = sb("xn0", [P, KT_, C])
        var2, std2, rstd2 = sb("var2", [P, KT_]), sb("std2", [P, KT_]), sb("rstd2", [P, KT_])
        tm = {k: sb(f"tm_{k}", [P, CJ]) for k in "kvr"}
        decay = sb("decay_row", [P, CJ * BT])
        wcol = sb("wcol", [P, CJ])
        dh = sb("dh", [P, CJ * BT])
        mix = {k: sb(f"mix_{k}", [P, CJ, BT]) for k in "kvr"}
        k_, v_, sr = sb("k", [P, CJ * BT]), sb("v", [P, CJ * BT]), sb("er", [P, CJ * BT])
        pp = sb("pp", [P, 1 + CJ * BT])
        aa = sb("aa", [P, 1 + CJ * BT])
        bb = sb("bb", [P, 1 + CJ * BT])
        z1, z2, z3, z4 = (sb(f"z{q}", [P, CJ * BT]) for q in range(1, 5))
        num, den = sb("num", [P, CJ * BT]), sb("den", [P, CJ * BT])
        gated = sb("gated", [P, CJ, BT])
        lin_ps = {k: [ps(f"{k}_ps{o}") for o in range(CJ)] for k in "kvr"}
        loaded, made = sem("loaded"), sem("made")
        V = Steps(sem("vector"), LN_V[:-1] + ["var2", "eps2", "both", ("norm", KT_), ("plain", KT_), "shift", "first",
                                              ("mix", 3 * CJ), "pp", "z2", ("z1", CJ), "cut_z1", "cut_pp",
                                              ("z4", CJ), ("z3", CJ), "e2", "z3b", "kv", "aa", "bb", "num", "den",
                                              "last_num", "last_num2", "den2", "inv", "gated", ("added", CJ)])
        A = Steps(sem("scalar"), LN_A[:1] + ["std2"] + LN_A[1:] + [("k", CJ), ("v", CJ), ("r", CJ), "e2b", "e1b", "e1", "e2"])
        T_ = Steps(sem("tensor"), LN_T + [("k", CJ), ("v", CJ), ("r", CJ), ("y", CJ)])
        block = ctx.enter_context(nc.Block())

        @block.sync
        def _(e):
            for k in "kvro":
                e.dma_start(w[k][:, :, :], c.d[f"l0_w{k}m"]).then_inc(loaded, 16)

        @block.tensor
        def _(e):
            T_.start(e)
            e.wait_ge(loaded, 64)
            with e.Fori(0, BLOCKS) as i:
                ln_tensor(e, V, T_, n, i, c, lambda: e.wait_ge(*V.at("added", i - 1)))
                for q, k in enumerate("kvr"):
                    e.wait_ge(*V.at("mix", i, 2 * q + 1))
                    for o in range(CJ):
                        e.wait_ge(*A.at(k, i - 1, o))
                        for j in range(CJ):
                            m = e.matmul(lin_ps[k][o][:, :], w[k][:, j, o * P:(o + 1) * P], mix[k][:, j, :],
                                         start=(j == 0), stop=(j == CJ - 1))
                        m.then_inc(T_(k), 1)
                e.wait_ge(*V.at("gated", i))
                e.wait_ge(*A.at("features", i))
                for b in range(CJ):
                    for k in (2 * b, 2 * b + 1):
                        for j in range(CJ):
                            m = e.matmul(n.ps[b][:, (k % 2) * C:(k % 2 + 1) * C], gated[:, j, k * P:(k + 1) * P],
                                         w["o"][:, j, :], start=(j == 0), stop=(j == CJ - 1))
                    m.then_inc(T_("y"), 1)

        @block.vector
        def _(e):
            V.start(e)
            for k in "kvr":
                e.tensor_scalar(tm[k][:, :], c.vec[f"tm_{k}"], 1.0, None, ALU.subtract).then_inc(made, 1)
            e.wait_ge(made, 4)
            e.tensor_scalar(wcol[:, :], wcol[:, :], -1.0, None, ALU.mult).then_inc(made, 1)
            e.memset(decay[:, :], 0.0).then_inc(made, 1)
            e.memset(pp[:, 0:1], FAR).then_inc(made, 1)
            e.memset(aa[:, 0:1], 0.0).then_inc(made, 1)
            e.memset(bb[:, 0:1], 0.0).then_inc(made, 1)
            e.wait_ge(made, 9)
            for j in range(CJ):
                e.tensor_scalar(decay[:, j * BT:(j + 1) * BT], decay[:, j * BT:(j + 1) * BT], wcol[:, j:j + 1], None,
                                ALU.add).then_inc(made, 1)
            e.wait_ge(made, 11)
            e.memset(by_batch(decay[:, :])[:, :, 0:1], FAR).then_inc(made, 1)
            e.wait_ge(made, 12)
            N = CJ * BT
            pp_now, pp_was, aa_was, bb_was = pp[:, 1:1 + N], pp[:, 0:N], aa[:, 0:N], bb[:, 0:N]
            first = c.vec["first"]

            def half(ap, j):
                return ap[:, j * BT:(j + 1) * BT]

            with e.Fori(0, BLOCKS) as i:
                def second():
                    e.wait_ge(*V.at("rstd", i))
                    e.tensor_tensor(var2[:, :], n.var[:, :], n.rstd[:, :], ALU.mult).then_inc(V("var2"), 1)
                    e.wait_ge(*V.at("var2", i))
                    e.tensor_tensor(var2[:, :], var2[:, :], n.rstd[:, :], ALU.mult).then_inc(V("eps2"), 1)
                    e.wait_ge(*A.at("std2", i))
                    e.reciprocal(rstd2[:, :], std2[:, :]).then_inc(V("both"), 1)
                    e.wait_ge(*V.at("both", i))
                    e.wait_ge(*T_.at("turned", i - 1))

                ln_vector(e, V, A, n, c.X, i, second)
                e.wait_ge(*V.at("norm", i))
                for k in range(KT_):
                    e.tensor_copy(xn0[:, k, :], n.xn[:, k, :]).then_inc(V("plain"), 1)
                e.wait_ge(*V.at("plain", i))
                h = n.hT[:, :, :].rearrange("p j t -> p (j t)")
                e.wait_ge(*A.at("features", i))
                e.tensor_tensor(by_batch(dh[:, :])[:, :, 1:T], by_batch(h)[:, :, 1:T], by_batch(h)[:, :, 0:T - 1],
                                ALU.subtract).then_inc(V("shift"), 1)
                e.tensor_copy(by_batch(dh[:, :])[:, :, 0:1], by_batch(h)[:, :, 0:1]).then_inc(V("first"), 1)
                e.wait_ge(*V.at("first", i))
                for k in "kvr":
                    e.wait_ge(*T_.at(k, i - 1))
                    for j in range(CJ):
                        e.scalar_tensor_tensor(mix[k][:, j, :], half(dh, j), tm[k][:, j:j + 1], n.hT[:, j, :],
                                               ALU.mult, ALU.add).then_inc(V("mix"), 1)
                e.wait_ge(*A.at("k", i))
                e.tensor_tensor_scan(pp_now, decay[:, :], k_[:, :], 0.0, ALU.add, ALU.max).then_inc(V("pp"), 1)
                e.wait_ge(*V.at("pp", i))
                e.tensor_tensor(z2[:, :], k_[:, :], pp_now, ALU.subtract).then_inc(V("z2"), 1)
                for j in range(CJ):
                    e.scalar_tensor_tensor(half(z1, j), half(pp_was, j), wcol[:, j:j + 1], half(pp_now, j), ALU.add,
                                           ALU.subtract).then_inc(V("z1"), 1)
                e.wait_ge(*V.at("z1", i))
                e.memset(by_batch(z1[:, :])[:, :, 0:1], FAR).then_inc(V("cut_z1"), 1)
                e.memset(by_batch(pp_was)[:, :, 0:1], FAR).then_inc(V("cut_pp"), 1)
                e.wait_ge(*V.at("cut_pp", i))
                for j in range(CJ):
                    e.scalar_tensor_tensor(half(z4, j), half(k_, j), first[:, j:j + 1], half(pp_was, j), ALU.add,
                                           ALU.max).then_inc(V("z4"), 1)
                e.wait_ge(*V.at("z4", i))
                for j in range(CJ):
                    e.scalar_tensor_tensor(half(z3, j), half(k_, j), first[:, j:j + 1], half(z4, j), ALU.add,
                                           ALU.subtract).then_inc(V("z3"), 1)
                e.wait_ge(*V.at("z3", i))
                e.tensor_tensor(z4[:, :], pp_was, z4[:, :], ALU.subtract).then_inc(V("e2"), 1)
                e.wait_ge(*A.at("v", i))
                e.wait_ge(*A.at("e2b", i))
                e.tensor_tensor(num[:, :], z2[:, :], v_[:, :], ALU.mult).then_inc(V("z3b"), 1)
                e.wait_ge(*V.at("z3b", i))
                e.wait_ge(*A.at("e1b", i))
                e.tensor_tensor_scan(aa[:, 1:1 + N], z1[:, :], num[:, :], 0.0, ALU.mult, ALU.add).then_inc(V("kv"), 1)
                e.tensor_tensor_scan(bb[:, 1:1 + N], z1[:, :], z2[:, :], 0.0, ALU.mult, ALU.add).then_inc(V("aa"), 1)
                e.wait_ge(*V.at("aa", i))
                e.wait_ge(*A.at("e2", i))
                e.tensor_tensor(num[:, :], z4[:, :], aa_was, ALU.mult).then_inc(V("bb"), 1)
                e.tensor_tensor(den[:, :], z4[:, :], bb_was, ALU.mult).then_inc(V("num"), 1)
                e.tensor_tensor(z2[:, :], z3[:, :], v_[:, :], ALU.mult).then_inc(V("den"), 1)
                e.wait_ge(*V.at("den", i))
                e.tensor_tensor(num[:, :], num[:, :], z2[:, :], ALU.add).then_inc(V("last_num"), 1)
                e.tensor_tensor(den[:, :], den[:, :], z3[:, :], ALU.add).then_inc(V("last_num2"), 1)
                e.wait_ge(*V.at("last_num2", i))
                e.wait_ge(*A.at("r", i))
                e.tensor_tensor(num[:, :], sr[:, :], num[:, :], ALU.mult).then_inc(V("den2"), 1)
                e.reciprocal(den[:, :], den[:, :]).then_inc(V("inv"), 1)
                e.wait_ge(*V.at("inv", i))
                e.wait_ge(*T_.at("y", i - 1))
                e.tensor_tensor(gated[:, :, :].rearrange("p j t -> p (j t)"), num[:, :], den[:, :],
                                ALU.mult).then_inc(V("gated"), 1)
                for b in range(CJ):
                    e.wait_ge(*T_.at("y", i, b))
                    e.tensor_tensor(c.XI[:, bass.ds(i * KT_ + 2 * b, 2), :], xn0[:, 2 * b:2 * b + 2, :],
                                    n.ps[b][:, :].rearrange("p (k f) -> p k f", k=2), ALU.add).then_inc(V("added"), 1)

        @block.scalar
        def _(e):
            A.start(e)
            e.activation(wcol[:, :], c.vec["decay"], ACT.Exp).then_inc(made, 1)
            with e.Fori(0, BLOCKS) as i:
                ln_scalar_std(e, V, A, n, i, c)
                e.wait_ge(*V.at("eps2", i))
                e.activation(std2[:, :], var2[:, :], ACT.Sqrt, bias=c.eps[:, 0:1]).then_inc(A("std2"), 1)
                ln_scalar_features(e, T_, A, n, i, lambda: e.wait_ge(*V.at("mix", i - 1)), c.vec["ln1_g"],
                                   c.vec["ln1_b"])
                for k, dst in (("k", k_), ("v", v_), ("r", sr)):
                    e.wait_ge(*V.at("den2", i - 1))
                    for o in range(CJ):
                        e.wait_ge(*T_.at(k, i, o))
                        e.activation(dst[:, o * BT:(o + 1) * BT], lin_ps[k][o][:, :],
                                     ACT.Sigmoid if k == "r" else ACT.Copy).then_inc(A(k), 1)
                e.wait_ge(*V.at("z2", i))
                e.activation(z2[:, :], z2[:, :], ACT.Exp).then_inc(A("e2b"), 1)
                e.wait_ge(*V.at("cut_z1", i))
                e.activation(z1[:, :], z1[:, :], ACT.Exp).then_inc(A("e1b"), 1)
                e.wait_ge(*V.at("z3", i))
                e.activation(z3[:, :], z3[:, :], ACT.Exp).then_inc(A("e1"), 1)
                e.wait_ge(*V.at("e2", i))
                e.activation(z4[:, :], z4[:, :], ACT.Exp).then_inc(A("e2"), 1)


def l0_channel_mix(nc, c):
    with ExitStack() as ctx:
        sb, ps, sem = tensors(nc, ctx, "cm")
        HC = HID // P
        wk, wv, wr = sb("wk", [P, CJ, HID]), sb("wv", [P, HC, C]), sb("wr", [P, CJ, C])
        n = Norm(sb, ps)
        tm = {k: sb(f"tm_{k}", [P, CJ]) for k in "kr"}
        dh = sb("dh", [P, CJ * BT])
        mix = {k: sb(f"mix_{k}", [P, CJ, BT]) for k in "kr"}
        relu = [sb(f"relu{u}", [P, BT]) for u in range(2)]
        kk = sb("kk", [P, HC, BT])
        gate = sb("gate", [P, KT_, C])
        k_ps = [ps(f"k_ps{u}") for u in range(2)]
        r_ps = [ps(f"r_ps{u}") for u in range(2)]
        v_ps = [ps(f"v_ps{u}") for u in range(2)]
        loaded, made = sem("loaded"), sem("made")
        V = Steps(sem("vector"), LN_V + ["shift", "first", ("mix", 2 * CJ), ("square", HC), ("rkv", 2), ("plus", 2), ("added", 2)])
        A = Steps(sem("scalar"), LN_A + [("relu", HC), ("gate", 2)])
        T_ = Steps(sem("tensor"), LN_T + [("k", HC), ("r", 2), ("v", 2)])
        block = ctx.enter_context(nc.Block())

        @block.sync
        def _(e):
            e.dma_start(wk[:, :, :], c.d["l0_wck"]).then_inc(loaded, 16)
            e.dma_start(wr[:, :, :], c.d["l0_wcr"]).then_inc(loaded, 16)
            e.dma_start(wv[:, :, :], c.d["l0_wcv"]).then_inc(loaded, 16)

        @block.tensor
        def _(e):
            T_.start(e)
            e.wait_ge(loaded, 48)
            with e.Fori(0, BLOCKS) as i:
                ln_tensor(e, V, T_, n, i, c, lambda: e.wait_ge(*A.at("features", i - 1)))
                e.wait_ge(*V.at("mix", i))
                for h in range(HC):
                    e.wait_ge(*(A.at("relu", i, h - 2) if h >= 2 else A.at("relu", i - 1)))
                    for j in range(CJ):
                        m = e.matmul(k_ps[h % 2][:, :], wk[:, j, h * P:(h + 1) * P], mix["k"][:, j, :],
                                     start=(j == 0), stop=(j == CJ - 1))
                    m.then_inc(T_("k"), 1)
                for b in range(2):
                    e.wait_ge(*A.at("gate", i - 1, b))
                    for k in (2 * b, 2 * b + 1):
                        for j in range(CJ):
                            m = e.matmul(r_ps[b][:, (k % 2) * C:(k % 2 + 1) * C], mix["r"][:, j, k * P:(k + 1) * P],
                                         wr[:, j, :], start=(j == 0), stop=(j == CJ - 1))
                    m.then_inc(T_("r"), 1)
                e.wait_ge(*V.at("square", i))
                for b in range(2):
                    e.wait_ge(*V.at("rkv", i - 1, b))
                    for k in (2 * b, 2 * b + 1):
                        for h in range(HC):
                            m = e.matmul(v_ps[b][:, (k % 2) * C:(k % 2 + 1) * C], kk[:, h, k * P:(k + 1) * P],
                                         wv[:, h, :], start=(h == 0), stop=(h == HC - 1))
                    m.then_inc(T_("v"), 1)

        @block.vector
        def _(e):
            V.start(e)
            for k in "kr":
                e.tensor_scalar(tm[k][:, :], c.vec[f"cm_{k}"], 1.0, None, ALU.subtract).then_inc(made, 1)
            e.wait_ge(made, 2)
            with e.Fori(0, BLOCKS) as i:
                ln_vector(e, V, A, n, c.XI, i, lambda: e.wait_ge(*T_.at("turned", i - 1)))
                h = n.hT[:, :, :].rearrange("p j t -> p (j t)")
                e.wait_ge(*A.at("features", i))
                e.tensor_tensor(by_batch(dh[:, :])[:, :, 1:T], by_batch(h)[:, :, 1:T], by_batch(h)[:, :, 0:T - 1],
                                ALU.subtract).then_inc(V("shift"), 1)
                e.tensor_copy(by_batch(dh[:, :])[:, :, 0:1], by_batch(h)[:, :, 0:1]).then_inc(V("first"), 1)
                e.wait_ge(*V.at("first", i))
                for k in "kr":
                    e.wait_ge(*T_.at(k, i - 1))
                    for j in range(CJ):
                        e.scalar_tensor_tensor(mix[k][:, j, :], dh[:, j * BT:(j + 1) * BT], tm[k][:, j:j + 1],
                                               n.hT[:, j, :], ALU.mult, ALU.add).then_inc(V("mix"), 1)
                e.wait_ge(*T_.at("v", i - 1))
                for q in range(HC):
                    e.wait_ge(*A.at("relu", i, q))
                    e.tensor_tensor(kk[:, q, :], relu[q % 2][:, :], relu[q % 2][:, :], ALU.mult).then_inc(V("square"), 1)
                for b in range(2):
                    e.wait_ge(*A.at("gate", i, b))
                    e.wait_ge(*T_.at("v", i, b))
                    g = gate[:, 2 * b:2 * b + 2, :]
                    e.tensor_tensor(g, g, v_ps[b][:, :].rearrange("p (k f) -> p k f", k=2), ALU.mult).then_inc(V("rkv"), 1)
                e.wait_ge(*V.at("rkv", i))
                for b in range(2):
                    tiles = bass.ds(i * KT_ + 2 * b, 2)
                    g = gate[:, 2 * b:2 * b + 2, :]
                    e.tensor_tensor(g, g, c.XI[:, tiles, :], ALU.add).then_inc(V("plus"), 1)
                e.wait_ge(*V.at("plus", i))
                for b in range(2):
                    tiles = bass.ds(i * KT_ + 2 * b, 2)
                    g = gate[:, 2 * b:2 * b + 2, :]
                    e.tensor_tensor(c.X[:, tiles, :], c.X[:, tiles, :], g, ALU.add).then_inc(V("added"), 1)

        @block.scalar
        def _(e):
            A.start(e)
            with e.Fori(0, BLOCKS) as i:
                ln_scalar_std(e, V, A, n, i, c)
                ln_scalar_features(e, T_, A, n, i, lambda: e.wait_ge(*V.at("mix", i - 1)), c.vec["ln2_g"],
                                   c.vec["ln2_b"])
                for h in range(HC):
                    e.wait_ge(*T_.at("k", i, h))
                    e.wait_ge(*(V.at("square", i, h - 2) if h >= 2 else V.at("square", i - 1)))
                    e.activation(relu[h % 2][:, :], k_ps[h % 2][:, :], ACT.Relu).then_inc(A("relu"), 1)
                for b in range(2):
                    e.wait_ge(*T_.at("r", i, b))
                    e.wait_ge(*V.at("added", i - 1))
                    e.activation(gate[:, 2 * b:2 * b + 2, :].rearrange("p k f -> p (k f)"), r_ps[b][:, :],
                                 ACT.Sigmoid).then_inc(A("gate"), 1)



def over(ap, shape, at):
    return ap.unsqueeze(at).broadcast_to(list(shape))


def l0_gates(nc, c):
    with ExitStack() as ctx:
        sb, ps, sem = tensors(nc, ctx, "mg")
        wg, we = sb("wg", [P, CJ, E]), [sb(f"we{j}", [P, E * C]) for j in range(CJ)]
        n = Norm(sb, ps, tiles=TILES)
        lg, prob, top = sb("lg", [P, TILES, E]), sb("prob", [P, TILES, E]), sb("top", [P, TILES, 8])
        idx, idf = sb("idx", [P, TILES, 8], U32), sb("idf", [P, TILES, 8])
        big, both = sb("big", [P, TILES]), sb("both", [P, TILES])
        g0, g1, gate = sb("g0", [P, TILES, E]), sb("g1", [P, TILES, E]), c.gate
        g_ps, t_ps = ps("g_ps"), [ps(f"t_ps{i}") for i in range(BLOCKS)]
        loaded, seen, w_loaded = sem("loaded"), sem("seen"), [sem(f"w_loaded{j}") for j in range(CJ)]
        V = Steps(sem("vector"), ALL_V + ["logits", "big", "less", ("top", TILES), ("index", TILES), "float", "sum",
                                          "flip", "hot0", "hot1", "part0", "part1", "join", "gate"])
        A = Steps(sem("scalar"), ALL_A + ["exp", ("gate_t", BLOCKS)])
        T_ = Steps(sem("tensor"), ALL_T + ["logits", ("gate_t", BLOCKS)])
        G = Steps(sem("pool"), CJ * ["scaled", "w0", "w1"] + ALL_G)
        block = ctx.enter_context(nc.Block())
        shape = [P, TILES, E]

        @block.sync
        def _(e):
            e.dma_start(wg[:, :, :], c.d["l0_wg"]).then_inc(loaded, 16)
            for j in range(CJ):
                e.dma_start(we[j][:, :], c.d["l0_we"][:, j, :]).then_inc(w_loaded[j], 16)

        @block.tensor
        def _(e):
            T_.start(e)
            all_tensor(e, V, A, T_, n, c)
            e.wait_ge(loaded, 16)
            for k in range(TILES):
                if k % KT_ == 0:
                    e.wait_ge(*A.at("features", 0, k // KT_ * CJ + CJ - 1))
                for j in range(CJ):
                    m = e.matmul(g_ps[:, k * E:(k + 1) * E], n.hT[:, j, k * P:(k + 1) * P], wg[:, j, :],
                                 start=(j == 0), stop=(j == CJ - 1))
            m.then_inc(T_("logits"), 1)
            e.wait_ge(*V.at("gate", 0))
            for i in range(BLOCKS):
                for k in range(KT_):
                    m = e.transpose(t_ps[i][0:E, k * P:(k + 1) * P], gate[:, i * KT_ + k, :], c.ident[:, :])
                m.then_inc(T_("gate_t"), 1)

        @block.gpsimd
        def _(e):
            G.start(e)
            for j in range(CJ):
                e.wait_ge(w_loaded[j], 16)
                e.tensor_scalar(we[j][:, :], we[j][:, :], W_SCALE, None, ALU.mult).then_inc(G("scaled"), 1)
                e.wait_ge(*G.at("scaled", 0, j))
                e.tensor_copy(c.we[0][:, j, :], we[j][:, :]).then_inc(G("w0"), 1)
                e.wait_ge(*G.at("w0", 0, j))
                e.tensor_tensor(c.we[1][:, j, :], we[j][:, :], c.we[0][:, j, :], ALU.subtract).then_inc(G("w1"), 1)
            all_pool(e, A, G, n, c.parts)

        @block.vector
        def _(e):
            V.start(e)
            ln_vector(e, V, A, n, c.X, 0, lambda: None)
            e.wait_ge(*T_.at("logits", 0))
            e.tensor_copy(lg[:, :, :].rearrange("p k e -> p (k e)"), g_ps[:, 0:TILES * E]).then_inc(V("logits"), 1)
            e.wait_ge(*V.at("logits", 0))
            e.tensor_reduce(big[:, :], lg[:, :, :], AX.X, ALU.max).then_inc(V("big"), 1)
            e.wait_ge(*V.at("big", 0))
            e.tensor_tensor(lg[:, :, :], lg[:, :, :], over(big[:, :], shape, 2), ALU.subtract).then_inc(V("less"), 1)
            e.wait_ge(*A.at("exp", 0))
            e.sem_inc(seen, 1)
            for k in range(TILES):
                e.max(top[:, k, :], prob[:, k, :]).then_inc(V("top"), 1)
            e.wait_ge(*V.at("top", 0))
            e.sem_inc(seen, 1)
            for k in range(TILES):
                e.max_index(idx[:, k, :], top[:, k, :], prob[:, k, :]).then_inc(V("index"), 1)
            e.wait_ge(*V.at("index", 0))
            e.tensor_copy(idf[:, :, :], idx[:, :, :]).then_inc(V("float"), 1)
            e.tensor_tensor(both[:, :], top[:, :, 0], top[:, :, 1], ALU.add).then_inc(V("sum"), 1)
            e.wait_ge(*V.at("sum", 0))
            e.reciprocal(both[:, :], both[:, :]).then_inc(V("flip"), 1)
            e.tensor_tensor(g0[:, :, :], over(c.iota, shape, 1), idf[:, :, 0:1].broadcast_to(shape),
                            ALU.is_equal).then_inc(V("hot0"), 1)
            e.tensor_tensor(g1[:, :, :], over(c.iota, shape, 1), idf[:, :, 1:2].broadcast_to(shape),
                            ALU.is_equal).then_inc(V("hot1"), 1)
            e.wait_ge(*V.at("hot1", 0))
            e.tensor_tensor(g0[:, :, :], g0[:, :, :], top[:, :, 0:1].broadcast_to(shape), ALU.mult).then_inc(V("part0"), 1)
            e.tensor_tensor(g1[:, :, :], g1[:, :, :], top[:, :, 1:2].broadcast_to(shape), ALU.mult).then_inc(V("part1"), 1)
            e.wait_ge(*V.at("part1", 0))
            e.tensor_tensor(g0[:, :, :], g0[:, :, :], g1[:, :, :], ALU.add).then_inc(V("join"), 1)
            e.wait_ge(*V.at("join", 0))
            e.tensor_tensor(gate[:, :, :], g0[:, :, :], over(both[:, :], shape, 2), ALU.mult).then_inc(V("gate"), 1)

        @block.scalar
        def _(e):
            A.start(e)
            ln_scalar_std(e, V, A, n, 0, c)
            all_scalar(e, T_, A, n, c.parts)
            e.wait_ge(*V.at("less", 0))
            e.activation(prob[:, :, :].rearrange("p k e -> p (k e)"), lg[:, :, :].rearrange("p k e -> p (k e)"),
                         ACT.Exp).then_inc(A("exp"), 1)
            for i in range(BLOCKS):
                e.wait_ge(*T_.at("gate_t", 0, i))
                e.activation(c.gate_t[:, i * BT:(i + 1) * BT], t_ps[i][0:E, :], ACT.Copy).then_inc(A("gate_t"), 1)


def l0_experts(nc, c):
    with ExitStack() as ctx:
        sb, ps, sem = tensors(nc, ctx, "mo")
        h = [sb(f"h{u}", [P, 2, CJ, P], FP16) for u in range(2)]
        gate_t = [sb(f"gate_t{u}", [E, P]) for u in range(2)]
        b_ps = ps("b_ps")
        e_ps = [ps(f"e_ps{q}") for q in range(E // 2)]
        V = Steps(sem("vector"), ["scaled"] + [("expert", E)] + ["bias"], 2)
        A = Steps(sem("scalar"), [("part", 2), "gate_t"], 2)
        T_ = Steps(sem("tensor"), [("expert", E // 2), "bias"], 2)
        g = [sb(f"g{u}", [P, E]) for u in range(2)]
        block = ctx.enter_context(nc.Block())

        @block.scalar
        def _(e):
            A.start(e)
            with e.Fori(0, TILES // 2) as i:
                for u in range(2):
                    t = i * 2 + u
                    e.wait_ge(*T_.at("bias", t - 2))
                    for x in range(2):
                        e.activation(h[u][:, x, :, :], c.parts[x][:, :, bass.ds(t * P, P)], ACT.Copy).then_inc(A("part"), 1)
                    e.activation(gate_t[u][:, :], c.gate_t[:, bass.ds(t * P, P)], ACT.Copy).then_inc(A("gate_t"), 1)

        @block.tensor
        def _(e):
            T_.start(e)
            with e.Fori(0, TILES // 2) as i:
                for u in range(2):
                    t = i * 2 + u
                    e.wait_ge(*A.at("part", t))
                    for q in range(E // 2):
                        e.wait_ge(*V.at("expert", t - 1, 2 * q + 1))
                        for j in range(CJ):
                            for x, w in ((0, 0), (0, 1), (1, 0)):
                                m = e.matmul(e_ps[q][:, :], h[u][:, x, j, :], c.we[w][:, j, q * 2 * C:(q + 1) * 2 * C],
                                             start=(j == 0 and x + w == 0), stop=(j == CJ - 1 and x == 1))
                        m.then_inc(T_("expert"), 1)
                    e.wait_ge(*A.at("gate_t", t))
                    e.wait_ge(*V.at("bias", t - 1))
                    e.matmul(b_ps[:, 0:C], gate_t[u][:, :], c.sm["be"][0:E, :], start=True, stop=True).then_inc(T_("bias"), 1)

        @block.vector
        def _(e):
            V.start(e)
            with e.Fori(0, TILES // 2) as i:
                for u in range(2):
                    t = i * 2 + u
                    x = c.X[:, t, :]
                    e.wait_ge(*V.at("expert", t - 2))
                    e.tensor_scalar(g[u][:, :], c.gate[:, t, :], 1.0 / W_SCALE, None, ALU.mult).then_inc(V("scaled"), 1)
                    e.wait_ge(*V.at("scaled", t))
                    for q in range(E):
                        if q % 2 == 0:
                            e.wait_ge(*T_.at("expert", t, q // 2))
                        if q:
                            e.wait_ge(*V.at("expert", t, q - 1))
                        e.scalar_tensor_tensor(x, e_ps[q // 2][:, (q % 2) * C:(q % 2 + 1) * C], g[u][:, q:q + 1], x,
                                               ALU.mult, ALU.add).then_inc(V("expert"), 1)
                    e.wait_ge(*T_.at("bias", t))
                    e.wait_ge(*V.at("expert", t))
                    e.tensor_tensor(x, x, b_ps[:, 0:C], ALU.add).then_inc(V("bias"), 1)



QUANT_V = ["amax", "guard", "inv", "scale", ("round", KT_), "int", "rt_inv", "dequant"]
QUANT_A = [("squares", KT_), "rt"]


class Quant:

    def __init__(self, sb):
        self.ss, self.amax, self.rt = (sb(f"q_{k}", [P, KT_]) for k in ("ss", "amax", "rt"))
        self.guard, self.scale, self.factor = (sb(f"q_{k}", [P, KT_]) for k in ("guard", "scale", "factor"))
        self.junk = sb("q_junk", [P, C])
        self.big = sb("q_big", [P, KT_, C])
        self.ints = sb("q_ints", [P, KT_, C], BF16)


def quant_vector(e, V, A, q, src, ready, i, free):
    e.wait_ge(*ready)
    e.tensor_reduce(q.amax[:, :], src[:, :, :], AX.X, ALU.max, apply_absolute_value=True).then_inc(V("amax"), 1)
    e.wait_ge(*V.at("amax", i))
    e.wait_ge(*A.at("rt", i))
    e.scalar_tensor_tensor(q.guard[:, :], q.rt[:, :], 1e-5, q.amax[:, :], ALU.mult, ALU.max).then_inc(V("guard"), 1)
    e.wait_ge(*V.at("guard", i))
    e.reciprocal(q.scale[:, :], q.guard[:, :]).then_inc(V("inv"), 1)
    e.wait_ge(*V.at("inv", i))
    e.tensor_scalar(q.scale[:, :], q.scale[:, :], 127.0, None, ALU.mult).then_inc(V("scale"), 1)
    e.wait_ge(*V.at("scale", i))
    for k in range(KT_):
        e.tensor_scalar(q.big[:, k, :], src[:, k, :], q.scale[:, k:k + 1], ROUND, ALU.mult, ALU.add).then_inc(V("round"), 1)
    e.wait_ge(*V.at("round", i))
    free()
    e.tensor_scalar(q.ints[:, :, :], q.big[:, :, :], ROUND, None, ALU.subtract).then_inc(V("int"), 1)
    e.reciprocal(q.rt[:, :], q.rt[:, :]).then_inc(V("rt_inv"), 1)
    e.wait_ge(*V.at("rt_inv", i))
    e.scalar_tensor_tensor(q.factor[:, :], q.guard[:, :], 1.0 / 127.0, q.rt[:, :], ALU.mult,
                           ALU.mult).then_inc(V("dequant"), 1)


def quant_scalar(e, V, A, q, src, ready, i, c):
    e.wait_ge(*ready)
    e.wait_ge(*V.at("dequant", i - 1))
    for k in range(KT_):
        e.wait_ge(*(A.at("squares", i, k - 1) if k else A.at("squares", i - 1)))
        e.activation(q.junk[:, :], src[:, k, :], ACT.Square, accum_out=q.ss[:, k:k + 1]).then_inc(A("squares"), 1)
    e.wait_ge(*A.at("squares", i))
    e.activation(q.rt[:, :], q.ss[:, :], ACT.Sqrt, scale=1.0 / C, bias=c.eps[:, 1:2]).then_inc(A("rt"), 1)


def l1_prepare(nc, c):
    with ExitStack() as ctx:
        sb, ps, sem = tensors(nc, ctx, "pr")
        names = [("q", C), ("k", P), ("v", P), ("o", C)]
        w = {k: sb(f"w{k}", [P, CJ, o]) for k, o in names}
        part, mean, inv = sb("part", [P, 4]), sb("mean", [P, 4]), sb("inv", [P, 4])
        big = {k: sb(f"big{k}", [P, CJ, o]) for k, o in names}
        rt, guard = sb("rt", [P, 2 * B]), sb("guard", [P, 2 * B])
        lastq = sb("lastq", [B, 4])
        lastf = sb("lastf", [B, 4])
        last, last_big = sb("last", [B, C]), sb("last_big", [B, C])
        last_i = sb("last_i", [B, C], BF16)
        last_t = sb("last_t", [P, CJ, B], BF16)
        kv = sb("kv", [B, 2 * P])
        k_parts = sb("k_parts", [B, 2, 2, P // 2], FP16)
        sum_ps, kv_ps, kt_ps = ps("sum_ps"), ps("kv_ps"), ps("kt_ps", (P, 2 * 512), FP16)
        t_ps = ps("t_ps", (P, 2 * 512), BF16)
        loaded, v, a, t, moved = sem("loaded"), sem("vector"), sem("scalar"), sem("tensor"), sem("moved")
        made, split = sem("made"), sem("split")
        block = ctx.enter_context(nc.Block())

        @block.sync
        def _(e):
            for k, _ in names:
                e.dma_start(w[k][:, :, :], c.d[f"l1_w{k}"]).then_inc(loaded, 16)
            e.dma_start(last[:, :], c.d["ctx_last"]).then_inc(loaded, 16)
            e.wait_ge(v, 26)
            e.dma_start(c.d["bounce"], kv[:, P:2 * P]).then_inc(moved, 16)
            e.wait_ge(moved, 16)

        @block.vector
        def _(e):
            e.wait_ge(loaded, 80)
            for q, (k, _) in enumerate(names):
                e.tensor_reduce(part[:, q:q + 1], w[k][:, :, :], AX.XY, ALU.add, apply_absolute_value=True).then_inc(v, 1)
            e.wait_ge(t, 1)
            for q, (_, o) in enumerate(names):
                e.tensor_scalar(mean[:, q:q + 1], sum_ps[:, q:q + 1], 1.0 / (C * o), 1e-5, ALU.mult, ALU.max).then_inc(v, 1)
            e.wait_ge(v, 8)
            e.reciprocal(inv[:, :], mean[:, :]).then_inc(v, 1)
            e.wait_ge(v, 9)
            for q, (k, _) in enumerate(names):
                e.tensor_scalar(big[k][:, :, :], w[k][:, :, :], inv[:, q:q + 1], ROUND, ALU.mult, ALU.add).then_inc(v, 1)
            e.wait_ge(v, 13)
            for k, _ in names:
                e.tensor_scalar(big[k][:, :, :], big[k][:, :, :], ROUND, 1.0, ALU.subtract, ALU.min).then_inc(v, 1)
            e.wait_ge(v, 17)
            e.tensor_scalar(c.wq[:, :, :], big["q"][:, :, :], -1.0, None, ALU.max).then_inc(v, 1)
            e.tensor_scalar(c.wkv[:, :, 0:P], big["k"][:, :, :], -1.0, None, ALU.max).then_inc(v, 1)
            e.tensor_scalar(c.wkv[:, :, P:2 * P], big["v"][:, :, :], -1.0, None, ALU.max).then_inc(v, 1)
            e.tensor_scalar(c.wo[:, :, :], big["o"][:, :, :], -1.0, None, ALU.max).then_inc(v, 1)
            e.tensor_scalar(c.wf[:, 0:1], mean[:, 0:1], HD ** -0.5, None, ALU.mult).then_inc(v, 1)
            e.tensor_copy(c.wf[:, 1:4], mean[:, 1:4]).then_inc(v, 1)
            e.tensor_reduce(lastq[:, 0:1], last[:, :], AX.X, ALU.max, apply_absolute_value=True).then_inc(v, 1)
            e.wait_ge(v, 24)
            e.wait_ge(a, 3)
            e.scalar_tensor_tensor(lastq[:, 2:3], lastq[:, 1:2], 1e-5, lastq[:, 0:1], ALU.mult, ALU.max).then_inc(made, 1)
            e.scalar_tensor_tensor(guard[:, :], rt[:, :], 1e-5, c.c_max[:, :], ALU.mult, ALU.max).then_inc(made, 1)
            e.wait_ge(made, 2)
            e.reciprocal(lastq[:, 3:4], lastq[:, 2:3]).then_inc(made, 1)
            e.reciprocal(rt[:, :], rt[:, :]).then_inc(made, 1)
            e.reciprocal(lastq[:, 1:2], lastq[:, 1:2]).then_inc(made, 1)
            e.wait_ge(made, 5)
            e.tensor_scalar(lastq[:, 3:4], lastq[:, 3:4], 127.0, None, ALU.mult).then_inc(made, 1)
            e.scalar_tensor_tensor(guard[:, :], guard[:, :], 1.0 / 127.0, rt[:, :], ALU.mult, ALU.mult).then_inc(made, 1)
            e.scalar_tensor_tensor(lastf[:, 1:2], lastq[:, 2:3], 1.0 / 127.0, lastq[:, 1:2], ALU.mult, ALU.mult).then_inc(made, 1)
            e.wait_ge(made, 8)
            e.tensor_scalar(c.kf[:, :], guard[:, :], mean[:, 1:2], None, ALU.mult).then_inc(made, 1)
            e.tensor_scalar(c.vf[:, :], guard[:, :], mean[:, 2:3], None, ALU.mult).then_inc(made, 1)
            e.tensor_scalar(lastf[:, 2:3], mean[0:B, 1:2], lastf[:, 1:2], None, ALU.mult).then_inc(made, 1)
            e.tensor_scalar(lastf[:, 3:4], mean[0:B, 2:3], lastf[:, 1:2], None, ALU.mult).then_inc(made, 1)
            e.tensor_scalar(last_big[:, :], last[:, :], lastq[:, 3:4], ROUND, ALU.mult, ALU.add).then_inc(made, 1)
            e.wait_ge(made, 13)
            e.tensor_scalar(last_i[:, :], last_big[:, :], ROUND, None, ALU.subtract).then_inc(made, 1)
            e.wait_ge(t, 2)
            e.tensor_copy(last_t[:, :, :].rearrange("p j b -> p (j b)"), t_ps[:, 0:CJ * B]).then_inc(made, 1)
            e.wait_ge(t, 3)
            e.tensor_scalar(kv[:, 0:P], kv_ps[0:B, 0:P], lastf[:, 2:3], None, ALU.mult).then_inc(v, 1)
            e.tensor_scalar(kv[:, P:2 * P], kv_ps[0:B, P:2 * P], lastf[:, 3:4], None, ALU.mult).then_inc(v, 1)
            k = kv[:, 0:P].rearrange("b (s f) -> b s f", s=2)
            e.wait_ge(v, 26)
            e.tensor_copy(k_parts[:, :, 0, :], k).then_inc(split, 1)
            e.wait_ge(split, 1)
            e.tensor_tensor(k_parts[:, :, 1, :], k, k_parts[:, :, 0, :], ALU.subtract).then_inc(split, 1)
            e.memset(c.v_last[:, :, :, :], 0.0).then_inc(split, 1)
            e.tensor_tensor(c.mask[:, :], c.group[:, 0:4], c.group[:, 4:8], ALU.add).then_inc(split, 1)
            e.wait_ge(t, 4)
            e.tensor_copy(c.k_last[:, :, :].rearrange("p s b -> p (s b)"), kt_ps[:, 0:2 * B]).then_inc(made, 1)

        @block.scalar
        def _(e):
            e.wait_ge(loaded, 80)
            e.activation(last_big[:, :], last[:, :], ACT.Square, accum_out=lastf[:, 0:1]).then_inc(a, 1)
            e.wait_ge(a, 1)
            e.activation(lastq[:, 1:2], lastf[:, 0:1], ACT.Sqrt, scale=1.0 / C, bias=c.eps[0:B, 1:2]).then_inc(a, 1)
            e.activation(rt[:, :], c.c_ss[:, :], ACT.Sqrt, scale=1.0 / C, bias=c.eps[:, 1:2]).then_inc(a, 1)

        @block.tensor
        def _(e):
            e.wait_ge(v, 4)
            e.matmul(sum_ps[:, 0:4], c.ones[:, :], part[:, :], start=True, stop=True).then_inc(t, 1)
            e.wait_ge(made, 14)
            for j in range(CJ):
                m = e.transpose(t_ps[:, j * B:(j + 1) * B], last_i[:, j * P:(j + 1) * P], c.identb[0:B, 0:B])
            m.then_inc(t, 1)
            e.wait_ge(made, 15)
            for j in range(CJ):
                m = e.matmul(kv_ps[0:B, 0:2 * P], last_t[:, j, :], c.wkv[:, j, :], start=(j == 0), stop=(j == CJ - 1))
            m.then_inc(t, 1)
            e.wait_ge(split, 2)
            for s in range(2):
                m = e.transpose(kt_ps[:, s * B:(s + 1) * B], k_parts[:, s, :, :].rearrange("b x f -> b (x f)"),
                                c.identh[0:B, 0:B])
            m.then_inc(t, 1)


def l1_queries(nc, c):
    with ExitStack() as ctx:
        sb, ps, sem = tensors(nc, ctx, "q1")
        parts_ps = [ps(f"parts_ps{j}", (P, 2 * 512), FP16) for j in range(2)]
        n, q = Norm(sb, ps, banks=parts_ps), Quant(sb)
        f = sb("f", [P, KT_])
        xT = sb("xT", [P, CJ, BT], BF16)
        qn = sb("qn", [P, KT_, C])
        parts = [sb(f"parts{x}", [P, KT_, 4, 2, P // 2], FP16) for x in range(2)]
        t_ps = [ps(f"t_ps{j}", (P, 2 * 512), BF16) for j in range(CJ)]
        q_ps = [ps(f"q_ps{b}") for b in range(2)]
        V = Steps(sem("vector"), LN_V + QUANT_V + ["factor", ("q", KT_)])
        A = Steps(sem("scalar"), LN_A[:1] + QUANT_A + [("xT", CJ), ("rounded", 2), ("features", 4)])
        T_ = Steps(sem("tensor"), [("ints_t", CJ), ("q", 2), ("turned", 4)])
        G = Steps(sem("pool"), [("rest", 2)])

        def copy_of(t, dup):
            return t[:, :, :, dup, :].rearrange("p k c f -> p (k c) f")

        def in_parts(t):
            return t[:, :, :].rearrange("p k (c f) -> p (k c) f", f=P // 2)

        block = ctx.enter_context(nc.Block())

        @block.vector
        def _(e):
            V.start(e)
            with e.Fori(0, BLOCKS) as i:
                ln_vector(e, V, A, n, c.X, i, lambda: None)
                quant_vector(e, V, A, q, n.xn, V.at("norm", i), i, lambda: e.wait_ge(*T_.at("ints_t", i - 1)))
                e.wait_ge(*V.at("dequant", i))
                e.tensor_scalar(f[:, :], q.factor[:, :], c.wf[:, 0:1], None, ALU.mult).then_inc(V("factor"), 1)
                e.wait_ge(*V.at("factor", i))
                e.wait_ge(*G.at("rest", i - 1))
                for k in range(KT_):
                    e.wait_ge(*T_.at("q", i, k // 2))
                    e.tensor_scalar(qn[:, k, :], q_ps[k // 2][:, (k % 2) * C:(k % 2 + 1) * C], f[:, k:k + 1], None,
                                    ALU.mult).then_inc(V("q"), 1)

        @block.scalar
        def _(e):
            A.start(e)
            with e.Fori(0, BLOCKS) as i:
                ln_scalar_std(e, V, A, n, i, c)
                quant_scalar(e, V, A, q, n.xn, V.at("norm", i), i, c)
                e.wait_ge(*T_.at("q", i - 1))
                for j in range(CJ):
                    e.wait_ge(*T_.at("ints_t", i, j))
                    e.activation(xT[:, j, :], t_ps[j][:, 0:BT], ACT.Copy).then_inc(A("xT"), 1)
                e.wait_ge(*V.at("q", i))
                e.wait_ge(*T_.at("turned", i - 1, 1))
                for dup in range(2):
                    e.activation(copy_of(parts[0], dup), in_parts(qn), ACT.Copy).then_inc(A("rounded"), 1)
                for r in range(4):
                    e.wait_ge(*T_.at("turned", i, r))
                    e.activation(c.qT[:, 2 * r:2 * r + 2, bass.ds(i * BT, BT)],
                                 parts_ps[r % 2][:, :].rearrange("p (s t) -> p s t", s=2), ACT.Copy)\
                        .then_inc(A("features"), 1)

        @block.gpsimd
        def _(e):
            G.start(e)
            with e.Fori(0, BLOCKS) as i:
                e.wait_ge(*A.at("rounded", i))
                e.wait_ge(*T_.at("turned", i - 1))
                for dup in range(2):
                    e.tensor_tensor(copy_of(parts[1], dup), in_parts(qn), copy_of(parts[0], dup),
                                    ALU.subtract).then_inc(G("rest"), 1)

        @block.tensor
        def _(e):
            T_.start(e)
            with e.Fori(0, BLOCKS) as i:
                e.wait_ge(*V.at("int", i))
                for j in range(CJ):
                    e.wait_ge(*A.at("xT", i - 1, j))
                    for k in range(KT_):
                        m = e.transpose(t_ps[j][:, k * P:(k + 1) * P], q.ints[:, k, j * P:(j + 1) * P], c.identb[:, :])
                    m.then_inc(T_("ints_t"), 1)
                e.wait_ge(*A.at("xT", i))
                for b in range(2):
                    e.wait_ge(*V.at("q", i - 1))
                    for k in (2 * b, 2 * b + 1):
                        for j in range(CJ):
                            m = e.matmul(q_ps[b][:, (k % 2) * C:(k % 2 + 1) * C], xT[:, j, k * P:(k + 1) * P],
                                         c.wq[:, j, :], start=(j == 0), stop=(j == CJ - 1))
                    m.then_inc(T_("q"), 1)
                for r in range(4):
                    e.wait_ge(*A.at("features", i if r >= 2 else i - 1, (r - 2) % 4))
                    e.wait_ge(*(A.at("rounded", i) if r < 2 else G.at("rest", i)))
                    for s in range(2):
                        for k in range(KT_):
                            m = e.transpose(parts_ps[r % 2][:, s * BT + k * P:s * BT + (k + 1) * P],
                                            parts[r // 2][:, k, 2 * (r % 2) + s, :, :].rearrange("p d f -> p (d f)"),
                                            c.identh[:, :])
                    m.then_inc(T_("turned"), 1)


BQ = B // 4


def l1_keys(nc, c, shared, quarter):
    with ExitStack() as ctx:
        sb, ps, _ = tensors(nc, ctx, f"k{quarter}")
        rows = [sb(f"rows{u}", [P, 2, C], BF16) for u in range(2)]
        xT = [sb(f"xT{u}", [P, CJ, 2 * P], BF16) for u in range(2)]
        kn = [sb(f"kn{u}", [P, 4, P // 2]) for u in range(2)]
        parts = [sb(f"parts{u}", [P, 4, 2, P // 2], FP16) for u in range(2)]
        t_ps = [ps(f"t_ps{u}", (P, 2 * 512), BF16) for u in range(2)]
        kv_ps = [ps(f"kv_ps{u}") for u in range(2)]
        kt_ps = [ps(f"kt_ps{u}", (P, 2 * 512), FP16) for u in range(2)]
        before = quarter * BQ
        made, last = shared.sem("made"), shared.sem("last")
        V = shared.steps("vector", ["k", "v", "rounded"], before)
        xT_kept, kT_kept = (shared.steps(f"{x}_kept", ["done"], before) for x in ("xT", "kT"))
        rows_t, kv_t, k_t = (shared.steps(f"{x}_t", ["done"], before) for x in ("rows", "kv", "k"))
        G = shared.steps("pool", ["rest"], before)
        fetched = [shared.sem(f"fetched{u}") for u in range(2)]
        block = ctx.enter_context(nc.Block())
        first = quarter * BQ

        @block.sync
        def _(e):
            for t in range(4):
                s = t // 2
                e.dma_start(c.v_last[t:t + 1, :, t, :],
                            c.d["bounce"][first:first + BQ, 64 * s:64 * s + 64].rearrange("(a b) f -> a b f", a=1))\
                    .then_inc(last, 16)
            with e.Fori(0, BQ // 2) as h:
                for u in range(2):
                    b = h * 2 + u
                    e.wait_ge(*rows_t.at("done", b - 2))
                    e.dma_start(rows[u][:, :, :], c.cq[:, bass.ds(b * 2 + 2 * first, 2), :]).then_inc(fetched[u], 16)
            e.wait_ge(last, 64 * (quarter + 1))

        @block.gpsimd
        def _(e):
            G.start(e)
            for s in range(2):
                e.tensor_copy(c.kT[:, :, s, 2 * P], c.k_last[:, s, first:first + BQ]).then_inc(made, 1)
            with e.Fori(0, BQ // 2) as h:
                for u in range(2):
                    b = h * 2 + u
                    e.wait_ge(*V.at("rounded", b))
                    e.wait_ge(*k_t.at("done", b - 2))
                    e.tensor_tensor(parts[u][:, :, 1, :], kn[u][:, :, :], parts[u][:, :, 0, :],
                                    ALU.subtract).then_inc(G("rest"), 1)

        @block.tensor
        def _(e):
            def turn_rows(b, u, nth):
                e.wait_ge(fetched[u], (nth + before // 2) * 16)
                e.wait_ge(*xT_kept.at("done", b - 2))
                for j in range(CJ):
                    for m in range(2):
                        t = e.transpose(t_ps[u][:, (2 * j + m) * P:(2 * j + m + 1) * P],
                                        rows[u][:, m, j * P:(j + 1) * P], c.identb[:, :])
                t.then_inc(rows_t("done"), 1)

            def project(b, u):
                e.wait_ge(*xT_kept.at("done", b))
                e.wait_ge(*V.at("v", b - 2))
                for m in range(2):
                    for j in range(CJ):
                        t = e.matmul(kv_ps[u][:, m * 2 * P:(m + 1) * 2 * P], xT[u][:, j, m * P:(m + 1) * P],
                                     c.wkv[:, j, :], start=(j == 0), stop=(j == CJ - 1))
                t.then_inc(kv_t("done"), 1)

            def turn_keys(b, u):
                e.wait_ge(*G.at("rest", b))
                e.wait_ge(*kT_kept.at("done", b - 2))
                for m in range(2):
                    for s in range(2):
                        t = e.transpose(kt_ps[u][:, (2 * s + m) * P:(2 * s + m + 1) * P],
                                        parts[u][:, 2 * m + s, :, :].rearrange("p x f -> p (x f)"), c.identh[:, :])
                t.then_inc(k_t("done"), 1)

            for s in (rows_t, kv_t, k_t):
                s.start(e)
            turn_rows(0, 0, 1)
            project(0, 0)
            turn_rows(1, 1, 1)
            with e.Fori(0, BQ // 2 - 1) as h:
                for w in range(2):
                    b, u = h * 2 + w + 1, 1 - w
                    project(b, u)
                    turn_rows(b + 1, 1 - u, h + 2)
                    turn_keys(b - 1, 1 - u)
            project(BQ - 1, 1)
            turn_keys(BQ - 2, 0)
            turn_keys(BQ - 1, 1)

        @block.scalar
        def _(e):
            def keep_rows(b, u):
                e.wait_ge(*rows_t.at("done", b))
                e.wait_ge(*kv_t.at("done", b - 2))
                e.activation(xT[u][:, :, :].rearrange("p j m -> p (j m)"), t_ps[u][:, 0:2 * C],
                             ACT.Copy).then_inc(xT_kept("done"), 1)

            def keep_keys(b, u):
                e.wait_ge(*k_t.at("done", b))
                e.activation(c.kT[:, b, :, 0:2 * P], kt_ps[u][:, 0:4 * P].rearrange("p (s m) -> p s m", s=2),
                             ACT.Copy).then_inc(kT_kept("done"), 1)

            xT_kept.start(e)
            kT_kept.start(e)
            keep_rows(0, 0)
            keep_rows(1, 1)
            with e.Fori(0, BQ // 2 - 1) as h:
                for u in range(2):
                    b = h * 2 + u
                    keep_keys(b, u)
                    keep_rows(b + 2, u)
            keep_keys(BQ - 2, 0)
            keep_keys(BQ - 1, 1)

        @block.vector
        def _(e):
            V.start(e)
            with e.Fori(0, BQ // 2) as h:
                for u in range(2):
                    b = h * 2 + u
                    r = bass.ds(b * 2 + 2 * first, 2)
                    kv = kv_ps[u][:, :].rearrange("p (m f) -> p m f", m=2)
                    e.wait_ge(*kv_t.at("done", b))
                    e.wait_ge(*G.at("rest", b - 2))
                    e.tensor_tensor(kn[u][:, :, :].rearrange("p (m s) f -> p m (s f)", m=2), kv[:, :, 0:P],
                                    over(c.kf[:, r], [P, 2, P], 2), ALU.mult).then_inc(V("k"), 1)
                    e.tensor_tensor(c.v[:, b, :, :], kv[:, :, P:2 * P], over(c.vf[:, r], [P, 2, P], 2),
                                    ALU.mult).then_inc(V("v"), 1)
                    e.wait_ge(*k_t.at("done", b - 2))
                    e.wait_ge(*V.at("k", b))
                    e.tensor_copy(parts[u][:, :, 0, :], kn[u][:, :, :]).then_inc(V("rounded"), 1)
            e.wait_ge(made, 2 * (quarter + 1))


def l1_attention(nc, c, shared, quarter):
    with ExitStack() as ctx:
        sb, ps, _ = tensors(nc, ctx, f"t{quarter}")
        qd = [[sb(f"qd{u}{s}", [P, 4, 4, T], FP16) for s in range(2)] for u in range(2)]
        p = [sb(f"p{u}", [P, 4, M]) for u in range(2)]
        pt = [[sb(f"pt{u}{s}", [P, 2, 2, P]) for s in range(2)] for u in range(2)]
        pl = [sb(f"pl{u}", [4, P]) for u in range(2)]
        mx = [sb(f"mx{u}", [P, 4]) for u in range(2)]
        tot = [sb(f"tot{u}", [P, 4]) for u in range(2)]
        inv = [sb(f"inv{u}", [P, 2, 2]) for u in range(2)]
        s_ps = [ps(f"s_ps{s}", (P, 1024)) for s in range(2)]
        pt_ps = [ps(f"pt_ps{s}") for s in range(2)]
        pl_ps, o_ps = ps("pl_ps"), ps("o_ps")

        def step(name, n=1):
            return shared.steps(name, [("done", n)], quarter * BQ)

        made_q = [step(f"made_q{s}") for s in range(2)]
        scores = [step(f"scores{s}") for s in range(2)]
        turned = [step(f"turned{s}") for s in range(2)]
        outs = step("outs")
        maxes = [step(f"max{s}") for s in range(2)]
        kept0, inverse, divided = step("kept0"), step("inverse"), step("divided", 4)
        exps = [step(f"exps{s}", 2) for s in range(2)]
        kept1, kept_last = step("kept1"), step("kept_last")
        block = ctx.enter_context(nc.Block())
        first = quarter * BQ

        @block.gpsimd
        def _(e):
            for s in range(2):
                made_q[s].start(e)
            with e.Fori(0, BQ // 2) as h:
                for u in range(2):
                    b = h * 2 + u
                    for s in range(2):
                        e.wait_ge(*scores[s].at("done", b - 2))
                        q = c.qT[:, :, bass.ds((b + first) * T, T)].rearrange("p (x s) t -> p x s t", s=2)[:, :, s, :]
                        e.tensor_tensor(qd[u][s][:, :, :, :], over(q, [P, 4, 4, T], 2),
                                        over(over(c.mask[:, :], [P, 4, T], 2), [P, 4, 4, T], 1),
                                        ALU.mult).then_inc(made_q[s]("done"), 1)

        @block.tensor
        def _(e):
            def score(b, u, s):
                e.wait_ge(*made_q[s].at("done", b))
                e.wait_ge(*exps[s].at("done", b - 1))
                for g in range(2):
                    for x in range(2):
                        m = e.matmul(s_ps[s][:, g * 512:g * 512 + M], qd[u][s][:, 2 * x + g, :, :], c.kT[:, b, s, :],
                                     start=(x == 0), stop=(x == 1))
                m.then_inc(scores[s]("done"), 1)

            def turn(b, u, s):
                e.wait_ge(*exps[s].at("done", b))
                e.wait_ge(*(kept1 if s else kept0).at("done", b - 1))
                for m in range(2):
                    for g in range(2):
                        t = e.transpose(pt_ps[s][:, (2 * m + g) * P:(2 * m + g + 1) * P],
                                        p[u][:, 2 * s + g, m * P:(m + 1) * P], c.ident[:, :])
                if s:
                    e.wait_ge(*kept_last.at("done", b - 1))
                    t = e.transpose(pl_ps[0:4, 0:P], p[u][:, :, 2 * P], c.ident[:, :])
                t.then_inc(turned[s]("done"), 1)

            def out(b, u):
                e.wait_ge(*divided.at("done", b - 1))
                e.wait_ge(*kept_last.at("done", b))
                e.wait_ge(*kept0.at("done", b))
                e.wait_ge(*kept1.at("done", b))
                e.matmul(o_ps[:, 0:4 * 64], pl[u][:, :], c.v_last[:, b, :, :].rearrange("t a f -> t (a f)"),
                         start=True, stop=False, skip_group_check=True)
                for t in range(4):
                    s, g = divmod(t, 2)
                    for m in range(2):
                        i = e.matmul(o_ps[:, t * 64:(t + 1) * 64], pt[u][s][:, m, g, :],
                                     c.v[:, b, m, 64 * s:64 * s + 64], start=False, stop=(m == 1),
                                     skip_group_check=True)
                i.then_inc(outs("done"), 1)

            def turns(b, u, last=BQ):
                turn(b, u, 1)
                if last > 1:
                    score(b + 1, 1 - u, 1)
                    turn(b + 1, 1 - u, 0)
                if last > 2:
                    score(b + 2, u, 0)
                out(b, u)

            for s in (*scores, *turned, outs):
                s.start(e)
            score(0, 0, 0)
            score(0, 0, 1)
            turn(0, 0, 0)
            score(1, 1, 0)
            with e.Fori(0, BQ // 2 - 1) as h:
                for u in range(2):
                    turns(h * 2 + u, u)
            turns(BQ - 2, 0, 2)
            turns(BQ - 1, 1, 1)

        @block.scalar
        def _(e):
            def exp(b, u, s):
                e.wait_ge(*maxes[s].at("done", b))
                e.wait_ge(*turned[s].at("done", b - 2))
                e.wait_ge(*inverse.at("done", b - 2))
                for g in range(2):
                    t = 2 * s + g
                    e.activation(p[u][:, t, :], s_ps[s][:, g * 512:g * 512 + M], ACT.Exp, bias=mx[u][:, t:t + 1],
                                 accum_out=tot[u][:, t:t + 1]).then_inc(exps[s]("done"), 1)

            def keep(b, u):
                e.wait_ge(*turned[1].at("done", b))
                e.wait_ge(*outs.at("done", b - 2))
                e.activation(pt[u][1][:, :, :, :].rearrange("p m g r -> p (m g r)"), pt_ps[1][:, :],
                             ACT.Copy).then_inc(kept1("done"), 1)
                e.activation(pl[u][:, :], pl_ps[0:4, 0:P], ACT.Copy).then_inc(kept_last("done"), 1)

            def turns(b, u, last=BQ):
                keep(b, u)
                if last > 1:
                    exp(b + 1, 1 - u, 1)
                if last > 2:
                    exp(b + 2, u, 0)

            for s in (*exps, kept1, kept_last):
                s.start(e)
            exp(0, 0, 0)
            exp(0, 0, 1)
            exp(1, 1, 0)
            with e.Fori(0, BQ // 2 - 1) as h:
                for u in range(2):
                    turns(h * 2 + u, u)
            turns(BQ - 2, 0, 2)
            turns(BQ - 1, 1, 1)

        @block.vector
        def _(e):
            def maximum(b, u, s):
                e.wait_ge(*scores[s].at("done", b))
                e.wait_ge(*exps[s].at("done", b - 2))
                e.tensor_reduce(mx[u][:, 2 * s:2 * s + 2], s_ps[s][:, :].rearrange("p (g m) -> p g m", g=2)[:, :, 0:M],
                                AX.X, ALU.max, negate=True).then_inc(maxes[s]("done"), 1)

            def keep(b, u):
                e.wait_ge(*turned[0].at("done", b))
                e.wait_ge(*outs.at("done", b - 2))
                e.tensor_copy(pt[u][0][:, :, :, :].rearrange("p m g r -> p (m g r)"),
                              pt_ps[0][:, :]).then_inc(kept0("done"), 1)

            def divide(b, w, tile):
                u = w % 2
                e.wait_ge(*exps[0].at("done", b))
                e.wait_ge(*exps[1].at("done", b))
                e.wait_ge(*divided.at("done", b - 2))
                e.reciprocal(inv[u][:, :, :].rearrange("p s g -> p (s g)"), tot[u][:, :]).then_inc(inverse("done"), 1)
                e.wait_ge(*inverse.at("done", b))
                e.wait_ge(*outs.at("done", b))
                o = o_ps[:, 0:256].rearrange("p (s g f) -> p s g f", s=2, g=2)
                x = c.XA[:, tile, :].rearrange("p (s k g d) -> p k s g d", s=2, k=4, g=2)
                for k in range(4):
                    q = slice(32 * k, 32 * k + 32)
                    e.tensor_tensor(x[32 * w:32 * w + 32, k, :, :, :], o[q, :, :, HD * k:HD * k + HD],
                                    over(inv[u][q, :, :], [T, 2, 2, HD], 3), ALU.mult).then_inc(divided("done"), 1)

            def turns(b, w, tile, last=BQ):
                u = w % 2
                if last > 1:
                    maximum(b + 1, 1 - u, 1)
                    keep(b + 1, 1 - u)
                if last > 2:
                    maximum(b + 2, u, 0)
                divide(b, w, tile)

            for s in (*maxes, kept0, inverse, divided):
                s.start(e)
            maximum(0, 0, 0)
            maximum(0, 0, 1)
            keep(0, 0)
            maximum(1, 1, 0)
            with e.Fori(0, BQ // BPT - 1) as h:
                for w in range(BPT):
                    turns(h * BPT + w, w, h)
            for w in range(BPT):
                turns(BQ - BPT + w, w, BQ // BPT - 1, BPT - w)


def l1_project(nc, c, shared, quarter):
    with ExitStack() as ctx:
        sb, ps, _ = tensors(nc, ctx, f"o{quarter}")
        n, q = Norm(sb, ps), Quant(sb)
        f = sb("f", [P, KT_])
        xT = sb("xT", [P, CJ, BT], BF16)
        t_ps = [ps(f"t_ps{j}", (P, 2 * 512), BF16) for j in range(CJ)]
        o_ps = [ps(f"o_ps{b}") for b in range(2)]
        V = shared.steps("vector", LN_V + ["gain", "shift"] + QUANT_V + ["factor", ("added", KT_)], quarter, 1)
        A = shared.steps("scalar", LN_A[:1] + QUANT_A + [("xT", CJ)], quarter, 1)
        T_ = shared.steps("tensor", [("ints_t", CJ), ("o", 2)], quarter, 1)
        block = ctx.enter_context(nc.Block())
        i = 0

        @block.vector
        def _(e):
            V.start(e)
            rows = [P, KT_, C]
            ln_vector(e, V, A, n, c.XA, i, lambda: None)
            e.wait_ge(*V.at("norm", i))
            y = n.xn[:, :, :]
            e.tensor_tensor(y, y, over(c.row["x_gamma"], rows, 1), ALU.mult).then_inc(V("gain"), 1)
            e.wait_ge(*V.at("gain", i))
            e.tensor_tensor(y, y, over(c.row["x_beta"], rows, 1), ALU.add).then_inc(V("shift"), 1)
            quant_vector(e, V, A, q, n.xn, V.at("shift", i), i, lambda: e.wait_ge(*T_.at("ints_t", i - 1)))
            e.wait_ge(*V.at("dequant", i))
            e.tensor_scalar(f[:, :], q.factor[:, :], c.wf[:, 3:4], None, ALU.mult).then_inc(V("factor"), 1)
            e.wait_ge(*V.at("factor", i))
            for k in range(KT_):
                x = c.X[:, quarter * KT_ + k, :]
                e.wait_ge(*T_.at("o", i, k // 2))
                e.scalar_tensor_tensor(x, o_ps[k // 2][:, (k % 2) * C:(k % 2 + 1) * C], f[:, k:k + 1], x,
                                       ALU.mult, ALU.add).then_inc(V("added"), 1)

        @block.scalar
        def _(e):
            A.start(e)
            ln_scalar_std(e, V, A, n, i, c)
            quant_scalar(e, V, A, q, n.xn, V.at("shift", i), i, c)
            e.wait_ge(*T_.at("o", i - 1))
            for j in range(CJ):
                e.wait_ge(*T_.at("ints_t", i, j))
                e.activation(xT[:, j, :], t_ps[j][:, 0:BT], ACT.Copy).then_inc(A("xT"), 1)

        @block.tensor
        def _(e):
            T_.start(e)
            e.wait_ge(*V.at("int", i))
            for j in range(CJ):
                e.wait_ge(*A.at("xT", i - 1, j))
                for k in range(KT_):
                    m = e.transpose(t_ps[j][:, k * P:(k + 1) * P], q.ints[:, k, j * P:(j + 1) * P], c.identb[:, :])
                m.then_inc(T_("ints_t"), 1)
            e.wait_ge(*A.at("xT", i))
            for b in range(2):
                e.wait_ge(*V.at("added", i - 1))
                for k in (2 * b, 2 * b + 1):
                    for j in range(CJ):
                        m = e.matmul(o_ps[b][:, (k % 2) * C:(k % 2 + 1) * C], xT[:, j, k * P:(k + 1) * P],
                                     c.wo[:, j, :], start=(j == 0), stop=(j == CJ - 1))
                m.then_inc(T_("o"), 1)



def l1_inner(nc, c):
    with ExitStack() as ctx:
        sb, ps, sem = tensors(nc, ctx, "mi")
        w_in, w_x = sb("w_in", [P, CJ, 2 * DI]), sb("w_x", [P, DC, NR])
        n = Norm(sb, ps, tiles=TILES, xn=c.xn)
        in_ps = [ps(f"in_ps{q}") for q in range(4)]
        ssm_ps, dt_ps = ps("ssm_ps"), ps("dt_ps")
        xm = sb("xm", [P, DC, BB, TAPS - 1 + T])
        acc = [sb(f"acc{u}", [P, BT]) for u in range(2)]
        ssm = sb("ssm", [NR, BT])
        rest, middle = sb("rest", [2 * NS, BT]), sb("middle", [2 * NS, BT], BF16)
        lg, na, ez, wz, lz, dz, mz, step = (sb(f"dt_{k}", [P, TILES]) for k in
                                            ("lg", "na", "ez", "wz", "lz", "dz", "mz", "step"))
        loaded, out_loaded, made = sem("loaded"), sem("out_loaded"), sem("made")
        N = Steps(sem("norm"), [(k[0], TILES) if isinstance(k, tuple) else k for k in LN_V])
        NA, NT = Steps(sem("norm_scalar"), ["std", ("features", CJ * BLOCKS)]), Steps(sem("norm_tensor"), ALL_T)
        CV = Steps(sem("conv"), [("conv", DC * TAPS)])
        V = Steps(sem("parts"), ["hi", "rest", "middle", "middle2", "low"])
        D = Steps(sem("step_vector"), ["na", "w", "d", "m", "d1", "inv", "l1", "zl", "t", "step"])
        DA = Steps(sem("step_scalar"), ["exp", "log", ("spread", BLOCKS)])
        xs, silus, zs, rows_kept, lg_kept = (Steps(sem(k), [("done", m)]) for k, m in
                                             (("xs", DC), ("silus", DC), ("zs", DC), ("rows_kept", 1), ("lg_kept", 1)))
        x_t, z_t, rows_t, lg_t = (Steps(sem(k), [("done", m)]) for k, m in
                                  (("x_t", DC), ("z_t", DC), ("rows_t", 1), ("lg_t", 1)))
        spread = sem("spread")
        block = ctx.enter_context(nc.Block())

        @block.sync
        def _(e):
            e.dma_start(w_in[:, :, :], c.d["l1_w_in"]).then_inc(loaded, 16)
            e.dma_start(w_x[:, :, :], c.d["l1_w_x"]).then_inc(loaded, 16)
            e.dma_start(c.w_out[:, :, :], c.d["l1_w_out"]).then_inc(out_loaded, 16)
            e.wait_ge(out_loaded, 16)

        @block.tensor
        def _(e):
            def project(i):
                for q in range(2 * DC):
                    e.wait_ge(*(xs.at("done", i, q - DC) if q >= DC else zs.at("done", i - 1, q)))
                    for j in range(CJ):
                        m = e.matmul(in_ps[q % 4][:, :], w_in[:, j, q * P:(q + 1) * P], n.hT[:, j, bass.ds(i * BT, BT)],
                                     start=(j == 0), stop=(j == CJ - 1))
                    m.then_inc((x_t if q < DC else z_t)("done"), 1)

            def rows(i):
                e.wait_ge(*silus.at("done", i))
                e.wait_ge(*rows_kept.at("done", i - 1))
                for q in range(DC):
                    m = e.matmul(ssm_ps[0:NR, :], w_x[:, q, :], c.xc[:, q, bass.ds(i * BT, BT)],
                                 start=(q == 0), stop=(q == DC - 1))
                m.then_inc(rows_t("done"), 1)

            def turn_step(i):
                e.wait_ge(*rows_kept.at("done", i))
                e.wait_ge(*lg_kept.at("done", i - 1))
                for k in range(KT_):
                    m = e.matmul(dt_ps[:, k:k + 1], ssm[2 * NS:NR, k * P:(k + 1) * P], c.ones[2 * NS:NR, 0:1],
                                 start=True, stop=True)
                m.then_inc(lg_t("done"), 1)

            for each in (NT, x_t, z_t, rows_t, lg_t):
                each.start(e)
            for i in range(BLOCKS):
                for j in range(CJ):
                    if i:
                        e.wait_ge(*NA.at("features", 0, (i - 1) * CJ + j))
                    e.wait_ge(*N.at("norm", 0, i * KT_ + KT_ - 1))
                    for k in range(KT_):
                        t = e.transpose(n.ps[j][:, k * P:(k + 1) * P], c.xn[:, i * KT_ + k, j * P:(j + 1) * P],
                                        c.ident[:, :])
                    t.then_inc(NT("turned"), 1)
            e.wait_ge(loaded, 32)
            e.wait_ge(*NA.at("features", 0))
            project(0)
            with e.Fori(0, BLOCKS - 1) as h:
                project(h + 1)
                rows(h)
                turn_step(h)
            rows(BLOCKS - 1)
            turn_step(BLOCKS - 1)
            e.wait_ge(*D.at("step", 0))
            e.wait_ge(*zs.at("done", BLOCKS - 1))
            for i in range(BLOCKS):
                for k in range(KT_):
                    m = e.matmul(in_ps[i][:, k * P:(k + 1) * P], step[:, i * KT_ + k:i * KT_ + k + 1].broadcast_to([P, P]),
                                 c.ident[:, :], start=True, stop=True)
                m.then_inc(spread, 1)

        @block.vector
        def _(e):
            N.start(e)
            V.start(e)
            CV.start(e)
            D.start(e)
            e.memset(xm[:, :, :, :], 0.0).then_inc(made, 1)
            ln_vector(e, N, NA, n, c.X, 0, lambda: None)
            e.tensor_tensor(c.sel[:, :], c.identb[0:6 * NS, 0:2 * NS], c.identb[0:6 * NS, 2 * NS:4 * NS],
                            ALU.add).then_inc(made, 1)
            e.wait_ge(made, 3)
            e.tensor_scalar(c.neg_a[:, :, :], c.neg_a[:, :, :], -1.0, None, ALU.mult).then_inc(made, 1)
            e.tensor_tensor(c.sel[:, :], c.sel[:, :], c.identb[0:6 * NS, 4 * NS:6 * NS], ALU.add).then_inc(made, 1)
            taps = c.vec["conv_w"]
            def convolve(i):
                for q in range(DC):
                    e.wait_ge(*xs.at("done", i, q))
                    e.wait_ge(*(silus.at("done", i, q - 2) if q >= 2 else silus.at("done", i - 1, DC - 2 + q)))
                    a = by_batch(acc[q % 2][:, :])
                    for k in range(TAPS):
                        x = xm[:, q, :, k:k + T]
                        w = taps[:, q * TAPS + k:q * TAPS + k + 1]
                        if k == 0:
                            e.tensor_scalar(a, x, w, None, ALU.mult).then_inc(CV("conv"), 1)
                        else:
                            e.wait_ge(*CV.at("conv", i, q * TAPS + k - 1))
                            e.scalar_tensor_tensor(a, x, w, a, ALU.mult, ALU.add).then_inc(CV("conv"), 1)

            def split_rows(i):
                at = bass.ds(i * BT, BT)
                e.wait_ge(*rows_kept.at("done", i))
                e.tensor_copy(c.rows3[0:2 * NS, at], ssm[0:2 * NS, :]).then_inc(V("hi"), 1)
                e.wait_ge(*V.at("hi", i))
                e.tensor_tensor(rest[:, :], ssm[0:2 * NS, :], c.rows3[0:2 * NS, at], ALU.subtract).then_inc(V("rest"), 1)
                e.wait_ge(*V.at("rest", i))
                e.tensor_copy(middle[:, :], rest[:, :]).then_inc(V("middle"), 1)
                e.tensor_copy(c.rows3[2 * NS:4 * NS, at], rest[:, :]).then_inc(V("middle2"), 1)
                e.wait_ge(*V.at("middle2", i))
                e.tensor_tensor(c.rows3[4 * NS:6 * NS, at], rest[:, :], middle[:, :], ALU.subtract).then_inc(V("low"), 1)

            convolve(0)
            with e.Fori(0, BLOCKS - 1) as h:
                convolve(h + 1)
                split_rows(h)
            split_rows(BLOCKS - 1)
            e.wait_ge(*lg_kept.at("done", BLOCKS - 1))
            e.scalar_tensor_tensor(na[:, :], lg[:, :], -1.0, lg[:, :], ALU.mult, ALU.min).then_inc(D("na"), 1)
            e.wait_ge(*DA.at("exp", 0))
            e.tensor_scalar(wz[:, :], ez[:, :], 1.0, None, ALU.add).then_inc(D("w"), 1)
            e.wait_ge(*D.at("w", 0))
            e.tensor_scalar(dz[:, :], wz[:, :], 1.0, None, ALU.subtract).then_inc(D("d"), 1)
            e.tensor_scalar(mz[:, :], wz[:, :], 1.0, None, ALU.is_equal).then_inc(D("m"), 1)
            e.wait_ge(*D.at("m", 0))
            e.tensor_tensor(dz[:, :], dz[:, :], mz[:, :], ALU.add).then_inc(D("d1"), 1)
            e.wait_ge(*D.at("d1", 0))
            e.reciprocal(dz[:, :], dz[:, :]).then_inc(D("inv"), 1)
            e.wait_ge(*DA.at("log", 0))
            e.tensor_tensor(lz[:, :], lz[:, :], mz[:, :], ALU.add).then_inc(D("l1"), 1)
            e.wait_ge(*D.at("l1", 0))
            e.tensor_tensor(lz[:, :], lz[:, :], dz[:, :], ALU.mult).then_inc(D("zl"), 1)
            e.wait_ge(*D.at("zl", 0))
            e.tensor_tensor(lz[:, :], lz[:, :], ez[:, :], ALU.mult).then_inc(D("t"), 1)
            e.wait_ge(*D.at("t", 0))
            e.scalar_tensor_tensor(step[:, :], lg[:, :], 0.0, lz[:, :], ALU.max, ALU.add).then_inc(D("step"), 1)

        @block.scalar
        def _(e):
            bias = c.vec["in_b"]

            def keep_x(i):
                e.wait_ge(*CV.at("conv", i - 1))
                for q in range(DC):
                    e.wait_ge(*x_t.at("done", i, q))
                    e.activation(xm[:, q, :, TAPS - 1:], by_batch(in_ps[q][:, :]), ACT.Identity,
                                 bias=bias[:, q:q + 1]).then_inc(xs("done"), 1)

            def keep_conv_and_z(i):
                at = bass.ds(i * BT, BT)
                for q in range(DC):
                    e.wait_ge(*CV.at("conv", i, q * TAPS + TAPS - 1))
                    e.activation(c.xc[:, q, at], acc[q % 2][:, :], ACT.Silu,
                                 bias=c.vec["conv_b"][:, q:q + 1]).then_inc(silus("done"), 1)
                    e.wait_ge(*z_t.at("done", i, q))
                    e.activation(c.sz[:, q, at], in_ps[q][:, :], ACT.Silu,
                                 bias=bias[:, DC + q:DC + q + 1]).then_inc(zs("done"), 1)

            def keep_rows(i):
                e.wait_ge(*rows_t.at("done", i))
                e.wait_ge(*V.at("rest", i - 1))
                e.wait_ge(*lg_t.at("done", i - 1))
                e.activation(ssm[:, :], ssm_ps[0:NR, :], ACT.Identity, bias=c.sm["xp_b"]).then_inc(rows_kept("done"), 1)
                e.wait_ge(*lg_t.at("done", i))
                e.activation(lg[:, bass.ds(i * KT_, KT_)], dt_ps[:, 0:KT_], ACT.Copy).then_inc(lg_kept("done"), 1)

            for each in (NA, DA, xs, silus, zs, rows_kept, lg_kept):
                each.start(e)
            e.activation(c.neg_a[:, :, :].rearrange("p q s -> p (q s)"), c.vec["A_log"], ACT.Exp).then_inc(made, 1)
            ln_scalar_std(e, N, NA, n, 0, c)
            for i in range(BLOCKS):
                for j in range(CJ):
                    e.wait_ge(*NT.at("turned", 0, i * CJ + j))
                    e.activation(n.hT[:, j, i * BT:(i + 1) * BT], n.ps[j][:, :], ACT.Copy).then_inc(NA("features"), 1)
            e.wait_ge(made, 1)
            keep_x(0)
            with e.Fori(0, BLOCKS - 1) as h:
                keep_conv_and_z(h)
                keep_x(h + 1)
                keep_rows(h)
            keep_conv_and_z(BLOCKS - 1)
            keep_rows(BLOCKS - 1)
            e.wait_ge(*D.at("na", 0))
            e.activation(ez[:, :], na[:, :], ACT.Exp).then_inc(DA("exp"), 1)
            e.wait_ge(*D.at("w", 0))
            e.activation(lz[:, :], wz[:, :], ACT.Ln).then_inc(DA("log"), 1)
            for i in range(BLOCKS):
                e.wait_ge(spread, i + 1)
                e.activation(c.dt[:, i * BT:(i + 1) * BT], in_ps[i][:, :], ACT.Copy).then_inc(DA("spread"), 1)


def l1_states(nc, c):
    with ExitStack() as ctx:
        sb, ps, sem = tensors(nc, ctx, "ms")
        y_ps = [ps(f"y_ps{q}") for q in range(DC)]
        b_ps, c_ps = [ps(f"b_ps{u}") for u in range(2)], [ps(f"c_ps{u}") for u in range(2)]
        xdt = sb("xdt", [P, DC, BT])
        dA, u_, h_, hc = ([sb(f"{k}{u}", [P, DC, BT]) for u in range(2)] for k in ("dA", "u", "h", "hc"))
        b_sb = [sb(f"b_sb{u}", [P, BT]) for u in range(2)]
        dt = sb("dt", [P, BT])
        seen = sem("seen")
        S = NS

        def each_state(name, n=1):
            return Steps(sem(name), [("done", n)], 2)

        us, hs, hcs, pool_us, cuts, dAs, b_kept, b_t, c_t, y_t = (
            each_state(k, m) for k, m in (("us", 1), ("hs", 1), ("hcs", 1), ("pool_us", 1), ("cuts", 1), ("dAs", DC),
                                          ("b_kept", 1), ("b_t", 1), ("c_t", 1), ("y_t", 1)))
        dt_kept = Steps(sem("dt_kept"), ["done"])
        B_ = Steps(sem("block"), ["xdt", ("skip", DC), ("gated", DC)])
        block = ctx.enter_context(nc.Block())
        flat = "p q t -> p (q t)"
        VQ = 2
        shape = [P, DC, BT]

        @block.tensor
        def _(e):
            def spread(bank, k, i):
                return e.matmul(bank[:, :], c.sel[:, k:k + 1].broadcast_to([6 * NS, P]), c.rows3[:, bass.ds(i * BT, BT)],
                                start=True, stop=True)

            def spread_b(i, s):
                e.wait_ge(*us.at("done", i * S + s - 2))
                e.wait_ge(*b_kept.at("done", i * S + s - 2))
                spread(b_ps[s % 2], s, i).then_inc(b_t("done"), 1)

            def spread_c(i, s):
                e.wait_ge(*hcs.at("done", i * S + s - 2))
                spread(c_ps[s % 2], NS + s, i).then_inc(c_t("done"), 1)

            for each in (b_t, c_t, y_t):
                each.start(e)

            def add_state(i, s):
                e.wait_ge(*hcs.at("done", i * S + s))
                for q in range(DC):
                    m = e.matmul(y_ps[q][:, :], c.ident[:, :], hc[s % 2][:, q, :], start=(s == 0), stop=(s == NS - 1))
                m.then_inc(y_t("done"), 1)

            with e.Fori(0, BLOCKS) as i:
                spread_b(i, 0)
                spread_c(i, 0)
                spread_b(i, 1)
                spread_c(i, 1)
                e.wait_ge(*B_.at("skip", i - 1))
                for s in range(1, NS):
                    if s + 1 < NS:
                        spread_b(i, s + 1)
                        spread_c(i, s + 1)
                    add_state(i, s - 1)
                add_state(i, NS - 1)

        @block.gpsimd
        def _(e):
            pool_us.start(e)
            cuts.start(e)
            with e.Fori(0, BLOCKS) as i:
                for s in range(NS):
                    t = i * S + s
                    if s == 0:
                        e.wait_ge(*B_.at("xdt", i))
                    e.wait_ge(*b_kept.at("done", t))
                    e.wait_ge(*hs.at("done", t - 1))
                    e.tensor_tensor(u_[s % 2][:, VQ:, :], xdt[:, VQ:, :], over(b_sb[s % 2][:, :], [P, DC - VQ, BT], 1),
                                    ALU.mult).then_inc(pool_us("done"), 1)
                    e.wait_ge(*dAs.at("done", t))
                    e.sem_inc(seen, 1)
                    e.memset(by_batch(dA[s % 2][:, :, :].rearrange(flat))[:, :, 0:1], 0.0).then_inc(cuts("done"), 1)

        @block.vector
        def _(e):
            def start_state(i, s):
                t = i * S + s
                e.wait_ge(*b_kept.at("done", t))
                e.wait_ge(*hs.at("done", t - 2))
                e.tensor_tensor(u_[s % 2][:, 0:VQ, :], xdt[:, 0:VQ, :], over(b_ps[s % 2][:, :], [P, VQ, BT], 1),
                                ALU.mult).then_inc(us("done"), 1)

            def scan(i, s):
                t = i * S + s
                e.wait_ge(*us.at("done", t))
                e.wait_ge(*pool_us.at("done", t))
                e.wait_ge(*cuts.at("done", t))
                e.wait_ge(*hcs.at("done", t - 2))
                e.tensor_tensor_scan(h_[s % 2][:, :, :].rearrange(flat), dA[s % 2][:, :, :].rearrange(flat),
                                     u_[s % 2][:, :, :].rearrange(flat), 0.0, ALU.mult, ALU.add).then_inc(hs("done"), 1)

            def weigh(i, s):
                t = i * S + s
                e.wait_ge(*hs.at("done", t))
                e.wait_ge(*c_t.at("done", t))
                e.wait_ge(*y_t.at("done", t - 2))
                e.tensor_tensor(hc[s % 2][:, :, :], h_[s % 2][:, :, :], over(c_ps[s % 2][:, :], shape, 1),
                                ALU.mult).then_inc(hcs("done"), 1)

            for each in (us, hs, hcs, B_):
                each.start(e)
            with e.Fori(0, BLOCKS) as i:
                at = bass.ds(i * BT, BT)
                e.wait_ge(*us.at("done", i * S - 1))
                e.wait_ge(*pool_us.at("done", i * S - 1))
                e.tensor_tensor(xdt[:, :, :], c.xc[:, :, at], over(c.dt[:, at], shape, 1), ALU.mult).then_inc(B_("xdt"), 1)
                e.wait_ge(*B_.at("xdt", i))
                start_state(i, 0)
                scan(i, 0)
                for s in range(1, NS):
                    start_state(i, s)
                    weigh(i, s - 1)
                    scan(i, s)
                weigh(i, NS - 1)
                e.wait_ge(*y_t.at("done", i * S + NS - 1))
                for q in range(DC):
                    xc = c.xc[:, q, at]
                    e.scalar_tensor_tensor(xc, xc, c.vec["D"][:, q:q + 1], y_ps[q][:, :], ALU.mult,
                                           ALU.add).then_inc(B_("skip"), 1)
                for q in range(DC):
                    e.wait_ge(*B_.at("skip", i, q))
                    e.tensor_tensor(c.sz[:, q, at], c.xc[:, q, at], c.sz[:, q, at], ALU.mult).then_inc(B_("gated"), 1)

        @block.scalar
        def _(e):
            dAs.start(e)
            b_kept.start(e)
            dt_kept.start(e)
            with e.Fori(0, BLOCKS) as i:
                e.wait_ge(*dAs.at("done", i * S - 1))
                e.activation(dt[:, :], c.dt[:, bass.ds(i * BT, BT)], ACT.Copy).then_inc(dt_kept("done"), 1)
                e.wait_ge(*dt_kept.at("done", i))
                for s in range(NS):
                    t = i * S + s
                    e.wait_ge(*b_t.at("done", t))
                    e.wait_ge(*pool_us.at("done", t - 2))
                    e.activation(b_sb[s % 2][:, :], b_ps[s % 2][:, :], ACT.Copy).then_inc(b_kept("done"), 1)
                    e.wait_ge(*hs.at("done", t - 2))
                    for q in range(DC):
                        e.activation(dA[s % 2][:, q, :], dt[:, :], ACT.Exp,
                                     scale=c.neg_a[:, q, s:s + 1]).then_inc(dAs("done"), 1)


def l1_state_space(nc, c):
    with ExitStack() as ctx:
        sb, ps, sem = tensors(nc, ctx, "my")
        y_ps = [ps(f"y_ps{q}") for q in range(8)]
        n = Norm(sb, ps, y_ps[:2], "ln2", tiles=TILES)
        r = n.src = sb("r", [P, TILES, C])
        V = Steps(sem("vector"), TILES // 2 * ["r1", ("stats", 2)] + [(k[0], TILES) if isinstance(k, tuple) else k for k in LN_V[1:]]
                  + [(k, BLOCKS) for k in ("gain", "shift", "added")])
        A = Steps(sem("scalar"), ["std"])
        T_ = Steps(sem("tensor"), [("out", TILES // 2)])
        block = ctx.enter_context(nc.Block())

        @block.tensor
        def _(e):
            T_.start(e)
            for b in range(TILES // 2):
                for k in (2 * b, 2 * b + 1):
                    out = y_ps[b][:, (k % 2) * C:(k % 2 + 1) * C]
                    for q in range(DC):
                        e.matmul(out, c.sz[:, q, k * P:(k + 1) * P], c.w_out[:, q, :], start=(q == 0), stop=False)
                    m = e.matmul(out, c.ones[0:1, 0:P], c.row["out_b"][0:1, :], start=False, stop=True)
                m.then_inc(T_("out"), 1)

        @block.vector
        def _(e):
            V.start(e)
            for b in range(TILES // 2):
                e.wait_ge(*T_.at("out", 0, b))
                e.tensor_tensor(r[:, 2 * b:2 * b + 2, :], c.xn[:, 2 * b:2 * b + 2, :],
                                y_ps[b][:, :].rearrange("p (k f) -> p k f", k=2), ALU.add).then_inc(V("r1"), 1)
                e.wait_ge(*V.at("r1", 0, b))
                for k in (2 * b, 2 * b + 1):
                    e.bn_stats(n.stats[:, k, :], r[:, k, :]).then_inc(V("stats"), 1)
            ln_vector(e, V, A, n, None, 0, lambda: None, stats=False)
            e.wait_ge(*V.at("norm", 0))
            rows = [P, KT_, C]
            blocks = [slice(i * KT_, (i + 1) * KT_) for i in range(BLOCKS)]
            for at in blocks:
                y = n.xn[:, at, :]
                e.tensor_tensor(y, y, over(c.row["m_gamma"], rows, 1), ALU.mult).then_inc(V("gain"), 1)
            for i, at in enumerate(blocks):
                y = n.xn[:, at, :]
                e.wait_ge(*V.at("gain", 0, i))
                e.tensor_tensor(y, y, over(c.row["m_beta"], rows, 1), ALU.add).then_inc(V("shift"), 1)
            for i, at in enumerate(blocks):
                e.wait_ge(*V.at("shift", 0, i))
                e.tensor_tensor(c.X[:, at, :], c.X[:, at, :], n.xn[:, at, :], ALU.add).then_inc(V("added"), 1)

        @block.scalar
        def _(e):
            A.start(e)
            ln_scalar_std(e, V, A, n, 0, c)



def l1_gates(nc, c):
    with ExitStack() as ctx:
        sb, ps, sem = tensors(nc, ctx, "fg")
        wg = sb("wg", [P, CJ, E])
        n = Norm(sb, ps, tiles=TILES)
        lg, sq = sb("lg", [P, TILES, E]), sb("sq", [P, TILES, E])
        ms, big, tot = sb("ms", [P, TILES]), sb("big", [P, TILES]), sb("tot", [P, TILES])
        g_ps = ps("g_ps")
        g_loaded = sem("g_loaded")
        V = Steps(sem("vector"), ALL_V + ["logits", "square", "mean_sq", "flip", "scaled", "weighted", "big", "less", "sum",
                                          "g", "g_eps", "g_inv", "norm_g"])
        A = Steps(sem("scalar"), ALL_A + ["rms", "exp"])
        T_ = Steps(sem("tensor"), ALL_T + ["logits"])
        G = Steps(sem("pool"), ALL_G)
        block = ctx.enter_context(nc.Block())
        shape = [P, TILES, E]
        flat = "p k e -> p (k e)"

        @block.sync
        def _(e):
            e.dma_start(wg[:, :, :], c.d["l1_wg"]).then_inc(g_loaded, 16)
            for q in range(E):
                e.dma_start(c.w1[q][:, :, :], c.d["l1_w1"][q]).then_inc(c.w_loaded[q], 16)
                e.dma_start(c.w2[q][:, :, :], c.d["l1_w2"][q]).then_inc(c.w_loaded[q], 16)

        @block.tensor
        def _(e):
            T_.start(e)
            all_tensor(e, V, A, T_, n, c)
            e.wait_ge(g_loaded, 16)
            for k in range(TILES):
                if k % KT_ == 0:
                    e.wait_ge(*A.at("features", 0, k // KT_ * CJ + CJ - 1))
                for j in range(CJ):
                    m = e.matmul(g_ps[:, k * E:(k + 1) * E], n.hT[:, j, k * P:(k + 1) * P], wg[:, j, :],
                                 start=(j == 0), stop=(j == CJ - 1))
            m.then_inc(T_("logits"), 1)

        @block.gpsimd
        def _(e):
            G.start(e)
            all_pool(e, A, G, n, c.parts)

        @block.scalar
        def _(e):
            A.start(e)
            ln_scalar_std(e, V, A, n, 0, c)
            all_scalar(e, T_, A, n, c.parts)
            e.wait_ge(*V.at("mean_sq", 0))
            e.activation(ms[:, :], ms[:, :], ACT.Sqrt, scale=1.0 / E, bias=c.eps[:, 3:4]).then_inc(A("rms"), 1)
            e.wait_ge(*V.at("less", 0))
            e.activation(sq[:, :, :].rearrange(flat), lg[:, :, :].rearrange(flat), ACT.Exp,
                         scale=2.0).then_inc(A("exp"), 1)

        @block.vector
        def _(e):
            V.start(e)
            ln_vector(e, V, A, n, c.X, 0, lambda: None)
            e.wait_ge(*T_.at("logits", 0))
            e.tensor_tensor(lg[:, :, :], g_ps[:, 0:TILES * E].rearrange("p (k e) -> p k e", k=TILES),
                            over(c.row["gate_b"], shape, 1), ALU.add).then_inc(V("logits"), 1)
            e.wait_ge(*V.at("logits", 0))
            e.tensor_tensor(sq[:, :, :], lg[:, :, :], lg[:, :, :], ALU.mult).then_inc(V("square"), 1)
            e.wait_ge(*V.at("square", 0))
            e.tensor_reduce(ms[:, :], sq[:, :, :], AX.X, ALU.add).then_inc(V("mean_sq"), 1)
            e.wait_ge(*A.at("rms", 0))
            e.reciprocal(ms[:, :], ms[:, :]).then_inc(V("flip"), 1)
            e.wait_ge(*V.at("flip", 0))
            e.tensor_tensor(lg[:, :, :], lg[:, :, :], over(ms[:, :], shape, 2), ALU.mult).then_inc(V("scaled"), 1)
            e.wait_ge(*V.at("scaled", 0))
            e.tensor_tensor(lg[:, :, :], lg[:, :, :], over(c.row["rms_w"], shape, 1), ALU.mult).then_inc(V("weighted"), 1)
            e.wait_ge(*V.at("weighted", 0))
            e.tensor_reduce(big[:, :], lg[:, :, :], AX.X, ALU.max).then_inc(V("big"), 1)
            e.wait_ge(*V.at("big", 0))
            e.tensor_tensor(lg[:, :, :], lg[:, :, :], over(big[:, :], shape, 2), ALU.subtract).then_inc(V("less"), 1)
            e.wait_ge(*A.at("exp", 0))
            e.tensor_reduce(tot[:, :], sq[:, :, :], AX.X, ALU.add).then_inc(V("sum"), 1)
            e.wait_ge(*V.at("sum", 0))
            e.reciprocal(tot[:, :], tot[:, :]).then_inc(V("g"), 1)
            e.wait_ge(*V.at("g", 0))
            e.tensor_scalar(big[:, :], tot[:, :], 1e-6, None, ALU.add).then_inc(V("g_eps"), 1)
            e.wait_ge(*V.at("g_eps", 0))
            e.reciprocal(big[:, :], big[:, :]).then_inc(V("g_inv"), 1)
            e.wait_ge(*V.at("g_inv", 0))
            e.scalar_tensor_tensor(c.norm_g[:, :], tot[:, :], 1.0 / W_SCALE, big[:, :], ALU.mult,
                                   ALU.mult).then_inc(V("norm_g"), 1)


def l1_experts(nc, c):
    with ExitStack() as ctx:
        sb, ps, sem = tensors(nc, ctx, "fe")
        w1 = [[sb(f"w1_{u}{x}", [P, CJ, FH], FP16) for x in range(2)] for u in range(E)]
        w2 = [[sb(f"w2_{u}{x}", [P, FJ, C], FP16) for x in range(2)] for u in range(E)]
        scale = sb("scale", [E, P])
        g = [sb(f"g{u}", [P, BT]) for u in range(2)]
        hid = [[sb(f"hid{u}{x}", [P, FJ, BT], FP16) for x in range(2)] for u in range(2)]
        h_ps = [ps(f"h_ps{u}") for u in range(4)]
        y_ps = [ps(f"y_ps{k}") for k in range(KT_)]
        N = E * FJ
        made = sem("made")
        V = Steps(sem("vector"), N * ["rounded", "rest"] + [("added", KT_)])
        A = Steps(sem("scalar"), [("gelu", N)])
        T_ = Steps(sem("tensor"), [("hidden", FJ)] + [("hidden", FJ), "y"] * (E - 1) + ["y"])
        G = Steps(sem("pool"), E * [f"{w}_{step}" for w in ("w1", "w2") for step in ("scaled", "rounded", "rest")])
        block = ctx.enter_context(nc.Block())
        products = ((0, 0), (0, 1), (1, 0))

        @block.gpsimd
        def _(e):
            G.start(e)
            for q in range(E):
                e.wait_ge(c.w_loaded[q], 32)
                for name, w, parts in (("w1", c.w1[q][:, :, :], w1[q]), ("w2", c.w2[q][:, :, :], w2[q])):
                    e.tensor_scalar(w, w, W_SCALE, None, ALU.mult).then_inc(G(f"{name}_scaled"), 1)
                    e.wait_ge(*G.at(f"{name}_scaled", 0, q))
                    e.tensor_copy(parts[0][:, :, :], w).then_inc(G(f"{name}_rounded"), 1)
                    e.wait_ge(*G.at(f"{name}_rounded", 0, q))
                    e.tensor_tensor(parts[1][:, :, :], w, parts[0][:, :, :], ALU.subtract).then_inc(G(f"{name}_rest"), 1)

        @block.tensor
        def _(e):
            T_.start(e)
            e.wait_ge(made, 1)

            def hidden(i, q):
                e.wait_ge(*G.at("w2_rest", 0, q))
                for f in range(FJ):
                    at = q * FJ + f
                    e.wait_ge(*(A.at("gelu", i, at - 4) if at >= 4 else A.at("gelu", i - 1, N - 4 + at)))
                    for j in range(CJ):
                        for w, x in products:
                            m = e.matmul(h_ps[f][:, :], w1[q][w][:, j, f * P:(f + 1) * P],
                                         c.parts[x][:, j, bass.ds(i * BT, BT)], start=(j == 0 and w + x == 0),
                                         stop=(j == CJ - 1 and w == 1))
                    m.then_inc(T_("hidden"), 1)

            def combine(i, q):
                e.wait_ge(*V.at("rest", i, q * FJ + FJ - 1))
                for k in range(KT_):
                    for f in range(FJ):
                        for x, w in products:
                            m = e.matmul(y_ps[k][:, 0:C], hid[q % 2][x][:, f, k * P:(k + 1) * P], w2[q][w][:, f, :],
                                         start=False, stop=(q == E - 1 and f == FJ - 1 and x == 1))
                m.then_inc(T_("y"), 1)

            with e.Fori(0, BLOCKS) as i:
                hidden(i, 0)
                for k in range(KT_):
                    e.wait_ge(*V.at("added", i - 1, k))
                    e.matmul(y_ps[k][:, 0:C], scale[:, :], c.sm["b2"][0:E, :], start=True, stop=False)
                for q in range(1, E):
                    hidden(i, q)
                    combine(i, q - 1)
                combine(i, E - 1)

        @block.scalar
        def _(e):
            A.start(e)
            with e.Fori(0, BLOCKS) as i:
                for q in range(E):
                    for f in range(FJ):
                        at = q * FJ + f
                        e.wait_ge(*T_.at("hidden", i, at))
                        e.wait_ge(*(V.at("rest", i, at - 2) if at >= 2 else V.at("rest", i - 1, N - 2 + at)))
                        e.activation(g[f % 2][:, :], h_ps[f][:, :], ACT.Gelu, scale=1.0 / W_SCALE,
                                     bias=c.vec["b1"][:, at:at + 1]).then_inc(A("gelu"), 1)

        @block.vector
        def _(e):
            V.start(e)
            e.memset(scale[:, :], W_SCALE).then_inc(made, 1)
            with e.Fori(0, BLOCKS) as i:
                for q in range(E):
                    for f in range(FJ):
                        at = q * FJ + f
                        part = hid[q % 2]
                        e.wait_ge(*A.at("gelu", i, at))
                        if f == 0:
                            e.wait_ge(*(T_.at("y", i, q - 2) if q >= 2 else T_.at("y", i - 1, E - 2 + q)))
                        e.tensor_copy(part[0][:, f, :], g[f % 2][:, :]).then_inc(V("rounded"), 1)
                        e.wait_ge(*V.at("rounded", i, at))
                        e.tensor_tensor(part[1][:, f, :], g[f % 2][:, :], part[0][:, f, :],
                                        ALU.subtract).then_inc(V("rest"), 1)
                e.wait_ge(*T_.at("y", i))
                for k in range(KT_):
                    x = c.X[:, i * KT_ + k, :]
                    e.scalar_tensor_tensor(x, y_ps[k][:, 0:C], c.norm_g[:, bass.ds(i * KT_ + k, 1)], x, ALU.mult,
                                           ALU.add).then_inc(V("added"), 1)



VECS = [("bq", 2), ("bk", 2), ("ln1_g", 2), ("ln1_b", 2), ("ln2_g", 2), ("ln2_b", 2), ("decay", 2), ("first", 2),
        ("tm_k", 2), ("tm_v", 2), ("tm_r", 2), ("cm_k", 2), ("cm_r", 2), ("in_b", 8), ("conv_w", 16), ("conv_b", 4),
        ("D", 4), ("A_log", 64), ("b1", 32)]
ROWS = [("bv", C), ("x_gamma", C), ("x_beta", C), ("out_b", C), ("m_gamma", C), ("m_beta", C), ("gate_b", E),
        ("rms_w", E), ("dt_b", 1)]
SMALL = [("be", C), ("b2", C), ("xp_b", 1)]


def named(tensor, table):
    out, at = {}, 0
    for name, n in table:
        out[name] = tensor[:, at:at + n]
        at += n
    return out, at


def build(nc, d, stages=range(1, 7)):
    c = Chip()
    c.d = d
    with ExitStack() as ctx:
        sb, ps, sem = tensors(nc, ctx, "c")
        c.X = sb("x", [P, TILES, C])
        c.vecs = sb("vecs", [P, sum(n for _, n in VECS)])
        c.rows = sb("rows", [P, sum(n for _, n in ROWS)])
        c.small = sb("small", [33, sum(n for _, n in SMALL)])
        c.vec, _ = named(c.vecs, VECS)
        c.row, _ = named(c.rows, ROWS)
        c.sm, _ = named(c.small, SMALL)
        c.consts = sb("consts", [P, P + 20])
        c.ident = c.consts[:, 0:P]
        c.own = c.consts[:, P:P + 4]
        c.group = c.consts[:, P + 4:P + 12]
        c.iota = c.consts[:, P + 12:P + 20]
        c.identb = sb("identb", [P, P], BF16)
        c.identh = sb("identh", [P, P], FP16)
        c.eps = sb("eps", [P, 4])
        c.ones = sb("ones", [P, P])
        c.c_max = sb("c_max", [P, 2 * B])
        c.c_ss = sb("c_ss", [P, 2 * B])
        load_all(nc, c)
        with ExitStack() as mid:
            c.cq = mid.enter_context(nc.sbuf_tensor("c_cq", [P, 2 * B, C], BF16))
            if 1 in stages:
                with ExitStack() as one:
                    c.qkT = one.enter_context(nc.sbuf_tensor("c_qkT", [P, CJ, B * T], FP32))
                    c.qc = one.enter_context(nc.sbuf_tensor("c_qc", [P, TILES], FP32))
                    l0_queries(nc, c)
                    l0_attention(nc, c)
            if 2 in stages:
                with ExitStack() as two:
                    c.XI = two.enter_context(nc.sbuf_tensor("c_XI", [P, TILES, C], FP32))
                    l0_time_mix(nc, c)
                    l0_channel_mix(nc, c)
            if 3 in stages:
                with ExitStack() as three:
                    def sb3(name, shape, dt=FP32):
                        return three.enter_context(nc.sbuf_tensor(f"c_{name}", shape, dt))

                    c.parts = [sb3(f"parts{x}", [P, CJ, B * T], FP16) for x in range(2)]
                    c.we = [sb3(f"we{x}", [P, CJ, E * C], FP16) for x in range(2)]
                    c.gate, c.gate_t = sb3("gate", [P, TILES, E]), sb3("gate_t", [E, B * T])
                    l0_gates(nc, c)
                    l0_experts(nc, c)
            if 4 in stages:
                with ExitStack() as four:
                    def sb4(name, shape, dt=FP32):
                        return four.enter_context(nc.sbuf_tensor(f"c_{name}", shape, dt))

                    c.wq, c.wkv, c.wo = (sb4(k, [P, CJ, C], BF16) for k in ("wq", "wkv", "wo"))
                    c.wf = sb4("wf", [P, 4])
                    c.kf, c.vf = sb4("kf", [P, 2 * B]), sb4("vf", [P, 2 * B])
                    c.k_last = sb4("k_last", [P, 2, B], FP16)
                    c.v_last = sb4("v_last", [4, BQ, 4, P // 2])
                    c.mask = sb4("mask", [P, 4])
                    c.qT = sb4("qT", [P, 8, B * T], FP16)
                    l1_prepare(nc, c)
                    l1_queries(nc, c)
                    c.XA = sb4("XA", [P, KT_, C])
                    with ExitStack() as kv:
                        c.kT = kv.enter_context(nc.sbuf_tensor("c_kT", [P, BQ, 2, M], FP16))
                        c.v = kv.enter_context(nc.sbuf_tensor("c_v", [P, BQ, 2, P], FP32))
                        shared = Shared(nc, kv, "keys"), Shared(nc, kv, "att"), Shared(nc, kv, "out")
                        for quarter in range(B // BQ):
                            l1_keys(nc, c, shared[0], quarter)
                            l1_attention(nc, c, shared[1], quarter)
                            l1_project(nc, c, shared[2], quarter)
        if 5 in stages:
            with ExitStack() as five:
                def sb5(name, shape, dt=FP32):
                    return five.enter_context(nc.sbuf_tensor(f"c_{name}", shape, dt))

                c.xn = sb5("xn", [P, TILES, C])
                c.xc, c.sz, c.dt = sb5("xc", [P, DC, B * T]), sb5("sz", [P, DC, B * T]), sb5("dt", [P, B * T])
                c.rows3, c.sel = sb5("rows3", [6 * NS, B * T], BF16), sb5("sel", [6 * NS, 2 * NS], BF16)
                c.neg_a = sb5("neg_a", [P, DC, NS])
                c.w_out = sb5("w_out", [P, DC, C])
                l1_inner(nc, c)
                l1_states(nc, c)
                l1_state_space(nc, c)
        if 6 in stages:
            with ExitStack() as six:
                def sb6(name, shape, dt=FP32):
                    return six.enter_context(nc.sbuf_tensor(f"c_{name}", shape, dt))

                c.w1 = [sb6(f"w1_{q}", [P, CJ, FH]) for q in range(E)]
                c.w2 = [sb6(f"w2_{q}", [P, FJ, C]) for q in range(E)]
                c.w_loaded = [six.enter_context(nc.semaphore(f"c_w_loaded{q}")) for q in range(E)]
                c.parts = [sb6(f"f_parts{x}", [P, CJ, B * T], FP16) for x in range(2)]
                c.norm_g = sb6("norm_g", [P, TILES])
                l1_gates(nc, c)
                l1_experts(nc, c)
        store(nc, c)


def store(nc, c):
    with ExitStack() as ctx:
        sb, ps, sem = tensors(nc, ctx, "st")
        stored = sem("stored")
        block = ctx.enter_context(nc.Block())

        @block.sync
        def _(e):
            e.dma_start(c.d["out"], c.X[:, :, :]).then_inc(stored, 16)
            e.wait_ge(stored, 16)


def layout(i):
    f = {k: np.asarray(v) for k, v in i.items()}

    def feat(w):
        w = w.T
        return np.ascontiguousarray(w.reshape(-1, P, w.shape[1]).transpose(1, 0, 2))

    def nat(w):
        return np.ascontiguousarray(w.reshape(-1, P, w.shape[1]).transpose(1, 0, 2))

    def vec(v):
        return v.reshape(-1, P).T

    ctxm = f["ctx_1024"]
    a = {}
    a["x"] = f["x"].reshape(TILES, P, C).transpose(1, 0, 2)
    main, last = ctxm[:, :2 * P, :], ctxm[:, 2 * P, :]
    a["ctx_n"] = main.reshape(TILES, BPT, 2, P, C).transpose(0, 3, 1, 2, 4)
    a["ctx_t"] = main.reshape(TILES, BPT, 2 * P, CJ, P).transpose(0, 4, 1, 3, 2)
    a["ctx_last_n"] = last.reshape(TILES, BPT, C).transpose(1, 0, 2)
    a["ctx_last_t"] = last.reshape(B, CJ, P).transpose(2, 1, 0)
    a["mask"] = f["mask_SxS2_ik1"]
    a["l0_wq"], a["l0_wk"], a["l0_wv"] = nat(f["L0_xattn_Wq"]), nat(f["L0_xattn_Wk"]), feat(f["L0_xattn_Wv"])
    for k, n in (("km", "Wk"), ("vm", "Wv"), ("rm", "Wr"), ("om", "Wo"), ("ck", "Wck"), ("cr", "Wcr"), ("cv", "Wcv")):
        a[f"l0_w{k}"] = feat(f[f"L0_attn_{n}"])
    a["l0_wg"] = nat(f["L0_ffn_Wg"])
    a["l0_we"] = f["L0_ffn_We"].reshape(E, CJ, P, C).transpose(2, 1, 0, 3).reshape(P, CJ, E * C)
    a["l1_wg"] = feat(f["L1_ffn_gate_w"])
    a["l1_w1"] = f["L1_ffn_w1"].reshape(E, CJ, P, FH).transpose(0, 2, 1, 3)
    a["l1_w2"] = f["L1_ffn_w2"].reshape(E, FH // P, P, C).transpose(0, 2, 1, 3)
    a["l1_w_in"], a["l1_w_x"] = feat(f["L1_attn_in_proj_w"]), feat(f["L1_attn_x_proj_w"])
    a["l1_w_out"] = feat(f["L1_attn_out_proj_w"])
    wq = f["L1_xattn_wq"].reshape(KVH, 2, HD, C).transpose(1, 0, 2, 3).reshape(C, C)
    a["l1_wq"], a["l1_wk"], a["l1_wv"], a["l1_wo"] = (feat(w) for w in (wq, f["L1_xattn_wk"], f["L1_xattn_wv"],
                                                                         f["L1_xattn_wo"]))
    a["ctx_last"] = last
    v = {"bq": f["L0_xattn_bq"], "bk": f["L0_xattn_bk"], "ln1_g": f["L0_attn_ln1_g"], "ln1_b": f["L0_attn_ln1_b"],
         "ln2_g": f["L0_attn_ln2_g"], "ln2_b": f["L0_attn_ln2_b"], "decay": f["L0_attn_time_decay"],
         "first": f["L0_attn_time_first"], "tm_k": f["L0_attn_tm_k"], "tm_v": f["L0_attn_tm_v"],
         "tm_r": f["L0_attn_tm_r"], "cm_k": f["L0_attn_cm_k"], "cm_r": f["L0_attn_cm_r"],
         "in_b": f["L1_attn_in_proj_b"], "conv_b": f["L1_attn_conv_b"], "D": f["L1_attn_D"]}
    v = {k: vec(x.reshape(-1)) for k, x in v.items()}
    v["conv_w"] = f["L1_attn_conv_w"].reshape(DC, P, TAPS).transpose(1, 0, 2).reshape(P, -1)
    v["A_log"] = f["L1_attn_A_log"].reshape(DC, P, NS).transpose(1, 0, 2).reshape(P, -1)
    v["b1"] = f["L1_ffn_b1"].reshape(E, FH // P, P).transpose(2, 0, 1).reshape(P, -1)
    a["vecs"] = np.concatenate([v[n] for n, _ in VECS], 1)
    r = {"bv": f["L0_xattn_bv"], "x_gamma": f["L1_xattn_ln_gamma"], "x_beta": f["L1_xattn_ln_beta"],
         "out_b": f["L1_attn_out_proj_b"], "m_gamma": f["L1_attn_ln_gamma"], "m_beta": f["L1_attn_ln_beta"],
         "gate_b": f["L1_ffn_gate_b"], "rms_w": f["L1_ffn_rms_w"],
         "dt_b": f["L1_attn_x_proj_b"][2 * NS:]}
    a["rows"] = np.broadcast_to(np.concatenate([r[n] for n, _ in ROWS])[None], (P, sum(n for _, n in ROWS)))
    small = np.zeros((33, sum(n for _, n in SMALL)), np.float32)
    small[:E, 0:C], small[:E, C:2 * C], small[:, 2 * C] = f["L0_ffn_be"], f["L1_ffn_b2"], f["L1_attn_x_proj_b"]
    a["small"] = small
    p = np.arange(P)[:, None]
    a["ident"] = np.concatenate([np.eye(P), p // T == np.arange(4), p // HD == np.arange(8),
                                 np.broadcast_to(np.arange(8), (P, 8))], 1).astype(np.float32)
    return {k: np.ascontiguousarray(x) for k, x in a.items()}


def kernel(**inputs):
    from concourse import bacc
    from concourse.bass_utils import run_bass_kernel_spmd

    nc = bacc.Bacc("TRN2", target_bir_lowering=False, num_devices=1)
    arrays = {f"in_{k}": a for k, a in layout(inputs).items()}
    d = {k[3:]: nc.dram_tensor(k, a.shape, mybir.dt.from_np(a.dtype), kind="ExternalInput").ap()
         for k, a in arrays.items()}
    out = nc.dram_tensor("out", (TILES, P, C), FP32, kind="ExternalOutput").ap()
    d["bounce"] = nc.dram_tensor("bounce", (B, P), FP32, kind="Internal").ap()
    d["out"] = out.rearrange("t p c -> p t c")
    build(nc, d)
    r = run_bass_kernel_spmd(nc, [arrays], core_ids=[0])
    return r.results[0]["out"].reshape(B, T, C)
```
